# Optimizing a Trainium2 kernel written in Bass

```python
import numpy as np
import jax
import jax.numpy as jnp

def _softmax(x, axis=-1):
    return jax.nn.softmax(x, axis=axis)

def _gelu(x):
    return jax.nn.gelu(x, approximate=True)

def _silu(x):
    return jax.nn.silu(x)

def _sigmoid(x):
    return jax.nn.sigmoid(x)

def _layernorm(x, axis=-1, eps=1e-05):
    m = jnp.mean(x, axis=axis, keepdims=True)
    v = jnp.var(x, axis=axis, keepdims=True)
    return (x - m) / jnp.sqrt(v + eps)

def _scatter_add(tgt, idx, src, axis=0):
    return tgt.at[idx].add(src)

def _segment_sum(src, seg, n):
    return jax.ops.segment_sum(src, seg, n)
kernel_name = 'mk_gps_d4_gnn_r16_dfd497'

def setup_inputs(seed: int=0):
    np.random.seed(seed)
    _w = jnp.asarray

    def _rec_inputs():
        import jax
        import jax.numpy as jnp
        _gk = jax.random.key(seed)
        x = -0.0001126 + 1 * jax.random.normal(jax.random.fold_in(_gk, 1), (625, 768), jnp.float32)
        src = jax.random.randint(jax.random.fold_in(_gk, 2), (20000,), 0, 625, jnp.int32)
        dst = jnp.minimum((625 * jax.random.uniform(jax.random.fold_in(_gk, 3), (20000,)) ** 2.0).astype(jnp.int32), 9999)
        _o = jnp.argsort(dst, stable=True)
        src = src[_o]
        dst = dst[_o]
        edge_weight1 = -0.00472126 + 0.997171 * jax.random.normal(jax.random.fold_in(_gk, 13), (20000, 1), jnp.float32)
        return (x, src, dst, edge_weight1)
    x, src, dst, edge_weight1 = _rec_inputs()

    def _L0_gnn_setup():
        import jax, jax.numpy as jnp
        import numpy as np
        N, E, D, H, C = (625, 6250, 768, 4, 192)
        NEG_SLOPE = 0.2

        def gat_conv(x, src, dst, W, a_src, a_dst, b):
            h = (x @ W).reshape(N, H, C)
            as_n = (h * a_src).sum(-1)
            ad_n = (h * a_dst).sum(-1)
            e = jax.nn.leaky_relu(as_n[src] + ad_n[dst], NEG_SLOPE)
            m = jax.ops.segment_max(e, dst, num_segments=N)
            p = jnp.exp(e - m[dst])
            s = jax.ops.segment_sum(p, dst, num_segments=N)
            alpha = p / (s[dst] + 1e-16)
            out = jax.ops.segment_sum(alpha[:, :, None] * h[src], dst, num_segments=N)
            return out.reshape(N, H * C) + b
        key = jax.random.key(seed)
        ks = jax.random.split(key, 16)
        w = lambda k, shape: jax.random.normal(k, shape, dtype=jnp.float32) * 0.02
        inp = {}
        inp['x'] = jax.random.normal(ks[0], (N, D), dtype=jnp.float32)
        inp['edge_index'] = jax.random.randint(ks[1], (2, E), 0, N, dtype=jnp.int32)
        inp['batch'] = jnp.zeros((N,), dtype=jnp.int32)
        inp['edge_attr'] = jax.random.normal(ks[2], (E, 1), dtype=jnp.float32)
        inp['W_ah'] = w(ks[3], (D, D))
        inp['b_ah'] = jnp.zeros((D,), jnp.float32)
        for i in range(3):
            inp[f'W{i}'] = w(ks[4 + 3 * i], (D, H * C))
            inp[f'a_src{i}'] = w(ks[5 + 3 * i], (H, C))
            inp[f'a_dst{i}'] = w(ks[6 + 3 * i], (H, C))
            inp[f'b{i}'] = jnp.zeros((H * C,), jnp.float32)
        inp['W_out'] = w(ks[13], (3 * D, D))
        inp['b_out'] = jnp.zeros((D,), jnp.float32)
        return inp
    _L0_gnn_all = _L0_gnn_setup()
    _L0_gnn_in = {k: v for k, v in _L0_gnn_all.items() if k in ('W_ah', 'b_ah', 'W0', 'a_src0', 'a_dst0', 'b0', 'W1', 'a_src1', 'a_dst1', 'b1', 'W2', 'a_src2', 'a_dst2', 'b2', 'W_out', 'b_out')}
    del _L0_gnn_all

    def _L0_mix_setup():
        import jax, jax.numpy as jnp
        import numpy as np
        DIM = 768
        HEADS = 12
        DIM_HEAD = 64
        INNER = HEADS * DIM_HEAD
        EPS = 1e-05

        def _layernorm(t, gamma, beta):
            mu = jnp.mean(t, axis=-1, keepdims=True)
            var = jnp.var(t, axis=-1, keepdims=True)
            return (t - mu) * jax.lax.rsqrt(var + EPS) * gamma + beta
        key = jax.random.key(seed)
        ks = jax.random.split(key, 5)
        x = jax.random.normal(ks[0], (8, 256, DIM), dtype=jnp.float32)
        w_map = jax.random.normal(ks[1], (3 * INNER, DIM), dtype=jnp.float32) * (1.0 / np.sqrt(DIM))
        g_k = jnp.ones((DIM_HEAD,), dtype=jnp.float32)
        b_k = jnp.zeros((DIM_HEAD,), dtype=jnp.float32)
        g_v = jnp.ones((DIM_HEAD,), dtype=jnp.float32)
        b_v = jnp.zeros((DIM_HEAD,), dtype=jnp.float32)
        w_out = jax.random.normal(ks[2], (DIM, INNER), dtype=jnp.float32) * (1.0 / np.sqrt(INNER))
        b_out = jax.random.normal(ks[3], (DIM,), dtype=jnp.float32) * 0.01
        return {'x': x, 'w_map': w_map, 'g_k': g_k, 'b_k': b_k, 'g_v': g_v, 'b_v': b_v, 'w_out': w_out, 'b_out': b_out}
    _L0_mix_all = _L0_mix_setup()
    _L0_mix_in = {k: v for k, v in _L0_mix_all.items() if k in ('w_map', 'g_k', 'b_k', 'g_v', 'b_v', 'w_out', 'b_out')}
    del _L0_mix_all

    def _L0_ffn_setup():
        import jax, jax.numpy as jnp
        import numpy as np
        B, M, D = (32, 196, 768)
        N, P, H = (64, 1, 192)
        EPS = 1e-12

        def _l2norm(v, axis):
            n = jnp.sqrt(jnp.sum(v * v, axis=axis, keepdims=True))
            return v / jnp.maximum(n, EPS)
        key = jax.random.key(seed)
        ks = jax.random.split(key, 7)
        x = jax.random.normal(ks[0], (B, M, D), dtype=jnp.float32)
        phi = jax.random.normal(ks[1], (D, N, P), dtype=jnp.float32) * (1.0 / D ** 0.5)
        scale = jnp.ones((1,), dtype=jnp.float32)
        w1 = jax.random.normal(ks[2], (N, D, H), dtype=jnp.float32) * (1.0 / D ** 0.5)
        b1 = jnp.zeros((N, H), dtype=jnp.float32)
        w2 = jax.random.normal(ks[3], (N, H, D), dtype=jnp.float32) * (1.0 / H ** 0.5)
        b2 = jnp.zeros((N, D), dtype=jnp.float32)
        return {'x': x, 'phi': phi, 'scale': scale, 'w1': w1, 'b1': b1, 'w2': w2, 'b2': b2}
    _L0_ffn_all = _L0_ffn_setup()
    _L0_ffn_in = {k: v for k, v in _L0_ffn_all.items() if k in ('phi', 'scale', 'w1', 'b1', 'w2', 'b2')}
    del _L0_ffn_all

    def _L1_gnn_setup():
        import jax, jax.numpy as jnp
        import numpy as np
        N_NODES = 625
        N_EDGES = 6250
        DIM = 768
        key = jax.random.key(seed)
        k1, k2, k3, k4 = jax.random.split(key, 4)
        x = jax.random.normal(k1, (N_NODES, DIM), dtype=jnp.float32)
        edge_index = jax.random.randint(k2, (2, N_EDGES), 0, N_NODES, dtype=jnp.int32)
        W = jax.random.normal(k3, (DIM, DIM), dtype=jnp.float32) / np.sqrt(DIM)
        b = jnp.zeros((DIM,), dtype=jnp.float32)
        return {'x': x, 'edge_index': edge_index, 'W': W, 'b': b}
    _L1_gnn_all = _L1_gnn_setup()
    _L1_gnn_in = {k: v for k, v in _L1_gnn_all.items() if k in ('W', 'b')}
    del _L1_gnn_all

    def _L1_mix_setup():
        import jax, jax.numpy as jnp
        import numpy as np
        import math
        H = 12
        HD = 64
        M = 32
        EPS = 1e-08

        def prm_exp(x, w):
            xd = 0.5 * jnp.sum(x * x, axis=-1, keepdims=True)
            wtx = jnp.einsum('bhti,hmi->bhtm', x, w)
            return jnp.exp(wtx - xd) / math.sqrt(M)
        key = jax.random.key(seed)
        ks = jax.random.split(key, 5)
        B, N, C = (8, 256, 768)
        x = jax.random.normal(ks[0], (B, N, C), dtype=jnp.float32)
        kqv_w = jax.random.normal(ks[1], (3 * C, C), dtype=jnp.float32) * (1.0 / math.sqrt(C))
        kqv_b = jnp.zeros((3 * C,), dtype=jnp.float32)
        proj_w = jax.random.normal(ks[2], (C, C), dtype=jnp.float32) * (1.0 / math.sqrt(C))
        proj_b = jnp.zeros((C,), dtype=jnp.float32)
        wr = jax.random.normal(ks[3], (H, M, HD), dtype=jnp.float32)
        q_ortho, _ = jnp.linalg.qr(jnp.swapaxes(wr, -1, -2))
        w = jnp.swapaxes(q_ortho, -1, -2) * math.sqrt(M)
        return {'x': x, 'kqv_w': kqv_w, 'kqv_b': kqv_b, 'proj_w': proj_w, 'proj_b': proj_b, 'w': w}
    _L1_mix_all = _L1_mix_setup()
    _L1_mix_in = {k: v for k, v in _L1_mix_all.items() if k in ('kqv_w', 'kqv_b', 'proj_w', 'proj_b', 'w')}
    del _L1_mix_all

    def _L1_ffn_setup():
        import jax, jax.numpy as jnp
        import numpy as np
        NUM_EXPERTS = 8
        TOP_K = 2
        CAP_FACTOR = 1.0
        D_MODEL = 768
        D_FF = 192
        key = jax.random.key(seed)
        k0, k1, k2, k3 = jax.random.split(key, 4)
        B, S, D = (1, 128, D_MODEL)
        inputs = jax.random.normal(k0, (B, S, D), dtype=jnp.float32)
        router_w = jax.random.normal(k1, (NUM_EXPERTS, D), dtype=jnp.float32) * D ** (-0.5)
        w1 = jax.random.normal(k2, (NUM_EXPERTS, D, D_FF), dtype=jnp.float32) * D ** (-0.5)
        w2 = jax.random.normal(k3, (NUM_EXPERTS, D_FF, D), dtype=jnp.float32) * D_FF ** (-0.5)
        return {'inputs': inputs, 'router_w': router_w, 'w1': w1, 'w2': w2}
    _L1_ffn_all = _L1_ffn_setup()
    _L1_ffn_in = {k: v for k, v in _L1_ffn_all.items() if k in ('router_w', 'w1', 'w2')}
    del _L1_ffn_all

    def _L2_gnn_setup():
        import jax, jax.numpy as jnp
        import numpy as np
        N_NODES = 625
        NEG_SLOPE = 0.2
        EPS = 1e-16

        def gat_layer(x, W, att_src, att_dst, bias, src, dst, heads, out_ch, concat):
            n = x.shape[0]
            h = (x @ W.T).reshape(n, heads, out_ch)
            a_src = jnp.einsum('nhc,hc->nh', h, att_src)
            a_dst = jnp.einsum('nhc,hc->nh', h, att_dst)
            e = a_src[src] + a_dst[dst]
            e = jax.nn.leaky_relu(e, NEG_SLOPE)
            m = jax.ops.segment_max(e, dst, num_segments=n)
            ex = jnp.exp(e - m[dst])
            denom = jax.ops.segment_sum(ex, dst, num_segments=n)
            alpha = ex / (denom[dst] + EPS)
            msg = alpha[:, :, None] * h[src]
            out = jax.ops.segment_sum(msg, dst, num_segments=n)
            if concat:
                out = out.reshape(n, heads * out_ch)
            else:
                out = out.mean(axis=1)
            return out + bias
        key = jax.random.key(seed)
        ks = jax.random.split(key, 12)
        x = jax.random.normal(ks[0], (N_NODES, 768), dtype=jnp.float32)
        edge_index = jax.random.randint(ks[1], (2, 10000), 0, N_NODES, dtype=jnp.int64)
        s1 = 1.0 / np.sqrt(768.0)
        W1 = jax.random.normal(ks[2], (8 * 128, 768), dtype=jnp.float32) * s1
        att_src1 = jax.random.normal(ks[3], (8, 128), dtype=jnp.float32) * (1.0 / np.sqrt(128.0))
        att_dst1 = jax.random.normal(ks[4], (8, 128), dtype=jnp.float32) * (1.0 / np.sqrt(128.0))
        b1 = jnp.zeros((8 * 128,), dtype=jnp.float32)
        s2 = 1.0 / np.sqrt(1024.0)
        W2 = jax.random.normal(ks[5], (1 * 768, 1024), dtype=jnp.float32) * s2
        att_src2 = jax.random.normal(ks[6], (1, 768), dtype=jnp.float32) * (1.0 / np.sqrt(768.0))
        att_dst2 = jax.random.normal(ks[7], (1, 768), dtype=jnp.float32) * (1.0 / np.sqrt(768.0))
        b2 = jnp.zeros((768,), dtype=jnp.float32)
        return {'x': x, 'edge_index': edge_index, 'W1': W1, 'att_src1': att_src1, 'att_dst1': att_dst1, 'b1': b1, 'W2': W2, 'att_src2': att_src2, 'att_dst2': att_dst2, 'b2': b2}
    _L2_gnn_all = _L2_gnn_setup()
    _L2_gnn_in = {k: v for k, v in _L2_gnn_all.items() if k in ('W1', 'att_src1', 'att_dst1', 'b1', 'W2', 'att_src2', 'att_dst2', 'b2')}
    del _L2_gnn_all

    def _L2_mix_setup():
        import jax, jax.numpy as jnp
        import numpy as np
        DIM = 768
        NUM_HEADS = 12
        HEAD_DIM = DIM // NUM_HEADS
        HIDDEN = int(DIM * 4.0)
        EPS = 1e-08

        def layer_norm(x, w, b):
            mu = jnp.mean(x, axis=-1, keepdims=True)
            var = jnp.mean(jnp.square(x - mu), axis=-1, keepdims=True)
            return (x - mu) * jax.lax.rsqrt(var + EPS) * w + b

        def linear_attention(x, qkv_w, qkv_b, proj_w, proj_b):
            B, N, C = x.shape
            qkv = (x @ qkv_w + qkv_b).reshape(B, N, 3, NUM_HEADS, HEAD_DIM)
            qkv = qkv.transpose(2, 0, 3, 1, 4)
            q, k, v = (qkv[0], qkv[1], qkv[2])
            q = jax.nn.elu(q) + 1.0
            k = jax.nn.elu(k) + 1.0
            kv = jnp.einsum('bhsd,bhse->bhde', k, v)
            z = 1.0 / jnp.einsum('bhsd,bhd->bhs', q, k.sum(axis=-2))
            out = jnp.einsum('bhde,bhsd,bhs->bhse', kv, q, z)
            out = out.transpose(0, 2, 1, 3).reshape(B, N, C)
            return out @ proj_w + proj_b
        key = jax.random.key(seed)
        ks = jax.random.split(key, 10)
        s = 0.02
        return {'x': jax.random.normal(ks[0], (16, 256, DIM), dtype=jnp.float32), 'qkv_w': jax.random.normal(ks[1], (DIM, 3 * DIM), dtype=jnp.float32) * s, 'qkv_b': jnp.zeros((3 * DIM,), dtype=jnp.float32), 'proj_w': jax.random.normal(ks[2], (DIM, DIM), dtype=jnp.float32) * s, 'proj_b': jnp.zeros((DIM,), dtype=jnp.float32), 'fc1_w': jax.random.normal(ks[3], (DIM, HIDDEN), dtype=jnp.float32) * s, 'fc1_b': jnp.zeros((HIDDEN,), dtype=jnp.float32), 'fc2_w': jax.random.normal(ks[4], (HIDDEN, DIM), dtype=jnp.float32) * s, 'fc2_b': jnp.zeros((DIM,), dtype=jnp.float32), 'ln1_w': jnp.ones((DIM,), dtype=jnp.float32), 'ln1_b': jnp.zeros((DIM,), dtype=jnp.float32), 'ln2_w': jnp.ones((DIM,), dtype=jnp.float32), 'ln2_b': jnp.zeros((DIM,), dtype=jnp.float32)}
    _L2_mix_all = _L2_mix_setup()
    _L2_mix_in = {k: v for k, v in _L2_mix_all.items() if k in ('qkv_w', 'qkv_b', 'proj_w', 'proj_b', 'fc1_w', 'fc1_b', 'fc2_w', 'fc2_b', 'ln1_w', 'ln1_b', 'ln2_w', 'ln2_b')}
    del _L2_mix_all

    def _L2_ffn_setup():
        import jax, jax.numpy as jnp
        import numpy as np
        E = 768
        H = 12
        D = E // H
        HID = 192
        NEXP = 4
        TOPK = 2
        EPS = 1e-05

        def _ln(x, g, b):
            m = jnp.mean(x, axis=-1, keepdims=True)
            v = jnp.mean(jnp.square(x - m), axis=-1, keepdims=True)
            return (x - m) * jax.lax.rsqrt(v + EPS) * g + b
        key = jax.random.key(seed)
        ks = jax.random.split(key, 10)
        s = 0.02
        return {'x': jax.random.normal(ks[0], (8, 1024, E), jnp.float32), 'ln1_g': jnp.ones((E,), jnp.float32), 'ln1_b': jnp.zeros((E,), jnp.float32), 'in_w': jax.random.normal(ks[1], (3 * E, E), jnp.float32) * s, 'in_b': jnp.zeros((3 * E,), jnp.float32), 'out_w': jax.random.normal(ks[2], (E, E), jnp.float32) * s, 'out_b': jnp.zeros((E,), jnp.float32), 'mlp_w1': jax.random.normal(ks[3], (E, HID), jnp.float32) * s, 'mlp_b1': jnp.zeros((HID,), jnp.float32), 'mlp_w2': jax.random.normal(ks[4], (HID, E), jnp.float32) * s, 'mlp_b2': jnp.zeros((E,), jnp.float32), 'ln2_g': jnp.ones((E,), jnp.float32), 'ln2_b': jnp.zeros((E,), jnp.float32), 'gate_w': jax.random.normal(ks[5], (NEXP, E), jnp.float32) * s, 'gate_b': jnp.zeros((NEXP,), jnp.float32), 'exp_w1': jax.random.normal(ks[6], (NEXP, E, HID), jnp.float32) * s, 'exp_b1': jnp.zeros((NEXP, HID), jnp.float32), 'exp_w2': jax.random.normal(ks[7], (NEXP, HID, E), jnp.float32) * s, 'exp_b2': jnp.zeros((NEXP, E), jnp.float32)}
    _L2_ffn_all = _L2_ffn_setup()
    _L2_ffn_in = {k: v for k, v in _L2_ffn_all.items() if k in ('ln1_g', 'ln1_b', 'in_w', 'in_b', 'out_w', 'out_b', 'mlp_w1', 'mlp_b1', 'mlp_w2', 'mlp_b2', 'ln2_g', 'ln2_b', 'gate_w', 'gate_b', 'exp_w1', 'exp_b1', 'exp_w2', 'exp_b2')}
    del _L2_ffn_all

    def _L3_gnn_setup():
        import jax, jax.numpy as jnp
        import numpy as np
        NEG_SLOPE = 0.2

        def _gat_layer(x, W, a_src, a_dst, b, src, dst, n_nodes):
            h = x @ W
            e_src = h @ a_src
            e_dst = h @ a_dst
            e = jax.nn.leaky_relu(e_src[src] + e_dst[dst], NEG_SLOPE)
            m = jax.ops.segment_max(e, dst, num_segments=n_nodes)
            w = jnp.exp(e - m[dst])
            z = jax.ops.segment_sum(w, dst, num_segments=n_nodes)
            alpha = w / z[dst]
            out = jax.ops.segment_sum(h[src] * alpha[:, None], dst, num_segments=n_nodes)
            return out + b
        key = jax.random.key(seed)
        ks = jax.random.split(key, 10)
        N, E, D = (625, 6250, 768)
        scale = 1.0 / np.sqrt(D)
        x = jax.random.normal(ks[0], (N, D), dtype=jnp.float32)
        edge_index = jax.random.randint(ks[1], (2, E), 0, N, dtype=jnp.int32)
        params = {}
        for i, nm in enumerate(['1', '2']):
            params[f'W{nm}'] = jax.random.normal(ks[2 + 4 * i], (D, D), jnp.float32) * scale
            params[f'att_src{nm}'] = jax.random.normal(ks[3 + 4 * i], (D,), jnp.float32) * scale
            params[f'att_dst{nm}'] = jax.random.normal(ks[4 + 4 * i], (D,), jnp.float32) * scale
            params[f'b{nm}'] = jnp.zeros((D,), jnp.float32)
        return {'x': x, 'edge_index': edge_index, **params}
    _L3_gnn_all = _L3_gnn_setup()
    _L3_gnn_in = {k: v for k, v in _L3_gnn_all.items() if k in ('W1', 'att_src1', 'att_dst1', 'b1', 'W2', 'att_src2', 'att_dst2', 'b2')}
    del _L3_gnn_all

    def _L3_mix_setup():
        import jax, jax.numpy as jnp
        import numpy as np
        import math
        B, N, C = (8, 256, 768)
        H = 12
        DH = C // H
        M = 256
        LN_EPS = 1e-05

        def _phi(t, random_features):
            norm_sq = 0.5 * jnp.sum(t * t, axis=-1, keepdims=True)
            proj = jnp.einsum('bhnd,md->bhnm', t, random_features)
            return jnp.exp(proj - norm_sq) * (1.0 / math.sqrt(M))
        key = jax.random.key(seed)
        ks = jax.random.split(key, 7)
        x = jax.random.normal(ks[0], (B, N, C), dtype=jnp.float32)
        W_qkv = jax.random.normal(ks[1], (C, 3 * C), dtype=jnp.float32) * (1.0 / math.sqrt(C))
        W_proj = jax.random.normal(ks[2], (C, C), dtype=jnp.float32) * (1.0 / math.sqrt(C))
        b_proj = jnp.zeros((C,), dtype=jnp.float32)
        gamma = jnp.ones((C,), dtype=jnp.float32)
        beta = jnp.zeros((C,), dtype=jnp.float32)
        random_features = jax.random.normal(ks[3], (M, DH), dtype=jnp.float32) / math.sqrt(DH)
        return {'x': x, 'W_qkv': W_qkv, 'W_proj': W_proj, 'b_proj': b_proj, 'gamma': gamma, 'beta': beta, 'random_features': random_features}
    _L3_mix_all = _L3_mix_setup()
    _L3_mix_in = {k: v for k, v in _L3_mix_all.items() if k in ('W_qkv', 'W_proj', 'b_proj', 'gamma', 'beta', 'random_features')}
    del _L3_mix_all

    def _L3_ffn_setup():
        import jax, jax.numpy as jnp
        import numpy as np
        E = 8
        TOP_K = 2
        CAP_RATIO = 1.2
        key = jax.random.key(seed)
        k1, k2, k3, k4 = jax.random.split(key, 4)
        B, L, D, H = (2, 128, 768, 128)
        x = jax.random.normal(k1, (B, L, D), dtype=jnp.float32)
        Wg = jax.random.normal(k2, (D, E), dtype=jnp.float32) * 0.02
        W1 = jax.random.normal(k3, (E, D, 2 * H), dtype=jnp.float32) * 0.02
        W2 = jax.random.normal(k4, (E, H, D), dtype=jnp.float32) * 0.02
        return {'x': x, 'Wg': Wg, 'W1': W1, 'W2': W2}
    _L3_ffn_all = _L3_ffn_setup()
    _L3_ffn_in = {k: v for k, v in _L3_ffn_all.items() if k in ('Wg', 'W1', 'W2')}
    del _L3_ffn_all
    return {'x': x, 'src': src, 'dst': dst, 'edge_weight1': edge_weight1, 'L0_gnn_W_ah': _L0_gnn_in['W_ah'], 'L0_gnn_b_ah': _L0_gnn_in['b_ah'], 'L0_gnn_W0': _L0_gnn_in['W0'], 'L0_gnn_a_src0': _L0_gnn_in['a_src0'], 'L0_gnn_a_dst0': _L0_gnn_in['a_dst0'], 'L0_gnn_b0': _L0_gnn_in['b0'], 'L0_gnn_W1': _L0_gnn_in['W1'], 'L0_gnn_a_src1': _L0_gnn_in['a_src1'], 'L0_gnn_a_dst1': _L0_gnn_in['a_dst1'], 'L0_gnn_b1': _L0_gnn_in['b1'], 'L0_gnn_W2': _L0_gnn_in['W2'], 'L0_gnn_a_src2': _L0_gnn_in['a_src2'], 'L0_gnn_a_dst2': _L0_gnn_in['a_dst2'], 'L0_gnn_b2': _L0_gnn_in['b2'], 'L0_gnn_W_out': _L0_gnn_in['W_out'], 'L0_gnn_b_out': _L0_gnn_in['b_out'], 'L0_mix_w_map': _L0_mix_in['w_map'], 'L0_mix_g_k': _L0_mix_in['g_k'], 'L0_mix_b_k': _L0_mix_in['b_k'], 'L0_mix_g_v': _L0_mix_in['g_v'], 'L0_mix_b_v': _L0_mix_in['b_v'], 'L0_mix_w_out': _L0_mix_in['w_out'], 'L0_mix_b_out': _L0_mix_in['b_out'], 'L0_ffn_phi': _L0_ffn_in['phi'], 'L0_ffn_scale': _L0_ffn_in['scale'], 'L0_ffn_w1': _L0_ffn_in['w1'], 'L0_ffn_b1': _L0_ffn_in['b1'], 'L0_ffn_w2': _L0_ffn_in['w2'], 'L0_ffn_b2': _L0_ffn_in['b2'], 'L1_gnn_W': _L1_gnn_in['W'], 'L1_gnn_b': _L1_gnn_in['b'], 'L1_mix_kqv_w': _L1_mix_in['kqv_w'], 'L1_mix_kqv_b': _L1_mix_in['kqv_b'], 'L1_mix_proj_w': _L1_mix_in['proj_w'], 'L1_mix_proj_b': _L1_mix_in['proj_b'], 'L1_mix_w': _L1_mix_in['w'], 'L1_ffn_router_w': _L1_ffn_in['router_w'], 'L1_ffn_w1': _L1_ffn_in['w1'], 'L1_ffn_w2': _L1_ffn_in['w2'], 'L2_gnn_W1': _L2_gnn_in['W1'], 'L2_gnn_att_src1': _L2_gnn_in['att_src1'], 'L2_gnn_att_dst1': _L2_gnn_in['att_dst1'], 'L2_gnn_b1': _L2_gnn_in['b1'], 'L2_gnn_W2': _L2_gnn_in['W2'], 'L2_gnn_att_src2': _L2_gnn_in['att_src2'], 'L2_gnn_att_dst2': _L2_gnn_in['att_dst2'], 'L2_gnn_b2': _L2_gnn_in['b2'], 'L2_mix_qkv_w': _L2_mix_in['qkv_w'], 'L2_mix_qkv_b': _L2_mix_in['qkv_b'], 'L2_mix_proj_w': _L2_mix_in['proj_w'], 'L2_mix_proj_b': _L2_mix_in['proj_b'], 'L2_mix_fc1_w': _L2_mix_in['fc1_w'], 'L2_mix_fc1_b': _L2_mix_in['fc1_b'], 'L2_mix_fc2_w': _L2_mix_in['fc2_w'], 'L2_mix_fc2_b': _L2_mix_in['fc2_b'], 'L2_mix_ln1_w': _L2_mix_in['ln1_w'], 'L2_mix_ln1_b': _L2_mix_in['ln1_b'], 'L2_mix_ln2_w': _L2_mix_in['ln2_w'], 'L2_mix_ln2_b': _L2_mix_in['ln2_b'], 'L2_ffn_ln1_g': _L2_ffn_in['ln1_g'], 'L2_ffn_ln1_b': _L2_ffn_in['ln1_b'], 'L2_ffn_in_w': _L2_ffn_in['in_w'], 'L2_ffn_in_b': _L2_ffn_in['in_b'], 'L2_ffn_out_w': _L2_ffn_in['out_w'], 'L2_ffn_out_b': _L2_ffn_in['out_b'], 'L2_ffn_mlp_w1': _L2_ffn_in['mlp_w1'], 'L2_ffn_mlp_b1': _L2_ffn_in['mlp_b1'], 'L2_ffn_mlp_w2': _L2_ffn_in['mlp_w2'], 'L2_ffn_mlp_b2': _L2_ffn_in['mlp_b2'], 'L2_ffn_ln2_g': _L2_ffn_in['ln2_g'], 'L2_ffn_ln2_b': _L2_ffn_in['ln2_b'], 'L2_ffn_gate_w': _L2_ffn_in['gate_w'], 'L2_ffn_gate_b': _L2_ffn_in['gate_b'], 'L2_ffn_exp_w1': _L2_ffn_in['exp_w1'], 'L2_ffn_exp_b1': _L2_ffn_in['exp_b1'], 'L2_ffn_exp_w2': _L2_ffn_in['exp_w2'], 'L2_ffn_exp_b2': _L2_ffn_in['exp_b2'], 'L3_gnn_W1': _L3_gnn_in['W1'], 'L3_gnn_att_src1': _L3_gnn_in['att_src1'], 'L3_gnn_att_dst1': _L3_gnn_in['att_dst1'], 'L3_gnn_b1': _L3_gnn_in['b1'], 'L3_gnn_W2': _L3_gnn_in['W2'], 'L3_gnn_att_src2': _L3_gnn_in['att_src2'], 'L3_gnn_att_dst2': _L3_gnn_in['att_dst2'], 'L3_gnn_b2': _L3_gnn_in['b2'], 'L3_mix_W_qkv': _L3_mix_in['W_qkv'], 'L3_mix_W_proj': _L3_mix_in['W_proj'], 'L3_mix_b_proj': _L3_mix_in['b_proj'], 'L3_mix_gamma': _L3_mix_in['gamma'], 'L3_mix_beta': _L3_mix_in['beta'], 'L3_mix_random_features': _L3_mix_in['random_features'], 'L3_ffn_Wg': _L3_ffn_in['Wg'], 'L3_ffn_W1': _L3_ffn_in['W1'], 'L3_ffn_W2': _L3_ffn_in['W2']}

def reference(x, src, dst, edge_weight1, L0_gnn_W_ah, L0_gnn_b_ah, L0_gnn_W0, L0_gnn_a_src0, L0_gnn_a_dst0, L0_gnn_b0, L0_gnn_W1, L0_gnn_a_src1, L0_gnn_a_dst1, L0_gnn_b1, L0_gnn_W2, L0_gnn_a_src2, L0_gnn_a_dst2, L0_gnn_b2, L0_gnn_W_out, L0_gnn_b_out, L0_mix_w_map, L0_mix_g_k, L0_mix_b_k, L0_mix_g_v, L0_mix_b_v, L0_mix_w_out, L0_mix_b_out, L0_ffn_phi, L0_ffn_scale, L0_ffn_w1, L0_ffn_b1, L0_ffn_w2, L0_ffn_b2, L1_gnn_W, L1_gnn_b, L1_mix_kqv_w, L1_mix_kqv_b, L1_mix_proj_w, L1_mix_proj_b, L1_mix_w, L1_ffn_router_w, L1_ffn_w1, L1_ffn_w2, L2_gnn_W1, L2_gnn_att_src1, L2_gnn_att_dst1, L2_gnn_b1, L2_gnn_W2, L2_gnn_att_src2, L2_gnn_att_dst2, L2_gnn_b2, L2_mix_qkv_w, L2_mix_qkv_b, L2_mix_proj_w, L2_mix_proj_b, L2_mix_fc1_w, L2_mix_fc1_b, L2_mix_fc2_w, L2_mix_fc2_b, L2_mix_ln1_w, L2_mix_ln1_b, L2_mix_ln2_w, L2_mix_ln2_b, L2_ffn_ln1_g, L2_ffn_ln1_b, L2_ffn_in_w, L2_ffn_in_b, L2_ffn_out_w, L2_ffn_out_b, L2_ffn_mlp_w1, L2_ffn_mlp_b1, L2_ffn_mlp_w2, L2_ffn_mlp_b2, L2_ffn_ln2_g, L2_ffn_ln2_b, L2_ffn_gate_w, L2_ffn_gate_b, L2_ffn_exp_w1, L2_ffn_exp_b1, L2_ffn_exp_w2, L2_ffn_exp_b2, L3_gnn_W1, L3_gnn_att_src1, L3_gnn_att_dst1, L3_gnn_b1, L3_gnn_W2, L3_gnn_att_src2, L3_gnn_att_dst2, L3_gnn_b2, L3_mix_W_qkv, L3_mix_W_proj, L3_mix_b_proj, L3_mix_gamma, L3_mix_beta, L3_mix_random_features, L3_ffn_Wg, L3_ffn_W1, L3_ffn_W2):
    import jax
    import jax.numpy as jnp

    def _L0_gnn_ref(x, edge_index, batch, edge_attr, W_ah, b_ah, W0, a_src0, a_dst0, b0, W1, a_src1, a_dst1, b1, W2, a_src2, a_dst2, b2, W_out, b_out):
        import jax, jax.numpy as jnp
        import numpy as np
        N, E, D, H, C = (625, 6250, 768, 4, 192)
        NEG_SLOPE = 0.2

        def gat_conv(x, src, dst, W, a_src, a_dst, b):
            h = (x @ W).reshape(N, H, C)
            as_n = (h * a_src).sum(-1)
            ad_n = (h * a_dst).sum(-1)
            e = jax.nn.leaky_relu(as_n[src] + ad_n[dst], NEG_SLOPE)
            m = jax.ops.segment_max(e, dst, num_segments=N)
            p = jnp.exp(e - m[dst])
            s = jax.ops.segment_sum(p, dst, num_segments=N)
            alpha = p / (s[dst] + 1e-16)
            out = jax.ops.segment_sum(alpha[:, :, None] * h[src], dst, num_segments=N)
            return out.reshape(N, H * C) + b
        loops = jnp.arange(N, dtype=edge_index.dtype)
        src = jnp.concatenate([edge_index[0], loops])
        dst = jnp.concatenate([edge_index[1], loops])
        x1 = jax.nn.relu(x @ W_ah + b_ah)
        xs = [jax.nn.relu(gat_conv(x1, src, dst, W, a_s, a_d, b)) for W, a_s, a_d, b in ((W0, a_src0, a_dst0, b0), (W1, a_src1, a_dst1, b1), (W2, a_src2, a_dst2, b2))]
        node_emb = jnp.concatenate(xs, axis=1)
        return jax.nn.relu(node_emb @ W_out + b_out)

    def _L0_mix_ref(x, w_map, g_k, b_k, g_v, b_v, w_out, b_out):
        import jax, jax.numpy as jnp
        import numpy as np
        DIM = 768
        HEADS = 12
        DIM_HEAD = 64
        INNER = HEADS * DIM_HEAD
        EPS = 1e-05

        def _layernorm(t, gamma, beta):
            mu = jnp.mean(t, axis=-1, keepdims=True)
            var = jnp.var(t, axis=-1, keepdims=True)
            return (t - mu) * jax.lax.rsqrt(var + EPS) * gamma + beta
        b, n, _ = x.shape
        qkv = x @ w_map.T
        q, k, v = jnp.split(qkv, 3, axis=-1)

        def to_heads(t):
            return t.reshape(b, n, HEADS, DIM_HEAD).transpose(0, 2, 1, 3)
        q, k, v = (to_heads(q), to_heads(k), to_heads(v))
        k = _layernorm(k, g_k, b_k)
        v = _layernorm(v, g_v, b_v)
        attn = jnp.einsum('bhnd,bhne->bhde', k, v) / n
        out = jnp.einsum('bhnd,bhde->bhne', q, attn)
        out = out.transpose(0, 2, 1, 3).reshape(b, n, INNER)
        return out @ w_out.T + b_out

    def _L0_ffn_ref(x, phi, scale, w1, b1, w2, b2):
        import jax, jax.numpy as jnp
        import numpy as np
        B, M, D = (32, 196, 768)
        N, P, H = (64, 1, 192)
        EPS = 1e-12

        def _l2norm(v, axis):
            n = jnp.sqrt(jnp.sum(v * v, axis=axis, keepdims=True))
            return v / jnp.maximum(n, EPS)
        xn = _l2norm(x, axis=2)
        phin = scale * _l2norm(phi, axis=0)
        logits = jnp.einsum('bmd,dnp->bmnp', xn, phin)
        d = jax.nn.softmax(logits, axis=1)
        b_, m_, n_, p_ = logits.shape
        c = jax.nn.softmax(logits.reshape(b_, m_, n_ * p_), axis=-1).reshape(b_, m_, n_, p_)
        xs = jnp.einsum('bmd,bmnp->bnpd', xn, d)
        h = jax.nn.gelu(jnp.einsum('bnpd,ndh->bnph', xs, w1) + b1[None, :, None, :], approximate=False)
        ys = jnp.einsum('bnph,nhd->bnpd', h, w2) + b2[None, :, None, :]
        y = jnp.einsum('bnpd,bmnp->bmd', ys, c)
        return y

    def _L1_gnn_ref(x, edge_index, W, b):
        import jax, jax.numpy as jnp
        import numpy as np
        N_NODES = 625
        N_EDGES = 6250
        DIM = 768
        n = x.shape[0]
        loop = jnp.arange(n, dtype=edge_index.dtype)
        src = jnp.concatenate([edge_index[0], loop])
        dst = jnp.concatenate([edge_index[1], loop])
        deg = jax.ops.segment_sum(jnp.ones_like(dst, dtype=x.dtype), dst, num_segments=n)
        deg_inv_sqrt = jnp.where(deg > 0, jax.lax.rsqrt(deg), 0.0)
        norm = deg_inv_sqrt[src] * deg_inv_sqrt[dst]
        h = x @ W
        msg = h[src] * norm[:, None]
        out = jax.ops.segment_sum(msg, dst, num_segments=n)
        return out + b

    def _L1_mix_ref(x, kqv_w, kqv_b, proj_w, proj_b, w):
        import jax, jax.numpy as jnp
        import numpy as np
        import math
        H = 12
        HD = 64
        M = 32
        EPS = 1e-08

        def prm_exp(x, w):
            xd = 0.5 * jnp.sum(x * x, axis=-1, keepdims=True)
            wtx = jnp.einsum('bhti,hmi->bhtm', x, w)
            return jnp.exp(wtx - xd) / math.sqrt(M)
        B, N, C = x.shape
        kqv = x @ kqv_w.T + kqv_b
        kqv = kqv.reshape(B, N, 3, H, HD).transpose(2, 0, 3, 1, 4)
        k, q, v = (kqv[0], kqv[1], kqv[2])
        kp = prm_exp(k, w)
        qp = prm_exp(q, w)
        D = jnp.einsum('bhtm,bhm->bht', qp, kp.sum(axis=2))[..., None]
        kptv = jnp.einsum('bhin,bhim->bhnm', v, kp)
        y = jnp.einsum('bhtm,bhnm->bhtn', qp, kptv) / (D + EPS)
        y = y.transpose(0, 2, 1, 3).reshape(B, N, C)
        y = y @ proj_w.T + proj_b
        return y

    def _L1_ffn_ref(inputs, router_w, w1, w2):
        import jax, jax.numpy as jnp
        import numpy as np
        NUM_EXPERTS = 8
        TOP_K = 2
        CAP_FACTOR = 1.0
        D_MODEL = 768
        D_FF = 192
        B, S, D = inputs.shape
        x = inputs.reshape(-1, D)
        N = x.shape[0]
        logits = x @ router_w.T
        probs = jax.nn.softmax(logits.astype(jnp.float32), axis=-1)
        weights, sel = jax.lax.top_k(probs, TOP_K)
        cap = int(CAP_FACTOR * N * TOP_K) + 1
        n_real = N * TOP_K
        expert_flat = sel.reshape(-1)
        weight_flat = weights.reshape(-1)
        token_idx = jnp.repeat(jnp.arange(N), TOP_K)
        pad = cap - n_real
        expert_flat = jnp.pad(expert_flat, (0, pad))
        weight_flat = jnp.pad(weight_flat, (0, pad))
        token_idx = jnp.pad(token_idx, (0, pad))
        valid = jnp.arange(cap) < n_real
        toks = x[token_idx]

        def mlp(w1e, w2e):
            return jax.nn.gelu(toks @ w1e) @ w2e
        ys = jax.vmap(mlp)(w1, w2)
        gate = (weight_flat * valid.astype(weight_flat.dtype)).astype(toks.dtype)
        res = ys[expert_flat, jnp.arange(cap)] * gate[:, None]
        out = jnp.zeros((N, D), dtype=inputs.dtype).at[token_idx].add(res)
        return out.reshape(B, S, D)

    def _L2_gnn_ref(x, edge_index, W1, att_src1, att_dst1, b1, W2, att_src2, att_dst2, b2):
        import jax, jax.numpy as jnp
        import numpy as np
        N_NODES = 625
        NEG_SLOPE = 0.2
        EPS = 1e-16

        def gat_layer(x, W, att_src, att_dst, bias, src, dst, heads, out_ch, concat):
            n = x.shape[0]
            h = (x @ W.T).reshape(n, heads, out_ch)
            a_src = jnp.einsum('nhc,hc->nh', h, att_src)
            a_dst = jnp.einsum('nhc,hc->nh', h, att_dst)
            e = a_src[src] + a_dst[dst]
            e = jax.nn.leaky_relu(e, NEG_SLOPE)
            m = jax.ops.segment_max(e, dst, num_segments=n)
            ex = jnp.exp(e - m[dst])
            denom = jax.ops.segment_sum(ex, dst, num_segments=n)
            alpha = ex / (denom[dst] + EPS)
            msg = alpha[:, :, None] * h[src]
            out = jax.ops.segment_sum(msg, dst, num_segments=n)
            if concat:
                out = out.reshape(n, heads * out_ch)
            else:
                out = out.mean(axis=1)
            return out + bias
        src, dst = (edge_index[0], edge_index[1])
        h = gat_layer(x, W1, att_src1, att_dst1, b1, src, dst, heads=8, out_ch=128, concat=True)
        h = jax.nn.relu(h)
        out = gat_layer(h, W2, att_src2, att_dst2, b2, src, dst, heads=1, out_ch=768, concat=True)
        return out

    def _L2_mix_ref(x, qkv_w, qkv_b, proj_w, proj_b, fc1_w, fc1_b, fc2_w, fc2_b, ln1_w, ln1_b, ln2_w, ln2_b):
        import jax, jax.numpy as jnp
        import numpy as np
        DIM = 768
        NUM_HEADS = 12
        HEAD_DIM = DIM // NUM_HEADS
        HIDDEN = int(DIM * 4.0)
        EPS = 1e-08

        def layer_norm(x, w, b):
            mu = jnp.mean(x, axis=-1, keepdims=True)
            var = jnp.mean(jnp.square(x - mu), axis=-1, keepdims=True)
            return (x - mu) * jax.lax.rsqrt(var + EPS) * w + b

        def linear_attention(x, qkv_w, qkv_b, proj_w, proj_b):
            B, N, C = x.shape
            qkv = (x @ qkv_w + qkv_b).reshape(B, N, 3, NUM_HEADS, HEAD_DIM)
            qkv = qkv.transpose(2, 0, 3, 1, 4)
            q, k, v = (qkv[0], qkv[1], qkv[2])
            q = jax.nn.elu(q) + 1.0
            k = jax.nn.elu(k) + 1.0
            kv = jnp.einsum('bhsd,bhse->bhde', k, v)
            z = 1.0 / jnp.einsum('bhsd,bhd->bhs', q, k.sum(axis=-2))
            out = jnp.einsum('bhde,bhsd,bhs->bhse', kv, q, z)
            out = out.transpose(0, 2, 1, 3).reshape(B, N, C)
            return out @ proj_w + proj_b
        y = linear_attention(layer_norm(x, ln1_w, ln1_b), qkv_w, qkv_b, proj_w, proj_b)
        x = x + y
        h = layer_norm(x, ln2_w, ln2_b)
        h = jax.nn.gelu(h @ fc1_w + fc1_b, approximate=False) @ fc2_w + fc2_b
        return x + h

    def _L2_ffn_ref(x, ln1_g, ln1_b, in_w, in_b, out_w, out_b, mlp_w1, mlp_b1, mlp_w2, mlp_b2, ln2_g, ln2_b, gate_w, gate_b, exp_w1, exp_b1, exp_w2, exp_b2):
        import jax, jax.numpy as jnp
        import numpy as np
        E = 768
        H = 12
        D = E // H
        HID = 192
        NEXP = 4
        TOPK = 2
        EPS = 1e-05

        def _ln(x, g, b):
            m = jnp.mean(x, axis=-1, keepdims=True)
            v = jnp.mean(jnp.square(x - m), axis=-1, keepdims=True)
            return (x - m) * jax.lax.rsqrt(v + EPS) * g + b
        B, N, _ = x.shape
        h = _ln(x, ln1_g, ln1_b)
        qkv = h @ in_w.T + in_b
        q, k, v = jnp.split(qkv, 3, axis=-1)
        q = q.reshape(B, N, H, D)
        k = k.reshape(B, N, H, D)
        v = v.reshape(B, N, H, D)
        scores = jnp.einsum('bqhd,bkhd->bhqk', q, k) / jnp.sqrt(jnp.float32(D))
        attn = jax.nn.softmax(scores, axis=-1)
        ctx = jnp.einsum('bhqk,bkhd->bqhd', attn, v).reshape(B, N, E)
        x = x + ctx @ out_w.T + out_b
        x = x + jax.nn.gelu(x @ mlp_w1 + mlp_b1, approximate=False) @ mlp_w2 + mlp_b2
        xm = _ln(x, ln2_g, ln2_b)
        logits = xm @ gate_w.T + gate_b
        topv, topi = jax.lax.top_k(logits, TOPK)
        gates = jax.nn.softmax(topv, axis=-1)
        onehot = jax.nn.one_hot(topi, NEXP, dtype=x.dtype)
        comb = jnp.einsum('bnk,bnke->bne', gates, onehot)
        moe_out = jnp.zeros_like(x)
        for e in range(NEXP):
            he = jax.nn.gelu(xm @ exp_w1[e] + exp_b1[e], approximate=False)
            oe = he @ exp_w2[e] + exp_b2[e]
            moe_out = moe_out + comb[..., e:e + 1] * oe
        return x + moe_out

    def _L3_gnn_ref(x, edge_index, W1, att_src1, att_dst1, b1, W2, att_src2, att_dst2, b2):
        import jax, jax.numpy as jnp
        import numpy as np
        NEG_SLOPE = 0.2

        def _gat_layer(x, W, a_src, a_dst, b, src, dst, n_nodes):
            h = x @ W
            e_src = h @ a_src
            e_dst = h @ a_dst
            e = jax.nn.leaky_relu(e_src[src] + e_dst[dst], NEG_SLOPE)
            m = jax.ops.segment_max(e, dst, num_segments=n_nodes)
            w = jnp.exp(e - m[dst])
            z = jax.ops.segment_sum(w, dst, num_segments=n_nodes)
            alpha = w / z[dst]
            out = jax.ops.segment_sum(h[src] * alpha[:, None], dst, num_segments=n_nodes)
            return out + b
        n_nodes = x.shape[0]
        loops = jnp.arange(n_nodes, dtype=edge_index.dtype)
        src = jnp.concatenate([edge_index[0], loops])
        dst = jnp.concatenate([edge_index[1], loops])
        h = _gat_layer(x, W1, att_src1, att_dst1, b1, src, dst, n_nodes)
        h = jax.nn.relu(h)
        out = _gat_layer(h, W2, att_src2, att_dst2, b2, src, dst, n_nodes)
        return out

    def _L3_mix_ref(x, W_qkv, W_proj, b_proj, gamma, beta, random_features):
        import jax, jax.numpy as jnp
        import numpy as np
        import math
        B, N, C = (8, 256, 768)
        H = 12
        DH = C // H
        M = 256
        LN_EPS = 1e-05

        def _phi(t, random_features):
            norm_sq = 0.5 * jnp.sum(t * t, axis=-1, keepdims=True)
            proj = jnp.einsum('bhnd,md->bhnm', t, random_features)
            return jnp.exp(proj - norm_sq) * (1.0 / math.sqrt(M))
        b, n, c = x.shape
        qkv = (x @ W_qkv).reshape(b, n, 3, H, DH)
        qkv = jnp.transpose(qkv, (2, 0, 3, 1, 4))
        q, k, v = (qkv[0], qkv[1], qkv[2])
        q_p = _phi(q, random_features)
        k_p = _phi(k, random_features)
        kv = jnp.einsum('bhnm,bhnd->bhmd', k_p, v)
        out = jnp.einsum('bhnm,bhmd->bhnd', q_p, kv)
        k_sum = jnp.sum(k_p, axis=2)
        normalizer = jnp.einsum('bhnm,bhm->bhn', q_p, k_sum)[..., None]
        out = out / (normalizer + 1e-06)
        x_attn = jnp.transpose(out, (0, 2, 1, 3)).reshape(b, n, c)
        x_attn = x_attn @ W_proj + b_proj
        y = x + x_attn
        mu = jnp.mean(y, axis=-1, keepdims=True)
        var = jnp.mean(jnp.square(y - mu), axis=-1, keepdims=True)
        return (y - mu) * jax.lax.rsqrt(var + LN_EPS) * gamma + beta

    def _L3_ffn_ref(x, Wg, W1, W2):
        import jax, jax.numpy as jnp
        import numpy as np
        E = 8
        TOP_K = 2
        CAP_RATIO = 1.2
        B, L, D = x.shape
        H = W2.shape[1]
        xf = x.reshape(-1, D)
        N = xf.shape[0]
        capacity = int(CAP_RATIO * N / E)
        logits = xf @ Wg
        scores, idx = jax.lax.top_k(logits, TOP_K)
        weights = jax.nn.softmax(scores, axis=-1)
        xpad = jnp.concatenate([xf, jnp.zeros((1, D), xf.dtype)], axis=0)
        wpad_zero = jnp.zeros((1,), weights.dtype)
        out = jnp.zeros((N, D), x.dtype)
        for k in range(TOP_K):
            ik = idx[:, k]
            onehot = ik[:, None] == jnp.arange(E)[None, :]
            pos = jnp.cumsum(onehot, axis=0) - 1
            posk = jnp.take_along_axis(pos, ik[:, None], axis=1)[:, 0]
            keep = posk < capacity
            buf = jnp.full((E, capacity), N, dtype=jnp.int32)
            buf = buf.at[ik, posk].set(jnp.arange(N, dtype=jnp.int32), mode='drop')
            xg = xpad[buf]
            h = jnp.einsum('ecd,edh->ech', xg, W1)
            act = h[..., :H] * jax.nn.silu(h[..., H:])
            ye = jnp.einsum('ech,ehd->ecd', act, W2)
            wk = jnp.where(keep, weights[:, k], 0.0)
            w_buf = jnp.concatenate([wk, wpad_zero])[buf]
            out = out.at[buf.reshape(-1)].add((w_buf[..., None] * ye).reshape(E * capacity, D), mode='drop')
        return out.reshape(B, L, D)
    edge_index = jnp.stack([src, dst])
    batch0 = jnp.zeros((625,), jnp.int32)
    xn = _layernorm(x, axis=-1)
    x = x + _L0_gnn_ref(xn, edge_index, batch0, edge_weight1, L0_gnn_W_ah, L0_gnn_b_ah, L0_gnn_W0, L0_gnn_a_src0, L0_gnn_a_dst0, L0_gnn_b0, L0_gnn_W1, L0_gnn_a_src1, L0_gnn_a_dst1, L0_gnn_b1, L0_gnn_W2, L0_gnn_a_src2, L0_gnn_a_dst2, L0_gnn_b2, L0_gnn_W_out, L0_gnn_b_out) + _L0_mix_ref(xn[None], L0_mix_w_map, L0_mix_g_k, L0_mix_b_k, L0_mix_g_v, L0_mix_b_v, L0_mix_w_out, L0_mix_b_out)[0]
    x = x + _L0_ffn_ref(_layernorm(x, axis=-1)[None], L0_ffn_phi, L0_ffn_scale, L0_ffn_w1, L0_ffn_b1, L0_ffn_w2, L0_ffn_b2)[0]
    xn = _layernorm(x, axis=-1)
    x = x + _L1_gnn_ref(xn, edge_index, L1_gnn_W, L1_gnn_b) + _L1_mix_ref(xn[None], L1_mix_kqv_w, L1_mix_kqv_b, L1_mix_proj_w, L1_mix_proj_b, L1_mix_w)[0]
    x = x + _L1_ffn_ref(_layernorm(x, axis=-1)[None], L1_ffn_router_w, L1_ffn_w1, L1_ffn_w2)[0]
    xn = _layernorm(x, axis=-1)
    x = x + _L2_gnn_ref(xn, edge_index, L2_gnn_W1, L2_gnn_att_src1, L2_gnn_att_dst1, L2_gnn_b1, L2_gnn_W2, L2_gnn_att_src2, L2_gnn_att_dst2, L2_gnn_b2) + _L2_mix_ref(xn[None], L2_mix_qkv_w, L2_mix_qkv_b, L2_mix_proj_w, L2_mix_proj_b, L2_mix_fc1_w, L2_mix_fc1_b, L2_mix_fc2_w, L2_mix_fc2_b, L2_mix_ln1_w, L2_mix_ln1_b, L2_mix_ln2_w, L2_mix_ln2_b)[0]
    x = x + _L2_ffn_ref(_layernorm(x, axis=-1)[None], L2_ffn_ln1_g, L2_ffn_ln1_b, L2_ffn_in_w, L2_ffn_in_b, L2_ffn_out_w, L2_ffn_out_b, L2_ffn_mlp_w1, L2_ffn_mlp_b1, L2_ffn_mlp_w2, L2_ffn_mlp_b2, L2_ffn_ln2_g, L2_ffn_ln2_b, L2_ffn_gate_w, L2_ffn_gate_b, L2_ffn_exp_w1, L2_ffn_exp_b1, L2_ffn_exp_w2, L2_ffn_exp_b2)[0]
    xn = _layernorm(x, axis=-1)
    x = x + _L3_gnn_ref(xn, edge_index, L3_gnn_W1, L3_gnn_att_src1, L3_gnn_att_dst1, L3_gnn_b1, L3_gnn_W2, L3_gnn_att_src2, L3_gnn_att_dst2, L3_gnn_b2) + _L3_mix_ref(xn[None], L3_mix_W_qkv, L3_mix_W_proj, L3_mix_b_proj, L3_mix_gamma, L3_mix_beta, L3_mix_random_features)[0]
    x = x + _L3_ffn_ref(_layernorm(x, axis=-1)[None], L3_ffn_Wg, L3_ffn_W1, L3_ffn_W2)[0]
    return x

_drawn_inputs = setup_inputs


def setup_inputs(seed=0):
    import zlib

    import numpy as np

    out = dict(_drawn_inputs(seed))
    spreads = {'L0_gnn_b_ah': (0.0, 0.302),
     'L0_gnn_b0': (0.0, 0.1),
     'L0_gnn_b1': (0.0, 0.1),
     'L0_gnn_b2': (0.0, 0.1),
     'L0_gnn_b_out': (0.0, 0.1),
     'L0_mix_g_k': (1.0, 0.2),
     'L0_mix_b_k': (0.0, 0.1),
     'L0_mix_g_v': (1.0, 0.2),
     'L0_mix_b_v': (0.0, 0.1),
     'L0_ffn_b1': (0.0, 0.459),
     'L0_ffn_b2': (0.0, 0.388),
     'L1_gnn_b': (0.0, 0.1),
     'L1_mix_kqv_b': (0.0, 0.614),
     'L1_mix_proj_b': (0.0, 0.1),
     'L2_gnn_b1': (0.0, 0.333),
     'L2_gnn_b2': (0.0, 0.1),
     'L2_mix_qkv_b': (0.0, 0.303),
     'L2_mix_proj_b': (0.0, 0.1),
     'L2_mix_fc1_b': (0.0, 0.273),
     'L2_mix_fc2_b': (0.0, 0.1),
     'L2_mix_ln1_w': (1.0, 0.6),
     'L2_mix_ln1_b': (0.0, 0.549),
     'L2_mix_ln2_w': (1.0, 0.2),
     'L2_mix_ln2_b': (0.0, 0.452),
     'L2_ffn_ln1_g': (1.0, 0.6),
     'L2_ffn_ln1_b': (0.0, 0.799),
     'L2_ffn_in_b': (0.0, 0.434),
     'L2_ffn_out_b': (0.0, 0.268),
     'L2_ffn_mlp_b1': (0.0, 0.8),
     'L2_ffn_mlp_b2': (0.0, 0.1),
     'L2_ffn_ln2_g': (1.0, 0.6),
     'L2_ffn_ln2_b': (0.0, 0.8),
     'L2_ffn_gate_b': (0.0, 0.8),
     'L2_ffn_exp_b1': (0.0, 0.8),
     'L2_ffn_exp_b2': (0.0, 0.36),
     'L3_gnn_b1': (0.0, 0.614),
     'L3_gnn_b2': (0.0, 0.355),
     'L3_mix_b_proj': (0.0, 0.344),
     'L3_mix_gamma': (1.0, 0.2),
     'L3_mix_beta': (0.0, 0.365)}
    factors = {'L0_gnn_a_src0': 8.0,
     'L0_gnn_a_dst0': 8.0,
     'L0_gnn_a_src1': 8.0,
     'L0_gnn_a_dst1': 8.0,
     'L0_gnn_a_src2': 8.0,
     'L0_gnn_a_dst2': 8.0,
     'L0_mix_b_out': 2.774,
     'L0_ffn_phi': 8.0,
     'L0_ffn_w1': 8.0,
     'L0_ffn_w2': 5.514,
     'L2_gnn_att_src1': 2.849,
     'L2_gnn_att_dst1': 8.0,
     'L2_gnn_att_src2': 8.0,
     'L2_gnn_att_dst2': 8.0,
     'L2_ffn_exp_w1': 2.848,
     'L3_gnn_att_src1': 5.627,
     'L3_gnn_att_dst1': 8.0,
     'L3_gnn_att_src2': 8.0,
     'L3_gnn_att_dst2': 8.0,
     'L3_mix_W_qkv': 8.0,
     'L3_mix_W_proj': 8.0,
     'L3_ffn_Wg': 8.0,
     'L3_ffn_W1': 8.0,
     'L3_ffn_W2': 8.0,
     'L1_mix_kqv_w': 8.0,
     'L1_mix_proj_w': 8.0,
     'L1_mix_w': 8.0}
    for name, (base, spread) in spreads.items():
        noise = np.random.default_rng([zlib.crc32(name.encode()), seed]).standard_normal(out[name].shape)
        drawn = base * np.exp(spread * noise) if base else spread * noise
        out[name] = jnp.asarray(drawn.astype(out[name].dtype))
    for name, factor in factors.items():
        out[name] = (out[name] * factor).astype(out[name].dtype)
    return out
```

```python
from contextlib import ExitStack

import concourse.bass as bass
from concourse import mybir

F32 = mybir.dt.float32
BF16 = mybir.dt.bfloat16
F16 = mybir.dt.float16
I32 = mybir.dt.int32
ALU = mybir.AluOpType
ACT = mybir.ActivationFunctionType
AX = mybir.AxisListType

N, D, E = 625, 768, 20000
TP = 125
NT = N // TP
KC = D // 128
HALVES = ((0, 3), (3, 5))
UNIT = 384
BUF = 3904
BANKS = 8
MASKED = -1.0e30
SLOPE = 0.2


class Ticks:

    def __init__(self, sem):
        self.sem, self.planned, self.issued = sem, 0, 0

    def reserve(self, n):
        base = self.planned
        self.planned += n
        return base

    def one(self):
        self.issued += 1
        return 1


class Load:

    def __init__(self, src, dst, sem, value, before):
        self.src, self.dst, self.sem, self.value, self.before, self.used = src, dst, sem, value, before, None


class Slot:

    def __init__(self, buf, sem):
        self.buf, self.sem, self.value, self.last = buf, sem, 0, None

    def take(self, n):
        before, base = self.last, self.value
        self.value += 16 * n
        return before, base


class Net:

    def __init__(self, nc, ctx, ins):
        self.nc, self.ins = nc, ins
        sb = lambda name, shape, dt=F32: ctx.enter_context(nc.sbuf_tensor(name, shape, dt))
        sem = lambda name: ctx.enter_context(nc.semaphore(name))
        self.pe, self.act, self.dve, self.pool = (Ticks(sem(n)) for n in ("pe_done", "act_done", "dve_done", "pool_done"))
        self.const_landed, self.stored = sem("const_landed"), sem("stored")
        self.ps = ctx.enter_context(nc.psum_tensor("ps", [128, BANKS, 512], F32))
        self.R, self.XT = sb("resid", [128, BUF]), sb("xT", [128, BUF])
        self.G = [sb(f"buf{i}", [128, BUF]) for i in range(6)]
        self.counts = sb("edge_counts", [128, NT, N])
        self.mask = sb("edge_mask", [128, NT, N], BF16)
        self.wslot = [sb(f"weights{i}", [128, 6 * UNIT]) for i in range(4)]
        self.wsem = [sem(f"weights_landed{i}") for i in range(4)]
        self.rslot = [sb(f"row{i}", [128, D]) for i in range(4)]
        self.rsem = [sem(f"row_landed{i}") for i in range(4)]
        self.ident = sb("ident", [128, 128])
        self.cols = sb("bias_cols", [128, 96])
        self.kv = sb("kv", [128, 24 * 65])
        self.fw = sb("feature_weights", [128, D])
        self.fn = sb("feature_norms", [128, 512])
        self.asb = sb("a_src_rows", [128, N])
        self.st = sb("stats", [128, 640])
        self.ones, self.zeros, self.iota64 = sb("ones", [128, 128]), sb("zeros", [128, UNIT]), sb("iota64", [128, 64])
        self.lnc, self.slot_scale = sb("lnc", [128, 2]), sb("slot_scale", [128, 1])
        self.stages, self.loads = [], []
        self.wring = [Slot(a, s) for a, s in zip(self.wslot, self.wsem)]
        self.rring = [Slot(a, s) for a, s in zip(self.rslot, self.rsem)]
        self.sem = sem
        self.freed, self.nbank = {}, 0
        self.consts, self.ncol = [], 0

    def now(self):
        return [(t.sem, t.planned) for t in (self.pe, self.act, self.dve, self.pool)]

    def add(self, stage):
        self.stages.append(stage)
        return stage

    def bank(self):
        self.nbank += 1
        return self.nbank - 1

    def _load(self, src, ring, shape):
        slot = ring.pop(0)
        ring.append(slot)
        p, c, w = shape
        before, base = slot.take(1)
        load = Load(src, slot.buf[:p, 0:c * w].rearrange("p (c w) -> p c w", c=c), slot.sem, base + 16, before)
        slot.last = load
        self.loads.append(load)
        return load

    def into(self, dst, src, after):
        free = Load(None, None, None, 0, None)
        free.used = after
        load = Load(src, dst, self.sem(f"landed_{len(self.loads)}"), 16, free)
        self.loads.append(load)
        return load

    def weights(self, src, kp=128):
        k, n = src.shape
        return self._load(src.rearrange("(c p) n -> p c n", p=kp), self.wring, (kp, k // kp, n))

    def row(self, src):
        n = src.shape[1]
        return self._load(src.to_broadcast([128, n]).unsqueeze(1), self.rring, (128, 1, n))

    def rows(self, src):
        return self._load(src.unsqueeze(1), self.rring, (src.shape[0], 1, src.shape[1]))

    def const(self, dst, src):
        self.consts.append((dst, src))

    def col(self, name, parts=128):
        src = self.ins[name]
        n = src.shape[1]
        dst = self.cols[:parts, self.ncol:self.ncol + n]
        self.ncol += n
        self.const(dst, src)
        return dst

    def tok(self, buf, w=D):
        return buf[:TP, 0:NT * w].rearrange("p (t w) -> p t w", t=NT)

    def feat(self, buf, c=KC, p=128):
        return buf[:p, 0:c * N].rearrange("p (c n) -> p c n", c=c)


class Stage:

    def __init__(self, net, after=None):
        self.net, self.nc = net, net.nc
        self.after = net.now() if after is None else after
        self.loads = []
        self.g = []

    def take(self, pe=0, act=0, dve=0, pool=0):
        n = self.net
        self.p0, self.a0, self.d0, self.l0 = (t.reserve(k) for t, k in ((n.pe, pe), (n.act, act), (n.dve, dve), (n.pool, pool)))
        self.done = n.now()
        for load in self.loads:
            load.used = self.done
        n.add(self)

    def groups(self, n, evac):
        net = self.net
        ca = cd = 0
        a0, d0 = net.act.planned, net.dve.planned
        for i in range(n):
            b, e = net.bank(), evac[i % len(evac)]
            if e == "a":
                ca += 1
                net.freed[b] = (net.act.sem, a0 + ca)
            else:
                cd += 1
                net.freed[b] = (net.dve.sem, d0 + cd)
            self.g.append((b, e))
        return ca, cd

    def free(self, b):
        return self.net.freed[b - BANKS]

    def begin(self, eng):
        for sem, value in self.after:
            if value > 0:
                eng.wait_ge(sem, value)

    def landed(self, eng):
        for load in self.loads:
            eng.wait_ge(load.sem, load.value)

    def tensor(self, pe):
        pass

    def scalar(self, act):
        pass

    def vector(self, dve):
        pass

    def gpsimd(self, pool):
        pass


def evacuate(nc, eng, kind, out, ps, bias=None, gate=None, add=None):
    if eng == "a":
        func = {"copy": ACT.Identity, "relu": ACT.Relu, "gelu": ACT.Gelu, "tanh_gelu": ACT.Gelu_apprx_tanh,
                "silu": ACT.Silu, "square": ACT.Square}[kind]
        if bias is None:
            return nc.scalar.activation(out, ps, func)
        return nc.scalar.activation(out, ps, func, bias=bias)
    if kind == "copy":
        if bias is None:
            return nc.vector.tensor_copy(out, ps)
        return nc.vector.tensor_scalar(out, ps, bias, None, ALU.add)
    if kind == "relu":
        if bias is None:
            return nc.vector.tensor_scalar(out, ps, 0.0, None, ALU.max)
        return nc.vector.tensor_scalar(out, ps, bias, 0.0, ALU.add, ALU.max)
    if kind == "mul":
        return nc.vector.tensor_tensor(out, ps, add, ALU.mult)
    if kind == "add":
        return nc.vector.tensor_tensor(out, ps, add, ALU.add)
    if kind == "gate":
        return nc.vector.scalar_tensor_tensor(out=out, in0=ps, scalar=gate, in1=add, op0=ALU.mult, op1=ALU.add)
    return nc.vector.tensor_scalar(out, ps, gate, None, ALU.mult)


class LinearT(Stage):

    def __init__(self, net, xT, parts, evac="ad", after=None):
        super().__init__(net, after)
        self.xT, self.parts = xT, parts
        a, d = self.groups(2 * len(parts), evac)
        self.loads = list(dict.fromkeys(q[0] for q in parts))
        self.take(pe=2 * len(parts), act=a, dve=d)
        for n, q in enumerate(parts):
            q[0].used = [(net.pe.sem, self.p0 + 2 * n + 2)]

    def tensor(self, pe):
        self.begin(pe)
        kp, kc = self.xT.shape[0], self.xT.shape[1]
        i = 0
        for load, c0, w, out, bias, kind in self.parts:
            pe.wait_ge(load.sem, load.value)
            for t0, t1 in HALVES:
                b = self.g[i][0]
                if b >= BANKS:
                    pe.wait_ge(*self.free(b))
                for k in range(kc):
                    mm = self.nc.tensor.matmul(self.net.ps[:w, b % BANKS, 0:(t1 - t0) * TP], load.dst[:kp, k, c0:c0 + w],
                                               self.xT[:, k, t0 * TP:t1 * TP], start=(k == 0), stop=(k == kc - 1))
                mm.then_inc(self.net.pe.sem, self.net.pe.one())
                i += 1

    def evac(self, eng, letter, ticks):
        self.begin(eng)
        for i, (b, e) in enumerate(self.g):
            if e == letter:
                load, c0, w, out, bias, kind = self.parts[i // 2]
                t0, t1 = HALVES[i % 2]
                eng.wait_ge(self.net.pe.sem, self.p0 + i + 1)
                evacuate(self.nc, letter, kind, out[:, t0 * TP:t1 * TP], self.net.ps[:w, b % BANKS, 0:(t1 - t0) * TP],
                         bias=bias).then_inc(ticks.sem, ticks.one())

    def scalar(self, act):
        self.evac(act, "a", self.net.act)

    def vector(self, dve):
        self.evac(dve, "d", self.net.dve)


class Linear(Stage):

    def __init__(self, net, xT, units, evac="ad", after=None, rows=()):
        super().__init__(net, after)
        self.xT, self.units, self.rows = xT, units, rows
        a, d = self.groups(NT * len(units), evac)
        self.loads = list(rows)
        self.take(pe=NT * len(units), act=a, dve=d)
        for n, u in enumerate(units):
            u["load"].used = [(net.pe.sem, self.p0 + NT * (n + 1))]

    def tensor(self, pe):
        self.begin(pe)
        kc = self.xT.shape[1]
        i = 0
        for u in self.units:
            load = u["load"]
            pe.wait_ge(load.sem, load.value)
            for t in range(NT):
                b = self.g[i][0]
                if b >= BANKS:
                    pe.wait_ge(*self.free(b))
                for k in range(kc):
                    mm = self.nc.tensor.matmul(self.net.ps[:TP, b % BANKS, 0:u["w"]], self.xT[:, k, t * TP:(t + 1) * TP],
                                               load.dst[:, k, u.get("c0", 0):u.get("c0", 0) + u["w"]],
                                               start=(k == 0), stop=(k == kc - 1))
                mm.then_inc(self.net.pe.sem, self.net.pe.one())
                i += 1

    def evac(self, eng, letter, ticks):
        self.begin(eng)
        for row in self.rows:
            eng.wait_ge(row.sem, row.value)
        for i, (b, e) in enumerate(self.g):
            if e == letter:
                u, t = self.units[i // NT], i % NT
                ps = self.net.ps[:TP, b % BANKS, 0:u["w"]]
                out, add = u["out"][:, t], u.get("add")
                if len(out.shape) == 3:
                    ps = ps.rearrange("p (h c) -> p h c", h=out.shape[1])
                if add is not None:
                    add = add[:, t] if u.get("by_tile", True) else add
                gate = u["gate"][:, t:t + 1] if "gate" in u else None
                eng.wait_ge(self.net.pe.sem, self.p0 + i + 1)
                evacuate(self.nc, letter, u["kind"], out, ps, add=add, gate=gate).then_inc(ticks.sem, ticks.one())

    def scalar(self, act):
        self.evac(act, "a", self.net.act)

    def vector(self, dve):
        self.evac(dve, "d", self.net.dve)


class ToFeatures(Stage):

    def __init__(self, net, x, out, func="copy", evac="ad", after=None):
        super().__init__(net, after)
        self.x, self.out, self.func = x, out, func
        self.c = out.shape[1]
        a, d = self.groups(2 * self.c, evac)
        self.take(pe=2 * self.c, act=a, dve=d)

    def tensor(self, pe):
        self.begin(pe)
        w = self.out.shape[0]
        for i, (b, e) in enumerate(self.g):
            c, (t0, t1) = i // 2, HALVES[i % 2]
            if b >= BANKS:
                pe.wait_ge(*self.free(b))
            for t in range(t0, t1):
                mm = self.nc.tensor.transpose(self.net.ps[:w, b % BANKS, (t - t0) * TP:(t - t0 + 1) * TP],
                                              self.x[:, t, c * w:(c + 1) * w], self.net.ident[:TP, :TP])
            mm.then_inc(self.net.pe.sem, self.net.pe.one())

    def evac(self, eng, letter, ticks):
        self.begin(eng)
        w = self.out.shape[0]
        for i, (b, e) in enumerate(self.g):
            if e == letter:
                c, (t0, t1) = i // 2, HALVES[i % 2]
                eng.wait_ge(self.net.pe.sem, self.p0 + i + 1)
                evacuate(self.nc, letter, self.func, self.out[:, c, t0 * TP:t1 * TP],
                         self.net.ps[:w, b % BANKS, 0:(t1 - t0) * TP]).then_inc(ticks.sem, ticks.one())

    def scalar(self, act):
        self.evac(act, "a", self.net.act)

    def vector(self, dve):
        self.evac(dve, "d", self.net.dve)


class LayerNorm(Stage):

    def __init__(self, net, x, out, eps, gamma=None, beta=None, after=None):
        super().__init__(net, after)
        self.x, self.out, self.eps, self.gamma, self.beta = x, out, eps, gamma, beta
        self.loads = [r for r in (gamma, beta) if r]
        self.stats = net.st[:TP, 0:60].rearrange("p (t s) -> p t s", t=NT)
        self.mv = net.st[:TP, 60:70].rearrange("p (t s) -> p t s", t=NT)
        self.rstd = net.st[:TP, 70:75]
        self.take(dve=3 * NT + 2 + NT + (NT if gamma else 0), act=1, pool=NT if gamma else 0)

    def vector(self, dve):
        self.begin(dve)
        done = self.net.dve
        for t in range(NT):
            for j in range(2):
                self.nc.vector.bn_stats(self.stats[:, t, 6 * j:6 * j + 6], self.x[:, t, j * UNIT:(j + 1) * UNIT]).then_inc(done.sem, done.one())
        for t in range(NT):
            dve.wait_ge(done.sem, self.d0 + 2 * t + 2)
            self.nc.vector.bn_aggr(self.mv[:, t, :], self.stats[:, t, :]).then_inc(done.sem, done.one())
        dve.wait_ge(done.sem, done.issued)
        self.nc.vector.tensor_scalar(self.rstd, self.mv[:, :, 1], self.eps, None, ALU.add).then_inc(done.sem, done.one())
        dve.wait_ge(self.net.act.sem, self.a0 + 1)
        self.nc.vector.reciprocal(self.rstd, self.rstd).then_inc(done.sem, done.one())
        dve.wait_ge(done.sem, done.issued)
        for t in range(NT):
            self.nc.vector.tensor_scalar(self.out[:, t], self.x[:, t], self.mv[:, t, 0:1], self.rstd[:, t:t + 1],
                                         ALU.subtract, ALU.mult).then_inc(done.sem, done.one())
        if self.gamma:
            self.landed(dve)
            for t in range(NT):
                dve.wait_ge(done.sem, self.d0 + 3 * NT + 2 + t + 1)
                self.nc.vector.tensor_tensor(self.out[:, t], self.out[:, t], self.gamma.dst[:TP, 0], ALU.mult).then_inc(done.sem, done.one())

    def scalar(self, act):
        self.begin(act)
        act.wait_ge(self.net.dve.sem, self.d0 + 3 * NT + 1)
        self.nc.scalar.activation(self.rstd, self.rstd, ACT.Sqrt).then_inc(self.net.act.sem, self.net.act.one())

    def gpsimd(self, pool):
        if not self.gamma:
            return
        self.begin(pool)
        self.landed(pool)
        for t in range(NT):
            pool.wait_ge(self.net.dve.sem, self.d0 + 4 * NT + 2 + t + 1)
            self.nc.gpsimd.tensor_tensor(self.out[:, t], self.out[:, t], self.beta.dst[:TP, 0], ALU.add).then_inc(self.net.pool.sem, self.net.pool.one())


class AddRow(Stage):

    def __init__(self, net, x, row, after=None):
        super().__init__(net, after)
        self.x, self.row, self.loads = x, row, [row]
        self.take(pool=NT)

    def gpsimd(self, pool):
        self.begin(pool)
        self.landed(pool)
        for t in range(NT):
            self.nc.gpsimd.tensor_tensor(self.x[:, t], self.x[:, t], self.row.dst[:TP, 0], ALU.add).then_inc(self.net.pool.sem, self.net.pool.one())


class ReluAdd(Stage):

    def __init__(self, net, x, y, after=None):
        super().__init__(net, after)
        self.x, self.y = x, y
        self.take(dve=NT)

    def vector(self, dve):
        self.begin(dve)
        for t in range(NT):
            self.nc.vector.scalar_tensor_tensor(out=self.x[:, t], in0=self.y[:, t], scalar=0.0, in1=self.x[:, t],
                                                op0=ALU.max, op1=ALU.add).then_inc(self.net.dve.sem, self.net.dve.one())


class Add(Stage):

    def __init__(self, net, out, x, y, after=None):
        super().__init__(net, after)
        self.out, self.x, self.y = out, x, y
        self.take(pool=NT)

    def gpsimd(self, pool):
        self.begin(pool)
        for t in range(NT):
            self.nc.gpsimd.tensor_tensor(self.out[:, t], self.x[:, t], self.y[:, t], ALU.add).then_inc(self.net.pool.sem, self.net.pool.one())


class EdgeCounts(Stage):
    CH = E // TP
    DEPTH = 4

    def __init__(self, net, after=None):
        super().__init__(net, after)
        g = net.G
        self.idx_i = g[0][:TP, 0:2 * self.CH].bitcast(I32).rearrange("p (s c) -> p s c", s=2)
        self.idx = g[1][:TP, 0:2 * self.CH].rearrange("p (s c) -> p s c", s=2)
        self.iota = g[2][:TP, 0:N]
        self.iota16 = g[2][:TP, N:N + 320].bitcast(F16)[:, 0:N]
        self.hot = [[g[3 + s][:TP, 320 * j:320 * j + 320].bitcast(F16)[:, 0:N] for s in range(2)] for j in range(self.DEPTH)]
        self.zero = g[5][:TP, 0:320].bitcast(F16)[:, 0:N]
        for s, name in enumerate(("src", "dst")):
            net.const(self.idx_i[:, s, :], net.ins[name].rearrange("(p c) -> p c", p=TP))
        net.const(self.iota, net.ins["iota"].to_broadcast([TP, N]))
        while net.nbank % BANKS:
            net.freed[net.bank()] = (net.dve.sem, net.dve.planned)
        n_dve = 3 + 2 * self.CH
        for i in range(BANKS):
            net.freed[net.bank()] = (net.dve.sem, net.dve.planned + n_dve + 2 * NT)
        self.take(pe=1 + self.CH + 1, dve=n_dve + 2 * NT)

    def products(self, lhs, rhs, start, stop):
        ps = self.net.ps
        for t in range(NT):
            self.nc.tensor.matmul(ps[:TP, t, 0:500], lhs[:, t * TP:(t + 1) * TP], rhs[:, 0:500], start=start, stop=stop, skip_group_check=True)
            b, c = (5, t * TP) if t < 4 else (6, 0)
            mm = self.nc.tensor.matmul(ps[:TP, b, c:c + TP], lhs[:, t * TP:(t + 1) * TP], rhs[:, 500:625], start=start, stop=stop, skip_group_check=True)
        return mm

    def tensor(self, pe):
        self.begin(pe)
        done, dve = self.net.pe, self.net.dve
        pe.wait_ge(dve.sem, self.d0 + 3)
        self.products(self.zero, self.zero, True, False).then_inc(done.sem, done.one())
        with self.nc.tensor.Fori(0, self.CH // self.DEPTH) as i:
            for j in range(self.DEPTH):
                pe.wait_ge(dve.sem, i * (2 * self.DEPTH) + (self.d0 + 3 + 2 * j + 2))
                self.products(self.hot[j][1], self.hot[j][0], False, False).then_inc(done.sem, 1)
        done.issued += self.CH
        self.products(self.zero, self.zero, False, True).then_inc(done.sem, done.one())

    def vector(self, dve):
        self.begin(dve)
        nc, done, pe = self.nc, self.net.dve, self.net.pe
        nc.vector.memset(self.zero, 0.0).then_inc(done.sem, done.one())
        nc.vector.tensor_copy(self.idx, self.idx_i).then_inc(done.sem, done.one())
        nc.vector.tensor_copy(self.iota16, self.iota).then_inc(done.sem, done.one())
        dve.wait_ge(done.sem, done.issued)
        for j in range(self.DEPTH):
            for s in range(2):
                nc.vector.tensor_scalar(self.hot[j][s], self.iota16, self.idx[:, s, j:j + 1], None, ALU.is_equal).then_inc(done.sem, 1)
        with nc.vector.Fori(1, self.CH // self.DEPTH) as i:
            for j in range(self.DEPTH):
                dve.wait_ge(pe.sem, i * self.DEPTH + (self.p0 + 1 + j + 1 - self.DEPTH))
                for s in range(2):
                    nc.vector.tensor_scalar(self.hot[j][s], self.iota16, self.idx[:, s, bass.ds(i * self.DEPTH + j, 1)], None,
                                            ALU.is_equal).then_inc(done.sem, 1)
        done.issued += 2 * self.CH
        dve.wait_ge(pe.sem, self.p0 + self.CH + 2)
        ps, counts = self.net.ps, self.net.counts
        for t in range(NT):
            nc.vector.tensor_copy(counts[:TP, t, 0:500], ps[:TP, t, 0:500]).then_inc(done.sem, done.one())
            b, c = (5, t * TP) if t < 4 else (6, 0)
            nc.vector.tensor_copy(counts[:TP, t, 500:625], ps[:TP, b, c:c + TP]).then_inc(done.sem, done.one())


class SelfLoops(Stage):

    def __init__(self, net, op, after=None):
        super().__init__(net, after)
        self.op = op
        self.take(dve=2 * NT)

    def vector(self, dve):
        self.begin(dve)
        nc, done, counts = self.nc, self.net.dve, self.net.counts
        for t in range(NT):
            diag = counts[:TP, t, t * TP:(t + 1) * TP]
            nc.vector.tensor_tensor(diag, diag, self.net.ident[:TP, :TP], self.op).then_inc(done.sem, done.one())
        dve.wait_ge(done.sem, done.issued)
        for t in range(NT):
            nc.vector.tensor_scalar(self.net.mask[:TP, t, :], counts[:TP, t, :], 0.0, MASKED, ALU.is_equal, ALU.mult).then_inc(done.sem, done.one())


class GatCoefs(Stage):

    def __init__(self, net, h, heads, c, head0, a_src, a_dst, coef, scratch, after=None):
        super().__init__(net, after)
        self.h, self.heads, self.c, self.head0, self.coef, self.scratch = h, heads, c, head0, coef, scratch
        self.loads = [a_src, a_dst]
        self.take(dve=2 * NT * heads)

    def vector(self, dve):
        self.begin(dve)
        self.landed(dve)
        done = self.net.dve
        for s in range(2):
            for t in range(NT):
                for hd in range(self.heads):
                    cs = slice(hd * self.c, (hd + 1) * self.c)
                    n = (s * NT + t) * self.heads + hd
                    if n > 1:
                        dve.wait_ge(done.sem, self.d0 + n - 1)
                    self.nc.vector.tensor_tensor_reduce(
                        out=self.scratch[:TP, (n % 2) * D:(n % 2) * D + self.c], in0=self.h[:, t, cs],
                        in1=self.loads[s].dst[:TP, 0, cs], scale=1.0, scalar=0.0, op0=ALU.mult, op1=ALU.add,
                        accum_out=self.coef[:, s, self.head0 + hd, t:t + 1]).then_inc(done.sem, done.one())


class GatScores(Stage):

    def __init__(self, net, coef, head, P, T, rinv, eps, after=None):
        super().__init__(net, after)
        self.src, self.dst, self.P, self.T, self.rinv, self.eps = coef[:, 0, head], coef[:, 1, head], P, T, rinv, eps
        self.groups(2, "a")
        o = 80
        self.mx, self.b1, self.b2, self.sum = (net.st[:TP, o + 5 * k:o + 5 * k + 5] for k in range(4))
        self.take(pe=2, act=2 + 2 * NT, dve=NT + 4 + NT + 2, pool=NT)
        self.relu_bias, self.exp_bias = self.b1, self.b2

    def tensor(self, pe):
        self.begin(pe)
        for i, (b, _) in enumerate(self.g):
            t0, t1 = HALVES[i]
            if b >= BANKS:
                pe.wait_ge(*self.free(b))
            for t in range(t0, t1):
                mm = self.nc.tensor.matmul(self.net.ps[:TP, b % BANKS, (t - t0) * TP:(t - t0 + 1) * TP],
                                           self.src[:, t:t + 1].to_broadcast([TP, TP]), self.net.ident[:TP, :TP], start=True, stop=True)
            mm.then_inc(self.net.pe.sem, self.net.pe.one())

    def scalar(self, act):
        self.begin(act)
        done = self.net.act
        for i, (b, _) in enumerate(self.g):
            t0, t1 = HALVES[i]
            act.wait_ge(self.net.pe.sem, self.p0 + i + 1)
            self.nc.scalar.activation(self.net.asb[:TP, t0 * TP:t1 * TP], self.net.ps[:TP, b % BANKS, 0:(t1 - t0) * TP],
                                      ACT.Identity).then_inc(done.sem, done.one())
        act.wait_ge(self.net.dve.sem, self.d0 + NT + 4)
        for t in range(NT):
            self.nc.scalar.activation(self.P[:, t], self.T[:, t], ACT.Relu, bias=self.b1[:, t:t + 1],
                                      scale=(1 - SLOPE) / SLOPE).then_inc(done.sem, done.one())
        for t in range(NT):
            act.wait_ge(self.net.pool.sem, self.l0 + t + 1)
            self.nc.scalar.activation(self.P[:, t], self.P[:, t], ACT.Exp, bias=self.b2[:, t:t + 1]).then_inc(done.sem, done.one())

    def vector(self, dve):
        self.begin(dve)
        nc, done = self.nc, self.net.dve
        dve.wait_ge(self.net.act.sem, self.a0 + 2)
        for t in range(NT):
            nc.vector.tensor_tensor_reduce(out=self.T[:, t], in0=self.net.asb[:TP, :], in1=self.net.mask[:TP, t, :], scale=SLOPE,
                                           scalar=2 * MASKED, op0=ALU.add, op1=ALU.max, accum_out=self.mx[:, t:t + 1]).then_inc(done.sem, done.one())
        nc.vector.tensor_scalar(self.b1, self.dst, 1 - SLOPE, None, ALU.mult).then_inc(done.sem, done.one())
        dve.wait_ge(done.sem, done.issued)
        nc.vector.scalar_tensor_tensor(out=self.b2, in0=self.dst, scalar=SLOPE, in1=self.mx, op0=ALU.mult, op1=ALU.add).then_inc(done.sem, done.one())
        dve.wait_ge(done.sem, done.issued)
        nc.vector.scalar_tensor_tensor(out=self.mx, in0=self.b2, scalar=1 / SLOPE, in1=self.b2, op0=ALU.mult, op1=ALU.max).then_inc(done.sem, done.one())
        dve.wait_ge(done.sem, done.issued)
        nc.vector.scalar_tensor_tensor(out=self.b2, in0=self.dst, scalar=SLOPE, in1=self.mx, op0=ALU.mult, op1=ALU.subtract).then_inc(done.sem, done.one())
        for t in range(NT):
            dve.wait_ge(self.net.act.sem, self.a0 + 2 + NT + t + 1)
            nc.vector.tensor_tensor_reduce(out=self.P[:, t], in0=self.P[:, t], in1=self.net.counts[:TP, t, :], scale=1.0,
                                           scalar=0.0, op0=ALU.mult, op1=ALU.add, accum_out=self.sum[:, t:t + 1]).then_inc(done.sem, done.one())
        dve.wait_ge(done.sem, done.issued)
        nc.vector.tensor_scalar(self.sum, self.sum, self.eps, None, ALU.add).then_inc(done.sem, done.one())
        dve.wait_ge(done.sem, done.issued)
        nc.vector.reciprocal(self.rinv, self.sum).then_inc(done.sem, done.one())

    def gpsimd(self, pool):
        self.begin(pool)
        for t in range(NT):
            pool.wait_ge(self.net.act.sem, self.a0 + 2 + t + 1)
            self.nc.gpsimd.tensor_tensor(self.P[:, t], self.P[:, t], self.T[:, t], ALU.add).then_inc(self.net.pool.sem, self.net.pool.one())


class Apply(Stage):

    def __init__(self, net, P, PT, h, rinv, out, add=None, by_tile=True, rows=(), after=None, evac="ad"):
        super().__init__(net, after)
        self.P, self.PT, self.h, self.rinv, self.out, self.add, self.by_tile, self.rows = P, PT, h, rinv, out, add, by_tile, rows
        self.loads = list(rows)
        c = h.shape[2]
        self.w = c if c <= 512 else UNIT
        self.nw = c // self.w
        a, d = self.groups(2 * NT, evac)
        self.turned = [(net.act.sem, net.act.planned + a), (net.dve.sem, net.dve.planned + d)]
        net.dve.planned += d
        _, d2 = self.groups(NT * self.nw, "d")
        net.dve.planned -= d
        self.d_turn = d
        self.take(pe=2 * NT + NT * self.nw, act=a, dve=d + d2)

    def tensor(self, pe):
        self.begin(pe)
        nc, done = self.nc, self.net.pe
        for i in range(2 * NT):
            b, s, (t0, t1) = self.g[i][0], i // 2, HALVES[i % 2]
            if b >= BANKS:
                pe.wait_ge(*self.free(b))
            for t in range(t0, t1):
                mm = nc.tensor.transpose(self.net.ps[:TP, b % BANKS, (t - t0) * TP:(t - t0 + 1) * TP],
                                         self.P[:, t, s * TP:(s + 1) * TP], self.net.ident[:TP, :TP])
            mm.then_inc(done.sem, done.one())
        for sem, value in self.turned:
            pe.wait_ge(sem, value)
        for i in range(NT * self.nw):
            b, t, j = self.g[2 * NT + i][0], i // self.nw, i % self.nw
            if b >= BANKS:
                pe.wait_ge(*self.free(b))
            for s in range(NT):
                mm = nc.tensor.matmul(self.net.ps[:TP, b % BANKS, 0:self.w], self.PT[:, s, t * TP:(t + 1) * TP],
                                      self.h[:, s, j * self.w:(j + 1) * self.w], start=(s == 0), stop=(s == NT - 1))
            mm.then_inc(done.sem, done.one())

    def turn(self, eng, letter, ticks):
        self.begin(eng)
        for i in range(2 * NT):
            b, e = self.g[i]
            if e == letter:
                s, (t0, t1) = i // 2, HALVES[i % 2]
                eng.wait_ge(self.net.pe.sem, self.p0 + i + 1)
                evacuate(self.nc, letter, "copy", self.PT[:, s, t0 * TP:t1 * TP],
                         self.net.ps[:TP, b % BANKS, 0:(t1 - t0) * TP]).then_inc(ticks.sem, ticks.one())

    def scalar(self, act):
        self.turn(act, "a", self.net.act)

    def vector(self, dve):
        self.turn(dve, "d", self.net.dve)
        self.landed(dve)
        done = self.net.dve
        for i in range(NT * self.nw):
            b, t, j = self.g[2 * NT + i][0], i // self.nw, i % self.nw
            cs = slice(j * self.w, (j + 1) * self.w)
            ps, out, r = self.net.ps[:TP, b % BANKS, 0:self.w], self.out[:, t, cs], self.rinv[:, t:t + 1]
            dve.wait_ge(self.net.pe.sem, self.p0 + 2 * NT + i + 1)
            if self.add is None:
                evacuate(self.nc, "d", "scale", out, ps, gate=r).then_inc(done.sem, done.one())
            else:
                add = self.add[:, t, cs] if self.by_tile else self.add[:, cs]
                evacuate(self.nc, "d", "gate", out, ps, gate=r, add=add).then_inc(done.sem, done.one())


class HeadNorm(Stage):

    def __init__(self, net, x, tmp, out, gamma, beta, eps, after=None):
        super().__init__(net, after)
        self.x, self.tmp, self.out, self.eps, self.loads = x, tmp, out, eps, [gamma, beta]
        self.mean, self.var = net.st[:TP, 270:330], net.st[:TP, 330:390]
        self.take(dve=9, act=2)

    def bc(self, small):
        return small.unsqueeze(2).to_broadcast([TP, 60, 64])

    def row(self, load):
        return load.dst[:TP, :, :].to_broadcast([TP, 60, 64])

    def vector(self, dve):
        self.begin(dve)
        nc, done, act = self.nc, self.net.dve, self.net.act
        nc.vector.tensor_reduce(self.mean, self.x, AX.X, ALU.add).then_inc(done.sem, done.one())
        dve.wait_ge(done.sem, done.issued)
        nc.vector.tensor_scalar(self.mean, self.mean, 1.0 / 64, None, ALU.mult).then_inc(done.sem, done.one())
        dve.wait_ge(done.sem, done.issued)
        nc.vector.tensor_tensor(self.x, self.x, self.bc(self.mean), ALU.subtract).then_inc(done.sem, done.one())
        dve.wait_ge(act.sem, self.a0 + 1)
        nc.vector.tensor_reduce(self.var, self.tmp, AX.X, ALU.add).then_inc(done.sem, done.one())
        dve.wait_ge(done.sem, done.issued)
        nc.vector.tensor_scalar(self.var, self.var, 1.0 / 64, self.eps, ALU.mult, ALU.add).then_inc(done.sem, done.one())
        dve.wait_ge(act.sem, self.a0 + 2)
        nc.vector.reciprocal(self.var, self.var).then_inc(done.sem, done.one())
        dve.wait_ge(done.sem, done.issued)
        nc.vector.tensor_tensor(self.x, self.x, self.bc(self.var), ALU.mult).then_inc(done.sem, done.one())
        self.landed(dve)
        dve.wait_ge(done.sem, done.issued)
        nc.vector.tensor_tensor(self.x, self.x, self.row(self.loads[0]), ALU.mult).then_inc(done.sem, done.one())
        dve.wait_ge(done.sem, done.issued)
        nc.vector.tensor_tensor(self.out, self.x, self.row(self.loads[1]), ALU.add).then_inc(done.sem, done.one())

    def scalar(self, act):
        self.begin(act)
        done, dve = self.net.act, self.net.dve
        act.wait_ge(dve.sem, self.d0 + 3)
        self.nc.scalar.activation(self.tmp, self.x, ACT.Square).then_inc(done.sem, done.one())
        act.wait_ge(dve.sem, self.d0 + 5)
        self.nc.scalar.activation(self.var, self.var, ACT.Sqrt).then_inc(done.sem, done.one())


class SetOnes(Stage):

    def __init__(self, net, v, after=None):
        super().__init__(net, after)
        self.v = v
        self.take(pool=1)

    def gpsimd(self, pool):
        self.begin(pool)
        self.nc.gpsimd.memset(self.v[:, :, 64:65], 1.0).then_inc(self.net.pool.sem, self.net.pool.one())


class Square(Stage):

    def __init__(self, net, x, out, after=None):
        super().__init__(net, after)
        self.x, self.out = x, out
        self.take(act=x.shape[1])

    def scalar(self, act):
        self.begin(act)
        for c in range(self.x.shape[1]):
            self.nc.scalar.activation(self.out[:, c], self.x[:, c], ACT.Square).then_inc(self.net.act.sem, self.net.act.one())


class Elu1(Stage):

    def __init__(self, net, x, tmp, after=None):
        super().__init__(net, after)
        self.x, self.tmp, self.c = x, tmp, x.shape[1]
        self.take(pool=self.c, act=self.c, dve=self.c)

    def gpsimd(self, pool):
        self.begin(pool)
        for c in range(self.c):
            self.nc.gpsimd.tensor_scalar(self.tmp[:, c], self.x[:, c], 0.0, None, ALU.min).then_inc(self.net.pool.sem, self.net.pool.one())

    def scalar(self, act):
        self.begin(act)
        for c in range(self.c):
            act.wait_ge(self.net.pool.sem, self.l0 + c + 1)
            self.nc.scalar.activation(self.tmp[:, c], self.tmp[:, c], ACT.Exp).then_inc(self.net.act.sem, self.net.act.one())

    def vector(self, dve):
        self.begin(dve)
        for c in range(self.c):
            dve.wait_ge(self.net.act.sem, self.a0 + c + 1)
            self.nc.vector.scalar_tensor_tensor(out=self.x[:, c], in0=self.x[:, c], scalar=0.0, in1=self.tmp[:, c],
                                                op0=ALU.max, op1=ALU.add).then_inc(self.net.dve.sem, self.net.dve.one())


class PhiTok(Stage):

    def __init__(self, net, xT, sqT, chunks, out, lnc, waits=(), after=None):
        super().__init__(net, after)
        self.xT, self.sqT, self.chunks, self.out, self.lnc, self.loads = xT, sqT, chunks, out, lnc, list(waits)
        self.groups(NT, "a")
        self.take(pe=NT, act=NT)

    def tensor(self, pe):
        self.begin(pe)
        self.landed(pe)
        for t in range(NT):
            b = self.g[t][0]
            if b >= BANKS:
                pe.wait_ge(*self.free(b))
            for j, terms in enumerate(self.chunks):
                for n, (c, w, norm) in enumerate(terms):
                    ps = self.net.ps[:TP, b % BANKS, j * 128:(j + 1) * 128]
                    self.nc.tensor.matmul(ps, self.xT[:, c, t * TP:(t + 1) * TP], w, start=(n == 0), stop=False)
                    mm = self.nc.tensor.matmul(ps, self.sqT[:, c, t * TP:(t + 1) * TP], norm, start=False, stop=(n == len(terms) - 1))
            mm.then_inc(self.net.pe.sem, self.net.pe.one())

    def scalar(self, act):
        self.begin(act)
        w = 128 * len(self.chunks)
        for t in range(NT):
            act.wait_ge(self.net.pe.sem, self.p0 + t + 1)
            self.nc.scalar.activation(self.out[:, t, 0:w], self.net.ps[:TP, self.g[t][0] % BANKS, 0:w], ACT.Exp,
                                      bias=self.lnc[:TP, :]).then_inc(self.net.act.sem, self.net.act.one())


class PhiFeat(Stage):

    def __init__(self, net, xT, sqT, chunks, out, lnc, waits=(), after=None):
        super().__init__(net, after)
        self.xT, self.sqT, self.chunks, self.out, self.lnc, self.loads = xT, sqT, chunks, out, lnc, list(waits)
        self.groups(2 * len(chunks), "a")
        self.take(pe=2 * len(chunks), act=2 * len(chunks))

    def tensor(self, pe):
        self.begin(pe)
        self.landed(pe)
        for i, (b, _) in enumerate(self.g):
            t0, t1 = HALVES[i % 2]
            terms = self.chunks[i // 2]
            if b >= BANKS:
                pe.wait_ge(*self.free(b))
            ps = self.net.ps[:, b % BANKS, 0:(t1 - t0) * TP]
            for n, (c, w, norm) in enumerate(terms):
                self.nc.tensor.matmul(ps, w, self.xT[:, c, t0 * TP:t1 * TP], start=(n == 0), stop=False)
                mm = self.nc.tensor.matmul(ps, norm, self.sqT[:, c, t0 * TP:t1 * TP], start=False, stop=(n == len(terms) - 1))
            mm.then_inc(self.net.pe.sem, self.net.pe.one())

    def scalar(self, act):
        self.begin(act)
        for i, (b, _) in enumerate(self.g):
            t0, t1 = HALVES[i % 2]
            act.wait_ge(self.net.pe.sem, self.p0 + i + 1)
            self.nc.scalar.activation(self.out[:, i // 2, t0 * TP:t1 * TP], self.net.ps[:, b % BANKS, 0:(t1 - t0) * TP], ACT.Exp,
                                      bias=self.lnc).then_inc(self.net.act.sem, self.net.act.one())


class KvSummary(Stage):

    def __init__(self, net, chunks, v, scale=1.0, clear=None, after=None):
        super().__init__(net, after)
        self.chunks, self.v, self.scale, self.clear = chunks, v, scale, clear
        base = net.dve.planned + (clear is not None)
        self.ends = []
        for phi, h0, nh, kv, rows in chunks:
            base += nh
            b = net.bank()
            net.freed[b] = (net.dve.sem, base)
            self.g.append((b, "d"))
        self.take(pe=len(chunks), dve=base - net.dve.planned)

    def tensor(self, pe):
        self.begin(pe)
        for (b, _), (phi, h0, nh, kv, rows) in zip(self.g, self.chunks):
            if b >= BANKS:
                pe.wait_ge(*self.free(b))
            for t in range(NT):
                mm = self.nc.tensor.matmul(self.net.ps[:, b % BANKS, 0:nh * 65], phi[:, t],
                                           self.v[:, t * 12 + h0:t * 12 + h0 + nh, :].rearrange("p h c -> p (h c)"),
                                           start=(t == 0), stop=(t == NT - 1))
            mm.then_inc(self.net.pe.sem, self.net.pe.one())

    def vector(self, dve):
        self.begin(dve)
        done = self.net.dve
        if self.clear is not None:
            self.nc.vector.memset(self.clear, 0.0).then_inc(done.sem, done.one())
            dve.wait_ge(done.sem, done.issued)
        for n, ((b, _), (phi, h0, nh, kv, rows)) in enumerate(zip(self.g, self.chunks)):
            dve.wait_ge(self.net.pe.sem, self.p0 + n + 1)
            for i in range(nh):
                r = slice(i * rows, (i + 1) * rows)
                self.nc.vector.tensor_scalar(kv[r, i * 65:(i + 1) * 65], self.net.ps[r, b % BANKS, i * 65:(i + 1) * 65],
                                             self.scale, None, ALU.mult).then_inc(done.sem, done.one())


class KvApply(Stage):

    def __init__(self, net, parts, y, eps, after=None):
        super().__init__(net, after)
        self.parts, self.y, self.eps = parts, y, eps
        self.per = 3 if eps is not None else 1
        n = NT * len(parts)
        for i in range(n):
            b = net.bank()
            net.freed[b] = (net.dve.sem, net.dve.planned + self.per * (i + 1))
            self.g.append((b, "d"))
        self.take(pe=n, dve=self.per * n)

    def tensor(self, pe):
        self.begin(pe)
        i = 0
        for part in self.parts:
            for t in range(NT):
                b, col = self.g[i][0], 0
                if b >= BANKS:
                    pe.wait_ge(*self.free(b))
                for h0, nh, terms in part:
                    for n, (phi, kv) in enumerate(terms):
                        mm = self.nc.tensor.matmul(self.net.ps[:TP, b % BANKS, col:col + nh * 65], phi[:, t * TP:(t + 1) * TP],
                                                   kv, start=(n == 0), stop=(n == len(terms) - 1))
                    col += nh * 65
                mm.then_inc(self.net.pe.sem, self.net.pe.one())
                i += 1

    def vector(self, dve):
        self.begin(dve)
        nc, done = self.nc, self.net.dve
        i = 0
        for part in self.parts:
            h0, nh = part[0][0], sum(q[1] for q in part)
            for t in range(NT):
                ps = self.net.ps[:TP, self.g[i][0] % BANKS, 0:nh * 65].rearrange("p (h c) -> p h c", h=nh)
                y = self.y[:, t, h0 * 64:(h0 + nh) * 64].rearrange("p (h c) -> p h c", h=nh)
                dve.wait_ge(self.net.pe.sem, self.p0 + i + 1)
                if self.eps is None:
                    nc.vector.tensor_copy(y, ps[:, :, 0:64]).then_inc(done.sem, done.one())
                else:
                    o = 270 + 12 * (i % 2)
                    den = self.net.st[:TP, o:o + nh]
                    if i > 1:
                        dve.wait_ge(done.sem, self.d0 + 3 * (i - 1))
                    nc.vector.tensor_scalar(den, ps[:, :, 64], self.eps, None, ALU.add).then_inc(done.sem, done.one())
                    dve.wait_ge(done.sem, done.issued)
                    nc.vector.reciprocal(den, den).then_inc(done.sem, done.one())
                    dve.wait_ge(done.sem, done.issued)
                    nc.vector.tensor_tensor(y, ps[:, :, 0:64], den.unsqueeze(2).to_broadcast([TP, nh, 64]), ALU.mult).then_inc(done.sem, done.one())
                i += 1


class AttnScores(Stage):

    def __init__(self, net, qT, kT, P, rinv, scale, after=None):
        super().__init__(net, after)
        self.qT, self.kT, self.P, self.rinv, self.scale = qT, kT, P, rinv, scale
        self.groups(2 * NT, "a")
        self.mx2 = net.st[:TP, 200:210].rearrange("p (t s) -> p t s", t=NT)
        self.nb = net.st[:TP, 210:215]
        self.sum2 = net.st[:TP, 215:225].rearrange("p (t s) -> p t s", t=NT)
        self.take(pe=2 * NT, act=2 * NT, dve=4 * NT + 2)

    def tensor(self, pe):
        self.begin(pe)
        for i, (b, _) in enumerate(self.g):
            t, (t0, t1) = i // 2, HALVES[i % 2]
            if b >= BANKS:
                pe.wait_ge(*self.free(b))
            self.nc.tensor.matmul(self.net.ps[:TP, b % BANKS, 0:(t1 - t0) * TP], self.qT[:, t * TP:(t + 1) * TP],
                                  self.kT[:, t0 * TP:t1 * TP], start=True, stop=True).then_inc(self.net.pe.sem, self.net.pe.one())

    def scalar(self, act):
        self.begin(act)
        for i, (b, _) in enumerate(self.g):
            t, (t0, t1) = i // 2, HALVES[i % 2]
            if i % 2 == 0:
                act.wait_ge(self.net.dve.sem, self.d0 + 4 * t + 4)
            self.nc.scalar.activation(self.P[:, t, t0 * TP:t1 * TP], self.net.ps[:TP, b % BANKS, 0:(t1 - t0) * TP], ACT.Exp,
                                      bias=self.nb[:, t:t + 1], scale=self.scale,
                                      accum_out=self.sum2[:, t, i % 2:i % 2 + 1]).then_inc(self.net.act.sem, self.net.act.one())

    def vector(self, dve):
        self.begin(dve)
        nc, done = self.nc, self.net.dve
        for t in range(NT):
            for j, (t0, t1) in enumerate(HALVES):
                dve.wait_ge(self.net.pe.sem, self.p0 + 2 * t + j + 1)
                nc.vector.tensor_reduce(self.mx2[:, t, j:j + 1], self.net.ps[:TP, self.g[2 * t + j][0] % BANKS, 0:(t1 - t0) * TP],
                                        AX.X, ALU.max).then_inc(done.sem, done.one())
            dve.wait_ge(done.sem, done.issued)
            nc.vector.tensor_reduce(self.nb[:, t:t + 1], self.mx2[:, t, :], AX.X, ALU.max).then_inc(done.sem, done.one())
            dve.wait_ge(done.sem, done.issued)
            nc.vector.tensor_scalar(self.nb[:, t:t + 1], self.nb[:, t:t + 1], -self.scale, None, ALU.mult).then_inc(done.sem, done.one())
        dve.wait_ge(self.net.act.sem, self.a0 + 2 * NT)
        nc.vector.tensor_reduce(self.rinv, self.sum2, AX.X, ALU.add).then_inc(done.sem, done.one())
        dve.wait_ge(done.sem, done.issued)
        nc.vector.reciprocal(self.rinv, self.rinv).then_inc(done.sem, done.one())


class L2Rows(Stage):

    def __init__(self, net, x, scratch, eps, after=None):
        super().__init__(net, after)
        self.x, self.scratch, self.eps = x, scratch, eps
        self.n = net.st[:TP, 270:275]
        self.take(dve=NT + 2 + NT, act=1)

    def vector(self, dve):
        self.begin(dve)
        nc, done = self.nc, self.net.dve
        for t in range(NT):
            nc.vector.tensor_tensor_reduce(out=self.scratch[:, t], in0=self.x[:, t], in1=self.x[:, t], scale=1.0, scalar=0.0,
                                           op0=ALU.mult, op1=ALU.add, accum_out=self.n[:, t:t + 1]).then_inc(done.sem, done.one())
        dve.wait_ge(self.net.act.sem, self.a0 + 1)
        nc.vector.tensor_scalar(self.n, self.n, self.eps, None, ALU.max).then_inc(done.sem, done.one())
        dve.wait_ge(done.sem, done.issued)
        nc.vector.reciprocal(self.n, self.n).then_inc(done.sem, done.one())
        dve.wait_ge(done.sem, done.issued)
        for t in range(NT):
            nc.vector.tensor_scalar(self.x[:, t], self.x[:, t], self.n[:, t:t + 1], None, ALU.mult).then_inc(done.sem, done.one())

    def scalar(self, act):
        self.begin(act)
        act.wait_ge(self.net.dve.sem, self.d0 + NT)
        self.nc.scalar.activation(self.n, self.n, ACT.Sqrt).then_inc(self.net.act.sem, self.net.act.one())


class PhiNorms(Stage):

    def __init__(self, net, phi, sq, rn, scale_col, eps, after=None):
        super().__init__(net, after)
        self.phi, self.sq, self.rn, self.scale_col, self.eps = phi, sq, rn, scale_col, eps
        self.loads = [phi]
        self.groups(1, "a")
        self.take(pe=1, act=1, dve=4)

    def tensor(self, pe):
        self.begin(pe)
        b = self.g[0][0]
        if b >= BANKS:
            pe.wait_ge(*self.free(b))
        pe.wait_ge(self.net.dve.sem, self.d0 + 1)
        for k in range(KC):
            mm = self.nc.tensor.matmul(self.net.ps[:TP, b % BANKS, 0:64], self.net.ones[:, 0:TP], self.sq[:, k, :], start=(k == 0), stop=(k == KC - 1))
        mm.then_inc(self.net.pe.sem, self.net.pe.one())

    def scalar(self, act):
        self.begin(act)
        act.wait_ge(self.net.pe.sem, self.p0 + 1)
        self.nc.scalar.activation(self.rn, self.net.ps[:TP, self.g[0][0] % BANKS, 0:64], ACT.Sqrt).then_inc(self.net.act.sem, self.net.act.one())

    def vector(self, dve):
        self.begin(dve)
        self.landed(dve)
        nc, done = self.nc, self.net.dve
        nc.vector.tensor_tensor(self.sq, self.phi.dst, self.phi.dst, ALU.mult).then_inc(done.sem, done.one())
        dve.wait_ge(self.net.act.sem, self.a0 + 1)
        nc.vector.tensor_scalar(self.rn, self.rn, self.eps, None, ALU.max).then_inc(done.sem, done.one())
        dve.wait_ge(done.sem, done.issued)
        nc.vector.reciprocal(self.rn, self.rn).then_inc(done.sem, done.one())
        dve.wait_ge(done.sem, done.issued)
        nc.vector.tensor_scalar(self.rn, self.rn, self.scale_col, None, ALU.mult).then_inc(done.sem, done.one())


class SoftmaxGroups(Stage):

    def __init__(self, net, x, out, after=None):
        super().__init__(net, after)
        self.x, self.out = x, out
        self.m, self.s = net.st[:TP, 275:280], net.st[:TP, 280:285]
        self.take(dve=5, act=1)

    def bc(self, small):
        return small.unsqueeze(2).to_broadcast(list(self.x.shape))

    def vector(self, dve):
        self.begin(dve)
        nc, done = self.nc, self.net.dve
        nc.vector.tensor_reduce(self.m, self.x, AX.X, ALU.max).then_inc(done.sem, done.one())
        dve.wait_ge(done.sem, done.issued)
        nc.vector.tensor_tensor(self.out, self.x, self.bc(self.m), ALU.subtract).then_inc(done.sem, done.one())
        dve.wait_ge(self.net.act.sem, self.a0 + 1)
        nc.vector.tensor_reduce(self.s, self.out, AX.X, ALU.add).then_inc(done.sem, done.one())
        dve.wait_ge(done.sem, done.issued)
        nc.vector.reciprocal(self.s, self.s).then_inc(done.sem, done.one())
        dve.wait_ge(done.sem, done.issued)
        nc.vector.tensor_tensor(self.out, self.out, self.bc(self.s), ALU.mult).then_inc(done.sem, done.one())

    def scalar(self, act):
        self.begin(act)
        act.wait_ge(self.net.dve.sem, self.d0 + 2)
        self.nc.scalar.activation(self.out, self.out, ACT.Exp).then_inc(self.net.act.sem, self.net.act.one())


class TokenSoftmax(Stage):

    def __init__(self, net, x, after=None):
        super().__init__(net, after)
        self.x = x
        self.m, self.s = net.st[:64, 285:286], net.st[:64, 286:287]
        self.take(dve=4, act=1)

    def vector(self, dve):
        self.begin(dve)
        nc, done = self.nc, self.net.dve
        nc.vector.tensor_reduce(self.m, self.x, AX.X, ALU.max).then_inc(done.sem, done.one())
        dve.wait_ge(done.sem, done.issued)
        nc.vector.tensor_scalar(self.m, self.m, -1.0, None, ALU.mult).then_inc(done.sem, done.one())
        dve.wait_ge(self.net.act.sem, self.a0 + 1)
        nc.vector.reciprocal(self.s, self.s).then_inc(done.sem, done.one())
        dve.wait_ge(done.sem, done.issued)
        nc.vector.tensor_scalar(self.x, self.x, self.s, None, ALU.mult).then_inc(done.sem, done.one())

    def scalar(self, act):
        self.begin(act)
        act.wait_ge(self.net.dve.sem, self.d0 + 2)
        self.nc.scalar.activation(self.x, self.x, ACT.Exp, bias=self.m, accum_out=self.s).then_inc(self.net.act.sem, self.net.act.one())


class ToTokens(Stage):

    def __init__(self, net, x, out, after=None):
        super().__init__(net, after)
        self.x, self.out = x, out
        self.groups(1, "d")
        self.take(pe=1, dve=1)

    def tensor(self, pe):
        self.begin(pe)
        b = self.g[0][0]
        if b >= BANKS:
            pe.wait_ge(*self.free(b))
        for t in range(NT):
            mm = self.nc.tensor.transpose(self.net.ps[:TP, b % BANKS, t * 64:(t + 1) * 64], self.x[:, t * TP:(t + 1) * TP], self.net.ident[:64, :64])
        mm.then_inc(self.net.pe.sem, self.net.pe.one())

    def vector(self, dve):
        self.begin(dve)
        dve.wait_ge(self.net.pe.sem, self.p0 + 1)
        self.nc.vector.tensor_copy(self.out, self.net.ps[:TP, self.g[0][0] % BANKS, 0:NT * 64].rearrange("p (t n) -> p t n", t=NT)).then_inc(self.net.dve.sem, self.net.dve.one())


class SlotInputs(Stage):

    def __init__(self, net, x, d, out, after=None):
        super().__init__(net, after)
        self.x, self.d, self.out = x, d, out
        self.groups(1, "d")
        self.take(pe=1, dve=1)

    def tensor(self, pe):
        self.begin(pe)
        b = self.g[0][0]
        if b >= BANKS:
            pe.wait_ge(*self.free(b))
        for c in range(KC):
            for t in range(NT):
                mm = self.nc.tensor.matmul(self.net.ps[:, b % BANKS, c * 64:(c + 1) * 64], self.x[:, t, c * 128:(c + 1) * 128], self.d[:, t, :],
                                           start=(t == 0), stop=(t == NT - 1))
        mm.then_inc(self.net.pe.sem, self.net.pe.one())

    def vector(self, dve):
        self.begin(dve)
        dve.wait_ge(self.net.pe.sem, self.p0 + 1)
        self.nc.vector.tensor_copy(self.out, self.net.ps[:, self.g[0][0] % BANKS, 0:KC * 64].rearrange("p (c n) -> p c n", c=KC)).then_inc(self.net.dve.sem, self.net.dve.one())


class SlotExperts(Stage):
    EXPERTS, DEPTH = 64, 4

    def __init__(self, net, xT, w, kp, masked, out, bias, func, after=None):
        super().__init__(net, after)
        self.xT, self.w, self.kp, self.masked, self.out, self.bias, self.func = xT, w, kp, masked, out, bias, func
        self.kc, self.n = w.shape[1] // kp, w.shape[2]
        self.loads = [bias]
        self.cols = self.n if self.n <= 512 else UNIT
        self.nb = self.n // self.cols
        self.slots = list(net.wring)
        self.taken = [s.take(self.EXPERTS // self.DEPTH) for s in self.slots]
        net.loads.append(self)
        E_, gelu = self.EXPERTS, func == "gelu"
        d_end = net.dve.planned + E_ + self.nb
        for _ in range(self.nb):
            b = net.bank()
            net.freed[b] = (net.dve.sem, d_end)
            self.g.append((b, "d"))
        self.take(pe=1 + E_ + 1, dve=E_ + self.nb, act=1 if gelu else 0)
        for s in self.slots:
            s.last = Load(None, None, None, 0, None)
            s.last.used = self.done

    def ps(self, q):
        return self.net.ps[:64, self.g[q][0] % BANKS, 0:self.cols]

    def clear(self, start):
        for q in range(self.nb):
            mm = self.nc.tensor.matmul(self.ps(q), self.net.zeros[:, 0:64], self.net.zeros[:, 0:self.cols], start=start, stop=not start, skip_group_check=True)
        return mm

    def sync(self, sp):
        for before, _ in self.taken:
            if before:
                for sem, value in before.used:
                    sp.wait_ge(sem, value)
        dsts = [s.buf[:self.kp, 0:self.kc * self.n].rearrange("p (c n) -> p c n", c=self.kc) for s in self.slots]
        for j in range(self.DEPTH):
            sp.dma_start(dsts[j], self.w[j].rearrange("(c p) n -> p c n", p=self.kp)).then_inc(self.slots[j].sem, 16)
        with self.nc.sync.Fori(1, self.EXPERTS // self.DEPTH) as i:
            for j in range(self.DEPTH):
                sp.wait_ge(self.net.pe.sem, i * self.DEPTH + (self.p0 + 1 + j + 1 - self.DEPTH))
                sp.dma_start(dsts[j], self.w[bass.ds(i * self.DEPTH + j, 1)].rearrange("e (c p) n -> (e p) c n", p=self.kp)).then_inc(self.slots[j].sem, 16)

    def tensor(self, pe):
        self.begin(pe)
        nc, done = self.nc, self.net.pe
        for b, _ in self.g:
            if b >= BANKS:
                pe.wait_ge(*self.free(b))
        self.clear(True).then_inc(done.sem, done.one())
        with nc.tensor.Fori(0, self.EXPERTS // self.DEPTH) as i:
            for j, s in enumerate(self.slots):
                w = s.buf[:self.kp, 0:self.kc * self.n].rearrange("p (c n) -> p c n", c=self.kc)
                pe.wait_ge(self.net.dve.sem, i * self.DEPTH + (self.d0 + j + 1))
                pe.wait_ge(s.sem, i * 16 + (self.taken[j][1] + 16))
                for k in range(self.kc):
                    for q in range(self.nb):
                        mm = nc.tensor.matmul(self.ps(q), self.masked[j][:, k, :], w[:, k, q * self.cols:(q + 1) * self.cols],
                                              start=False, stop=False, skip_group_check=True)
                mm.then_inc(done.sem, 1)
        done.issued += self.EXPERTS
        self.clear(False).then_inc(done.sem, done.one())

    def vector(self, dve):
        self.begin(dve)
        nc, done = self.nc, self.net.dve
        with nc.vector.Fori(0, self.EXPERTS // self.DEPTH) as i:
            for j in range(self.DEPTH):
                dve.wait_ge(self.net.pe.sem, i * self.DEPTH + (self.p0 + 1 + j + 1 - self.DEPTH))
                nc.vector.scalar_tensor_tensor(out=self.masked[j], in0=self.net.iota64[:self.kp, :].unsqueeze(1).to_broadcast([self.kp, self.kc, 64]),
                                               scalar=self.net.iota64[:self.kp, bass.ds(i * self.DEPTH + j, 1)], in1=self.xT,
                                               op0=ALU.is_equal, op1=ALU.mult).then_inc(done.sem, 1)
        done.issued += self.EXPERTS
        self.landed(dve)
        dve.wait_ge(self.net.pe.sem, self.p0 + self.EXPERTS + 2)
        for q in range(self.nb):
            cs = slice(q * self.cols, (q + 1) * self.cols)
            nc.vector.tensor_tensor(self.out[:, cs], self.ps(q), self.bias.dst[:64, 0, cs], ALU.add).then_inc(done.sem, done.one())

    def scalar(self, act):
        if self.func == "gelu":
            self.begin(act)
            act.wait_ge(self.net.dve.sem, self.d0 + self.EXPERTS + self.nb)
            self.nc.scalar.activation(self.out, self.out, ACT.Gelu).then_inc(self.net.act.sem, self.net.act.one())


class SlotHidden(Stage):

    def __init__(self, net, x, out, after=None):
        super().__init__(net, after)
        self.x, self.out = x, out
        self.groups(1, "d")
        self.take(pe=1, dve=1)

    def tensor(self, pe):
        self.begin(pe)
        b = self.g[0][0]
        if b >= BANKS:
            pe.wait_ge(*self.free(b))
        for c in range(2):
            mm = self.nc.tensor.transpose(self.net.ps[:96, b % BANKS, c * 64:(c + 1) * 64], self.x[:, c * 96:(c + 1) * 96], self.net.ident[:64, :64])
        mm.then_inc(self.net.pe.sem, self.net.pe.one())

    def vector(self, dve):
        self.begin(dve)
        dve.wait_ge(self.net.pe.sem, self.p0 + 1)
        self.nc.vector.tensor_copy(self.out, self.net.ps[:96, self.g[0][0] % BANKS, 0:128].rearrange("p (c n) -> p c n", c=2)).then_inc(self.net.dve.sem, self.net.dve.one())


class TopTwo(Stage):
    ABSENT = 3.0e38

    def __init__(self, net, logits, gates, norm, sel, first=None, after=None):
        super().__init__(net, after)
        self.x, self.gates, self.norm, self.sel, self.first = logits, gates, norm, sel, first
        s = lambda o, w: net.st[:TP, o:o + NT * w].rearrange("p (t w) -> p t w", t=NT)
        self.top, self.want, self.rep, self.sum = s(310, 8), s(350, 8), s(390, 8), net.st[:TP, 430:435]
        self.n_first = 2 + NT if first is not None else 0
        self.take(dve=NT + 2 + NT + 1 + self.n_first + 1 + 1 + 3, act=1)

    def bc(self, small):
        return small.to_broadcast([TP, NT, 8])

    def vector(self, dve):
        self.begin(dve)
        nc, done = self.nc, self.net.dve
        nc.vector.memset(self.want, self.ABSENT).then_inc(done.sem, done.one())
        for t in range(NT):
            nc.vector.max(self.top[:, t, :], self.x[:, t, :]).then_inc(done.sem, done.one())
        dve.wait_ge(done.sem, done.issued)
        if self.first is not None:
            nc.vector.tensor_copy(self.want[:, :, 0:1], self.top[:, :, 0:1]).then_inc(done.sem, done.one())
            dve.wait_ge(done.sem, done.issued)
            for t in range(NT):
                nc.vector.match_replace(self.first[:, t, :], self.want[:, t, :], self.x[:, t, :], -self.ABSENT).then_inc(done.sem, done.one())
            dve.wait_ge(done.sem, done.issued)
            nc.vector.tensor_tensor(self.first, self.first, self.x, ALU.not_equal).then_inc(done.sem, done.one())
            dve.wait_ge(done.sem, done.issued)
        nc.vector.tensor_copy(self.want[:, :, 0:2], self.top[:, :, 0:2]).then_inc(done.sem, done.one())
        dve.wait_ge(done.sem, done.issued)
        for t in range(NT):
            nc.vector.match_replace(self.rep[:, t, :], self.want[:, t, :], self.x[:, t, :], -self.ABSENT).then_inc(done.sem, done.one())
        nc.vector.tensor_tensor(self.gates, self.x, self.bc(self.top[:, :, 0:1]), ALU.subtract).then_inc(done.sem, done.one())
        dve.wait_ge(done.sem, done.issued)
        nc.vector.tensor_tensor(self.sel, self.rep, self.x, ALU.not_equal).then_inc(done.sem, done.one())
        dve.wait_ge(done.sem, done.issued)
        dve.wait_ge(self.net.act.sem, self.a0 + 1)
        if self.norm == "all":
            nc.vector.tensor_reduce(self.sum, self.gates, AX.X, ALU.add).then_inc(done.sem, done.one())
            dve.wait_ge(done.sem, done.issued)
            nc.vector.tensor_tensor(self.gates, self.gates, self.sel, ALU.mult).then_inc(done.sem, done.one())
        else:
            nc.vector.tensor_tensor(self.gates, self.gates, self.sel, ALU.mult).then_inc(done.sem, done.one())
            dve.wait_ge(done.sem, done.issued)
            nc.vector.tensor_reduce(self.sum, self.gates, AX.X, ALU.add).then_inc(done.sem, done.one())
        dve.wait_ge(done.sem, done.issued)
        nc.vector.reciprocal(self.sum, self.sum).then_inc(done.sem, done.one())
        dve.wait_ge(done.sem, done.issued)
        nc.vector.tensor_tensor(self.gates, self.gates, self.bc(self.sum.unsqueeze(2)), ALU.mult).then_inc(done.sem, done.one())

    def scalar(self, act):
        self.begin(act)
        act.wait_ge(self.net.dve.sem, self.d0 + 1 + NT + self.n_first + 1 + NT + 1)
        self.nc.scalar.activation(self.gates, self.gates, ACT.Exp).then_inc(self.net.act.sem, self.net.act.one())


class Capacity(Stage):

    def __init__(self, net, gates, sel, first, tri, capacity, after=None):
        super().__init__(net, after)
        self.gates, self.sel, self.first, self.tri, self.capacity = gates, sel, first, tri, capacity
        self.hot = net.st[:TP, 350:430].rearrange("p (t k e) -> p t k e", t=NT, k=2)
        self.loads = [tri]
        self.groups(1, "d")
        self.take(pe=1, dve=6)

    def vector(self, dve):
        self.begin(dve)
        nc, done, ps = self.nc, self.net.dve, self.net.ps
        nc.vector.tensor_copy(self.hot[:, :, 0, :], self.first).then_inc(done.sem, done.one())
        nc.vector.tensor_tensor(self.hot[:, :, 1, :], self.sel, self.first, ALU.subtract).then_inc(done.sem, done.one())
        dve.wait_ge(done.sem, done.issued)
        dve.wait_ge(self.net.pe.sem, self.p0 + 1)
        count = ps[:TP, self.g[0][0] % BANKS, 0:NT * 16].rearrange("p (t k e) -> p t k e", t=NT, k=2)
        for k in range(2):
            nc.vector.scalar_tensor_tensor(out=self.hot[:, :, k, :], in0=count[:, :, k, :], scalar=float(self.capacity), in1=self.hot[:, :, k, :],
                                           op0=ALU.is_le, op1=ALU.mult).then_inc(done.sem, done.one())
        dve.wait_ge(done.sem, done.issued)
        nc.vector.tensor_tensor(self.sel, self.hot[:, :, 0, :], self.hot[:, :, 1, :], ALU.add).then_inc(done.sem, done.one())
        dve.wait_ge(done.sem, done.issued)
        nc.vector.tensor_tensor(self.gates, self.gates, self.sel, ALU.mult).then_inc(done.sem, done.one())

    def tensor(self, pe):
        self.begin(pe)
        self.landed(pe)
        b = self.g[0][0]
        if b >= BANKS:
            pe.wait_ge(*self.free(b))
        pe.wait_ge(self.net.dve.sem, self.d0 + 2)
        for t in range(NT):
            for s in range(t + 1):
                lhs = self.tri.dst[:TP, 0, 0:TP] if s == t else self.net.ones[:TP, 0:TP]
                mm = self.nc.tensor.matmul(self.net.ps[:TP, b % BANKS, t * 16:(t + 1) * 16], lhs, self.hot[:, s].rearrange("p k e -> p (k e)"),
                                           start=(s == 0), stop=(s == t))
        mm.then_inc(self.net.pe.sem, self.net.pe.one())


class GatedRows(Stage):

    def __init__(self, net, x, gate, row, after=None):
        super().__init__(net, after)
        self.x, self.gate, self.row, self.loads = x, gate, row, [row]
        self.take(dve=NT)

    def vector(self, dve):
        self.begin(dve)
        self.landed(dve)
        for t in range(NT):
            self.nc.vector.scalar_tensor_tensor(out=self.x[:, t], in0=self.row.dst[:TP, 0], scalar=self.gate[:, t:t + 1], in1=self.x[:, t],
                                                op0=ALU.mult, op1=ALU.add).then_inc(self.net.dve.sem, self.net.dve.one())


class Multiply(Stage):

    def __init__(self, net, x, y, after=None):
        super().__init__(net, after)
        self.x, self.y = x, y
        self.take(dve=1)

    def vector(self, dve):
        self.begin(dve)
        self.nc.vector.tensor_tensor(self.x, self.x, self.y, ALU.mult).then_inc(self.net.dve.sem, self.net.dve.one())


class Clear(Stage):

    def __init__(self, net, x, value=0.0, after=None):
        super().__init__(net, after)
        self.x, self.value = x, value
        self.take(dve=1)

    def vector(self, dve):
        self.begin(dve)
        self.nc.vector.memset(self.x, self.value).then_inc(self.net.dve.sem, self.net.dve.one())


class Degrees(Stage):

    def __init__(self, net, rdeg, after=None):
        super().__init__(net, after)
        self.rdeg = rdeg
        self.take(dve=2, act=1)

    def vector(self, dve):
        self.begin(dve)
        done = self.net.dve
        self.nc.vector.tensor_reduce(self.rdeg, self.net.counts[:TP], AX.X, ALU.add).then_inc(done.sem, done.one())
        dve.wait_ge(self.net.act.sem, self.a0 + 1)
        self.nc.vector.reciprocal(self.rdeg, self.rdeg).then_inc(done.sem, done.one())

    def scalar(self, act):
        self.begin(act)
        act.wait_ge(self.net.dve.sem, self.d0 + 1)
        self.nc.scalar.activation(self.rdeg, self.rdeg, ACT.Sqrt).then_inc(self.net.act.sem, self.net.act.one())


def weight_units(net, w, rows=None, cols=None):
    r0, r1 = rows or (0, w.shape[0])
    c0, c1 = cols or (0, w.shape[1])
    return [net.weights(w[r0:r1, c:min(c + UNIT, c1)]) for c in range(c0, c1, UNIT)]


def linear_T(net, xT, w, out, bias=None, kind="copy", rows=None, cols=None, evac="ad"):
    m = 0
    for load in weight_units(net, w, rows, cols):
        parts = []
        for c0 in range(0, load.dst.shape[2], 128):
            parts.append((load, c0, 128, out[:, m], bias[:, m:m + 1] if bias is not None else None, kind))
            m += 1
        LinearT(net, xT, parts, evac)


def linear(net, xT, w, out, kind="copy", add=None, rows=None, cols=None, bias=None, gate=None, evac="ad", kp=128):
    f = 0
    r0, r1 = rows or (0, w.shape[0])
    c0, c1 = cols or (0, w.shape[1])
    for c in range(c0, c1, UNIT):
        load = net.weights(w[r0:r1, c:min(c + UNIT, c1)], kp)
        n = load.dst.shape[2]
        u = dict(load=load, w=n, out=out[:, :, f:f + n], kind=kind)
        if kind == "row":
            u.update(kind="add", add=bias.dst[:TP, 0, f:f + n], by_tile=False)
        elif kind in ("add", "gate"):
            u["add"] = add[:, :, f:f + n]
        if gate is not None:
            u["gate"] = gate
        Linear(net, xT, [u], evac if kind in ("copy", "relu") else "d", rows=[bias] if bias else ())
        f += n


def linear_heads(net, xT, w, cols, v4, bias=None):
    for j, c in enumerate(range(cols[0], cols[1], UNIT)):
        load = net.weights(w[:, c:c + UNIT])
        u = dict(load=load, w=UNIT, out=v4[:, :, 6 * j:6 * j + 6, 0:64], kind="copy")
        if bias:
            u.update(kind="add", by_tile=False, add=bias.dst[:TP, 0, j * UNIT:(j + 1) * UNIT].rearrange("p (h c) -> p h c", h=6))
        Linear(net, xT, [u], "d" if bias else "ad", rows=[bias] if bias else ())


def gat_layer(net, h_parts, heads, c, a_src, a_dst, P, T, eps, outs, bias_rows=None, add=None):
    coef = net.st[:TP, 100:180].rearrange("p (s h t) -> p s h t", s=2, h=8)
    head = 0
    for h, nh in h_parts:
        cs = slice(head * c, (head + nh) * c)
        GatCoefs(net, h, nh, c, head, net.row(a_src[:, cs]), net.row(a_dst[:, cs]), coef, P)
        head += nh
    head = 0
    for (h, nh), out, k in zip(h_parts, outs, range(len(h_parts))):
        row = net.row(bias_rows[:, head * c:(head + nh) * c]) if bias_rows is not None else None
        for i in range(nh):
            rinv = net.st[:TP, 180 + 5 * (head % 2):185 + 5 * (head % 2)]
            GatScores(net, coef, head, net.feat(P, NT, TP), net.feat(T, NT, TP), rinv, eps)
            cs = slice(i * c, (i + 1) * c)
            if row:
                Apply(net, net.feat(P, NT, TP), net.feat(T, NT, TP), h[:, :, cs], rinv, out[:, :, cs], add=row.dst[:TP, 0, cs], by_tile=False, rows=[row])
            else:
                Apply(net, net.feat(P, NT, TP), net.feat(T, NT, TP), h[:, :, cs], rinv, out[:, :, cs], add=add)
            head += 1


def network(net, upto):
    ins, G = net.ins, net.G
    tok, feat = net.tok, net.feat
    R, XT = tok(net.R), feat(net.XT)
    P_, T_ = G[2], G[3]
    net.const(net.ident[:, :], ins["ident"])
    net.const(net.lnc[:, :], ins["lnc"])
    net.const(net.slot_scale[:, :], ins["L0_ffn_scale"].to_broadcast([128, 1]))
    net.const(net.iota64[:, :], ins["iota"][:, 0:64].to_broadcast([128, 64]))
    net.const(R, ins["x"].rearrange("(t p) d -> p t d", p=TP))
    col = {n: net.col(n) for n in ("b_ah_c", "kqv_b_c", "qkv_b_c", "fc1_b_c", "in_b_c")}
    col.update({n: net.col(n, 96) for n in ("mlp_b1_c", "exp_b1_c")})
    Clear(net, net.ones[:, :], 1.0)
    Clear(net, net.zeros[:, :], 0.0)
    EdgeCounts(net)
    SelfLoops(net, ALU.add)

    LayerNorm(net, R, tok(G[0]), 1e-5)
    ToFeatures(net, tok(G[0]), XT)
    w = ins["L0_mix_w_mapT"]
    heads = lambda b: b[:TP, 0:NT * D].rearrange("p (t c) -> p t c", c=64)
    v = G[2][:TP, 0:NT * 12 * 65].rearrange("p (t c) -> p t c", c=65)
    v4 = v.rearrange("p (t h) c -> p t h c", t=NT)
    linear_T(net, XT, w, feat(G[0]), cols=(0, D))
    linear(net, XT, w, tok(G[1]), cols=(D, 2 * D))
    HeadNorm(net, heads(G[1]), heads(G[4]), heads(G[1]), net.row(ins["L0_mix_g_k"]), net.row(ins["L0_mix_b_k"]), 1e-5)
    linear(net, XT, w, tok(G[3]), cols=(2 * D, 3 * D))
    HeadNorm(net, heads(G[3]), heads(G[4]), v[:, :, 0:64], net.row(ins["L0_mix_g_v"]), net.row(ins["L0_mix_b_v"]), 1e-5)
    SetOnes(net, v)
    kv = net.kv[:, 0:780].rearrange("p (c w) -> p c w", c=6)
    KvSummary(net, [(tok(G[1])[:, :, j * 128:(j + 1) * 128], 2 * j, 2, kv[:, j], 64) for j in range(6)], v, 1.0 / N, clear=net.kv[:, 0:780])
    pairs = lambda phi: [[(2 * j, 2, ((phi[:, j], kv[:, j]),)) for j in range(3 * q, 3 * q + 3)] for q in range(2)]
    KvApply(net, pairs(feat(G[0])), tok(G[3]), None)
    ToFeatures(net, tok(G[3]), feat(G[4]))
    AddRow(net, R, net.row(ins["L0_mix_b_out"]))
    linear(net, feat(G[4]), ins["L0_mix_w_outT"], R, "add", add=R)
    linear_T(net, XT, ins["L0_gnn_W_ah"], feat(G[0]), bias=col["b_ah_c"], kind="relu")
    Clear(net, tok(G[5]))
    AddRow(net, tok(G[5]), net.row(ins["L0_gnn_b_out"]))
    for i in range(3):
        linear(net, feat(G[0]), ins[f"L0_gnn_W{i}"], tok(G[1]))
        gat_layer(net, [(tok(G[1]), 4)], 4, 192, ins[f"L0_gnn_a_src{i}"], ins[f"L0_gnn_a_dst{i}"], P_, T_, 1e-16, [tok(G[4])], ins[f"L0_gnn_b{i}"])
        ToFeatures(net, tok(G[4]), XT, "relu")
        linear(net, XT, ins["L0_gnn_W_out"], tok(G[5]), "add", add=tok(G[5]), rows=(i * D, (i + 1) * D))
    ReluAdd(net, R, tok(G[5]))
    if upto == 1:
        return
    LayerNorm(net, R, tok(G[0]), 1e-5)
    L2Rows(net, tok(G[0]), tok(G[1]), 1e-12)
    ToFeatures(net, tok(G[0]), XT)
    phi = net.weights(ins["L0_ffn_phi"])
    c64 = lambda b, p=TP, c=NT: b[:p, 0:c * 64].rearrange("p (t n) -> p t n", t=c)
    rn = G[2][:TP, 0:64]
    PhiNorms(net, phi, c64(G[1], 128, KC), rn, net.slot_scale[:TP, :], 1e-12)
    Linear(net, XT, [dict(load=phi, w=64, out=c64(G[3]), kind="mul", add=rn, by_tile=False)], "d")
    ToFeatures(net, c64(G[3]), feat(G[4], 1, 64))
    TokenSoftmax(net, G[4][:64, 0:N])
    ToTokens(net, G[4][:64, 0:N], c64(G[5]))
    SoftmaxGroups(net, c64(G[3]), c64(G[3]))
    ToFeatures(net, c64(G[3]), feat(G[4], 1, 64))
    xsT = c64(G[1], 128, KC)
    SlotInputs(net, tok(G[0]), c64(G[5]), xsT)
    hid = G[5][:64, 0:192]
    masked = [G[2][:, j * UNIT:(j + 1) * UNIT].rearrange("p (c n) -> p c n", c=KC) for j in range(4)]
    SlotExperts(net, xsT, ins["L0_ffn_w1"], 128, masked, hid, net.rows(ins["L0_ffn_b1"]), "gelu")
    hidT = c64(G[3], 96, 2)
    SlotHidden(net, hid, hidT)
    masked = [G[2][:96, j * 128:(j + 1) * 128].rearrange("p (c n) -> p c n", c=2) for j in range(4)]
    ys = G[0][:64, 0:D]
    SlotExperts(net, hidT, ins["L0_ffn_w2"], 96, masked, ys, net.rows(ins["L0_ffn_b2"]), "copy")
    for j in range(2):
        held = Load(None, G[0][:64, j * UNIT:(j + 1) * UNIT].unsqueeze(1), net.pe.sem, 0, None)
        Linear(net, feat(G[4], 1, 64), [dict(load=held, w=UNIT, out=R[:, :, j * UNIT:(j + 1) * UNIT], kind="add", add=R[:, :, j * UNIT:(j + 1) * UNIT])], "d")
    if upto == 2:
        return

    LayerNorm(net, R, tok(G[0]), 1e-5)
    ToFeatures(net, tok(G[0]), XT)
    Clear(net, net.fw[:, :])
    fw = net.fw[:, :].rearrange("p (c m) -> p c m", c=6)
    fn = net.fn[:, 0:256].rearrange("p (i m) -> p i m", i=2)
    fws = [net.into(net.fn[:, 0:256], ins["norms1"], net.now())]
    for i in range(2):
        for s in range(2):
            dst = net.fw[64 * s:64 * s + 64, :].rearrange("p (j i m) -> p j i m", j=3, i=2)[:, :, i, 64 * i + 32 * s:64 * i + 32 * s + 32]
            fws.append(net.into(dst, ins["L1_mix_wT"].rearrange("(j i s) d m -> i s d j m", i=2, s=2)[i, s], net.now()))
    chunks = [[(2 * j + i, fw[:, 2 * j + i], fn[:, i]) for i in range(2)] for j in range(3)]
    w = ins["L1_mix_kqv_wT"]
    linear_T(net, XT, w, feat(G[0]), bias=col["kqv_b_c"][:, 0:6], cols=(0, D))
    Square(net, feat(G[0]), feat(G[1]))
    phik = G[2][:TP, 0:NT * UNIT].rearrange("p (t m) -> p t m", t=NT)
    PhiTok(net, feat(G[0]), feat(G[1]), chunks, phik, net.lnc[:, 0:1], fws)
    linear_T(net, XT, w, feat(G[0]), bias=col["kqv_b_c"][:, 6:12], cols=(D, 2 * D))
    Square(net, feat(G[0]), feat(G[1]))
    phiq = feat(G[3], 3)
    PhiFeat(net, feat(G[0]), feat(G[1]), chunks, phiq, net.lnc[:, 0:1])
    v = G[4][:TP, 0:NT * 12 * 65].rearrange("p (t c) -> p t c", c=65)
    v4 = v.rearrange("p (t h) c -> p t h c", t=NT)
    SetOnes(net, v)
    linear_heads(net, XT, w, (2 * D, 3 * D), v4, net.row(ins["L1_mix_kqv_b_v"]))
    kv = net.kv[:, 0:780].rearrange("p (c w) -> p c w", c=3)
    KvSummary(net, [(phik[:, :, j * 128:(j + 1) * 128], 4 * j, 4, kv[:, j], 32) for j in range(3)], v, 1.0, clear=net.kv[:, 0:780])
    KvApply(net, [[(4 * j, 4, ((phiq[:, j], kv[:, j]),))] for j in range(3)], tok(G[5]), 1e-8)
    ToFeatures(net, tok(G[5]), feat(G[0]))
    AddRow(net, R, net.row(ins["L1_mix_proj_b"]))
    linear(net, feat(G[0]), ins["L1_mix_proj_wT"], R, "add", add=R)
    rdeg = net.st[:TP, 180:185]
    Degrees(net, rdeg)
    AddRow(net, R, net.row(ins["L1_gnn_b"]))
    for j, load in enumerate(weight_units(net, ins["L1_gnn_W"])):
        Linear(net, XT, [dict(load=load, w=UNIT, out=tok(G[1])[:, :, j * UNIT:(j + 1) * UNIT], kind="scale", gate=rdeg)], "d")
    Apply(net, net.counts[:TP], feat(G[3], NT, TP), tok(G[1]), rdeg, R, add=R)
    if upto == 3:
        return
    gates, logits = (net.st[:TP, o:o + 40].rearrange("p (t e) -> p t e", t=NT) for o in (230, 520))
    sel, first = (net.st[:TP, o:o + 40].rearrange("p (t e) -> p t e", t=NT) for o in (440, 480))
    LayerNorm(net, R, tok(G[0]), 1e-5)
    ToFeatures(net, tok(G[0]), XT)
    Linear(net, XT, [dict(load=net.weights(ins["L1_ffn_router_wT"]), w=8, out=logits, kind="copy")], "d")
    TopTwo(net, logits, gates, "all", sel)
    for e in range(8):
        hT = feat(G[e % 2], 2, 96)
        load = net.weights(ins["L1_ffn_w1"][e])
        LinearT(net, XT, [(load, 96 * k, 96, hT[:, k], None, "tanh_gelu") for k in range(2)], "a")
        for j in range(2):
            load = net.weights(ins["L1_ffn_w2"][e][:, j * UNIT:(j + 1) * UNIT], 96)
            cs = slice(j * UNIT, (j + 1) * UNIT)
            Linear(net, hT, [dict(load=load, w=UNIT, out=R[:, :, cs], kind="gate", gate=gates[:, :, e], add=R[:, :, cs])], "d")
    if upto == 4:
        return

    LayerNorm(net, R, tok(G[5]), 1e-5)
    ToFeatures(net, tok(G[5]), XT)
    SelfLoops(net, ALU.subtract)
    w = ins["L2_gnn_W1T"]
    hA, hB = tok(G[0]), tok(G[1], 256)
    linear(net, XT, w, hA, cols=(0, D))
    linear(net, XT, w, hB, cols=(D, 1024))
    outB = G[1][:TP, 1280:2560].rearrange("p (t w) -> p t w", t=NT)
    gat_layer(net, [(hA, 6), (hB, 2)], 8, 128, ins["L2_gnn_att_src1"], ins["L2_gnn_att_dst1"], P_, T_, 1e-16, [tok(G[4]), outB], ins["L2_gnn_b1"])
    ToFeatures(net, tok(G[4]), feat(G[0]), "relu")
    ToFeatures(net, outB, feat(G[2], 2), "relu")
    linear(net, feat(G[0]), ins["L2_gnn_W2T"], tok(G[4]), rows=(0, D))
    linear(net, feat(G[2], 2), ins["L2_gnn_W2T"], tok(G[4]), "add", add=tok(G[4]), rows=(D, 1024))
    AddRow(net, R, net.row(ins["L2_gnn_b2"]))
    gat_layer(net, [(tok(G[4]), 1)], 1, D, ins["L2_gnn_att_src2"], ins["L2_gnn_att_dst2"], P_, T_, 1e-16, [R], add=R)
    SelfLoops(net, ALU.add)
    LayerNorm(net, tok(G[5]), tok(G[0]), 1e-8, net.row(ins["L2_mix_ln1_w"]), net.row(ins["L2_mix_ln1_b"]))
    ToFeatures(net, tok(G[0]), XT)
    w = ins["L2_mix_qkv_w"]
    linear_T(net, XT, w, feat(G[0]), bias=col["qkv_b_c"], cols=(0, D))
    Elu1(net, feat(G[0]), feat(G[1]))
    linear(net, XT, w, tok(G[2]), "row", bias=net.row(ins["L2_mix_qkv_b"][:, D:2 * D]), cols=(D, 2 * D))
    Elu1(net, tok(G[2]), tok(G[1]))
    v = G[3][:TP, 0:NT * 12 * 65].rearrange("p (t c) -> p t c", c=65)
    v4 = v.rearrange("p (t h) c -> p t h c", t=NT)
    SetOnes(net, v)
    linear_heads(net, XT, w, (2 * D, 3 * D), v4, net.row(ins["L2_mix_qkv_b"][:, 2 * D:3 * D]))
    kv = net.kv[:, 0:780].rearrange("p (c w) -> p c w", c=6)
    KvSummary(net, [(tok(G[2])[:, :, j * 128:(j + 1) * 128], 2 * j, 2, kv[:, j], 64) for j in range(6)], v, 1.0, clear=net.kv[:, 0:780])
    KvApply(net, pairs_of(feat(G[0]), kv), tok(G[1]), 0.0)
    ToFeatures(net, tok(G[1]), feat(G[0]))
    AddRow(net, tok(G[5]), net.row(ins["L2_mix_proj_b"]))
    linear(net, feat(G[0]), ins["L2_mix_proj_w"], tok(G[5]), "add", add=tok(G[5]))
    LayerNorm(net, tok(G[5]), tok(G[0]), 1e-8, net.row(ins["L2_mix_ln2_w"]), net.row(ins["L2_mix_ln2_b"]))
    ToFeatures(net, tok(G[0]), XT)
    Add(net, R, R, tok(G[5]))
    AddRow(net, R, net.row(ins["L2_mix_fc2_b"]))
    for q in range(4):
        linear_T(net, XT, ins["L2_mix_fc1_w"], feat(G[q % 2]), bias=col["fc1_b_c"][:, 6 * q:6 * q + 6], kind="gelu", cols=(q * D, (q + 1) * D), evac="a")
        linear(net, feat(G[q % 2]), ins["L2_mix_fc2_w"], R, "add", add=R, rows=(q * D, (q + 1) * D))
    if upto == 5:
        return
    X = tok(G[5])
    LayerNorm(net, R, X, 1e-5)
    LayerNorm(net, X, tok(G[0]), 1e-5, net.row(ins["L2_ffn_ln1_g"]), net.row(ins["L2_ffn_ln1_b"]))
    ToFeatures(net, tok(G[0]), XT)
    w = ins["L2_ffn_in_wT"]
    linear_T(net, XT, w, feat(G[0]), bias=col["in_b_c"][:, 0:6], cols=(0, D))
    linear_T(net, XT, w, feat(G[1]), bias=col["in_b_c"][:, 6:12], cols=(D, 2 * D))
    linear(net, XT, w, tok(G[2]), "row", bias=net.row(ins["L2_ffn_in_b"][:, 2 * D:3 * D]), cols=(2 * D, 3 * D))
    P, T, ctx = feat(G[3], NT, TP), feat(G[4], NT, TP), tok(net.XT)
    for h in range(12):
        r = slice(64 * (h % 2), 64 * (h % 2) + 64)
        rinv = net.st[:TP, 180 + 5 * (h % 2):185 + 5 * (h % 2)]
        AttnScores(net, feat(G[0])[r, h // 2], feat(G[1])[r, h // 2], P, rinv, 0.125)
        Apply(net, P, T, tok(G[2])[:, :, h * 64:(h + 1) * 64], rinv, ctx[:, :, h * 64:(h + 1) * 64])
    ToFeatures(net, ctx, feat(G[0]))
    AddRow(net, X, net.row(ins["L2_ffn_out_b"]))
    linear(net, feat(G[0]), ins["L2_ffn_out_wT"], X, "add", add=X)
    ToFeatures(net, X, feat(G[0]))
    load = net.weights(ins["L2_ffn_mlp_w1"])
    LinearT(net, feat(G[0]), [(load, 96 * k, 96, feat(G[1], 2, 96)[:, k], col["mlp_b1_c"][:, k:k + 1], "gelu") for k in range(2)], "a")
    AddRow(net, X, net.row(ins["L2_ffn_mlp_b2"]))
    linear(net, feat(G[1], 2, 96), ins["L2_ffn_mlp_w2"], X, "add", add=X, kp=96)
    LayerNorm(net, X, tok(G[0]), 1e-5, net.row(ins["L2_ffn_ln2_g"]), net.row(ins["L2_ffn_ln2_b"]))
    ToFeatures(net, tok(G[0]), XT)
    Add(net, R, R, X)
    Clear(net, logits, -1.0e38)
    gb = net.row(ins["L2_ffn_gate_b"])
    Linear(net, XT, [dict(load=net.weights(ins["L2_ffn_gate_wT"]), w=4, out=logits[:, :, 0:4], kind="add", by_tile=False, add=gb.dst[:TP, 0, :])], "d", rows=[gb])
    TopTwo(net, logits, gates, "top", sel)
    for e in range(4):
        hT = feat(G[e % 2], 2, 96)
        load = net.weights(ins["L2_ffn_exp_w1"][e])
        LinearT(net, XT, [(load, 96 * k, 96, hT[:, k], col["exp_b1_c"][:, 2 * e + k:2 * e + k + 1], "gelu") for k in range(2)], "a")
        GatedRows(net, R, gates[:, :, e], net.row(ins["L2_ffn_exp_b2"][e:e + 1, :]))
        for j in range(2):
            load = net.weights(ins["L2_ffn_exp_w2"][e][:, j * UNIT:(j + 1) * UNIT], 96)
            cs = slice(j * UNIT, (j + 1) * UNIT)
            Linear(net, hT, [dict(load=load, w=UNIT, out=R[:, :, cs], kind="gate", gate=gates[:, :, e], add=R[:, :, cs])], "d")
    if upto == 6:
        return

    LayerNorm(net, R, tok(G[5]), 1e-5)
    ToFeatures(net, tok(G[5]), XT)
    linear(net, XT, ins["L3_gnn_W1"], tok(G[0]))
    gat_layer(net, [(tok(G[0]), 1)], 1, D, ins["L3_gnn_att_src1"], ins["L3_gnn_att_dst1"], P_, T_, 0.0, [tok(G[4])], ins["L3_gnn_b1"])
    ToFeatures(net, tok(G[4]), feat(G[1]), "relu")
    linear(net, feat(G[1]), ins["L3_gnn_W2"], tok(G[0]))
    AddRow(net, R, net.row(ins["L3_gnn_b2"]))
    gat_layer(net, [(tok(G[0]), 1)], 1, D, ins["L3_gnn_att_src2"], ins["L3_gnn_att_dst2"], P_, T_, 0.0, [R], add=R)
    w = ins["L3_mix_W_qkv"]
    Clear(net, net.fw[:, :])
    fws = [net.into(net.fn[:, :], ins["norms3"], net.now())]
    for s in range(2):
        fws.append(net.into(net.fw[64 * s:64 * s + 64, 256 * s:256 * s + 256], ins["L3_mix_rfT"], net.now()))
    wc = lambda m: net.fw[:, m * 128:(m + 1) * 128]
    nc_ = lambda m: net.fn[:, m * 128:(m + 1) * 128]
    v = G[4][:TP, 0:NT * 12 * 65].rearrange("p (t c) -> p t c", c=65)
    v4 = v.rearrange("p (t h) c -> p t h c", t=NT)
    SetOnes(net, v)
    linear_heads(net, XT, w, (2 * D, 3 * D), v4)
    kv = net.kv[:, :].rearrange("p (c w) -> p c w", c=24)
    linear_T(net, XT, w, feat(G[0]), cols=(D, 2 * D))
    Square(net, feat(G[0]), feat(G[1]))
    for c in range(6):
        phik = G[2 + c % 2][:TP, 0:NT * 512].rearrange("p (t m) -> p t m", t=NT)
        PhiTok(net, feat(G[0]), feat(G[1]), [[(c, wc(m), nc_(m))] for m in range(4)], phik, net.lnc[:, 1:2], fws)
        KvSummary(net, [(phik[:, :, m * 128:(m + 1) * 128], 2 * c + m // 2, 1, kv[:, 4 * c + m], 128) for m in range(4)], v)
    linear_T(net, XT, w, feat(G[0]), cols=(0, D))
    Square(net, feat(G[0]), feat(G[1]))
    for c in range(6):
        phiq = feat(G[2 + c % 2], 4)
        PhiFeat(net, feat(G[0]), feat(G[1]), [[(c, wc(m), nc_(m))] for m in range(4)], phiq, net.lnc[:, 1:2])
        KvApply(net, [[(2 * c + s, 1, tuple((phiq[:, 2 * s + m], kv[:, 4 * c + 2 * s + m]) for m in range(2))) for s in range(2)]], tok(G[4]) if False else tok(net.XT), 1e-6)
    ToFeatures(net, tok(net.XT), feat(G[0]))
    AddRow(net, tok(G[5]), net.row(ins["L3_mix_b_proj"]))
    linear(net, feat(G[0]), ins["L3_mix_W_proj"], tok(G[5]), "add", add=tok(G[5]))
    LayerNorm(net, tok(G[5]), tok(G[0]), 1e-5, net.row(ins["L3_mix_gamma"]), net.row(ins["L3_mix_beta"]))
    Add(net, R, R, tok(G[0]))
    if upto == 7:
        return
    LayerNorm(net, R, tok(G[0]), 1e-5)
    ToFeatures(net, tok(G[0]), XT)
    Linear(net, XT, [dict(load=net.weights(ins["L3_ffn_Wg"]), w=8, out=logits, kind="copy")], "d")
    TopTwo(net, logits, gates, "top", sel, first)
    Capacity(net, gates, sel, first, net.rows(ins["tri"]), int(1.2 * N / 8))
    for e in range(8):
        hT = feat(G[e % 2], 2)
        load = net.weights(ins["L3_ffn_W1"][e])
        LinearT(net, XT, [(load, 0, 128, hT[:, 0], None, "copy"), (load, 128, 128, hT[:, 1], None, "silu")], "a")
        Multiply(net, hT[:, 0], hT[:, 1])
        for j in range(2):
            load = net.weights(ins["L3_ffn_W2"][e][:, j * UNIT:(j + 1) * UNIT])
            cs = slice(j * UNIT, (j + 1) * UNIT)
            Linear(net, hT[:, 0:1], [dict(load=load, w=UNIT, out=R[:, :, cs], kind="gate", gate=gates[:, :, e], add=R[:, :, cs])], "d")


def pairs_of(phi, kv):
    return [[(2 * j, 2, ((phi[:, j], kv[:, j]),)) for j in range(3 * q, 3 * q + 3)] for q in range(2)]


def bass_gps_kernel(nc, ins, out, upto=99):
    with ExitStack() as ctx:
        net = Net(nc, ctx, ins)
        network(net, upto)
        block = ctx.enter_context(nc.Block())
        n_const = 16 * len(net.consts)

        @block.sync
        def _(sp):
            for dst, src in net.consts:
                sp.dma_start(dst, src).then_inc(net.const_landed, 16)
            for load in net.loads:
                if isinstance(load, SlotExperts):
                    load.sync(sp)
                    continue
                if load.before:
                    for sem, value in load.before.used:
                        if value:
                            sp.wait_ge(sem, value)
                sp.dma_start(load.dst, load.src).then_inc(load.sem, 16)
            for sem, value in net.now():
                sp.wait_ge(sem, value)
            sp.dma_start(out.rearrange("(t p) d -> p t d", p=TP), net.tok(net.R)).then_inc(net.stored, 16)
            sp.wait_ge(net.stored, 16)

        @block.tensor
        def _(pe):
            pe.wait_ge(net.const_landed, n_const)
            for stage in net.stages:
                stage.tensor(pe)
                assert net.pe.issued <= net.pe.planned, stage

        @block.scalar
        def _(act):
            act.wait_ge(net.const_landed, n_const)
            for stage in net.stages:
                stage.scalar(act)

        @block.vector
        def _(dve):
            dve.wait_ge(net.const_landed, n_const)
            for stage in net.stages:
                assert net.dve.issued == stage.d0, stage
                stage.vector(dve)

        @block.gpsimd
        def _(pool):
            pool.wait_ge(net.const_landed, n_const)
            for stage in net.stages:
                stage.gpsimd(pool)

        for ticks in (net.pe, net.act, net.dve, net.pool):
            assert ticks.issued == ticks.planned, (ticks.sem, ticks.issued, ticks.planned)


_TURNED = {"L0_mix_w_mapT": "L0_mix_w_map", "L0_mix_w_outT": "L0_mix_w_out", "L1_mix_kqv_wT": "L1_mix_kqv_w", "L1_mix_proj_wT": "L1_mix_proj_w",
           "L1_ffn_router_wT": "L1_ffn_router_w", "L2_gnn_W1T": "L2_gnn_W1", "L2_gnn_W2T": "L2_gnn_W2", "L2_ffn_in_wT": "L2_ffn_in_w",
           "L2_ffn_out_wT": "L2_ffn_out_w", "L2_ffn_gate_wT": "L2_ffn_gate_w", "L3_mix_rfT": "L3_mix_random_features"}
_ROWS = ["L0_gnn_a_src0", "L0_gnn_a_dst0", "L0_gnn_b0", "L0_gnn_a_src1", "L0_gnn_a_dst1", "L0_gnn_b1", "L0_gnn_a_src2", "L0_gnn_a_dst2", "L0_gnn_b2",
         "L0_gnn_b_out", "L0_mix_g_k", "L0_mix_b_k", "L0_mix_g_v", "L0_mix_b_v", "L0_mix_b_out", "L1_gnn_b", "L1_mix_proj_b",
         "L2_gnn_att_src1", "L2_gnn_att_dst1", "L2_gnn_b1", "L2_gnn_att_src2", "L2_gnn_att_dst2", "L2_gnn_b2", "L2_mix_qkv_b", "L2_mix_proj_b",
         "L2_mix_fc2_b", "L2_mix_ln1_w", "L2_mix_ln1_b", "L2_mix_ln2_w", "L2_mix_ln2_b", "L2_ffn_ln1_g", "L2_ffn_ln1_b", "L2_ffn_in_b",
         "L2_ffn_out_b", "L2_ffn_mlp_b2", "L2_ffn_ln2_g", "L2_ffn_ln2_b", "L2_ffn_gate_b", "L3_gnn_att_src1", "L3_gnn_att_dst1", "L3_gnn_b1",
         "L3_gnn_att_src2", "L3_gnn_att_dst2", "L3_gnn_b2", "L3_mix_b_proj", "L3_mix_gamma", "L3_mix_beta"]
_PLAIN = ["x", "src", "dst", "L0_gnn_W_ah", "L0_gnn_W0", "L0_gnn_W1", "L0_gnn_W2", "L0_gnn_W_out", "L0_ffn_w1", "L0_ffn_b1", "L0_ffn_w2",
          "L0_ffn_b2", "L1_gnn_W", "L1_ffn_w1", "L1_ffn_w2", "L2_mix_qkv_w", "L2_mix_proj_w", "L2_mix_fc1_w", "L2_mix_fc2_w", "L2_ffn_mlp_w1",
          "L2_ffn_mlp_w2", "L2_ffn_exp_w1", "L2_ffn_exp_w2", "L2_ffn_exp_b2", "L3_gnn_W1", "L3_gnn_W2", "L3_mix_W_qkv", "L3_mix_W_proj",
          "L3_ffn_Wg", "L3_ffn_W1", "L3_ffn_W2"]


def kernel(**inputs):
    import math

    import numpy as np
    import concourse.bacc as bacc
    from concourse.bass_utils import run_bass_kernel_spmd

    lay = np.ascontiguousarray
    a = {name: np.asarray(v) for name, v in inputs.items()}
    columns = lambda v, p: lay(v.reshape(-1, p).T)
    arrays = {n: lay(a[n]) for n in _PLAIN}
    arrays.update({n: lay(a[o].T) for n, o in _TURNED.items()})
    arrays.update({n: lay(a[n].reshape(1, -1)) for n in _ROWS})
    arrays["L0_ffn_scale"] = lay(a["L0_ffn_scale"].reshape(1, 1))
    arrays["L0_ffn_phi"] = lay(a["L0_ffn_phi"].reshape(D, 64))
    arrays["L1_mix_wT"] = lay(a["L1_mix_w"].transpose(0, 2, 1))
    arrays["L1_mix_kqv_b_v"] = lay(a["L1_mix_kqv_b"][2 * D:].reshape(1, -1))
    arrays["b_ah_c"] = columns(a["L0_gnn_b_ah"], 128)
    arrays["kqv_b_c"] = columns(a["L1_mix_kqv_b"][:2 * D], 128)
    arrays["qkv_b_c"] = columns(a["L2_mix_qkv_b"][:D], 128)
    arrays["fc1_b_c"] = columns(a["L2_mix_fc1_b"], 128)
    arrays["in_b_c"] = columns(a["L2_ffn_in_b"][:2 * D], 128)
    arrays["mlp_b1_c"] = columns(a["L2_ffn_mlp_b1"], 96)
    arrays["exp_b1_c"] = columns(a["L2_ffn_exp_b1"], 96)
    arrays["ident"] = np.eye(128, dtype=np.float32)
    arrays["iota"] = np.arange(N, dtype=np.float32).reshape(1, N)
    arrays["tri"] = np.triu(np.ones((128, 128), np.float32))
    arrays["lnc"] = np.tile(np.array([[-0.5 * math.log(32.0), -0.5 * math.log(256.0)]], np.float32), (128, 1))
    norms1 = np.zeros((128, 2, 128), np.float32)
    norms3 = np.zeros((128, 512), np.float32)
    for s in range(2):
        norms3[64 * s:64 * s + 64, 256 * s:256 * s + 256] = -0.5
        for i in range(2):
            norms1[64 * s:64 * s + 64, i, 64 * i + 32 * s:64 * i + 32 * s + 32] = -0.5
    arrays["norms1"], arrays["norms3"] = norms1.reshape(128, 256), norms3

    nc = bacc.Bacc("TRN2", target_bir_lowering=False, num_devices=1)
    ins = {n: nc.dram_tensor(f"in_{n}", v.shape, mybir.dt.from_np(v.dtype), kind="ExternalInput").ap() for n, v in arrays.items()}
    out = nc.dram_tensor("out", (N, D), F32, kind="ExternalOutput").ap()
    bass_gps_kernel(nc, ins, out, UPTO)
    r = run_bass_kernel_spmd(nc, [{f"in_{n}": v for n, v in arrays.items()}], core_ids=[0])
    return r.results[0]["out"]


UPTO = 99
```

```python
from contextlib import ExitStack

import concourse.bass as bass
from concourse import mybir

F32 = mybir.dt.float32
BF16 = mybir.dt.bfloat16
F16 = mybir.dt.float16
I32 = mybir.dt.int32
ALU = mybir.AluOpType
ACT = mybir.ActivationFunctionType
AX = mybir.AxisListType

N, D, E = 625, 768, 20000
TP = 125
NT = N // TP
KC = D // 128
HALVES = ((0, 3), (3, 5))
UNIT = 384
BUF = 3904
BANKS = 8
WSLOTS = 3
MASKED = -1.0e30
SLOPE = 0.2


class Ticks:

    def __init__(self, sem):
        self.sem, self.planned, self.issued, self.joined = sem, 0, 0, 0

    def reserve(self, n):
        base = self.planned
        self.planned += n
        return base

    def one(self):
        self.issued += 1
        return 1


class Load:

    def __init__(self, src, dst, sem, value, before):
        self.src, self.dst, self.sem, self.value, self.before, self.used = src, dst, sem, value, before, None


class Slot:

    def __init__(self, buf, sem):
        self.buf, self.sem, self.value, self.last = buf, sem, 0, None

    def take(self, n):
        before, base = self.last, self.value
        self.value += 16 * n
        return before, base


class Net:

    def __init__(self, nc, ctx, ins):
        self.nc, self.ins = nc, ins
        sb = lambda name, shape, dt=F32: ctx.enter_context(nc.sbuf_tensor(name, shape, dt))
        sem = lambda name: ctx.enter_context(nc.semaphore(name))
        self.pe, self.act, self.dve, self.pool = (Ticks(sem(n)) for n in ("pe_done", "act_done", "dve_done", "pool_done"))
        self.const_landed, self.stored = sem("const_landed"), sem("stored")
        self.ps = ctx.enter_context(nc.psum_tensor("ps", [128, BANKS, 512], F32))
        self.R, self.XT = sb("resid", [128, BUF]), sb("xT", [128, BUF])
        self.G = [sb(f"buf{i}", [128, BUF]) for i in range(6)]
        self.counts = sb("edge_counts", [128, NT, N])
        self.mask = sb("edge_mask", [128, NT, N], BF16)
        self.P1 = sb("head_weights1", [128, NT * N])
        self.wbuf = sb("weights", [128, WSLOTS * 6 * UNIT])
        self.wslot = [self.wbuf[:, i * 6 * UNIT:(i + 1) * 6 * UNIT] for i in range(WSLOTS)]
        self.wsem = [sem(f"weights_landed{i}") for i in range(WSLOTS)]
        self.rslot = [sb(f"row{i}", [128, D]) for i in range(3)]
        self.rsem = [sem(f"row_landed{i}") for i in range(3)]
        self.ident = sb("ident", [128, 128])
        self.cols = sb("bias_cols", [128, 96])
        self.kv = sb("kv", [128, 24 * 65])
        self.misc = sb("misc", [128, D + 512])
        self.fw, self.fn = self.misc[:, 0:D], self.misc[:, D:D + 512]
        self.asb = sb("a_src_rows", [128, N])
        self.st = sb("stats", [128, 640])
        self.bn = self.st[:TP, 0:60].rearrange("p (t s) -> p t s", t=NT)
        self.mv = self.st[:TP, 60:70].rearrange("p (t s) -> p t s", t=NT)
        self.ones, self.zeros, self.iota64 = sb("ones", [128, 128]), sb("zeros", [128, UNIT]), sb("iota64", [128, 64])
        self.lnc, self.slot_scale = sb("lnc", [128, 2]), sb("slot_scale", [128, 1])
        self.stages, self.loads = [], []
        self.wring = [Slot(a, s) for a, s in zip(self.wslot, self.wsem)]
        self.rring = [Slot(a, s) for a, s in zip(self.rslot, self.rsem)]
        self.sem, self.expert_loads = sem, 0
        self.esem = [sem(f"expert_landed{j}") for j in range(4)]
        self.freed, self.nbank = {}, 0
        self.consts, self.ncol = [], 0

    def now(self):
        return [(t.sem, t.joined) for t in (self.pe, self.act, self.dve, self.pool)]

    def end(self):
        return [(t.sem, t.planned) for t in (self.pe, self.act, self.dve, self.pool)]

    def add(self, stage):
        self.stages.append(stage)
        return stage

    def bank(self):
        self.nbank += 1
        return self.nbank - 1

    def _load(self, src, ring, shape):
        slot = ring.pop(0)
        ring.append(slot)
        p, c, w = shape
        before, base = slot.take(1)
        load = Load(src, slot.buf[:p, 0:c * w].rearrange("p (c w) -> p c w", c=c), slot.sem, base + 16, before)
        slot.last = load
        self.loads.append(load)
        return load

    def into(self, dst, src, after):
        free = Load(None, None, None, 0, None)
        free.used = after
        load = Load(src, dst, self.sem(f"landed_{len(self.loads)}"), 16, free)
        self.loads.append(load)
        return load

    def weights(self, src, kp=128):
        k, n = src.shape
        return self._load(src.rearrange("(c p) n -> p c n", p=kp), self.wring, (kp, k // kp, n))

    def row(self, src):
        n = src.shape[1]
        return self._load(src.to_broadcast([128, n]).unsqueeze(1), self.rring, (128, 1, n))

    def rows(self, src):
        return self._load(src.unsqueeze(1), self.rring, (src.shape[0], 1, src.shape[1]))

    def const(self, dst, src):
        self.consts.append((dst, src))

    def col(self, name, parts=128):
        src = self.ins[name]
        n = src.shape[1]
        dst = self.cols[:parts, self.ncol:self.ncol + n]
        self.ncol += n
        self.const(dst, src)
        return dst

    def tok(self, buf, w=D):
        return buf[:TP, 0:NT * w].rearrange("p (t w) -> p t w", t=NT)

    def feat(self, buf, c=KC, p=128):
        return buf[:p, 0:c * N].rearrange("p (c n) -> p c n", c=c)


class Stage:

    side = False

    def __init__(self, net, after=None):
        self.net, self.nc = net, net.nc
        self.after = net.now() if after is None else after
        self.loads = []
        self.g = []

    def take(self, pe=0, act=0, dve=0, pool=0):
        n = self.net
        self.p0, self.a0, self.d0, self.l0 = (t.reserve(k) for t, k in ((n.pe, pe), (n.act, act), (n.dve, dve), (n.pool, pool)))
        self.size = (pe, act, dve, pool)
        for t, k in ((n.pe, pe), (n.act, act), (n.dve, dve), (n.pool, pool)):
            if k and not self.side:
                t.joined = t.planned
        self.done = self.ends()
        for load in self.loads:
            load.used = self.done
        n.add(self)

    def groups(self, n, evac):
        net = self.net
        ca = cd = 0
        a0, d0 = net.act.planned, net.dve.planned
        for i in range(n):
            b, e = net.bank(), evac[i % len(evac)]
            if e == "a":
                ca += 1
                net.freed[b] = (net.act.sem, a0 + ca)
            else:
                cd += 1
                net.freed[b] = (net.dve.sem, d0 + cd)
            self.g.append((b, e))
        return ca, cd

    def free(self, b):
        return self.net.freed[b - BANKS]

    def ends(self):
        return [(t.sem, b + k) for t, b, k in zip((self.net.pe, self.net.act, self.net.dve, self.net.pool), (self.p0, self.a0, self.d0, self.l0), self.size) if k]

    def begin(self, eng):
        for sem, value in self.after:
            if value > 0:
                eng.wait_ge(sem, value)

    def landed(self, eng):
        for load in self.loads:
            eng.wait_ge(load.sem, load.value)

    def tensor(self, pe):
        pass

    def scalar(self, act):
        pass

    def vector(self, dve):
        pass

    def gpsimd(self, pool):
        pass


def evacuate(nc, eng, kind, out, ps, bias=None, gate=None, add=None):
    if eng == "a":
        func = {"copy": ACT.Identity, "relu": ACT.Relu, "gelu": ACT.Gelu, "tanh_gelu": ACT.Gelu_apprx_tanh,
                "silu": ACT.Silu, "square": ACT.Square}[kind]
        if bias is None:
            return nc.scalar.activation(out, ps, func)
        return nc.scalar.activation(out, ps, func, bias=bias)
    if kind == "copy":
        if bias is None:
            return nc.vector.tensor_copy(out, ps)
        return nc.vector.tensor_scalar(out, ps, bias, None, ALU.add)
    if kind == "relu":
        if bias is None:
            return nc.vector.tensor_scalar(out, ps, 0.0, None, ALU.max)
        return nc.vector.tensor_scalar(out, ps, bias, 0.0, ALU.add, ALU.max)
    if kind == "mul":
        return nc.vector.tensor_tensor(out, ps, add, ALU.mult)
    if kind == "add":
        return nc.vector.tensor_tensor(out, ps, add, ALU.add)
    if kind == "gate":
        return nc.vector.scalar_tensor_tensor(out=out, in0=ps, scalar=gate, in1=add, op0=ALU.mult, op1=ALU.add)
    return nc.vector.tensor_scalar(out, ps, gate, None, ALU.mult)


def tile_stats(net, dve, x, t):
    done = net.dve
    dve.wait_ge(done.sem, done.issued)
    for j in range(2):
        net.nc.vector.bn_stats(net.bn[:, t, 6 * j:6 * j + 6], x[:, t, j * UNIT:(j + 1) * UNIT]).then_inc(done.sem, done.one())
    dve.wait_ge(done.sem, done.issued)
    net.nc.vector.bn_aggr(net.mv[:, t, :], net.bn[:, t, :]).then_inc(done.sem, done.one())


class LinearT(Stage):

    def __init__(self, net, xT, parts, evac="ad", after=None):
        super().__init__(net, after)
        self.xT, self.parts = xT, parts
        a, d = self.groups(2 * len(parts), evac)
        self.loads = list(dict.fromkeys(q[0] for q in parts))
        self.take(pe=2 * len(parts), act=a, dve=d)
        for n, q in enumerate(parts):
            q[0].used = [(net.pe.sem, self.p0 + 2 * n + 2)]

    def chunk_done(self, m):
        return [self.net.freed[b] for b, _ in self.g[2 * m:2 * m + 2]]

    def tensor(self, pe):
        self.begin(pe)
        kp, kc = self.xT.shape[0], self.xT.shape[1]
        i = 0
        for load, c0, w, out, bias, kind in self.parts:
            pe.wait_ge(load.sem, load.value)
            for t0, t1 in HALVES:
                b = self.g[i][0]
                if b >= BANKS:
                    pe.wait_ge(*self.free(b))
                for k in range(kc):
                    mm = self.nc.tensor.matmul(self.net.ps[:w, b % BANKS, 0:(t1 - t0) * TP], load.dst[:kp, k, c0:c0 + w],
                                               self.xT[:, k, t0 * TP:t1 * TP], start=(k == 0), stop=(k == kc - 1))
                mm.then_inc(self.net.pe.sem, self.net.pe.one())
                i += 1

    def evac(self, eng, letter, ticks):
        self.begin(eng)
        for i, (b, e) in enumerate(self.g):
            if e == letter:
                load, c0, w, out, bias, kind = self.parts[i // 2]
                t0, t1 = HALVES[i % 2]
                eng.wait_ge(self.net.pe.sem, self.p0 + i + 1)
                evacuate(self.nc, letter, kind, out[:, t0 * TP:t1 * TP], self.net.ps[:w, b % BANKS, 0:(t1 - t0) * TP],
                         bias=bias).then_inc(ticks.sem, ticks.one())

    def scalar(self, act):
        self.evac(act, "a", self.net.act)

    def vector(self, dve):
        self.evac(dve, "d", self.net.dve)


class Linear(Stage):

    def __init__(self, net, xT, units, evac="ad", after=None, rows=(), stats=None):
        super().__init__(net, after)
        self.xT, self.units, self.rows, self.stats = xT, units, rows, stats
        a = d = 0
        for i in range(NT * len(units)):
            b, e = net.bank(), evac[i % len(evac)]
            a, d = a + (e == "a"), d + (e == "d")
            net.freed[b] = (net.act.sem, net.act.planned + a) if e == "a" else (net.dve.sem, net.dve.planned + d)
            if stats is not None and i >= NT * (len(units) - 1):
                d += 3
            self.g.append((b, e))
        self.loads = list(rows)
        self.take(pe=NT * len(units), act=a, dve=d)
        for n, u in enumerate(units):
            u["load"].used = [(net.pe.sem, self.p0 + NT * (n + 1))]

    def tensor(self, pe):
        self.begin(pe)
        kc = self.xT.shape[1]
        i = 0
        for u in self.units:
            load = u["load"]
            pe.wait_ge(load.sem, load.value)
            for t in range(NT):
                b = self.g[i][0]
                if b >= BANKS:
                    pe.wait_ge(*self.free(b))
                for k in range(kc):
                    mm = self.nc.tensor.matmul(self.net.ps[:TP, b % BANKS, 0:u["w"]], self.xT[:, k, t * TP:(t + 1) * TP],
                                               load.dst[:, k, u.get("c0", 0):u.get("c0", 0) + u["w"]],
                                               start=(k == 0), stop=(k == kc - 1))
                mm.then_inc(self.net.pe.sem, self.net.pe.one())
                i += 1

    def evac(self, eng, letter, ticks):
        self.begin(eng)
        for row in self.rows:
            eng.wait_ge(row.sem, row.value)
        for i, (b, e) in enumerate(self.g):
            if e == letter:
                u, t = self.units[i // NT], i % NT
                ps = self.net.ps[:TP, b % BANKS, 0:u["w"]]
                out, add = u["out"][:, t], u.get("add")
                if len(out.shape) == 3:
                    ps = ps.rearrange("p (h c) -> p h c", h=out.shape[1])
                if add is not None:
                    add = add[:, t] if u.get("by_tile", True) else add
                gate = u["gate"][:, t:t + 1] if "gate" in u else None
                eng.wait_ge(self.net.pe.sem, self.p0 + i + 1)
                evacuate(self.nc, letter, u["kind"], out, ps, add=add, gate=gate).then_inc(ticks.sem, ticks.one())
                if self.stats is not None and i >= NT * (len(self.units) - 1):
                    tile_stats(self.net, eng, self.stats, t)

    def scalar(self, act):
        self.evac(act, "a", self.net.act)

    def vector(self, dve):
        self.evac(dve, "d", self.net.dve)


class ToFeatures(Stage):

    def __init__(self, net, x, out, func="copy", evac="ad", after=None, tiles=None):
        super().__init__(net, after)
        self.x, self.out, self.func, self.tiles = x, out, func, tiles
        self.c = out.shape[1]
        self.per = 3 if self.c % 3 == 0 else self.c
        self.ng = self.c // self.per
        a, d = self.groups(NT * self.ng, evac)
        self.take(pe=NT * self.ng, act=a, dve=d)

    def tensor(self, pe):
        self.begin(pe)
        w = self.out.shape[0]
        for i, (b, e) in enumerate(self.g):
            t, c0 = i // self.ng, i % self.ng * self.per
            if b >= BANKS:
                pe.wait_ge(*self.free(b))
            if self.tiles and c0 == 0:
                pe.wait_ge(*self.tiles[t])
            for c in range(c0, c0 + self.per):
                mm = self.nc.tensor.transpose(self.net.ps[:w, b % BANKS, (c - c0) * TP:(c - c0 + 1) * TP],
                                              self.x[:, t, c * w:(c + 1) * w], self.net.ident[:TP, :TP])
            mm.then_inc(self.net.pe.sem, self.net.pe.one())

    def evac(self, eng, letter, ticks):
        self.begin(eng)
        w = self.out.shape[0]
        for i, (b, e) in enumerate(self.g):
            if e == letter:
                t, c0 = i // self.ng, i % self.ng * self.per
                eng.wait_ge(self.net.pe.sem, self.p0 + i + 1)
                evacuate(self.nc, letter, self.func, self.out[:, c0:c0 + self.per, t * TP:(t + 1) * TP],
                         self.net.ps[:w, b % BANKS, 0:self.per * TP].rearrange("p (c n) -> p c n", c=self.per)).then_inc(ticks.sem, ticks.one())

    def scalar(self, act):
        self.evac(act, "a", self.net.act)

    def vector(self, dve):
        self.evac(dve, "d", self.net.dve)


class LayerNorm(Stage):

    def __init__(self, net, x, out, eps, gamma=None, beta=None, ready=False, after=None):
        super().__init__(net, after)
        self.x, self.out, self.eps, self.gamma, self.beta, self.ready = x, out, eps, gamma, beta, ready
        self.loads = [r for r in (gamma, beta) if r]
        self.rstd = net.st[:TP, 70:75]
        n = 0 if ready else 3 * NT
        self.root = net.dve.planned + n + 1
        self.tiles = [(net.dve.sem, net.dve.planned + n + 2 + (t + 1 if not gamma else min(2 * t + 3, 2 * NT))) for t in range(NT)]
        self.take(dve=n + 2 + (2 * NT if gamma else NT), act=1)

    def vector(self, dve):
        self.begin(dve)
        nc, done, mv = self.nc, self.net.dve, self.net.mv
        if not self.ready:
            for t in range(NT):
                tile_stats(self.net, dve, self.x, t)
        dve.wait_ge(done.sem, done.issued)
        nc.vector.tensor_scalar(self.rstd, mv[:, :, 1], self.eps, None, ALU.add).then_inc(done.sem, done.one())
        dve.wait_ge(self.net.act.sem, self.a0 + 1)
        nc.vector.reciprocal(self.rstd, self.rstd).then_inc(done.sem, done.one())
        if not self.gamma:
            dve.wait_ge(done.sem, done.issued)
            for t in range(NT):
                nc.vector.tensor_scalar(self.out[:, t], self.x[:, t], mv[:, t, 0:1], self.rstd[:, t:t + 1],
                                        ALU.subtract, ALU.mult).then_inc(done.sem, done.one())
            return
        self.landed(dve)
        first = done.issued
        for t in range(NT + 1):
            if t < NT:
                nc.vector.scalar_tensor_tensor(out=self.out[:, t], in0=self.x[:, t], scalar=mv[:, t, 0:1], in1=self.gamma.dst[:TP, 0],
                                               op0=ALU.subtract, op1=ALU.mult).then_inc(done.sem, done.one())
            if t > 0:
                dve.wait_ge(done.sem, first + (1 if t == 1 else 2 * t - 2))
                nc.vector.scalar_tensor_tensor(out=self.out[:, t - 1], in0=self.out[:, t - 1], scalar=self.rstd[:, t - 1:t], in1=self.beta.dst[:TP, 0],
                                               op0=ALU.mult, op1=ALU.add).then_inc(done.sem, done.one())

    def scalar(self, act):
        self.begin(act)
        act.wait_ge(self.net.dve.sem, self.root)
        self.nc.scalar.activation(self.rstd, self.rstd, ACT.Sqrt).then_inc(self.net.act.sem, self.net.act.one())


def norm_T(net, x, out, outT, eps, gamma=None, beta=None, ready=False):
    start = net.now()
    norm = LayerNorm(net, x, out, eps, gamma, beta, ready)
    ToFeatures(net, out, outT, evac="aaaaaaaadd" if gamma is None else "a", after=start, tiles=norm.tiles)
    return norm


class AddRow(Stage):
    side = True

    def __init__(self, net, x, row, after=None):
        super().__init__(net, after)
        self.x, self.row, self.loads = x, row, [row]
        self.take(pool=NT)

    def gpsimd(self, pool):
        self.begin(pool)
        self.landed(pool)
        for t in range(NT):
            self.nc.gpsimd.tensor_tensor(self.x[:, t], self.x[:, t], self.row.dst[:TP, 0], ALU.add).then_inc(self.net.pool.sem, self.net.pool.one())


class ReluAdd(Stage):

    def __init__(self, net, x, y, after=None):
        super().__init__(net, after)
        self.x, self.y = x, y
        self.take(dve=NT)

    def vector(self, dve):
        self.begin(dve)
        for t in range(NT):
            self.nc.vector.scalar_tensor_tensor(out=self.x[:, t], in0=self.y[:, t], scalar=0.0, in1=self.x[:, t],
                                                op0=ALU.max, op1=ALU.add).then_inc(self.net.dve.sem, self.net.dve.one())


class Add(Stage):
    side = True

    def __init__(self, net, out, x, y, after=None, side=True):
        super().__init__(net, after)
        self.out, self.x, self.y, self.side = out, x, y, side
        self.take(pool=NT)

    def gpsimd(self, pool):
        self.begin(pool)
        for t in range(NT):
            self.nc.gpsimd.tensor_tensor(self.out[:, t], self.x[:, t], self.y[:, t], ALU.add).then_inc(self.net.pool.sem, self.net.pool.one())


class EdgeCounts(Stage):
    CH = E // TP
    DEPTH = 4

    def __init__(self, net, after=None):
        super().__init__(net, after)
        g = net.G
        self.idx_i = g[0][:TP, 0:2 * self.CH].bitcast(I32).rearrange("p (s c) -> p s c", s=2)
        self.idx = g[1][:TP, 0:2 * self.CH].rearrange("p (s c) -> p s c", s=2)
        self.iota = g[2][:TP, 0:N]
        self.iota16 = g[2][:TP, N:N + 320].bitcast(F16)[:, 0:N]
        self.hot = [[g[3 + s][:TP, 320 * j:320 * j + 320].bitcast(F16)[:, 0:N] for s in range(2)] for j in range(self.DEPTH)]
        self.zero = g[5][:TP, 0:320].bitcast(F16)[:, 0:N]
        for s, name in enumerate(("src", "dst")):
            net.const(self.idx_i[:, s, :], net.ins[name].rearrange("(p c) -> p c", p=TP))
        net.const(self.iota, net.ins["iota"].to_broadcast([TP, N]))
        while net.nbank % BANKS:
            net.freed[net.bank()] = (net.dve.sem, net.dve.planned)
        n_dve = 3 + 2 * self.CH
        for i in range(BANKS):
            net.freed[net.bank()] = (net.dve.sem, net.dve.planned + n_dve + 2 * NT)
        self.take(pe=1 + self.CH + 1, dve=n_dve + 2 * NT)

    def products(self, lhs, rhs, start, stop):
        ps = self.net.ps
        for t in range(NT):
            self.nc.tensor.matmul(ps[:TP, t, 0:500], lhs[:, t * TP:(t + 1) * TP], rhs[:, 0:500], start=start, stop=stop, skip_group_check=True)
            b, c = (5, t * TP) if t < 4 else (6, 0)
            mm = self.nc.tensor.matmul(ps[:TP, b, c:c + TP], lhs[:, t * TP:(t + 1) * TP], rhs[:, 500:625], start=start, stop=stop, skip_group_check=True)
        return mm

    def tensor(self, pe):
        self.begin(pe)
        done, dve = self.net.pe, self.net.dve
        pe.wait_ge(dve.sem, self.d0 + 3)
        self.products(self.zero, self.zero, True, False).then_inc(done.sem, done.one())
        with self.nc.tensor.Fori(0, self.CH // self.DEPTH) as i:
            for j in range(self.DEPTH):
                pe.wait_ge(dve.sem, i * (2 * self.DEPTH) + (self.d0 + 3 + 2 * j + 2))
                self.products(self.hot[j][1], self.hot[j][0], False, False).then_inc(done.sem, 1)
        done.issued += self.CH
        self.products(self.zero, self.zero, False, True).then_inc(done.sem, done.one())

    def vector(self, dve):
        self.begin(dve)
        nc, done, pe = self.nc, self.net.dve, self.net.pe
        nc.vector.memset(self.zero, 0.0).then_inc(done.sem, done.one())
        nc.vector.tensor_copy(self.idx, self.idx_i).then_inc(done.sem, done.one())
        nc.vector.tensor_copy(self.iota16, self.iota).then_inc(done.sem, done.one())
        dve.wait_ge(done.sem, done.issued)
        for j in range(self.DEPTH):
            for s in range(2):
                nc.vector.tensor_scalar(self.hot[j][s], self.iota16, self.idx[:, s, j:j + 1], None, ALU.is_equal).then_inc(done.sem, 1)
        with nc.vector.Fori(1, self.CH // self.DEPTH) as i:
            for j in range(self.DEPTH):
                dve.wait_ge(pe.sem, i * self.DEPTH + (self.p0 + 1 + j + 1 - self.DEPTH))
                for s in range(2):
                    nc.vector.tensor_scalar(self.hot[j][s], self.iota16, self.idx[:, s, bass.ds(i * self.DEPTH + j, 1)], None,
                                            ALU.is_equal).then_inc(done.sem, 1)
        done.issued += 2 * self.CH
        dve.wait_ge(pe.sem, self.p0 + self.CH + 2)
        ps, counts = self.net.ps, self.net.counts
        for t in range(NT):
            nc.vector.tensor_copy(counts[:TP, t, 0:500], ps[:TP, t, 0:500]).then_inc(done.sem, done.one())
            b, c = (5, t * TP) if t < 4 else (6, 0)
            nc.vector.tensor_copy(counts[:TP, t, 500:625], ps[:TP, b, c:c + TP]).then_inc(done.sem, done.one())


class SelfLoops(Stage):
    side = True

    def __init__(self, net, op, after=None):
        super().__init__(net, after)
        self.op = op
        self.take(dve=2 * NT)

    def vector(self, dve):
        self.begin(dve)
        nc, done, counts = self.nc, self.net.dve, self.net.counts
        for t in range(NT):
            diag = counts[:TP, t, t * TP:(t + 1) * TP]
            nc.vector.tensor_tensor(diag, diag, self.net.ident[:TP, :TP], self.op).then_inc(done.sem, done.one())
        dve.wait_ge(done.sem, done.issued)
        for t in range(NT):
            nc.vector.tensor_scalar(self.net.mask[:TP, t, :], counts[:TP, t, :], 0.0, MASKED, ALU.is_equal, ALU.mult).then_inc(done.sem, done.one())


class GatCoefs(Stage):
    side = True

    def __init__(self, net, h, heads, c, head0, a_src, a_dst, coef, scratch, after=None):
        super().__init__(net, after)
        self.h, self.heads, self.c, self.head0, self.coef, self.scratch = h, heads, c, head0, coef, scratch
        self.loads = [a_src, a_dst]
        self.take(dve=2 * NT * heads)

    def vector(self, dve):
        self.begin(dve)
        self.landed(dve)
        done = self.net.dve
        for s in range(2):
            for t in range(NT):
                for hd in range(self.heads):
                    cs = slice(hd * self.c, (hd + 1) * self.c)
                    n = (s * NT + t) * self.heads + hd
                    if n > 1:
                        dve.wait_ge(done.sem, self.d0 + n - 1)
                    self.nc.vector.tensor_tensor_reduce(
                        out=self.scratch[:TP, (n % 2) * D:(n % 2) * D + self.c], in0=self.h[:, t, cs],
                        in1=self.loads[s].dst[:TP, 0, cs], scale=1.0, scalar=0.0, op0=ALU.mult, op1=ALU.add,
                        accum_out=self.coef[:, s, self.head0 + hd, t:t + 1]).then_inc(done.sem, done.one())


FIRST = "first"


class Heads(Stage):

    def schedule(self, n_heads, first, prior):
        net = self.net
        self.order = {e: [] for e in ("pe", "act", "dve", "pool")}
        self.side = last = first < 0 and prior is FIRST
        for k in range(first, 0 if last else n_heads):
            self.step(k, k + 1 < n_heads, k >= 0)
        bases = dict(pe=net.pe.planned, act=net.act.planned, dve=net.dve.planned, pool=net.pool.planned)
        self.at = {e: {q: bases[e] + i + 1 for i, q in enumerate(seq)} for e, seq in self.order.items()}
        if first >= 0:
            for e in self.at:
                self.at[e].update(prior.at[e])
        self.bank = {}
        for q in self.order["pe"]:
            b = self.bank[q] = net.bank()
            engine, entry = self.reader(q)
            net.freed[b] = ({"act": net.act, "dve": net.dve}[engine].sem, self.at[engine][entry])
        self.take(**{e: len(seq) for e, seq in self.order.items()})

    def ps(self, q, p, w):
        return self.net.ps[:p, self.bank[q] % BANKS, 0:w]

    def wait(self, eng, engine, *entry):
        ticks = {"pe": self.net.pe, "act": self.net.act, "dve": self.net.dve, "pool": self.net.pool}[engine]
        eng.wait_ge(ticks.sem, self.at[engine][entry])

    def wait_bank(self, pe, q):
        if self.bank[q] >= BANKS:
            pe.wait_ge(*self.free(self.bank[q]))

    def turn_group(self, P, s, t0, t1, q):
        ps = self.ps(q, TP, (t1 - t0) * TP)
        for t in range(t0, t1):
            mm = self.nc.tensor.transpose(ps[:, (t - t0) * TP:(t - t0 + 1) * TP], P[:, t, s * TP:(s + 1) * TP], self.net.ident[:TP, :TP])
        return mm


class GatHeads(Heads):

    def __init__(self, net, heads, P, PT, eps, rows=(), after=None, first=-1, prior=None):
        super().__init__(net, after)
        self.heads, self.P, self.PT, self.eps, self.rows = heads, P, PT, eps, list(rows)
        self.loads = self.rows
        o = 80
        self.mx, self.b1, self.b2, self.sum = (net.st[:TP, o + 5 * k:o + 5 * k + 5] for k in range(4))
        self.rinv = [net.st[:TP, 180 + 5 * k:185 + 5 * k] for k in range(2)]
        self.relu = [net.misc[:TP, N * k:N * (k + 1)] for k in range(2)]
        c = heads[0][2].shape[2]
        self.w = c if c <= 512 else UNIT
        self.nw = c // self.w
        self.schedule(len(heads), first, prior)

    def step(self, k, scores, apply):
        pe, act, dve, pool = (self.order[e] for e in ("pe", "act", "dve", "pool"))
        n = k + 1
        if scores:
            pe += [("row", n, j) for j in range(2)]
            act += [("row", n, j) for j in range(2)]
            dve += [("max", n, t) for t in range(NT)] + [("small", n, j) for j in range(4)]
        if apply:
            pe += [("turn", k, s, j) for s in range(NT) for j in range(2)] + [("apply", k, t, j) for t in range(NT) for j in range(self.nw)]
            act += [("turn", k, s, j) for s in range(NT) for j in range(2)]
        if scores:
            act += [("relu", n, 0), ("relu", n, 1)]
            for t in range(NT):
                pool.append(("add", n, t))
                act.append(("exp", n, t))
                if t + 2 < NT:
                    act.append(("relu", n, t + 2))
        for t in range(NT):
            if apply:
                dve += [("out", k, t, j) for j in range(self.nw)]
            if scores:
                dve.append(("count", n, t))
        if scores:
            dve += [("sum", n), ("rinv", n)]

    def reader(self, q):
        return {"row": ("act", q), "turn": ("act", q), "apply": ("dve", ("out",) + q[1:])}[q[0]]

    def tensor(self, pe):
        self.begin(pe)
        nc, done = self.nc, self.net.pe
        for q in self.order["pe"]:
            self.wait_bank(pe, q)
            k = q[1]
            if q[0] == "row":
                t0, t1 = HALVES[q[2]]
                ps = self.ps(q, TP, (t1 - t0) * TP)
                for t in range(t0, t1):
                    mm = nc.tensor.matmul(ps[:, (t - t0) * TP:(t - t0 + 1) * TP], self.heads[k][0][:, t:t + 1].to_broadcast([TP, TP]),
                                          self.net.ident[:TP, :TP], start=True, stop=True)
            elif q[0] == "turn":
                t0, t1 = HALVES[q[3]]
                if q[2] == 0:
                    self.wait(pe, "dve", "count", k, t1 - 1)
                mm = self.turn_group(self.P[k % 2], q[2], t0, t1, q)
            else:
                t, j = q[2], q[3]
                for s in range(NT):
                    if t == 0 and j == 0:
                        self.wait(pe, "act", "turn", k, s, 1)
                    mm = nc.tensor.matmul(self.ps(q, TP, self.w), self.PT[:, s, t * TP:(t + 1) * TP],
                                          self.heads[k][2][:, s, j * self.w:(j + 1) * self.w], start=(s == 0), stop=(s == NT - 1))
            mm.then_inc(done.sem, done.one())

    def scalar(self, act):
        self.begin(act)
        nc, done = self.nc, self.net.act
        for q in self.order["act"]:
            k = q[1]
            if q[0] == "row":
                t0, t1 = HALVES[q[2]]
                self.wait(act, "pe", *q)
                ins = nc.scalar.activation(self.net.asb[:TP, t0 * TP:t1 * TP], self.ps(q, TP, (t1 - t0) * TP), ACT.Identity)
            elif q[0] == "turn":
                t0, t1 = HALVES[q[3]]
                self.wait(act, "pe", *q)
                ins = nc.scalar.activation(self.PT[:, q[2], t0 * TP:t1 * TP], self.ps(q, TP, (t1 - t0) * TP), ACT.Identity)
            elif q[0] == "relu":
                t = q[2]
                if t == 0:
                    self.wait(act, "dve", "small", k, 3)
                if t >= 2:
                    self.wait(act, "pool", "add", k, t - 2)
                ins = nc.scalar.activation(self.relu[t % 2], self.P[k % 2][:, t], ACT.Relu, bias=self.b1[:, t:t + 1], scale=(1 - SLOPE) / SLOPE)
            else:
                t = q[2]
                self.wait(act, "pool", "add", k, t)
                ins = nc.scalar.activation(self.P[k % 2][:, t], self.P[k % 2][:, t], ACT.Exp, bias=self.b2[:, t:t + 1])
            ins.then_inc(done.sem, done.one())

    def vector(self, dve):
        self.begin(dve)
        self.landed(dve)
        nc, done, stt = self.nc, self.net.dve, self.nc.vector.scalar_tensor_tensor
        for q in self.order["dve"]:
            k = q[1]
            src, dst, h, out, add, by_tile = self.heads[k]
            if q[0] == "max":
                t = q[2]
                if t == 0:
                    self.wait(dve, "act", "row", k, 1)
                ins = nc.vector.tensor_tensor_reduce(out=self.P[k % 2][:, t], in0=self.net.asb[:TP, :], in1=self.net.mask[:TP, t, :], scale=SLOPE,
                                                     scalar=2 * MASKED, op0=ALU.add, op1=ALU.max, accum_out=self.mx[:, t:t + 1])
            elif q[0] == "small":
                dve.wait_ge(done.sem, done.issued)
                ins = [lambda: nc.vector.tensor_scalar(self.b1, dst, 1 - SLOPE, None, ALU.mult),
                       lambda: stt(out=self.b2, in0=dst, scalar=SLOPE, in1=self.mx, op0=ALU.mult, op1=ALU.add),
                       lambda: stt(out=self.mx, in0=self.b2, scalar=1 / SLOPE, in1=self.b2, op0=ALU.mult, op1=ALU.max),
                       lambda: stt(out=self.b2, in0=dst, scalar=SLOPE, in1=self.mx, op0=ALU.mult, op1=ALU.subtract)][q[2]]()
            elif q[0] == "count":
                t = q[2]
                self.wait(dve, "act", "exp", k, t)
                ins = nc.vector.tensor_tensor_reduce(out=self.P[k % 2][:, t], in0=self.P[k % 2][:, t], in1=self.net.counts[:TP, t, :], scale=1.0,
                                                     scalar=0.0, op0=ALU.mult, op1=ALU.add, accum_out=self.sum[:, t:t + 1])
            elif q[0] == "sum":
                dve.wait_ge(done.sem, done.issued)
                ins = nc.vector.tensor_scalar(self.sum, self.sum, self.eps, None, ALU.add)
            elif q[0] == "rinv":
                dve.wait_ge(done.sem, done.issued)
                ins = nc.vector.reciprocal(self.rinv[k % 2], self.sum)
            else:
                t, j = q[2], q[3]
                cs = slice(j * self.w, (j + 1) * self.w)
                self.wait(dve, "pe", "apply", k, t, j)
                if t == 0 and j == 0:
                    self.wait(dve, "dve", "rinv", k)
                if add is None:
                    ins = nc.vector.tensor_scalar(out[:, t, cs], self.ps(("apply", k, t, j), TP, self.w), self.rinv[k % 2][:, t:t + 1], None, ALU.mult)
                else:
                    ins = stt(out=out[:, t, cs], in0=self.ps(("apply", k, t, j), TP, self.w), scalar=self.rinv[k % 2][:, t:t + 1],
                              in1=add[:, t, cs] if by_tile else add[:, cs], op0=ALU.mult, op1=ALU.add)
            ins.then_inc(done.sem, done.one())

    def gpsimd(self, pool):
        self.begin(pool)
        for q in self.order["pool"]:
            k, t = q[1], q[2]
            self.wait(pool, "act", "relu", k, t)
            self.nc.gpsimd.tensor_tensor(self.P[k % 2][:, t], self.P[k % 2][:, t], self.relu[t % 2], ALU.add).then_inc(self.net.pool.sem, self.net.pool.one())


class SoftmaxHeads(Heads):

    def __init__(self, net, heads, P, PT, scale, after=None):
        super().__init__(net, after)
        self.heads, self.P, self.PT, self.scale = heads, P, PT, scale
        self.mx2 = net.st[:TP, 200:210].rearrange("p (t s) -> p t s", t=NT)
        self.nb = net.st[:TP, 210:215]
        self.sum2 = net.st[:TP, 215:225].rearrange("p (t s) -> p t s", t=NT)
        self.rinv = [net.st[:TP, 180 + 5 * k:185 + 5 * k] for k in range(2)]
        self.schedule(len(heads), -1, None)

    def step(self, k, scores, apply):
        pe, act, dve = (self.order[e] for e in ("pe", "act", "dve"))
        n = k + 1
        for t in range(NT):
            if scores:
                pe += [("score", n, t, j) for j in range(2)]
                dve += [("max", n, t, j) for j in range(2)] + [("top", n, t), ("neg", n, t)]
            if apply:
                pe += [("turn", k, t, j) for j in range(2)]
                act.append(("turn", k, t, 0))
                dve.append(("turn", k, t, 1))
            if scores:
                act += [("exp", n, t, j) for j in range(2)]
        if apply:
            pe.append(("apply", k))
            dve.append(("out", k))
        if scores:
            dve += [("sum", n), ("rinv", n)]

    def reader(self, q):
        if q[0] == "score":
            return "act", ("exp",) + q[1:]
        if q[0] == "turn":
            return ("act", "dve")[q[3]], q
        return "dve", ("out", q[1])

    def tensor(self, pe):
        self.begin(pe)
        nc, done = self.nc, self.net.pe
        for q in self.order["pe"]:
            self.wait_bank(pe, q)
            k = q[1]
            qT, kT, v, out = self.heads[k]
            if q[0] == "score":
                t0, t1 = HALVES[q[3]]
                mm = nc.tensor.matmul(self.ps(q, TP, (t1 - t0) * TP), qT[:, q[2] * TP:(q[2] + 1) * TP], kT[:, t0 * TP:t1 * TP], start=True, stop=True)
            elif q[0] == "turn":
                if q[2] == 0:
                    self.wait(pe, "act", "exp", k, HALVES[q[3]][1] - 1, 1)
                mm = self.turn_group(self.P[k % 2], q[2], *HALVES[q[3]], q)
            else:
                self.wait(pe, "act", "turn", k, NT - 1, 0)
                self.wait(pe, "dve", "turn", k, NT - 1, 1)
                for t in range(NT):
                    for s in range(NT):
                        mm = nc.tensor.matmul(self.ps(q, TP, NT * 64)[:, t * 64:(t + 1) * 64], self.PT[:, s, t * TP:(t + 1) * TP], v[:, s, :],
                                              start=(s == 0), stop=(s == NT - 1))
            mm.then_inc(done.sem, done.one())

    def scalar(self, act):
        self.begin(act)
        nc, done = self.nc, self.net.act
        for q in self.order["act"]:
            k, t, j = q[1:]
            t0, t1 = HALVES[j]
            if q[0] == "turn":
                self.wait(act, "pe", *q)
                ins = nc.scalar.activation(self.PT[:, t, t0 * TP:t1 * TP], self.ps(q, TP, (t1 - t0) * TP), ACT.Identity)
            else:
                self.wait(act, "dve", "neg", k, t)
                ins = nc.scalar.activation(self.P[k % 2][:, t, t0 * TP:t1 * TP], self.ps(("score", k, t, j), TP, (t1 - t0) * TP), ACT.Exp,
                                           bias=self.nb[:, t:t + 1], scale=self.scale, accum_out=self.sum2[:, t, j:j + 1])
            ins.then_inc(done.sem, done.one())

    def vector(self, dve):
        self.begin(dve)
        nc, done = self.nc, self.net.dve
        for q in self.order["dve"]:
            k = q[1]
            if q[0] == "max":
                t, (t0, t1) = q[2], HALVES[q[3]]
                self.wait(dve, "pe", "score", *q[1:])
                ins = nc.vector.tensor_reduce(self.mx2[:, t, q[3]:q[3] + 1], self.ps(("score",) + q[1:], TP, (t1 - t0) * TP), AX.X, ALU.max)
            elif q[0] == "top":
                dve.wait_ge(done.sem, done.issued)
                ins = nc.vector.tensor_reduce(self.nb[:, q[2]:q[2] + 1], self.mx2[:, q[2], :], AX.X, ALU.max)
            elif q[0] == "neg":
                dve.wait_ge(done.sem, done.issued)
                ins = nc.vector.tensor_scalar(self.nb[:, q[2]:q[2] + 1], self.nb[:, q[2]:q[2] + 1], -self.scale, None, ALU.mult)
            elif q[0] == "turn":
                t0, t1 = HALVES[q[3]]
                self.wait(dve, "pe", *q)
                ins = nc.vector.tensor_copy(self.PT[:, q[2], t0 * TP:t1 * TP], self.ps(q, TP, (t1 - t0) * TP))
            elif q[0] == "out":
                self.wait(dve, "pe", "apply", k)
                ins = nc.vector.tensor_tensor(self.heads[k][3], self.ps(("apply", k), TP, NT * 64).rearrange("p (t c) -> p t c", t=NT),
                                              self.rinv[k % 2].unsqueeze(2).to_broadcast([TP, NT, 64]), ALU.mult)
            elif q[0] == "sum":
                self.wait(dve, "act", "exp", k, NT - 1, 1)
                ins = nc.vector.tensor_reduce(self.rinv[k % 2], self.sum2, AX.X, ALU.add)
            else:
                dve.wait_ge(done.sem, done.issued)
                ins = nc.vector.reciprocal(self.rinv[k % 2], self.rinv[k % 2])
            ins.then_inc(done.sem, done.one())


class Apply(Stage):

    def __init__(self, net, P, PT, h, rinv, out, add=None, by_tile=True, rows=(), after=None, evac="ad"):
        super().__init__(net, after)
        self.P, self.PT, self.h, self.rinv, self.out, self.add, self.by_tile, self.rows = P, PT, h, rinv, out, add, by_tile, rows
        self.loads = list(rows)
        c = h.shape[2]
        self.w = c if c <= 512 else UNIT
        self.nw = c // self.w
        a, d = self.groups(2 * NT, evac)
        self.turned = [(net.act.sem, net.act.planned + a), (net.dve.sem, net.dve.planned + d)]
        net.dve.planned += d
        _, d2 = self.groups(NT * self.nw, "d")
        net.dve.planned -= d
        self.d_turn = d
        self.take(pe=2 * NT + NT * self.nw, act=a, dve=d + d2)

    def tensor(self, pe):
        self.begin(pe)
        nc, done = self.nc, self.net.pe
        for i in range(2 * NT):
            b, s, (t0, t1) = self.g[i][0], i // 2, HALVES[i % 2]
            if b >= BANKS:
                pe.wait_ge(*self.free(b))
            for t in range(t0, t1):
                mm = nc.tensor.transpose(self.net.ps[:TP, b % BANKS, (t - t0) * TP:(t - t0 + 1) * TP],
                                         self.P[:, t, s * TP:(s + 1) * TP], self.net.ident[:TP, :TP])
            mm.then_inc(done.sem, done.one())
        for sem, value in self.turned:
            pe.wait_ge(sem, value)
        for i in range(NT * self.nw):
            b, t, j = self.g[2 * NT + i][0], i // self.nw, i % self.nw
            if b >= BANKS:
                pe.wait_ge(*self.free(b))
            for s in range(NT):
                mm = nc.tensor.matmul(self.net.ps[:TP, b % BANKS, 0:self.w], self.PT[:, s, t * TP:(t + 1) * TP],
                                      self.h[:, s, j * self.w:(j + 1) * self.w], start=(s == 0), stop=(s == NT - 1))
            mm.then_inc(done.sem, done.one())

    def turn(self, eng, letter, ticks):
        self.begin(eng)
        for i in range(2 * NT):
            b, e = self.g[i]
            if e == letter:
                s, (t0, t1) = i // 2, HALVES[i % 2]
                eng.wait_ge(self.net.pe.sem, self.p0 + i + 1)
                evacuate(self.nc, letter, "copy", self.PT[:, s, t0 * TP:t1 * TP],
                         self.net.ps[:TP, b % BANKS, 0:(t1 - t0) * TP]).then_inc(ticks.sem, ticks.one())

    def scalar(self, act):
        self.turn(act, "a", self.net.act)

    def vector(self, dve):
        self.turn(dve, "d", self.net.dve)
        self.landed(dve)
        done = self.net.dve
        for i in range(NT * self.nw):
            b, t, j = self.g[2 * NT + i][0], i // self.nw, i % self.nw
            cs = slice(j * self.w, (j + 1) * self.w)
            ps, out, r = self.net.ps[:TP, b % BANKS, 0:self.w], self.out[:, t, cs], self.rinv[:, t:t + 1]
            dve.wait_ge(self.net.pe.sem, self.p0 + 2 * NT + i + 1)
            if self.add is None:
                evacuate(self.nc, "d", "scale", out, ps, gate=r).then_inc(done.sem, done.one())
            else:
                add = self.add[:, t, cs] if self.by_tile else self.add[:, cs]
                evacuate(self.nc, "d", "gate", out, ps, gate=r, add=add).then_inc(done.sem, done.one())


class HeadNorm(Stage):
    side = True

    def __init__(self, net, x, tmp, out, gamma, beta, eps, after=None):
        super().__init__(net, after)
        self.x, self.tmp, self.out, self.eps, self.loads = x, tmp, out, eps, [gamma, beta]
        self.mean, self.var = net.st[:TP, 270:330], net.st[:TP, 330:390]
        self.take(dve=9, act=2)

    def bc(self, small):
        return small.unsqueeze(2).to_broadcast([TP, 60, 64])

    def row(self, load):
        return load.dst[:TP, :, :].to_broadcast([TP, 60, 64])

    def vector(self, dve):
        self.begin(dve)
        nc, done, act = self.nc, self.net.dve, self.net.act
        nc.vector.tensor_reduce(self.mean, self.x, AX.X, ALU.add).then_inc(done.sem, done.one())
        dve.wait_ge(done.sem, done.issued)
        nc.vector.tensor_scalar(self.mean, self.mean, 1.0 / 64, None, ALU.mult).then_inc(done.sem, done.one())
        dve.wait_ge(done.sem, done.issued)
        nc.vector.tensor_tensor(self.x, self.x, self.bc(self.mean), ALU.subtract).then_inc(done.sem, done.one())
        dve.wait_ge(act.sem, self.a0 + 1)
        nc.vector.tensor_reduce(self.var, self.tmp, AX.X, ALU.add).then_inc(done.sem, done.one())
        dve.wait_ge(done.sem, done.issued)
        nc.vector.tensor_scalar(self.var, self.var, 1.0 / 64, self.eps, ALU.mult, ALU.add).then_inc(done.sem, done.one())
        dve.wait_ge(act.sem, self.a0 + 2)
        nc.vector.reciprocal(self.var, self.var).then_inc(done.sem, done.one())
        dve.wait_ge(done.sem, done.issued)
        nc.vector.tensor_tensor(self.x, self.x, self.bc(self.var), ALU.mult).then_inc(done.sem, done.one())
        self.landed(dve)
        dve.wait_ge(done.sem, done.issued)
        nc.vector.tensor_tensor(self.x, self.x, self.row(self.loads[0]), ALU.mult).then_inc(done.sem, done.one())
        dve.wait_ge(done.sem, done.issued)
        nc.vector.tensor_tensor(self.out, self.x, self.row(self.loads[1]), ALU.add).then_inc(done.sem, done.one())

    def scalar(self, act):
        self.begin(act)
        done, dve = self.net.act, self.net.dve
        act.wait_ge(dve.sem, self.d0 + 3)
        self.nc.scalar.activation(self.tmp, self.x, ACT.Square).then_inc(done.sem, done.one())
        act.wait_ge(dve.sem, self.d0 + 5)
        self.nc.scalar.activation(self.var, self.var, ACT.Sqrt).then_inc(done.sem, done.one())


class SetOnes(Stage):
    side = True

    def __init__(self, net, v, after=None):
        super().__init__(net, after)
        self.v = v
        self.take(pool=1)

    def gpsimd(self, pool):
        self.begin(pool)
        self.nc.gpsimd.memset(self.v[:, :, 64:65], 1.0).then_inc(self.net.pool.sem, self.net.pool.one())


class Square(Stage):

    def __init__(self, net, x, out, made, after):
        super().__init__(net, after)
        self.x, self.out, self.made = x, out, made
        self.take(pool=x.shape[1])

    def gpsimd(self, pool):
        self.begin(pool)
        for c in range(self.x.shape[1]):
            for sem, value in self.made.chunk_done(c):
                pool.wait_ge(sem, value)
            self.nc.gpsimd.tensor_tensor(self.out[:, c], self.x[:, c], self.x[:, c], ALU.mult).then_inc(self.net.pool.sem, self.net.pool.one())


class Elu1(Stage):
    side = True

    def __init__(self, net, x, tmp, after=None):
        super().__init__(net, after)
        self.x, self.tmp, self.c = x, tmp, x.shape[1]
        self.take(pool=self.c, act=self.c, dve=self.c)

    def gpsimd(self, pool):
        self.begin(pool)
        for c in range(self.c):
            self.nc.gpsimd.tensor_scalar(self.tmp[:, c], self.x[:, c], 0.0, None, ALU.min).then_inc(self.net.pool.sem, self.net.pool.one())

    def scalar(self, act):
        self.begin(act)
        for c in range(self.c):
            act.wait_ge(self.net.pool.sem, self.l0 + c + 1)
            self.nc.scalar.activation(self.tmp[:, c], self.tmp[:, c], ACT.Exp).then_inc(self.net.act.sem, self.net.act.one())

    def vector(self, dve):
        self.begin(dve)
        for c in range(self.c):
            dve.wait_ge(self.net.act.sem, self.a0 + c + 1)
            self.nc.vector.scalar_tensor_tensor(out=self.x[:, c], in0=self.x[:, c], scalar=0.0, in1=self.tmp[:, c],
                                                op0=ALU.max, op1=ALU.add).then_inc(self.net.dve.sem, self.net.dve.one())


class PhiTok(Stage):

    def __init__(self, net, xT, sqT, chunks, out, lnc, waits=(), after=None):
        super().__init__(net, after)
        self.xT, self.sqT, self.chunks, self.out, self.lnc, self.loads = xT, sqT, chunks, out, lnc, list(waits)
        self.groups(NT, "a")
        self.take(pe=NT, act=NT)

    def tensor(self, pe):
        self.begin(pe)
        self.landed(pe)
        for t in range(NT):
            b = self.g[t][0]
            if b >= BANKS:
                pe.wait_ge(*self.free(b))
            for j, terms in enumerate(self.chunks):
                for n, (c, w, norm) in enumerate(terms):
                    ps = self.net.ps[:TP, b % BANKS, j * 128:(j + 1) * 128]
                    self.nc.tensor.matmul(ps, self.xT[:, c, t * TP:(t + 1) * TP], w, start=(n == 0), stop=False)
                    mm = self.nc.tensor.matmul(ps, self.sqT[:, c, t * TP:(t + 1) * TP], norm, start=False, stop=(n == len(terms) - 1))
            mm.then_inc(self.net.pe.sem, self.net.pe.one())

    def scalar(self, act):
        self.begin(act)
        w = 128 * len(self.chunks)
        for t in range(NT):
            act.wait_ge(self.net.pe.sem, self.p0 + t + 1)
            self.nc.scalar.activation(self.out[:, t, 0:w], self.net.ps[:TP, self.g[t][0] % BANKS, 0:w], ACT.Exp,
                                      bias=self.lnc[:TP, :]).then_inc(self.net.act.sem, self.net.act.one())


class PhiFeat(Stage):

    def __init__(self, net, xT, sqT, chunks, out, lnc, waits=(), after=None):
        super().__init__(net, after)
        self.xT, self.sqT, self.chunks, self.out, self.lnc, self.loads = xT, sqT, chunks, out, lnc, list(waits)
        self.groups(2 * len(chunks), "a")
        self.take(pe=2 * len(chunks), act=2 * len(chunks))

    def tensor(self, pe):
        self.begin(pe)
        self.landed(pe)
        for i, (b, _) in enumerate(self.g):
            t0, t1 = HALVES[i % 2]
            terms = self.chunks[i // 2]
            if b >= BANKS:
                pe.wait_ge(*self.free(b))
            ps = self.net.ps[:, b % BANKS, 0:(t1 - t0) * TP]
            for n, (c, w, norm) in enumerate(terms):
                self.nc.tensor.matmul(ps, w, self.xT[:, c, t0 * TP:t1 * TP], start=(n == 0), stop=False)
                mm = self.nc.tensor.matmul(ps, norm, self.sqT[:, c, t0 * TP:t1 * TP], start=False, stop=(n == len(terms) - 1))
            mm.then_inc(self.net.pe.sem, self.net.pe.one())

    def scalar(self, act):
        self.begin(act)
        for i, (b, _) in enumerate(self.g):
            t0, t1 = HALVES[i % 2]
            act.wait_ge(self.net.pe.sem, self.p0 + i + 1)
            self.nc.scalar.activation(self.out[:, i // 2, t0 * TP:t1 * TP], self.net.ps[:, b % BANKS, 0:(t1 - t0) * TP], ACT.Exp,
                                      bias=self.lnc).then_inc(self.net.act.sem, self.net.act.one())


class KvSummary(Stage):

    def __init__(self, net, chunks, v, scale=1.0, clear=None, after=None):
        super().__init__(net, after)
        self.chunks, self.v, self.scale, self.clear = chunks, v, scale, clear
        base = net.dve.planned + (clear is not None)
        for phi, h0, nh, kv, rows in chunks:
            base += nh
            b = net.bank()
            net.freed[b] = (net.dve.sem, base)
            self.g.append((b, "d"))
        self.take(pe=len(chunks), dve=base - net.dve.planned)

    def tensor(self, pe):
        self.begin(pe)
        for (b, _), (phi, h0, nh, kv, rows) in zip(self.g, self.chunks):
            if b >= BANKS:
                pe.wait_ge(*self.free(b))
            for t in range(NT):
                mm = self.nc.tensor.matmul(self.net.ps[:, b % BANKS, 0:nh * 65], phi[:, t],
                                           self.v[:, t * 12 + h0:t * 12 + h0 + nh, :].rearrange("p h c -> p (h c)"),
                                           start=(t == 0), stop=(t == NT - 1))
            mm.then_inc(self.net.pe.sem, self.net.pe.one())

    def vector(self, dve):
        self.begin(dve)
        done = self.net.dve
        if self.clear is not None:
            self.nc.vector.memset(self.clear, 0.0).then_inc(done.sem, done.one())
            dve.wait_ge(done.sem, done.issued)
        for n, ((b, _), (phi, h0, nh, kv, rows)) in enumerate(zip(self.g, self.chunks)):
            dve.wait_ge(self.net.pe.sem, self.p0 + n + 1)
            for i in range(nh):
                r = slice(i * rows, (i + 1) * rows)
                self.nc.vector.tensor_scalar(kv[r, i * 65:(i + 1) * 65], self.net.ps[r, b % BANKS, i * 65:(i + 1) * 65],
                                             self.scale, None, ALU.mult).then_inc(done.sem, done.one())


class KvApply(Stage):

    def __init__(self, net, parts, y, eps, after=None):
        super().__init__(net, after)
        self.parts, self.y, self.eps = parts, y, eps
        self.per = 3 if eps is not None else 1
        n = NT * len(parts)
        for i in range(n):
            b = net.bank()
            net.freed[b] = (net.dve.sem, net.dve.planned + self.per * (i + 1))
            self.g.append((b, "d"))
        self.take(pe=n, dve=self.per * n)

    def tensor(self, pe):
        self.begin(pe)
        i = 0
        for part in self.parts:
            for t in range(NT):
                b, col = self.g[i][0], 0
                if b >= BANKS:
                    pe.wait_ge(*self.free(b))
                for h0, nh, terms in part:
                    for n, (phi, kv) in enumerate(terms):
                        mm = self.nc.tensor.matmul(self.net.ps[:TP, b % BANKS, col:col + nh * 65], phi[:, t * TP:(t + 1) * TP],
                                                   kv, start=(n == 0), stop=(n == len(terms) - 1))
                    col += nh * 65
                mm.then_inc(self.net.pe.sem, self.net.pe.one())
                i += 1

    def vector(self, dve):
        self.begin(dve)
        nc, done = self.nc, self.net.dve
        i = 0
        for part in self.parts:
            h0, nh = part[0][0], sum(q[1] for q in part)
            for t in range(NT):
                ps = self.net.ps[:TP, self.g[i][0] % BANKS, 0:nh * 65].rearrange("p (h c) -> p h c", h=nh)
                y = self.y[:, t, h0 * 64:(h0 + nh) * 64].rearrange("p (h c) -> p h c", h=nh)
                dve.wait_ge(self.net.pe.sem, self.p0 + i + 1)
                if self.eps is None:
                    nc.vector.tensor_copy(y, ps[:, :, 0:64]).then_inc(done.sem, done.one())
                else:
                    o = 270 + 12 * (i % 2)
                    den = self.net.st[:TP, o:o + nh]
                    if i > 1:
                        dve.wait_ge(done.sem, self.d0 + 3 * (i - 1))
                    nc.vector.tensor_scalar(den, ps[:, :, 64], self.eps, None, ALU.add).then_inc(done.sem, done.one())
                    dve.wait_ge(done.sem, done.issued)
                    nc.vector.reciprocal(den, den).then_inc(done.sem, done.one())
                    dve.wait_ge(done.sem, done.issued)
                    nc.vector.tensor_tensor(y, ps[:, :, 0:64], den.unsqueeze(2).to_broadcast([TP, nh, 64]), ALU.mult).then_inc(done.sem, done.one())
                i += 1


class L2Rows(Stage):

    def __init__(self, net, x, scratch, eps, after=None):
        super().__init__(net, after)
        self.x, self.scratch, self.eps = x, scratch, eps
        self.n = net.st[:TP, 270:275]
        self.take(dve=NT + 2 + NT, act=1)

    def vector(self, dve):
        self.begin(dve)
        nc, done = self.nc, self.net.dve
        for t in range(NT):
            nc.vector.tensor_tensor_reduce(out=self.scratch[:, t], in0=self.x[:, t], in1=self.x[:, t], scale=1.0, scalar=0.0,
                                           op0=ALU.mult, op1=ALU.add, accum_out=self.n[:, t:t + 1]).then_inc(done.sem, done.one())
        dve.wait_ge(self.net.act.sem, self.a0 + 1)
        nc.vector.tensor_scalar(self.n, self.n, self.eps, None, ALU.max).then_inc(done.sem, done.one())
        dve.wait_ge(done.sem, done.issued)
        nc.vector.reciprocal(self.n, self.n).then_inc(done.sem, done.one())
        dve.wait_ge(done.sem, done.issued)
        for t in range(NT):
            nc.vector.tensor_scalar(self.x[:, t], self.x[:, t], self.n[:, t:t + 1], None, ALU.mult).then_inc(done.sem, done.one())

    def scalar(self, act):
        self.begin(act)
        act.wait_ge(self.net.dve.sem, self.d0 + NT)
        self.nc.scalar.activation(self.n, self.n, ACT.Sqrt).then_inc(self.net.act.sem, self.net.act.one())


class PhiNorms(Stage):

    def __init__(self, net, phi, sq, rn, scale_col, eps, after=None):
        super().__init__(net, after)
        self.phi, self.sq, self.rn, self.scale_col, self.eps = phi, sq, rn, scale_col, eps
        self.loads = [phi]
        self.groups(1, "a")
        self.take(pe=1, act=1, dve=4)

    def tensor(self, pe):
        self.begin(pe)
        b = self.g[0][0]
        if b >= BANKS:
            pe.wait_ge(*self.free(b))
        pe.wait_ge(self.net.dve.sem, self.d0 + 1)
        for k in range(KC):
            mm = self.nc.tensor.matmul(self.net.ps[:TP, b % BANKS, 0:64], self.net.ones[:, 0:TP], self.sq[:, k, :], start=(k == 0), stop=(k == KC - 1))
        mm.then_inc(self.net.pe.sem, self.net.pe.one())

    def scalar(self, act):
        self.begin(act)
        act.wait_ge(self.net.pe.sem, self.p0 + 1)
        self.nc.scalar.activation(self.rn, self.net.ps[:TP, self.g[0][0] % BANKS, 0:64], ACT.Sqrt).then_inc(self.net.act.sem, self.net.act.one())

    def vector(self, dve):
        self.begin(dve)
        self.landed(dve)
        nc, done = self.nc, self.net.dve
        nc.vector.tensor_tensor(self.sq, self.phi.dst, self.phi.dst, ALU.mult).then_inc(done.sem, done.one())
        dve.wait_ge(self.net.act.sem, self.a0 + 1)
        nc.vector.tensor_scalar(self.rn, self.rn, self.eps, None, ALU.max).then_inc(done.sem, done.one())
        dve.wait_ge(done.sem, done.issued)
        nc.vector.reciprocal(self.rn, self.rn).then_inc(done.sem, done.one())
        dve.wait_ge(done.sem, done.issued)
        nc.vector.tensor_scalar(self.rn, self.rn, self.scale_col, None, ALU.mult).then_inc(done.sem, done.one())


class SoftmaxGroups(Stage):

    def __init__(self, net, x, out, after=None):
        super().__init__(net, after)
        self.x, self.out = x, out
        self.m, self.s = net.st[:TP, 275:280], net.st[:TP, 280:285]
        self.take(dve=5, act=1)

    def bc(self, small):
        return small.unsqueeze(2).to_broadcast(list(self.x.shape))

    def vector(self, dve):
        self.begin(dve)
        nc, done = self.nc, self.net.dve
        nc.vector.tensor_reduce(self.m, self.x, AX.X, ALU.max).then_inc(done.sem, done.one())
        dve.wait_ge(done.sem, done.issued)
        nc.vector.tensor_tensor(self.out, self.x, self.bc(self.m), ALU.subtract).then_inc(done.sem, done.one())
        dve.wait_ge(self.net.act.sem, self.a0 + 1)
        nc.vector.tensor_reduce(self.s, self.out, AX.X, ALU.add).then_inc(done.sem, done.one())
        dve.wait_ge(done.sem, done.issued)
        nc.vector.reciprocal(self.s, self.s).then_inc(done.sem, done.one())
        dve.wait_ge(done.sem, done.issued)
        nc.vector.tensor_tensor(self.out, self.out, self.bc(self.s), ALU.mult).then_inc(done.sem, done.one())

    def scalar(self, act):
        self.begin(act)
        act.wait_ge(self.net.dve.sem, self.d0 + 2)
        self.nc.scalar.activation(self.out, self.out, ACT.Exp).then_inc(self.net.act.sem, self.net.act.one())


class TokenSoftmax(Stage):

    def __init__(self, net, x, after=None):
        super().__init__(net, after)
        self.x = x
        self.m, self.s = net.st[:64, 285:286], net.st[:64, 286:287]
        self.take(dve=4, act=1)

    def vector(self, dve):
        self.begin(dve)
        nc, done = self.nc, self.net.dve
        nc.vector.tensor_reduce(self.m, self.x, AX.X, ALU.max).then_inc(done.sem, done.one())
        dve.wait_ge(done.sem, done.issued)
        nc.vector.tensor_scalar(self.m, self.m, -1.0, None, ALU.mult).then_inc(done.sem, done.one())
        dve.wait_ge(self.net.act.sem, self.a0 + 1)
        nc.vector.reciprocal(self.s, self.s).then_inc(done.sem, done.one())
        dve.wait_ge(done.sem, done.issued)
        nc.vector.tensor_scalar(self.x, self.x, self.s, None, ALU.mult).then_inc(done.sem, done.one())

    def scalar(self, act):
        self.begin(act)
        act.wait_ge(self.net.dve.sem, self.d0 + 2)
        self.nc.scalar.activation(self.x, self.x, ACT.Exp, bias=self.m, accum_out=self.s).then_inc(self.net.act.sem, self.net.act.one())


class ToTokens(Stage):

    def __init__(self, net, x, out, after=None):
        super().__init__(net, after)
        self.x, self.out = x, out
        self.groups(1, "d")
        self.take(pe=1, dve=1)

    def tensor(self, pe):
        self.begin(pe)
        b = self.g[0][0]
        if b >= BANKS:
            pe.wait_ge(*self.free(b))
        for t in range(NT):
            mm = self.nc.tensor.transpose(self.net.ps[:TP, b % BANKS, t * 64:(t + 1) * 64], self.x[:, t * TP:(t + 1) * TP], self.net.ident[:64, :64])
        mm.then_inc(self.net.pe.sem, self.net.pe.one())

    def vector(self, dve):
        self.begin(dve)
        dve.wait_ge(self.net.pe.sem, self.p0 + 1)
        self.nc.vector.tensor_copy(self.out, self.net.ps[:TP, self.g[0][0] % BANKS, 0:NT * 64].rearrange("p (t n) -> p t n", t=NT)).then_inc(self.net.dve.sem, self.net.dve.one())


class SlotInputs(Stage):

    def __init__(self, net, x, d, out, after=None):
        super().__init__(net, after)
        self.x, self.d, self.out = x, d, out
        self.groups(1, "d")
        self.take(pe=1, dve=1)

    def tensor(self, pe):
        self.begin(pe)
        b = self.g[0][0]
        if b >= BANKS:
            pe.wait_ge(*self.free(b))
        for c in range(KC):
            for t in range(NT):
                mm = self.nc.tensor.matmul(self.net.ps[:, b % BANKS, c * 64:(c + 1) * 64], self.x[:, t, c * 128:(c + 1) * 128], self.d[:, t, :],
                                           start=(t == 0), stop=(t == NT - 1))
        mm.then_inc(self.net.pe.sem, self.net.pe.one())

    def vector(self, dve):
        self.begin(dve)
        dve.wait_ge(self.net.pe.sem, self.p0 + 1)
        self.nc.vector.tensor_copy(self.out, self.net.ps[:, self.g[0][0] % BANKS, 0:KC * 64].rearrange("p (c n) -> p c n", c=KC)).then_inc(self.net.dve.sem, self.net.dve.one())


class SlotExperts(Stage):
    EXPERTS, DEPTH = 64, 4

    def __init__(self, net, xT, w, kp, masked, out, bias, func, after=None):
        super().__init__(net, after)
        self.xT, self.w, self.kp, self.masked, self.out, self.bias, self.func = xT, w, kp, masked, out, bias, func
        self.kc, self.n = w.shape[1] // kp, w.shape[2]
        self.loads = [bias]
        self.cols = self.n if self.n <= 512 else UNIT
        self.nb = self.n // self.cols
        self.held = [s.take(0)[0] for s in net.wring]
        self.dsts = [net.wbuf[:kp, 1728 * j:1728 * j + self.kc * self.n].rearrange("p (c n) -> p c n", c=self.kc) for j in range(self.DEPTH)]
        self.base = net.expert_loads
        net.expert_loads += 16 * (self.EXPERTS // self.DEPTH)
        net.loads.append(self)
        E_, gelu = self.EXPERTS, func == "gelu"
        d_end = net.dve.planned + E_ + self.nb
        for _ in range(self.nb):
            b = net.bank()
            net.freed[b] = (net.dve.sem, d_end)
            self.g.append((b, "d"))
        self.take(pe=1 + E_ + 1, dve=E_ + self.nb, act=1 if gelu else 0)
        for s in net.wring:
            s.last = Load(None, None, None, 0, None)
            s.last.used = self.done

    def ps(self, q):
        return self.net.ps[:64, self.g[q][0] % BANKS, 0:self.cols]

    def clear(self, start):
        for q in range(self.nb):
            mm = self.nc.tensor.matmul(self.ps(q), self.net.zeros[:, 0:64], self.net.zeros[:, 0:self.cols], start=start, stop=not start, skip_group_check=True)
        return mm

    def sync(self, sp):
        for before in self.held:
            if before:
                for sem, value in before.used:
                    sp.wait_ge(sem, value)
        dsts, sems = self.dsts, self.net.esem
        for j in range(self.DEPTH):
            sp.dma_start(dsts[j], self.w[j].rearrange("(c p) n -> p c n", p=self.kp)).then_inc(sems[j], 16)
        with self.nc.sync.Fori(1, self.EXPERTS // self.DEPTH) as i:
            for j in range(self.DEPTH):
                sp.wait_ge(self.net.pe.sem, i * self.DEPTH + (self.p0 + 1 + j + 1 - self.DEPTH))
                sp.dma_start(dsts[j], self.w[bass.ds(i * self.DEPTH + j, 1)].rearrange("e (c p) n -> (e p) c n", p=self.kp)).then_inc(sems[j], 16)

    def tensor(self, pe):
        self.begin(pe)
        nc, done = self.nc, self.net.pe
        for b, _ in self.g:
            if b >= BANKS:
                pe.wait_ge(*self.free(b))
        self.clear(True).then_inc(done.sem, done.one())
        with nc.tensor.Fori(0, self.EXPERTS // self.DEPTH) as i:
            for j, w in enumerate(self.dsts):
                pe.wait_ge(self.net.dve.sem, i * self.DEPTH + (self.d0 + j + 1))
                pe.wait_ge(self.net.esem[j], i * 16 + (self.base + 16))
                for k in range(self.kc):
                    for q in range(self.nb):
                        mm = nc.tensor.matmul(self.ps(q), self.masked[j][:, k, :], w[:, k, q * self.cols:(q + 1) * self.cols],
                                              start=False, stop=False, skip_group_check=True)
                mm.then_inc(done.sem, 1)
        done.issued += self.EXPERTS
        self.clear(False).then_inc(done.sem, done.one())

    def vector(self, dve):
        self.begin(dve)
        nc, done = self.nc, self.net.dve
        with nc.vector.Fori(0, self.EXPERTS // self.DEPTH) as i:
            for j in range(self.DEPTH):
                dve.wait_ge(self.net.pe.sem, i * self.DEPTH + (self.p0 + 1 + j + 1 - self.DEPTH))
                nc.vector.scalar_tensor_tensor(out=self.masked[j], in0=self.net.iota64[:self.kp, :].unsqueeze(1).to_broadcast([self.kp, self.kc, 64]),
                                               scalar=self.net.iota64[:self.kp, bass.ds(i * self.DEPTH + j, 1)], in1=self.xT,
                                               op0=ALU.is_equal, op1=ALU.mult).then_inc(done.sem, 1)
        done.issued += self.EXPERTS
        self.landed(dve)
        dve.wait_ge(self.net.pe.sem, self.p0 + self.EXPERTS + 2)
        for q in range(self.nb):
            cs = slice(q * self.cols, (q + 1) * self.cols)
            nc.vector.tensor_tensor(self.out[:, cs], self.ps(q), self.bias.dst[:64, 0, cs], ALU.add).then_inc(done.sem, done.one())

    def scalar(self, act):
        if self.func == "gelu":
            self.begin(act)
            act.wait_ge(self.net.dve.sem, self.d0 + self.EXPERTS + self.nb)
            self.nc.scalar.activation(self.out, self.out, ACT.Gelu).then_inc(self.net.act.sem, self.net.act.one())


class SlotHidden(Stage):

    def __init__(self, net, x, out, after=None):
        super().__init__(net, after)
        self.x, self.out = x, out
        self.groups(1, "d")
        self.take(pe=1, dve=1)

    def tensor(self, pe):
        self.begin(pe)
        b = self.g[0][0]
        if b >= BANKS:
            pe.wait_ge(*self.free(b))
        for c in range(2):
            mm = self.nc.tensor.transpose(self.net.ps[:96, b % BANKS, c * 64:(c + 1) * 64], self.x[:, c * 96:(c + 1) * 96], self.net.ident[:64, :64])
        mm.then_inc(self.net.pe.sem, self.net.pe.one())

    def vector(self, dve):
        self.begin(dve)
        dve.wait_ge(self.net.pe.sem, self.p0 + 1)
        self.nc.vector.tensor_copy(self.out, self.net.ps[:96, self.g[0][0] % BANKS, 0:128].rearrange("p (c n) -> p c n", c=2)).then_inc(self.net.dve.sem, self.net.dve.one())


class TopTwo(Stage):
    ABSENT = 3.0e38

    def __init__(self, net, logits, gates, norm, sel, first=None, after=None):
        super().__init__(net, after)
        self.x, self.gates, self.norm, self.sel, self.first = logits, gates, norm, sel, first
        s = lambda o, w: net.st[:TP, o:o + NT * w].rearrange("p (t w) -> p t w", t=NT)
        self.top, self.want, self.rep, self.sum = s(310, 8), s(350, 8), s(390, 8), net.st[:TP, 430:435]
        self.n_first = 2 + NT if first is not None else 0
        self.take(dve=NT + 2 + NT + 1 + self.n_first + 1 + 1 + 3, act=1)

    def bc(self, small):
        return small.to_broadcast([TP, NT, 8])

    def vector(self, dve):
        self.begin(dve)
        nc, done = self.nc, self.net.dve
        nc.vector.memset(self.want, self.ABSENT).then_inc(done.sem, done.one())
        for t in range(NT):
            nc.vector.max(self.top[:, t, :], self.x[:, t, :]).then_inc(done.sem, done.one())
        dve.wait_ge(done.sem, done.issued)
        if self.first is not None:
            nc.vector.tensor_copy(self.want[:, :, 0:1], self.top[:, :, 0:1]).then_inc(done.sem, done.one())
            dve.wait_ge(done.sem, done.issued)
            for t in range(NT):
                nc.vector.match_replace(self.first[:, t, :], self.want[:, t, :], self.x[:, t, :], -self.ABSENT).then_inc(done.sem, done.one())
            dve.wait_ge(done.sem, done.issued)
            nc.vector.tensor_tensor(self.first, self.first, self.x, ALU.not_equal).then_inc(done.sem, done.one())
            dve.wait_ge(done.sem, done.issued)
        nc.vector.tensor_copy(self.want[:, :, 0:2], self.top[:, :, 0:2]).then_inc(done.sem, done.one())
        dve.wait_ge(done.sem, done.issued)
        for t in range(NT):
            nc.vector.match_replace(self.rep[:, t, :], self.want[:, t, :], self.x[:, t, :], -self.ABSENT).then_inc(done.sem, done.one())
        nc.vector.tensor_tensor(self.gates, self.x, self.bc(self.top[:, :, 0:1]), ALU.subtract).then_inc(done.sem, done.one())
        dve.wait_ge(done.sem, done.issued)
        nc.vector.tensor_tensor(self.sel, self.rep, self.x, ALU.not_equal).then_inc(done.sem, done.one())
        dve.wait_ge(done.sem, done.issued)
        dve.wait_ge(self.net.act.sem, self.a0 + 1)
        if self.norm == "all":
            nc.vector.tensor_reduce(self.sum, self.gates, AX.X, ALU.add).then_inc(done.sem, done.one())
            dve.wait_ge(done.sem, done.issued)
            nc.vector.tensor_tensor(self.gates, self.gates, self.sel, ALU.mult).then_inc(done.sem, done.one())
        else:
            nc.vector.tensor_tensor(self.gates, self.gates, self.sel, ALU.mult).then_inc(done.sem, done.one())
            dve.wait_ge(done.sem, done.issued)
            nc.vector.tensor_reduce(self.sum, self.gates, AX.X, ALU.add).then_inc(done.sem, done.one())
        dve.wait_ge(done.sem, done.issued)
        nc.vector.reciprocal(self.sum, self.sum).then_inc(done.sem, done.one())
        dve.wait_ge(done.sem, done.issued)
        nc.vector.tensor_tensor(self.gates, self.gates, self.bc(self.sum.unsqueeze(2)), ALU.mult).then_inc(done.sem, done.one())

    def scalar(self, act):
        self.begin(act)
        act.wait_ge(self.net.dve.sem, self.d0 + 1 + NT + self.n_first + 1 + NT + 1)
        self.nc.scalar.activation(self.gates, self.gates, ACT.Exp).then_inc(self.net.act.sem, self.net.act.one())


class Capacity(Stage):

    def __init__(self, net, gates, sel, first, tri, capacity, after=None):
        super().__init__(net, after)
        self.gates, self.sel, self.first, self.tri, self.capacity = gates, sel, first, tri, capacity
        self.hot = net.st[:TP, 350:430].rearrange("p (t k e) -> p t k e", t=NT, k=2)
        self.loads = [tri]
        self.groups(1, "d")
        net.freed[self.g[0][0]] = (net.dve.sem, net.dve.planned + 4)
        self.take(pe=1, dve=6)

    def vector(self, dve):
        self.begin(dve)
        nc, done, ps = self.nc, self.net.dve, self.net.ps
        nc.vector.tensor_copy(self.hot[:, :, 0, :], self.first).then_inc(done.sem, done.one())
        nc.vector.tensor_tensor(self.hot[:, :, 1, :], self.sel, self.first, ALU.subtract).then_inc(done.sem, done.one())
        dve.wait_ge(done.sem, done.issued)
        dve.wait_ge(self.net.pe.sem, self.p0 + 1)
        count = ps[:TP, self.g[0][0] % BANKS, 0:NT * 16].rearrange("p (t k e) -> p t k e", t=NT, k=2)
        for k in range(2):
            nc.vector.scalar_tensor_tensor(out=self.hot[:, :, k, :], in0=count[:, :, k, :], scalar=float(self.capacity), in1=self.hot[:, :, k, :],
                                           op0=ALU.is_le, op1=ALU.mult).then_inc(done.sem, done.one())
        dve.wait_ge(done.sem, done.issued)
        nc.vector.tensor_tensor(self.sel, self.hot[:, :, 0, :], self.hot[:, :, 1, :], ALU.add).then_inc(done.sem, done.one())
        dve.wait_ge(done.sem, done.issued)
        nc.vector.tensor_tensor(self.gates, self.gates, self.sel, ALU.mult).then_inc(done.sem, done.one())

    def tensor(self, pe):
        self.begin(pe)
        self.landed(pe)
        b = self.g[0][0]
        if b >= BANKS:
            pe.wait_ge(*self.free(b))
        pe.wait_ge(self.net.dve.sem, self.d0 + 2)
        for t in range(NT):
            for s in range(t + 1):
                lhs = self.tri.dst[:TP, 0, 0:TP] if s == t else self.net.ones[:TP, 0:TP]
                mm = self.nc.tensor.matmul(self.net.ps[:TP, b % BANKS, t * 16:(t + 1) * 16], lhs, self.hot[:, s].rearrange("p k e -> p (k e)"),
                                           start=(s == 0), stop=(s == t))
        mm.then_inc(self.net.pe.sem, self.net.pe.one())


class GatedRows(Stage):

    def __init__(self, net, x, gate, row, after=None):
        super().__init__(net, after)
        self.x, self.gate, self.row, self.loads = x, gate, row, [row]
        self.take(dve=NT)

    def vector(self, dve):
        self.begin(dve)
        self.landed(dve)
        for t in range(NT):
            self.nc.vector.scalar_tensor_tensor(out=self.x[:, t], in0=self.row.dst[:TP, 0], scalar=self.gate[:, t:t + 1], in1=self.x[:, t],
                                                op0=ALU.mult, op1=ALU.add).then_inc(self.net.dve.sem, self.net.dve.one())


class Multiply(Stage):

    def __init__(self, net, x, y, after=None):
        super().__init__(net, after)
        self.x, self.y = x, y
        self.take(dve=1)

    def vector(self, dve):
        self.begin(dve)
        self.nc.vector.tensor_tensor(self.x, self.x, self.y, ALU.mult).then_inc(self.net.dve.sem, self.net.dve.one())


class Clear(Stage):

    def __init__(self, net, x, value=0.0, after=None):
        super().__init__(net, after)
        self.x, self.value = x, value
        self.take(dve=1)

    def vector(self, dve):
        self.begin(dve)
        self.nc.vector.memset(self.x, self.value).then_inc(self.net.dve.sem, self.net.dve.one())


class Degrees(Stage):
    side = True

    def __init__(self, net, rdeg, after=None):
        super().__init__(net, after)
        self.rdeg = rdeg
        self.take(dve=2, act=1)

    def vector(self, dve):
        self.begin(dve)
        done = self.net.dve
        self.nc.vector.tensor_reduce(self.rdeg, self.net.counts[:TP], AX.X, ALU.add).then_inc(done.sem, done.one())
        dve.wait_ge(self.net.act.sem, self.a0 + 1)
        self.nc.vector.reciprocal(self.rdeg, self.rdeg).then_inc(done.sem, done.one())

    def scalar(self, act):
        self.begin(act)
        act.wait_ge(self.net.dve.sem, self.d0 + 1)
        self.nc.scalar.activation(self.rdeg, self.rdeg, ACT.Sqrt).then_inc(self.net.act.sem, self.net.act.one())


def weight_units(net, w, rows=None, cols=None):
    r0, r1 = rows or (0, w.shape[0])
    c0, c1 = cols or (0, w.shape[1])
    return [net.weights(w[r0:r1, c:min(c + UNIT, c1)]) for c in range(c0, c1, UNIT)]


def linear_T(net, xT, w, out, bias=None, kind="copy", rows=None, cols=None, evac="ad", after=None):
    parts, m = [], 0
    for load in weight_units(net, w, rows, cols):
        for c0 in range(0, load.dst.shape[2], 128):
            parts.append((load, c0, 128, out[:, m], bias[:, m:m + 1] if bias is not None else None, kind))
            m += 1
    return LinearT(net, xT, parts, evac, after)


def linear(net, xT, w, out, kind="copy", add=None, rows=None, cols=None, bias=None, gate=None, evac="ad", kp=128, after=None, stats=None):
    f, units = 0, []
    r0, r1 = rows or (0, w.shape[0])
    c0, c1 = cols or (0, w.shape[1])
    for c in range(c0, c1, UNIT):
        load = net.weights(w[r0:r1, c:min(c + UNIT, c1)], kp)
        n = load.dst.shape[2]
        u = dict(load=load, w=n, out=out[:, :, f:f + n], kind=kind)
        if kind == "row":
            u.update(kind="add", add=bias.dst[:TP, 0, f:f + n], by_tile=False)
        elif kind in ("add", "gate"):
            u["add"] = add[:, :, f:f + n]
        if gate is not None:
            u["gate"] = gate
        units.append(u)
        f += n
    return Linear(net, xT, units, evac if kind in ("copy", "relu") else "d", rows=[bias] if bias else (), after=after, stats=stats)


def linear_heads(net, xT, w, cols, v4, bias=None, evac="ad"):
    units = []
    for j, c in enumerate(range(cols[0], cols[1], UNIT)):
        u = dict(load=net.weights(w[:, c:c + UNIT]), w=UNIT, out=v4[:, :, 6 * j:6 * j + 6, 0:64], kind="copy")
        if bias:
            u.update(kind="add", by_tile=False, add=bias.dst[:TP, 0, j * UNIT:(j + 1) * UNIT].rearrange("p (h c) -> p h c", h=6))
        units.append(u)
    Linear(net, xT, units, "d" if bias else evac, rows=[bias] if bias else ())


def expert_layers(net, xT, n, hidden, gates, out, w2, kp, start):
    gated = net.now()
    made, used = [], []
    for e in range(n + 1):
        if e < n:
            made.append(hidden(e, start if e < 2 else used[e - 2]))
        if e > 0:
            stage, hT = made[e - 1]
            units = []
            for j in range(2):
                cs = slice(j * UNIT, (j + 1) * UNIT)
                load = net.weights(w2[e - 1][:, cs], kp)
                units.append(dict(load=load, w=UNIT, out=out[:, :, cs], kind="gate", gate=gates[:, :, e - 1], add=out[:, :, cs]))
            product = Linear(net, hT, units, "d", after=gated + stage.ends(), stats=out if e == n else None)
            used.append(product.ends())


def gat_coefs(net, h_parts, c, a_src, a_dst, coef, scratch, after=None):
    head, last = 0, None
    for h, nh in h_parts:
        cs = slice(head * c, (head + nh) * c)
        last = GatCoefs(net, h, nh, c, head, net.row(a_src[:, cs]), net.row(a_dst[:, cs]), coef, scratch, after)
        head += nh
    return last


def gat_heads(net, h_parts, c, coef, P, PT, eps, outs, bias_rows=None, add=None, coefs=()):
    heads, rows, head = [], [], 0
    for (h, nh), out in zip(h_parts, outs):
        row = net.row(bias_rows[:, head * c:(head + nh) * c]) if bias_rows is not None else None
        rows += [row] if row else []
        for i in range(nh):
            cs = slice(i * c, (i + 1) * c)
            heads.append((coef[:, 0, head], coef[:, 1, head], h[:, :, cs], out[:, :, cs], row.dst[:TP, 0, cs] if row else add, not row))
            head += 1
    buffers = [net.feat(b, NT, TP) for b in (P, net.P1)]
    first = GatHeads(net, heads, buffers, net.feat(PT, NT, TP), eps, (), net.now() + list(coefs), -1, FIRST)
    return lambda after=(): GatHeads(net, heads, buffers, net.feat(PT, NT, TP), eps, rows, net.now() + first.ends() + list(after), 0, first)


def network(net, upto):
    ins, G, now = net.ins, net.G, net.now
    tok, feat = net.tok, net.feat
    R, XT = tok(net.R), feat(net.XT)
    net.const(net.ident[:, :], ins["ident"])
    net.const(net.lnc[:, :], ins["lnc"])
    net.const(net.slot_scale[:, :], ins["L0_ffn_scale"].to_broadcast([128, 1]))
    net.const(net.iota64[:, :], ins["iota"][:, 0:64].to_broadcast([128, 64]))
    net.const(R, ins["x"].rearrange("(t p) d -> p t d", p=TP))
    col = {n: net.col(n) for n in ("b_ah_c", "kqv_b_c", "qkv_b_c", "fc1_b_c", "in_b_c")}
    col.update({n: net.col(n, 96) for n in ("mlp_b1_c", "exp_b1_c")})
    heads = lambda b: b[:TP, 0:NT * D].rearrange("p (t c) -> p t c", c=64)
    heads65 = lambda b: b[:TP, 0:NT * 12 * 65].rearrange("p (t c) -> p t c", c=65)
    by_head = lambda v: v.rearrange("p (t h) c -> p t h c", t=NT)
    coef = net.st[:TP, 100:180].rearrange("p (s h t) -> p s h t", s=2, h=8)
    Clear(net, net.ones[:, :], 1.0)
    Clear(net, net.zeros[:, :], 0.0)
    EdgeCounts(net)
    start = now()
    norm_T(net, R, tok(G[0]), XT, 1e-5)
    loops = SelfLoops(net, ALU.add, start)
    bias_out = AddRow(net, R, net.row(ins["L0_mix_b_out"]))
    w = ins["L0_mix_w_mapT"]
    v = heads65(G[2])
    linear(net, XT, w, tok(G[1]), cols=(D, 2 * D), evac="a")
    head_norm = HeadNorm(net, heads(G[1]), heads(G[4]), heads(G[1]), net.row(ins["L0_mix_g_k"]), net.row(ins["L0_mix_b_k"]), 1e-5)
    linear(net, XT, w, tok(G[3]), cols=(2 * D, 3 * D), evac="a")
    head_norm = HeadNorm(net, heads(G[3]), heads(G[4]), v[:, :, 0:64], net.row(ins["L0_mix_g_v"]), net.row(ins["L0_mix_b_v"]), 1e-5,
                         now() + head_norm.ends())
    ones = SetOnes(net, v, now())
    linear_T(net, XT, w, feat(G[0]), cols=(0, D), evac="a")
    linear_T(net, XT, ins["L0_gnn_W_ah"], feat(G[5]), bias=col["b_ah_c"], kind="relu", evac="a")
    kv = net.kv[:, 0:780].rearrange("p (c w) -> p c w", c=6)
    KvSummary(net, [(tok(G[1])[:, :, j * 128:(j + 1) * 128], 2 * j, 2, kv[:, j], 64) for j in range(6)], v, 1.0 / N, clear=net.kv[:, 0:780],
              after=now() + head_norm.ends() + ones.ends())
    KvApply(net, pairs_of(feat(G[0]), kv), tok(G[3]), None)
    ToFeatures(net, tok(G[3]), feat(G[4]))
    linear(net, feat(G[4]), ins["L0_mix_w_outT"], R, "add", add=R, after=now() + bias_out.ends())
    x1T = feat(G[5])
    hs = [tok(net.XT), tok(G[0]), tok(G[1])]
    coefs3, marks = [net.st[:TP, o:o + 40].rearrange("p (s h t) -> p s h t", s=2, h=4) for o in (100, 140, 600)], []
    for i in range(3):
        made = linear(net, x1T, ins[f"L0_gnn_W{i}"], hs[i], evac="a")
        marks.append(gat_coefs(net, [(hs[i], 4)], 192, ins[f"L0_gnn_a_src{i}"], ins[f"L0_gnn_a_dst{i}"], coefs3[i], G[2]))
    Clear(net, tok(G[5]))
    bias_out = AddRow(net, tok(G[5]), net.row(ins["L0_gnn_b_out"]))
    rest = gat_heads(net, [(hs[0], 4)], 192, coefs3[0], G[2], G[3], 1e-16, [tok(G[4])], ins["L0_gnn_b0"], coefs=marks[0].ends() + loops.ends())
    for i in range(3):
        rest()
        outT = feat((net.XT, G[0], G[1])[i])
        ToFeatures(net, tok(G[4]), outT, "relu")
        if i < 2:
            rest = gat_heads(net, [(hs[i + 1], 4)], 192, coefs3[i + 1], G[2], G[3], 1e-16, [tok(G[4])], ins[f"L0_gnn_b{i + 1}"], coefs=marks[i + 1].ends())
        linear(net, outT, ins["L0_gnn_W_out"], tok(G[5]), "add", add=tok(G[5]), rows=(i * D, (i + 1) * D), after=now() + bias_out.ends())
    ReluAdd(net, R, tok(G[5]))
    if upto == 1:
        return
    LayerNorm(net, R, tok(G[0]), 1e-5)
    L2Rows(net, tok(G[0]), tok(G[1]), 1e-12)
    ToFeatures(net, tok(G[0]), XT)
    phi = net.weights(ins["L0_ffn_phi"])
    c64 = lambda b, p=TP, c=NT: b[:p, 0:c * 64].rearrange("p (t n) -> p t n", t=c)
    rn = G[2][:TP, 0:64]
    PhiNorms(net, phi, c64(G[1], 128, KC), rn, net.slot_scale[:TP, :], 1e-12)
    Linear(net, XT, [dict(load=phi, w=64, out=c64(G[3]), kind="mul", add=rn, by_tile=False)], "d")
    ToFeatures(net, c64(G[3]), feat(G[4], 1, 64))
    TokenSoftmax(net, G[4][:64, 0:N])
    ToTokens(net, G[4][:64, 0:N], c64(G[5]))
    xsT = c64(G[1], 128, KC)
    SlotInputs(net, tok(G[0]), c64(G[5]), xsT)
    SoftmaxGroups(net, c64(G[3]), c64(G[3]))
    ToFeatures(net, c64(G[3]), feat(G[4], 1, 64))
    hid = G[5][:64, 0:192]
    masked = [G[2][:, j * UNIT:(j + 1) * UNIT].rearrange("p (c n) -> p c n", c=KC) for j in range(4)]
    SlotExperts(net, xsT, ins["L0_ffn_w1"], 128, masked, hid, net.rows(ins["L0_ffn_b1"]), "gelu")
    hidT = c64(G[3], 96, 2)
    SlotHidden(net, hid, hidT)
    masked = [G[2][:96, j * 128:(j + 1) * 128].rearrange("p (c n) -> p c n", c=2) for j in range(4)]
    ys = G[0][:64, 0:D]
    SlotExperts(net, hidT, ins["L0_ffn_w2"], 96, masked, ys, net.rows(ins["L0_ffn_b2"]), "copy")
    halves2 = [(Load(None, ys[:, cs].unsqueeze(1), net.pe.sem, 0, None), R[:, :, cs]) for cs in (slice(0, UNIT), slice(UNIT, D))]
    Linear(net, feat(G[4], 1, 64), [dict(load=held, w=UNIT, out=out, kind="add", add=out) for held, out in halves2], "d", stats=R)
    if upto == 2:
        return

    clear = Clear(net, net.fw)
    fw = net.fw.rearrange("p (c m) -> p c m", c=6)
    fn = net.fn[:, 0:256].rearrange("p (i m) -> p i m", i=2)
    fws = [net.into(net.fn[:, 0:256], ins["norms1"], now())]
    for i in range(2):
        for s in range(2):
            dst = net.fw[64 * s:64 * s + 64, :].rearrange("p (j i m) -> p j i m", j=3, i=2)[:, :, i, 64 * i + 32 * s:64 * i + 32 * s + 32]
            fws.append(net.into(dst, ins["L1_mix_wT"].rearrange("(j i s) d m -> i s d j m", i=2, s=2)[i, s], now()))
    norm_T(net, R, tok(G[0]), XT, 1e-5, ready=True)
    bias_out = AddRow(net, R, net.row(ins["L1_mix_proj_b"]))
    bias_out2 = AddRow(net, R, net.row(ins["L1_gnn_b"]), now() + bias_out.ends())
    ones = SetOnes(net, heads65(G[4]), now())
    rdeg = net.st[:TP, 180:185]
    degrees = Degrees(net, rdeg)
    chunks = [[(2 * j + i, fw[:, 2 * j + i], fn[:, i]) for i in range(2)] for j in range(3)]
    w = ins["L1_mix_kqv_wT"]
    start = now()
    made = linear_T(net, XT, w, feat(G[0]), bias=col["kqv_b_c"][:, 0:6], cols=(0, D))
    square = Square(net, feat(G[0]), feat(G[1]), made, start)
    made = linear_T(net, XT, w, feat(G[5]), bias=col["kqv_b_c"][:, 6:12], cols=(D, 2 * D))
    phik = G[2][:TP, 0:NT * UNIT].rearrange("p (t m) -> p t m", t=NT)
    phi = PhiTok(net, feat(G[0]), feat(G[1]), chunks, phik, net.lnc[:, 0:1], fws)
    v = heads65(G[4])
    linear_heads(net, XT, w, (2 * D, 3 * D), by_head(v), net.row(ins["L1_mix_kqv_b_v"]))
    square = Square(net, feat(G[5]), feat(G[0]), made, phi.ends())
    phiq = feat(G[3], 3)
    PhiFeat(net, feat(G[5]), feat(G[0]), chunks, phiq, net.lnc[:, 0:1])
    kv = net.kv[:, 0:780].rearrange("p (c w) -> p c w", c=3)
    KvSummary(net, [(phik[:, :, j * 128:(j + 1) * 128], 4 * j, 4, kv[:, j], 32) for j in range(3)], v, 1.0, clear=net.kv[:, 0:780])
    KvApply(net, [[(4 * j, 4, ((phiq[:, j], kv[:, j]),))] for j in range(3)], tok(G[5]), 1e-8)
    units = [dict(load=load, w=UNIT, out=tok(G[1])[:, :, j * UNIT:(j + 1) * UNIT], kind="scale", gate=rdeg) for j, load in enumerate(weight_units(net, ins["L1_gnn_W"]))]
    Linear(net, XT, units, "d")
    ToFeatures(net, tok(G[5]), feat(G[0]))
    linear(net, feat(G[0]), ins["L1_mix_proj_wT"], R, "add", add=R, after=now() + bias_out2.ends())
    Apply(net, net.counts[:TP], feat(G[3], NT, TP), tok(G[1]), rdeg, R, add=R)
    if upto == 3:
        return
    gates, logits = (net.st[:TP, o:o + 40].rearrange("p (t e) -> p t e", t=NT) for o in (230, 520))
    sel, first = (net.st[:TP, o:o + 40].rearrange("p (t e) -> p t e", t=NT) for o in (440, 480))
    norm_T(net, R, tok(G[0]), XT, 1e-5)
    start = now()
    Linear(net, XT, [dict(load=net.weights(ins["L1_ffn_router_wT"]), w=8, out=logits, kind="copy")], "d")
    TopTwo(net, logits, gates, "all", sel)

    def hidden1(e, after):
        hT = feat(G[e % 2], 2, 96)
        load = net.weights(ins["L1_ffn_w1"][e])
        return LinearT(net, XT, [(load, 96 * k, 96, hT[:, k], None, "tanh_gelu") for k in range(2)], "a", after), hT

    expert_layers(net, XT, 8, hidden1, gates, R, ins["L1_ffn_w2"], 96, start)
    if upto == 4:
        return

    loops = SelfLoops(net, ALU.subtract)
    norm_T(net, R, tok(G[5]), XT, 1e-5, ready=True)
    bias2 = AddRow(net, R, net.row(ins["L2_gnn_b2"]))
    bias2 = AddRow(net, R, net.row(ins["L2_mix_fc2_b"]), now() + bias2.ends())
    w = ins["L2_gnn_W1T"]
    hA, hB = tok(G[0]), tok(G[1], 256)
    linear(net, XT, w, hA, cols=(0, D), evac="a")
    marks = gat_coefs(net, [(hA, 6)], 128, ins["L2_gnn_att_src1"], ins["L2_gnn_att_dst1"], coef, G[2])
    linear(net, XT, w, hB, cols=(D, 1024), evac="a")
    marks = gat_coefs(net, [(hB, 2)], 128, ins["L2_gnn_att_src1"][:, D:], ins["L2_gnn_att_dst1"][:, D:], coef[:, :, 6:8], G[2], now() + marks.ends())
    outB = G[1][:TP, 1280:2560].rearrange("p (t w) -> p t w", t=NT)
    gat_heads(net, [(hA, 6), (hB, 2)], 128, coef, G[2], G[3], 1e-16, [tok(G[4]), outB], ins["L2_gnn_b1"], coefs=marks.ends())()
    ToFeatures(net, tok(G[4]), feat(G[0]), "relu")
    ToFeatures(net, outB, feat(G[2], 2), "relu")
    linear(net, feat(G[0]), ins["L2_gnn_W2T"], tok(G[4]), rows=(0, D))
    linear(net, feat(G[2], 2), ins["L2_gnn_W2T"], tok(G[4]), "add", add=tok(G[4]), rows=(D, 1024))
    norm_T(net, tok(G[5]), tok(G[0]), XT, 1e-8, net.row(ins["L2_mix_ln1_w"]), net.row(ins["L2_mix_ln1_b"]))
    marks = gat_coefs(net, [(tok(G[4]), 1)], D, ins["L2_gnn_att_src2"], ins["L2_gnn_att_dst2"], coef, G[2])
    rest = gat_heads(net, [(tok(G[4]), 1)], D, coef, G[2], G[3], 1e-16, [R], add=R, coefs=marks.ends())
    bias_p = AddRow(net, tok(G[5]), net.row(ins["L2_mix_proj_b"]))
    w = ins["L2_mix_qkv_w"]
    linear_T(net, XT, w, feat(G[0]), bias=col["qkv_b_c"], cols=(0, D))
    rest(bias2.ends())
    loops = SelfLoops(net, ALU.add)
    elu = Elu1(net, feat(G[0]), feat(G[1]))
    linear(net, XT, w, tok(G[2]), "row", bias=net.row(ins["L2_mix_qkv_b"][:, D:2 * D]), cols=(D, 2 * D))
    v = heads65(G[3])
    ones = SetOnes(net, v, now())
    elu = Elu1(net, tok(G[2]), tok(G[1]), now() + elu.ends())
    linear_heads(net, XT, w, (2 * D, 3 * D), by_head(v), net.row(ins["L2_mix_qkv_b"][:, 2 * D:3 * D]))
    kv = net.kv[:, 0:780].rearrange("p (c w) -> p c w", c=6)
    KvSummary(net, [(tok(G[2])[:, :, j * 128:(j + 1) * 128], 2 * j, 2, kv[:, j], 64) for j in range(6)], v, 1.0, clear=net.kv[:, 0:780],
              after=now() + elu.ends() + ones.ends())
    KvApply(net, pairs_of(feat(G[0]), kv), tok(G[1]), 0.0)
    ToFeatures(net, tok(G[1]), feat(G[0]))
    linear(net, feat(G[0]), ins["L2_mix_proj_w"], tok(G[5]), "add", add=tok(G[5]), after=now() + bias_p.ends(), stats=tok(G[5]))
    norm_T(net, tok(G[5]), tok(G[0]), XT, 1e-8, net.row(ins["L2_mix_ln2_w"]), net.row(ins["L2_mix_ln2_b"]), ready=True)
    added = Add(net, R, R, tok(G[5]))
    start = now()
    made, used = [], []
    for q in range(5):
        if q < 4:
            made.append(linear_T(net, XT, ins["L2_mix_fc1_w"], feat(G[q % 2]), bias=col["fc1_b_c"][:, 6 * q:6 * q + 6], kind="gelu",
                                 cols=(q * D, (q + 1) * D), evac="a", after=start if q < 2 else used[q - 2]))
        if q > 0:
            used.append(linear(net, feat(G[(q - 1) % 2]), ins["L2_mix_fc2_w"], R, "add", add=R, rows=((q - 1) * D, q * D),
                               after=start + made[q - 1].ends() + added.ends(), stats=R if q == 4 else None).ends())
    if upto == 5:
        return
    X = tok(G[5])
    LayerNorm(net, R, X, 1e-5, ready=True)
    norm_T(net, X, tok(G[0]), XT, 1e-5, net.row(ins["L2_ffn_ln1_g"]), net.row(ins["L2_ffn_ln1_b"]))
    bias_out = AddRow(net, X, net.row(ins["L2_ffn_out_b"]))
    w = ins["L2_ffn_in_wT"]
    linear_T(net, XT, w, feat(G[0]), bias=col["in_b_c"][:, 0:6], cols=(0, D))
    linear_T(net, XT, w, feat(G[1]), bias=col["in_b_c"][:, 6:12], cols=(D, 2 * D))
    linear(net, XT, w, tok(G[2]), "row", bias=net.row(ins["L2_ffn_in_b"][:, 2 * D:3 * D]), cols=(2 * D, 3 * D))
    ctx = tok(net.XT)
    halves = [slice(64 * i, 64 * i + 64) for i in range(2)]
    SoftmaxHeads(net, [(feat(G[0])[halves[h % 2], h // 2], feat(G[1])[halves[h % 2], h // 2], tok(G[2])[:, :, h * 64:(h + 1) * 64],
                        ctx[:, :, h * 64:(h + 1) * 64]) for h in range(12)],
                 [feat(b, NT, TP) for b in (G[3], net.P1)], feat(G[4], NT, TP), 0.125)
    ToFeatures(net, ctx, feat(G[0]))
    linear(net, feat(G[0]), ins["L2_ffn_out_wT"], X, "add", add=X, after=now() + bias_out.ends())
    ToFeatures(net, X, feat(G[0]))
    bias_out = AddRow(net, X, net.row(ins["L2_ffn_mlp_b2"]))
    load = net.weights(ins["L2_ffn_mlp_w1"])
    LinearT(net, feat(G[0]), [(load, 96 * k, 96, feat(G[1], 2, 96)[:, k], col["mlp_b1_c"][:, k:k + 1], "gelu") for k in range(2)], "a")
    linear(net, feat(G[1], 2, 96), ins["L2_ffn_mlp_w2"], X, "add", add=X, kp=96, after=now() + bias_out.ends(), stats=X)
    Clear(net, logits, -1.0e38)
    norm_T(net, X, tok(G[0]), XT, 1e-5, net.row(ins["L2_ffn_ln2_g"]), net.row(ins["L2_ffn_ln2_b"]), ready=True)
    added = Add(net, R, R, X)
    start = now()
    gb = net.row(ins["L2_ffn_gate_b"])
    Linear(net, XT, [dict(load=net.weights(ins["L2_ffn_gate_wT"]), w=4, out=logits[:, :, 0:4], kind="add", by_tile=False, add=gb.dst[:TP, 0, :])], "d", rows=[gb])
    TopTwo(net, logits, gates, "top", sel)
    for e in range(4):
        GatedRows(net, R, gates[:, :, e], net.row(ins["L2_ffn_exp_b2"][e:e + 1, :]), now() + added.ends())

    def hidden2(e, after):
        hT = feat(G[e % 2], 2, 96)
        load = net.weights(ins["L2_ffn_exp_w1"][e])
        return LinearT(net, XT, [(load, 96 * k, 96, hT[:, k], col["exp_b1_c"][:, 2 * e + k:2 * e + k + 1], "gelu") for k in range(2)], "a", after), hT

    expert_layers(net, XT, 4, hidden2, gates, R, ins["L2_ffn_exp_w2"], 96, start)
    if upto == 6:
        return

    norm_T(net, R, tok(G[5]), XT, 1e-5, ready=True)
    bias2 = AddRow(net, R, net.row(ins["L3_gnn_b2"]))
    w = ins["L3_mix_W_qkv"]
    linear(net, XT, ins["L3_gnn_W1"], tok(G[0]), evac="a")
    marks = gat_coefs(net, [(tok(G[0]), 1)], D, ins["L3_gnn_att_src1"], ins["L3_gnn_att_dst1"], coef, G[2], now() + loops.ends())
    rest = gat_heads(net, [(tok(G[0]), 1)], D, coef, G[2], G[3], 0.0, [tok(G[1])], ins["L3_gnn_b1"], coefs=marks.ends())
    v = heads65(G[4])
    ones = SetOnes(net, v, now())
    linear_heads(net, XT, w, (2 * D, 3 * D), by_head(v), evac="a")
    rest()
    ToFeatures(net, tok(G[1]), feat(G[3]), "relu")
    linear(net, feat(G[3]), ins["L3_gnn_W2"], tok(G[0]), evac="a")
    marks = gat_coefs(net, [(tok(G[0]), 1)], D, ins["L3_gnn_att_src2"], ins["L3_gnn_att_dst2"], coef, G[2])
    rest = gat_heads(net, [(tok(G[0]), 1)], D, coef, G[2], G[3], 0.0, [R], add=R, coefs=marks.ends())
    start = now()
    made = linear_T(net, XT, w, feat(G[1]), cols=(D, 2 * D), evac="a")
    rest(bias2.ends())
    Clear(net, net.fw)
    fws = [net.into(net.fn, ins["norms3"], now())]
    for s in range(2):
        fws.append(net.into(net.fw[64 * s:64 * s + 64, 256 * s:256 * s + 256], ins["L3_mix_rfT"], now()))
    wc = lambda m: net.fw[:, m * 128:(m + 1) * 128]
    nc_ = lambda m: net.fn[:, m * 128:(m + 1) * 128]
    square = Square(net, feat(G[1]), feat(G[0]), made, now())
    kv = net.kv[:, :].rearrange("p (c w) -> p c w", c=24)
    kT, kT2 = feat(G[1]), feat(G[0])
    for c in range(6):
        phik = G[2 + c % 2][:TP, 0:NT * 512].rearrange("p (t m) -> p t m", t=NT)
        PhiTok(net, kT, kT2, [[(c, wc(m), nc_(m))] for m in range(4)], phik, net.lnc[:, 1:2], fws, now() + ones.ends())
        KvSummary(net, [(phik[:, :, m * 128:(m + 1) * 128], 2 * c + m // 2, 1, kv[:, 4 * c + m], 128) for m in range(4)], v)
    start = now()
    made = linear_T(net, XT, w, feat(G[1]), cols=(0, D))
    square = Square(net, feat(G[1]), feat(G[0]), made, start)
    for c in range(6):
        phiq = feat(G[2 + c % 2], 4)
        PhiFeat(net, feat(G[1]), feat(G[0]), [[(c, wc(m), nc_(m))] for m in range(4)], phiq, net.lnc[:, 1:2])
        KvApply(net, [[(2 * c + s, 1, tuple((phiq[:, 2 * s + m], kv[:, 4 * c + 2 * s + m]) for m in range(2))) for s in range(2)]], tok(net.XT), 1e-6)
    bias_out = AddRow(net, tok(G[5]), net.row(ins["L3_mix_b_proj"]))
    ToFeatures(net, tok(net.XT), feat(G[0]))
    linear(net, feat(G[0]), ins["L3_mix_W_proj"], tok(G[5]), "add", add=tok(G[5]), after=now() + bias_out.ends(), stats=tok(G[5]))
    LayerNorm(net, tok(G[5]), tok(G[0]), 1e-5, net.row(ins["L3_mix_gamma"]), net.row(ins["L3_mix_beta"]), ready=True)
    Add(net, R, R, tok(G[0]), side=False)
    if upto == 7:
        return
    norm_T(net, R, tok(G[0]), XT, 1e-5)
    start = now()
    Linear(net, XT, [dict(load=net.weights(ins["L3_ffn_Wg"]), w=8, out=logits, kind="copy")], "d")
    TopTwo(net, logits, gates, "top", sel, first)
    Capacity(net, gates, sel, first, net.rows(ins["tri"]), int(1.2 * N / 8))

    def hidden3(e, after):
        hT = feat(G[e % 2], 2)
        load = net.weights(ins["L3_ffn_W1"][e])
        made = LinearT(net, XT, [(load, 0, 128, hT[:, 0], None, "copy"), (load, 128, 128, hT[:, 1], None, "silu")], "a", after)
        return Multiply(net, hT[:, 0], hT[:, 1], made.ends()), hT[:, 0:1]

    expert_layers(net, XT, 8, hidden3, gates, R, ins["L3_ffn_W2"], 128, start)


def pairs_of(phi, kv):
    return [[(2 * j, 2, ((phi[:, j], kv[:, j]),)) for j in range(3 * q, 3 * q + 3)] for q in range(2)]


def bass_gps_kernel(nc, ins, out, upto=99):
    with ExitStack() as ctx:
        net = Net(nc, ctx, ins)
        network(net, upto)
        block = ctx.enter_context(nc.Block())
        n_const = 16 * len(net.consts)

        @block.sync
        def _(sp):
            for dst, src in net.consts:
                sp.dma_start(dst, src).then_inc(net.const_landed, 16)
            for load in net.loads:
                if isinstance(load, SlotExperts):
                    load.sync(sp)
                    continue
                if load.before:
                    for sem, value in load.before.used:
                        if value:
                            sp.wait_ge(sem, value)
                sp.dma_start(load.dst, load.src).then_inc(load.sem, 16)
            for sem, value in net.end():
                sp.wait_ge(sem, value)
            sp.dma_start(out.rearrange("(t p) d -> p t d", p=TP), net.tok(net.R)).then_inc(net.stored, 16)
            sp.wait_ge(net.stored, 16)

        @block.tensor
        def _(pe):
            pe.wait_ge(net.const_landed, n_const)
            for stage in net.stages:
                stage.tensor(pe)
                assert net.pe.issued <= net.pe.planned, stage

        @block.scalar
        def _(act):
            act.wait_ge(net.const_landed, n_const)
            for stage in net.stages:
                stage.scalar(act)

        @block.vector
        def _(dve):
            dve.wait_ge(net.const_landed, n_const)
            for stage in net.stages:
                assert net.dve.issued == stage.d0, stage
                stage.vector(dve)

        @block.gpsimd
        def _(pool):
            pool.wait_ge(net.const_landed, n_const)
            for stage in net.stages:
                stage.gpsimd(pool)

        for ticks in (net.pe, net.act, net.dve, net.pool):
            assert ticks.issued == ticks.planned, (ticks.sem, ticks.issued, ticks.planned)


_TURNED = {"L0_mix_w_mapT": "L0_mix_w_map", "L0_mix_w_outT": "L0_mix_w_out", "L1_mix_kqv_wT": "L1_mix_kqv_w", "L1_mix_proj_wT": "L1_mix_proj_w",
           "L1_ffn_router_wT": "L1_ffn_router_w", "L2_gnn_W1T": "L2_gnn_W1", "L2_gnn_W2T": "L2_gnn_W2", "L2_ffn_in_wT": "L2_ffn_in_w",
           "L2_ffn_out_wT": "L2_ffn_out_w", "L2_ffn_gate_wT": "L2_ffn_gate_w", "L3_mix_rfT": "L3_mix_random_features"}
_ROWS = ["L0_gnn_a_src0", "L0_gnn_a_dst0", "L0_gnn_b0", "L0_gnn_a_src1", "L0_gnn_a_dst1", "L0_gnn_b1", "L0_gnn_a_src2", "L0_gnn_a_dst2", "L0_gnn_b2",
         "L0_gnn_b_out", "L0_mix_g_k", "L0_mix_b_k", "L0_mix_g_v", "L0_mix_b_v", "L0_mix_b_out", "L1_gnn_b", "L1_mix_proj_b",
         "L2_gnn_att_src1", "L2_gnn_att_dst1", "L2_gnn_b1", "L2_gnn_att_src2", "L2_gnn_att_dst2", "L2_gnn_b2", "L2_mix_qkv_b", "L2_mix_proj_b",
         "L2_mix_fc2_b", "L2_mix_ln1_w", "L2_mix_ln1_b", "L2_mix_ln2_w", "L2_mix_ln2_b", "L2_ffn_ln1_g", "L2_ffn_ln1_b", "L2_ffn_in_b",
         "L2_ffn_out_b", "L2_ffn_mlp_b2", "L2_ffn_ln2_g", "L2_ffn_ln2_b", "L2_ffn_gate_b", "L3_gnn_att_src1", "L3_gnn_att_dst1", "L3_gnn_b1",
         "L3_gnn_att_src2", "L3_gnn_att_dst2", "L3_gnn_b2", "L3_mix_b_proj", "L3_mix_gamma", "L3_mix_beta"]
_PLAIN = ["x", "src", "dst", "L0_gnn_W_ah", "L0_gnn_W0", "L0_gnn_W1", "L0_gnn_W2", "L0_gnn_W_out", "L0_ffn_w1", "L0_ffn_b1", "L0_ffn_w2",
          "L0_ffn_b2", "L1_gnn_W", "L1_ffn_w1", "L1_ffn_w2", "L2_mix_qkv_w", "L2_mix_proj_w", "L2_mix_fc1_w", "L2_mix_fc2_w", "L2_ffn_mlp_w1",
          "L2_ffn_mlp_w2", "L2_ffn_exp_w1", "L2_ffn_exp_w2", "L2_ffn_exp_b2", "L3_gnn_W1", "L3_gnn_W2", "L3_mix_W_qkv", "L3_mix_W_proj",
          "L3_ffn_Wg", "L3_ffn_W1", "L3_ffn_W2"]


def kernel(**inputs):
    import math

    import numpy as np
    import concourse.bacc as bacc
    from concourse.bass_utils import run_bass_kernel_spmd

    lay = np.ascontiguousarray
    a = {name: np.asarray(v) for name, v in inputs.items()}
    columns = lambda v, p: lay(v.reshape(-1, p).T)
    arrays = {n: lay(a[n]) for n in _PLAIN}
    arrays.update({n: lay(a[o].T) for n, o in _TURNED.items()})
    arrays.update({n: lay(a[n].reshape(1, -1)) for n in _ROWS})
    arrays["L0_ffn_scale"] = lay(a["L0_ffn_scale"].reshape(1, 1))
    arrays["L0_ffn_phi"] = lay(a["L0_ffn_phi"].reshape(D, 64))
    arrays["L1_mix_wT"] = lay(a["L1_mix_w"].transpose(0, 2, 1))
    arrays["L1_mix_kqv_b_v"] = lay(a["L1_mix_kqv_b"][2 * D:].reshape(1, -1))
    arrays["b_ah_c"] = columns(a["L0_gnn_b_ah"], 128)
    arrays["kqv_b_c"] = columns(a["L1_mix_kqv_b"][:2 * D], 128)
    arrays["qkv_b_c"] = columns(a["L2_mix_qkv_b"][:D], 128)
    arrays["fc1_b_c"] = columns(a["L2_mix_fc1_b"], 128)
    arrays["in_b_c"] = columns(a["L2_ffn_in_b"][:2 * D], 128)
    arrays["mlp_b1_c"] = columns(a["L2_ffn_mlp_b1"], 96)
    arrays["exp_b1_c"] = columns(a["L2_ffn_exp_b1"], 96)
    arrays["ident"] = np.eye(128, dtype=np.float32)
    arrays["iota"] = np.arange(N, dtype=np.float32).reshape(1, N)
    arrays["tri"] = np.triu(np.ones((128, 128), np.float32))
    arrays["lnc"] = np.tile(np.array([[-0.5 * math.log(32.0), -0.5 * math.log(256.0)]], np.float32), (128, 1))
    norms1 = np.zeros((128, 2, 128), np.float32)
    norms3 = np.zeros((128, 512), np.float32)
    for s in range(2):
        norms3[64 * s:64 * s + 64, 256 * s:256 * s + 256] = -0.5
        for i in range(2):
            norms1[64 * s:64 * s + 64, i, 64 * i + 32 * s:64 * i + 32 * s + 32] = -0.5
    arrays["norms1"], arrays["norms3"] = norms1.reshape(128, 256), norms3

    nc = bacc.Bacc("TRN2", target_bir_lowering=False, num_devices=1)
    ins = {n: nc.dram_tensor(f"in_{n}", v.shape, mybir.dt.from_np(v.dtype), kind="ExternalInput").ap() for n, v in arrays.items()}
    out = nc.dram_tensor("out", (N, D), F32, kind="ExternalOutput").ap()
    bass_gps_kernel(nc, ins, out, UPTO)
    r = run_bass_kernel_spmd(nc, [{f"in_{n}": v for n, v in arrays.items()}], core_ids=[0])
    return r.results[0]["out"]


UPTO = 99
```

```python
from contextlib import ExitStack

import concourse.bass as bass
from concourse import mybir

F32 = mybir.dt.float32
F32R = mybir.dt.float32r
BF16 = mybir.dt.bfloat16
F16 = mybir.dt.float16
I32 = mybir.dt.int32
ALU = mybir.AluOpType
ACT = mybir.ActivationFunctionType
AX = mybir.AxisListType

N, D, E = 625, 768, 20000
TP = 125
NT = N // TP
KC = D // 128
HALVES = ((0, 3), (3, 5))
UNIT = 256
HALF = D // 2
SLOT = KC * UNIT
BUF = 3904
BANKS = 8
WSLOTS = 3
MASKED = -1.0e30
SLOPE = 0.2


class Pair:

    def __init__(self, hi, lo):
        self.hi, self.lo, self.shape = hi, lo, hi.shape

    def chunk(self, c):
        return Pair(self.hi[:, c], self.lo[:, c])


def products(net, ps, kc, stationary, moving):
    for n, (s, m) in enumerate((("hi", "lo"), ("lo", "hi"), ("hi", "hi"))):
        for k in range(kc):
            mm = net.nc.tensor.matmul(ps, net.r(stationary(s, k)), net.r(moving(m, k)), start=(n == 0 and k == 0), stop=(n == 2 and k == kc - 1))
    return mm


class Ticks:

    def __init__(self, sem):
        self.sem, self.planned, self.issued, self.joined = sem, 0, 0, 0

    def reserve(self, n):
        base = self.planned
        self.planned += n
        return base

    def one(self):
        self.issued += 1
        return 1


class Load:

    def __init__(self, src, dst, sem, value, before):
        self.src, self.dst, self.sem, self.value, self.before, self.used = src, dst, sem, value, before, None
        self.unit = None
        self.used_at = (-1, 0)


class Slot:

    def __init__(self, buf, sem):
        self.buf, self.sem, self.value, self.last = buf, sem, 0, None

    def take(self, n):
        before, base = self.last, self.value
        self.value += 16 * n
        return before, base


class Net:

    def __init__(self, nc, ctx, ins):
        self.nc, self.ins = nc, ins
        sb = lambda name, shape, dt=F32: ctx.enter_context(nc.sbuf_tensor(name, shape, dt))
        sem = lambda name: ctx.enter_context(nc.semaphore(name))
        self.pe, self.act, self.dve, self.pool = (Ticks(sem(n)) for n in ("pe_done", "act_done", "dve_done", "pool_done"))
        self.const_landed, self.stored = sem("const_landed"), sem("stored")
        self.ps = ctx.enter_context(nc.psum_tensor("ps", [128, BANKS, 512], F32))
        sizes = dict(xT=BUF, **{f"buf{i}": BUF for i in range(6)}, head_weights1=NT * N + 3, weights=(WSLOTS + 1) * SLOT)
        at, plain, self.rounded = -(-nc.sbuf_base // 32) * 32, {}, {}
        sb("arena", [128, sum(sizes.values())])
        for name, n in sizes.items():
            plain[name] = nc.alloc_sbuf_tensor_at(name, [128, n], F32, offset=at)
            self.rounded[plain[name].name] = nc.alloc_sbuf_tensor_at(name + "_r", [128, n], F32R, offset=at)
            at += 4 * n
        self.R, self.XT = sb("resid", [128, BUF]), plain["xT"]
        self.G = [plain[f"buf{i}"] for i in range(6)]
        self.counts = sb("edge_counts", [128, NT, N])
        self.mask = sb("edge_mask", [128, NT, N], BF16)
        self.P1 = plain["head_weights1"]
        self.wbuf = plain["weights"]
        self.wslot = [self.wbuf[:, i * SLOT:(i + 1) * SLOT] for i in range(WSLOTS)]
        self.high = [self.wbuf[:, WSLOTS * SLOT:(WSLOTS + 1) * SLOT], self.P1[:, 0:SLOT]]
        self.high_made, self.low_made = sem("weights_high_made"), sem("weights_low_made")
        self.units, self.high_used, self.segment = [], [[], []], 0
        self.wsem = [sem(f"weights_landed{i}") for i in range(WSLOTS)]
        self.rslot = [sb(f"row{i}", [128, D]) for i in range(3)]
        self.rsem = [sem(f"row_landed{i}") for i in range(3)]
        self.ident = sb("ident", [128, 128])
        self.cols = sb("bias_cols", [128, 96])
        self.kv = sb("kv", [128, 24 * 65])
        self.misc = sb("misc", [128, D + 512])
        self.fw, self.fn = self.misc[:, 0:D], self.misc[:, D:D + 512]
        self.asb = sb("a_src_rows", [128, N])
        self.st = sb("stats", [128, 640])
        self.bn = self.st[:TP, 0:60].rearrange("p (t s) -> p t s", t=NT)
        self.mv = self.st[:TP, 60:70].rearrange("p (t s) -> p t s", t=NT)
        self.ones, self.zeros, self.iota64 = sb("ones", [128, 128]), sb("zeros", [128, HALF]), sb("iota64", [128, 64])
        self.lnc, self.slot_scale = sb("lnc", [128, 2]), sb("slot_scale", [128, 1])
        self.stages, self.loads = [], []
        self.wring = [Slot(a, s) for a, s in zip(self.wslot, self.wsem)]
        self.rring = [Slot(a, s) for a, s in zip(self.rslot, self.rsem)]
        self.sem, self.expert_loads = sem, 0
        self.esem = [sem(f"expert_landed{j}") for j in range(4)]
        self.freed, self.nbank = {}, 0
        self.consts, self.edges, self.ncol = [], [], 0
        self.edges_landed = sem("edges_landed")

    def now(self):
        return [(t.sem, t.joined) for t in (self.pe, self.act, self.dve, self.pool)]

    def end(self):
        return [(t.sem, t.planned) for t in (self.pe, self.act, self.dve, self.pool)]

    def add(self, stage):
        self.stages.append(stage)
        return stage

    def bank(self):
        self.nbank += 1
        return self.nbank - 1

    def _load(self, src, ring, shape):
        slot = ring.pop(0)
        ring.append(slot)
        p, c, w = shape
        before, base = slot.take(1)
        load = Load(src, slot.buf[:p, 0:c * w].rearrange("p (c w) -> p c w", c=c), slot.sem, base + 16, before)
        slot.last = load
        self.loads.append(load)
        return load

    def into(self, dst, src, after):
        free = Load(None, None, None, 0, None)
        free.used, free.used_at = after, (len(self.stages) - 1, 1 << 20)
        load = Load(src, dst, self.sem(f"landed_{len(self.loads)}"), 16, free)
        self.loads.append(load)
        return load

    def weights(self, src, kp=128):
        k, n = src.shape
        return self._load(src.rearrange("(c p) n -> p c n", p=kp), self.wring, (kp, k // kp, n))

    def row(self, src):
        n = src.shape[1]
        return self._load(src.to_broadcast([128, n]).unsqueeze(1), self.rring, (128, 1, n))

    def rows(self, src):
        return self._load(src.unsqueeze(1), self.rring, (src.shape[0], 1, src.shape[1]))

    def r(self, ap):
        return bass.AP(self.rounded[ap.tensor.name], ap.offset, ap.ap)

    def split(self, load):
        p, c, w = load.dst.shape
        slot = load.unit = len(self.units)
        load.high = self.high[slot % 2][:p, 0:c * w].rearrange("p (c w) -> p c w", c=c)
        load.high_free, load.segment = self.high_used[slot % 2], self.segment
        self.high_used[slot % 2] = list(load.used)
        self.units.append(load)

    def barrier(self, stage):
        self.high_used = [used + stage.ends() for used in self.high_used]
        self.segment += 1
        stage.next_unit, stage.next_segment = len(self.units), self.segment

    def split_high(self, u, segment):
        if u < len(self.units) and self.units[u].segment == segment:
            load = self.units[u]
            self.nc.scalar.wait_ge(load.sem, load.value)
            for sem, value in load.high_free:
                self.nc.scalar.wait_ge(sem, value)
            self.nc.scalar.activation(self.r(load.high), load.dst, ACT.Identity).then_inc(self.high_made, 1)

    def split_low(self, u, segment):
        if u < len(self.units) and self.units[u].segment == segment:
            load = self.units[u]
            self.nc.gpsimd.wait_ge(self.high_made, u + 1)
            self.nc.gpsimd.tensor_tensor(self.r(load.dst), load.dst, self.r(load.high), ALU.subtract).then_inc(self.low_made, 1)

    def const(self, dst, src):
        self.consts.append((dst, src))

    def col(self, name, parts=128):
        src = self.ins[name]
        n = src.shape[1]
        dst = self.cols[:parts, self.ncol:self.ncol + n]
        self.ncol += n
        self.const(dst, src)
        return dst

    def tok(self, buf, w=D):
        return buf[:TP, 0:NT * w].rearrange("p (t w) -> p t w", t=NT)

    def feat(self, buf, c=KC, p=128):
        return buf[:p, 0:c * N].rearrange("p (c n) -> p c n", c=c)


class Stage:

    next_unit = None
    side = False

    def __init__(self, net, after=None):
        self.net, self.nc = net, net.nc
        self.after = net.now() if after is None else after
        self.loads = []
        self.g = []

    def take(self, pe=0, act=0, dve=0, pool=0):
        n = self.net
        self.p0, self.a0, self.d0, self.l0 = (t.reserve(k) for t, k in ((n.pe, pe), (n.act, act), (n.dve, dve), (n.pool, pool)))
        self.size = (pe, act, dve, pool)
        for t, k in ((n.pe, pe), (n.act, act), (n.dve, dve), (n.pool, pool)):
            if k and not self.side:
                t.joined = t.planned
        self.done = self.ends()
        for load in self.loads:
            load.used, load.used_at = self.done, (len(n.stages), 1 << 20)
        n.add(self)

    def groups(self, n, evac):
        net = self.net
        ca = cd = 0
        a0, d0 = net.act.planned, net.dve.planned
        for i in range(n):
            b, e = net.bank(), evac[i % len(evac)]
            if e == "a":
                ca += 1
                net.freed[b] = (net.act.sem, a0 + ca)
            else:
                cd += 1
                net.freed[b] = (net.dve.sem, d0 + cd)
            self.g.append((b, e))
        return ca, cd

    def free(self, b):
        return self.net.freed[b - BANKS]

    def ends(self):
        return [(t.sem, b + k) for t, b, k in zip((self.net.pe, self.net.act, self.net.dve, self.net.pool), (self.p0, self.a0, self.d0, self.l0), self.size) if k]

    def split_next(self, split):
        if self.next_unit is not None:
            for u in range(2):
                split(self.next_unit + u, self.next_segment)

    def begin(self, eng):
        for sem, value in self.after:
            if value > 0:
                eng.wait_ge(sem, value)

    def landed(self, eng):
        for load in self.loads:
            eng.wait_ge(load.sem, load.value)

    def tensor(self, pe):
        pass

    def scalar(self, act):
        pass

    def vector(self, dve):
        pass

    def gpsimd(self, pool):
        pass


def evacuate(nc, eng, kind, out, ps, bias=None, gate=None, add=None):
    if eng == "a":
        func = {"copy": ACT.Identity, "relu": ACT.Relu, "gelu": ACT.Gelu, "tanh_gelu": ACT.Gelu_apprx_tanh,
                "silu": ACT.Silu, "square": ACT.Square}[kind]
        if bias is None:
            return nc.scalar.activation(out, ps, func)
        return nc.scalar.activation(out, ps, func, bias=bias)
    if kind == "copy":
        if bias is None:
            return nc.vector.tensor_copy(out, ps)
        return nc.vector.tensor_scalar(out, ps, bias, None, ALU.add)
    if kind == "relu":
        if bias is None:
            return nc.vector.tensor_scalar(out, ps, 0.0, None, ALU.max)
        return nc.vector.tensor_scalar(out, ps, bias, 0.0, ALU.add, ALU.max)
    if kind == "mul":
        return nc.vector.tensor_tensor(out, ps, add, ALU.mult)
    if kind == "add":
        return nc.vector.tensor_tensor(out, ps, add, ALU.add)
    if kind == "gate":
        return nc.vector.scalar_tensor_tensor(out=out, in0=ps, scalar=gate, in1=add, op0=ALU.mult, op1=ALU.add)
    return nc.vector.tensor_scalar(out, ps, gate, None, ALU.mult)


def tile_stats(net, dve, x, t):
    done = net.dve
    dve.wait_ge(done.sem, done.issued)
    for j in range(2):
        net.nc.vector.bn_stats(net.bn[:, t, 6 * j:6 * j + 6], x[:, t, j * HALF:(j + 1) * HALF]).then_inc(done.sem, done.one())
    dve.wait_ge(done.sem, done.issued)
    net.nc.vector.bn_aggr(net.mv[:, t, :], net.bn[:, t, :]).then_inc(done.sem, done.one())


class LinearT(Stage):

    def __init__(self, net, xT, parts, evac="ad", after=None):
        super().__init__(net, after)
        self.xT, self.parts = xT, parts
        self.pairs = isinstance(parts[0][3], Pair)
        if self.pairs:
            for i in range(2 * len(parts)):
                b = net.bank()
                net.freed[b] = (net.act.sem, net.act.planned + 2 * i + 1)
                self.g.append((b, "a"))
            a, d = 4 * len(parts), 2 * len(parts)
        else:
            a, d = self.groups(2 * len(parts), evac)
        self.loads = list(dict.fromkeys(q[0] for q in parts))
        self.take(pe=2 * len(parts), act=a, dve=d)
        for n, q in enumerate(parts):
            q[0].used, q[0].used_at = [(net.pe.sem, self.p0 + 2 * n + 2)], (len(net.stages) - 1, n)
        for load in self.loads:
            net.split(load)

    def chunk_done(self, m):
        return [self.net.freed[b] for b, _ in self.g[2 * m:2 * m + 2]]

    def tensor(self, pe):
        self.begin(pe)
        kp, kc = self.xT.shape[0], self.xT.shape[1]
        i = 0
        for load, c0, w, out, bias, kind in self.parts:
            pe.wait_ge(self.net.low_made, load.unit + 1)
            weights = {"hi": load.high, "lo": load.dst}
            for t0, t1 in HALVES:
                b = self.g[i][0]
                if b >= BANKS:
                    pe.wait_ge(*self.free(b))
                n = (t1 - t0) * TP + (t1 - t0) * TP % 2
                mm = products(self.net, self.net.ps[:w, b % BANKS, 0:n], kc, lambda s, k: weights[s][:kp, k, c0:c0 + w],
                              lambda m, k: (self.xT.hi if m == "hi" else self.xT.lo)[:, k, t0 * TP:t0 * TP + n])
                mm.then_inc(self.net.pe.sem, self.net.pe.one())
                i += 1

    def last(self, i):
        return i % 2 == 1 and (i // 2 + 1 == len(self.parts) or self.parts[i // 2 + 1][0] is not self.parts[i // 2][0])

    def evac(self, eng, letter, ticks):
        self.begin(eng)
        for i, (b, e) in enumerate(self.g):
            load, c0, w, out, bias, kind = self.parts[i // 2]
            t0, t1 = HALVES[i % 2]
            ts, ps = slice(t0 * TP, t1 * TP), self.net.ps[:w, b % BANKS, 0:(t1 - t0) * TP]
            if self.pairs and letter == "a":
                eng.wait_ge(self.net.pe.sem, self.p0 + i + 1)
                evacuate(self.nc, letter, kind, out.lo[:, ts], ps, bias=bias).then_inc(ticks.sem, ticks.one())
                eng.wait_ge(ticks.sem, ticks.issued)
                self.nc.scalar.activation(self.net.r(out.hi[:, ts]), out.lo[:, ts], ACT.Identity).then_inc(ticks.sem, ticks.one())
            elif self.pairs:
                eng.wait_ge(self.net.act.sem, self.a0 + 2 * i + 2)
                self.nc.vector.tensor_tensor(self.net.r(out.lo[:, ts]), out.lo[:, ts], self.net.r(out.hi[:, ts]), ALU.subtract).then_inc(ticks.sem, ticks.one())
            elif e == letter:
                eng.wait_ge(self.net.pe.sem, self.p0 + i + 1)
                evacuate(self.nc, letter, kind, out[:, ts], ps, bias=bias).then_inc(ticks.sem, ticks.one())
            if letter == "a" and self.last(i):
                self.net.split_high(load.unit + 2, load.segment)

    def scalar(self, act):
        self.evac(act, "a", self.net.act)

    def vector(self, dve):
        self.evac(dve, "d", self.net.dve)

    def gpsimd(self, pool):
        for load in dict.fromkeys(q[0] for q in self.parts):
            self.net.split_low(load.unit + 2, load.segment)


class Linear(Stage):

    def __init__(self, net, xT, units, evac="ad", after=None, rows=(), stats=None):
        super().__init__(net, after)
        self.xT, self.units, self.rows, self.stats = xT, units, rows, stats
        a = d = 0
        for i in range(NT * len(units)):
            b, e = net.bank(), evac[i % len(evac)]
            a, d = a + (e == "a"), d + (e == "d")
            net.freed[b] = (net.act.sem, net.act.planned + a) if e == "a" else (net.dve.sem, net.dve.planned + d)
            if stats is not None and i >= NT * (len(units) - 1):
                d += 3
            self.g.append((b, e))
        self.loads = list(rows)
        self.take(pe=NT * len(units), act=a, dve=d)
        for n, u in enumerate(units):
            u["load"].used, u["load"].used_at = [(net.pe.sem, self.p0 + NT * (n + 1))], (len(net.stages) - 1, n)
        if isinstance(xT, Pair):
            for load in dict.fromkeys(u["load"] for u in units):
                net.split(load)

    def tensor(self, pe):
        self.begin(pe)
        kc = self.xT.shape[1]
        i = 0
        for u in self.units:
            load = u["load"]
            if load.unit is None:
                pe.wait_ge(load.sem, load.value)
            else:
                pe.wait_ge(self.net.low_made, load.unit + 1)
                weights = {"hi": load.high, "lo": load.dst}
            for t in range(NT):
                b = self.g[i][0]
                if b >= BANKS:
                    pe.wait_ge(*self.free(b))
                if load.unit is not None:
                    mm = products(self.net, self.net.ps[:TP, b % BANKS, 0:u["w"]], kc,
                                  lambda s, k: (self.xT.hi if s == "hi" else self.xT.lo)[:, k, t * TP:(t + 1) * TP],
                                  lambda m, k: weights[m][:, k, u.get("c0", 0):u.get("c0", 0) + u["w"]])
                for k in range(kc if load.unit is None else 0):
                    mm = self.nc.tensor.matmul(self.net.ps[:TP, b % BANKS, 0:u["w"]], self.xT[:, k, t * TP:(t + 1) * TP],
                                               load.dst[:, k, 0:u["w"]],
                                               start=(k == 0), stop=(k == kc - 1))
                mm.then_inc(self.net.pe.sem, self.net.pe.one())
                i += 1

    def evac(self, eng, letter, ticks):
        self.begin(eng)
        for row in self.rows:
            eng.wait_ge(row.sem, row.value)
        for i, (b, e) in enumerate(self.g):
            if e == letter:
                u, t = self.units[i // NT], i % NT
                ps = self.net.ps[:TP, b % BANKS, 0:u["w"]]
                out, add = u["out"][:, t], u.get("add")
                if len(out.shape) == 3:
                    ps = ps.rearrange("p (h c) -> p h c", h=out.shape[1])
                if add is not None:
                    add = add[:, t] if u.get("by_tile", True) else add
                gate = u["gate"][:, t:t + 1] if "gate" in u else None
                eng.wait_ge(self.net.pe.sem, self.p0 + i + 1)
                evacuate(self.nc, letter, u["kind"], out, ps, add=add, gate=gate).then_inc(ticks.sem, ticks.one())
                if self.stats is not None and i >= NT * (len(self.units) - 1):
                    tile_stats(self.net, eng, self.stats, t)
            load = self.units[i // NT]["load"]
            last = i + 1 == len(self.g) or self.units[(i + 1) // NT]["load"] is not load
            if letter == "a" and last and load.unit is not None:
                self.net.split_high(load.unit + 2, load.segment)

    def scalar(self, act):
        self.evac(act, "a", self.net.act)

    def vector(self, dve):
        self.evac(dve, "d", self.net.dve)

    def gpsimd(self, pool):
        for load in dict.fromkeys(u["load"] for u in self.units):
            if load.unit is not None:
                self.net.split_low(load.unit + 2, load.segment)


class ToFeatures(Stage):

    def __init__(self, net, x, out, func="copy", evac="ad", after=None, tiles=None):
        super().__init__(net, after)
        self.x, self.out, self.func, self.tiles = x, out, func, tiles
        self.c = out.shape[1]
        self.per = 3 if self.c % 3 == 0 else self.c
        self.ng = self.c // self.per
        self.pairs = isinstance(out, Pair)
        if self.pairs:
            a = d = NT * self.ng
            for i in range(a):
                b = net.bank()
                net.freed[b] = (net.dve.sem, net.dve.planned + i + 1)
                self.g.append((b, "ad"))
        else:
            a, d = self.groups(NT * self.ng, evac)
        self.take(pe=NT * self.ng, act=a, dve=d)

    def tensor(self, pe):
        self.begin(pe)
        w = self.out.shape[0]
        for i, (b, e) in enumerate(self.g):
            t, c0 = i // self.ng, i % self.ng * self.per
            if b >= BANKS:
                pe.wait_ge(*self.free(b))
            if self.tiles and c0 == 0:
                pe.wait_ge(*self.tiles[t])
            for c in range(c0, c0 + self.per):
                mm = self.nc.tensor.transpose(self.net.ps[:w, b % BANKS, (c - c0) * TP:(c - c0 + 1) * TP],
                                              self.x[:, t, c * w:(c + 1) * w], self.net.ident[:TP, :TP])
            mm.then_inc(self.net.pe.sem, self.net.pe.one())

    def evac(self, eng, letter, ticks):
        self.begin(eng)
        w = self.out.shape[0]
        for i, (b, e) in enumerate(self.g):
            t, c0 = i // self.ng, i % self.ng * self.per
            if self.pairs:
                hi, lo = (self.net.r(x[:, c0:c0 + self.per, t * TP:(t + 1) * TP]) for x in (self.out.hi, self.out.lo))
                ps = self.net.ps[:w, b % BANKS, 0:self.per * TP].rearrange("p (c n) -> p c n", c=self.per)
                if letter == "a":
                    eng.wait_ge(self.net.pe.sem, self.p0 + i + 1)
                    evacuate(self.nc, letter, self.func, hi, ps).then_inc(ticks.sem, ticks.one())
                    continue
                eng.wait_ge(self.net.act.sem, self.a0 + i + 1)
                if self.func == "relu":
                    self.nc.vector.scalar_tensor_tensor(out=lo, in0=ps, scalar=0.0, in1=hi, op0=ALU.max, op1=ALU.subtract).then_inc(ticks.sem, ticks.one())
                else:
                    self.nc.vector.tensor_tensor(lo, ps, hi, ALU.subtract).then_inc(ticks.sem, ticks.one())
            elif e == letter:
                eng.wait_ge(self.net.pe.sem, self.p0 + i + 1)
                evacuate(self.nc, letter, self.func, self.out[:, c0:c0 + self.per, t * TP:(t + 1) * TP],
                         self.net.ps[:w, b % BANKS, 0:self.per * TP].rearrange("p (c n) -> p c n", c=self.per)).then_inc(ticks.sem, ticks.one())

    def scalar(self, act):
        self.evac(act, "a", self.net.act)

    def vector(self, dve):
        self.evac(dve, "d", self.net.dve)


class LayerNorm(Stage):

    def __init__(self, net, x, out, eps, gamma=None, beta=None, ready=False, after=None, made=None):
        super().__init__(net, after)
        self.made = made
        self.x, self.out, self.eps, self.gamma, self.beta, self.ready = x, out, eps, gamma, beta, ready
        self.loads = [r for r in (gamma, beta) if r]
        self.rstd = net.st[:TP, 70:75]
        n = 0 if ready else 3 * NT
        self.root = net.dve.planned + n + 1
        self.tiles = [(net.dve.sem, net.dve.planned + n + 2 + (t + 1 if not gamma else min(2 * t + 3, 2 * NT))) for t in range(NT)]
        self.take(dve=n + 2 + (2 * NT if gamma else NT), act=1)

    def vector(self, dve):
        self.begin(dve)
        nc, done, mv = self.nc, self.net.dve, self.net.mv
        if not self.ready:
            for t in range(NT):
                if self.made:
                    dve.wait_ge(*self.made[t])
                tile_stats(self.net, dve, self.x, t)
        dve.wait_ge(done.sem, done.issued)
        nc.vector.tensor_scalar(self.rstd, mv[:, :, 1], self.eps, None, ALU.add).then_inc(done.sem, done.one())
        dve.wait_ge(self.net.act.sem, self.a0 + 1)
        nc.vector.reciprocal(self.rstd, self.rstd).then_inc(done.sem, done.one())
        if not self.gamma:
            dve.wait_ge(done.sem, done.issued)
            for t in range(NT):
                nc.vector.tensor_scalar(self.out[:, t], self.x[:, t], mv[:, t, 0:1], self.rstd[:, t:t + 1],
                                        ALU.subtract, ALU.mult).then_inc(done.sem, done.one())
            return
        self.landed(dve)
        first = done.issued
        for t in range(NT + 1):
            if t < NT:
                nc.vector.scalar_tensor_tensor(out=self.out[:, t], in0=self.x[:, t], scalar=mv[:, t, 0:1], in1=self.gamma.dst[:TP, 0],
                                               op0=ALU.subtract, op1=ALU.mult).then_inc(done.sem, done.one())
            if t > 0:
                dve.wait_ge(done.sem, first + (1 if t == 1 else 2 * t - 2))
                nc.vector.scalar_tensor_tensor(out=self.out[:, t - 1], in0=self.out[:, t - 1], scalar=self.rstd[:, t - 1:t], in1=self.beta.dst[:TP, 0],
                                               op0=ALU.mult, op1=ALU.add).then_inc(done.sem, done.one())

    def scalar(self, act):
        self.begin(act)
        act.wait_ge(self.net.dve.sem, self.root)
        self.nc.scalar.activation(self.rstd, self.rstd, ACT.Sqrt).then_inc(self.net.act.sem, self.net.act.one())


def norm_T(net, x, out, outT, eps, gamma=None, beta=None, ready=False, made=None):
    start = net.now()
    norm = LayerNorm(net, x, out, eps, gamma, beta, ready, made=made)
    ToFeatures(net, out, outT, evac="aaaaaaaadd" if gamma is None else "a", after=start, tiles=norm.tiles)
    return norm


class AddRow(Stage):
    side = True

    def __init__(self, net, x, row, after=None):
        super().__init__(net, after)
        self.x, self.row, self.loads = x, row, [row]
        self.take(pool=NT)

    def gpsimd(self, pool):
        self.begin(pool)
        self.landed(pool)
        for t in range(NT):
            self.nc.gpsimd.tensor_tensor(self.x[:, t], self.x[:, t], self.row.dst[:TP, 0], ALU.add).then_inc(self.net.pool.sem, self.net.pool.one())


class Split(Stage):
    side = True

    def __init__(self, net, x, hi, after=None):
        super().__init__(net, after)
        self.x, self.hi = x, hi
        self.take(act=x.shape[1], dve=x.shape[1])

    def scalar(self, act):
        self.begin(act)
        for c in range(self.x.shape[1]):
            self.nc.scalar.activation(self.net.r(self.hi[:, c]), self.x[:, c], ACT.Identity).then_inc(self.net.act.sem, self.net.act.one())

    def vector(self, dve):
        self.begin(dve)
        for c in range(self.x.shape[1]):
            dve.wait_ge(self.net.act.sem, self.a0 + c + 1)
            self.nc.vector.tensor_tensor(self.net.r(self.x[:, c]), self.x[:, c], self.net.r(self.hi[:, c]), ALU.subtract).then_inc(self.net.dve.sem, self.net.dve.one())


class ReluAdd(Stage):

    def __init__(self, net, x, y, after=None):
        super().__init__(net, after)
        self.x, self.y = x, y
        self.take(dve=NT)

    def vector(self, dve):
        self.begin(dve)
        for t in range(NT):
            self.nc.vector.scalar_tensor_tensor(out=self.x[:, t], in0=self.y[:, t], scalar=0.0, in1=self.x[:, t],
                                                op0=ALU.max, op1=ALU.add).then_inc(self.net.dve.sem, self.net.dve.one())


class Add(Stage):
    side = True

    def __init__(self, net, out, x, y, after=None, tiles=None):
        super().__init__(net, after)
        self.out, self.x, self.y, self.tiles = out, x, y, tiles
        self.made = [(net.pool.sem, net.pool.planned + t + 1) for t in range(NT)]
        self.take(pool=NT)

    def gpsimd(self, pool):
        self.begin(pool)
        for t in range(NT):
            if self.tiles:
                pool.wait_ge(*self.tiles[t])
            self.nc.gpsimd.tensor_tensor(self.out[:, t], self.x[:, t], self.y[:, t], ALU.add).then_inc(self.net.pool.sem, self.net.pool.one())


class EdgeCounts(Stage):
    CH = E // TP
    DEPTH = 4

    def __init__(self, net, after=None):
        super().__init__(net, after)
        g = net.G
        self.idx_i = g[0][:TP, 0:2 * self.CH].bitcast(I32).rearrange("p (s c) -> p s c", s=2)
        self.idx = g[1][:TP, 0:2 * self.CH].rearrange("p (s c) -> p s c", s=2)
        self.iota = g[2][:TP, 0:N]
        self.iota16 = g[2][:TP, N:N + 320].bitcast(F16)[:, 0:N]
        self.hot = [[g[3 + s][:TP, 320 * j:320 * j + 320].bitcast(F16)[:, 0:N] for s in range(2)] for j in range(self.DEPTH)]
        self.zero = g[5][:TP, 0:320].bitcast(F16)[:, 0:N]
        for s, name in enumerate(("src", "dst")):
            net.edges.append((self.idx_i[:, s, :], net.ins[name].rearrange("(p c) -> p c", p=TP)))
        net.edges.append((self.iota, net.ins["iota"].to_broadcast([TP, N])))
        while net.nbank % BANKS:
            net.freed[net.bank()] = (net.dve.sem, net.dve.planned)
        n_dve = 3 + 2 * self.CH
        for i in range(BANKS):
            net.freed[net.bank()] = (net.dve.sem, net.dve.planned + n_dve + 2 * NT)
        self.take(pe=1 + self.CH + 1, dve=n_dve + 2 * NT)

    def products(self, lhs, rhs, start, stop):
        ps = self.net.ps
        for t in range(NT):
            self.nc.tensor.matmul(ps[:TP, t, 0:500], lhs[:, t * TP:(t + 1) * TP], rhs[:, 0:500], start=start, stop=stop, skip_group_check=True)
            b, c = (5, t * TP) if t < 4 else (6, 0)
            mm = self.nc.tensor.matmul(ps[:TP, b, c:c + TP], lhs[:, t * TP:(t + 1) * TP], rhs[:, 500:625], start=start, stop=stop, skip_group_check=True)
        return mm

    def tensor(self, pe):
        self.begin(pe)
        done, dve = self.net.pe, self.net.dve
        pe.wait_ge(dve.sem, self.d0 + 3)
        self.products(self.zero, self.zero, True, False).then_inc(done.sem, done.one())
        with self.nc.tensor.Fori(0, self.CH // self.DEPTH) as i:
            for j in range(self.DEPTH):
                pe.wait_ge(dve.sem, i * (2 * self.DEPTH) + (self.d0 + 3 + 2 * j + 2))
                self.products(self.hot[j][1], self.hot[j][0], False, False).then_inc(done.sem, 1)
        done.issued += self.CH
        self.products(self.zero, self.zero, False, True).then_inc(done.sem, done.one())
        pe.wait_ge(self.net.const_landed, 16 * len(self.net.consts))

    def vector(self, dve):
        self.begin(dve)
        nc, done, pe = self.nc, self.net.dve, self.net.pe
        nc.vector.memset(self.zero, 0.0).then_inc(done.sem, done.one())
        dve.wait_ge(self.net.edges_landed, 16 * len(self.net.edges))
        nc.vector.tensor_copy(self.idx, self.idx_i).then_inc(done.sem, done.one())
        nc.vector.tensor_copy(self.iota16, self.iota).then_inc(done.sem, done.one())
        dve.wait_ge(done.sem, done.issued)
        for j in range(self.DEPTH):
            for s in range(2):
                nc.vector.tensor_scalar(self.hot[j][s], self.iota16, self.idx[:, s, j:j + 1], None, ALU.is_equal).then_inc(done.sem, 1)
        with nc.vector.Fori(1, self.CH // self.DEPTH) as i:
            for j in range(self.DEPTH):
                dve.wait_ge(pe.sem, i * self.DEPTH + (self.p0 + 1 + j + 1 - self.DEPTH))
                for s in range(2):
                    nc.vector.tensor_scalar(self.hot[j][s], self.iota16, self.idx[:, s, bass.ds(i * self.DEPTH + j, 1)], None,
                                            ALU.is_equal).then_inc(done.sem, 1)
        done.issued += 2 * self.CH
        dve.wait_ge(pe.sem, self.p0 + self.CH + 2)
        ps, counts = self.net.ps, self.net.counts
        for t in range(NT):
            nc.vector.tensor_copy(counts[:TP, t, 0:500], ps[:TP, t, 0:500]).then_inc(done.sem, done.one())
            b, c = (5, t * TP) if t < 4 else (6, 0)
            nc.vector.tensor_copy(counts[:TP, t, 500:625], ps[:TP, b, c:c + TP]).then_inc(done.sem, done.one())
        dve.wait_ge(self.net.const_landed, 16 * len(self.net.consts))


class SelfLoops(Stage):
    side = True

    def __init__(self, net, op, after=None):
        super().__init__(net, after)
        self.op = op
        self.take(dve=2 * NT)

    def vector(self, dve):
        self.begin(dve)
        nc, done, counts = self.nc, self.net.dve, self.net.counts
        for t in range(NT):
            diag = counts[:TP, t, t * TP:(t + 1) * TP]
            nc.vector.tensor_tensor(diag, diag, self.net.ident[:TP, :TP], self.op).then_inc(done.sem, done.one())
        dve.wait_ge(done.sem, done.issued)
        for t in range(NT):
            nc.vector.tensor_scalar(self.net.mask[:TP, t, :], counts[:TP, t, :], 0.0, MASKED, ALU.is_equal, ALU.mult).then_inc(done.sem, done.one())


class GatCoefs(Stage):
    side = True

    def __init__(self, net, h, heads, c, head0, a_src, a_dst, coef, scratch, after=None):
        super().__init__(net, after)
        self.h, self.heads, self.c, self.head0, self.coef, self.scratch = h, heads, c, head0, coef, scratch
        self.loads = [a_src, a_dst]
        self.take(dve=2 * NT * heads)

    def vector(self, dve):
        self.begin(dve)
        self.landed(dve)
        done = self.net.dve
        for s in range(2):
            for t in range(NT):
                for hd in range(self.heads):
                    cs = slice(hd * self.c, (hd + 1) * self.c)
                    n = (s * NT + t) * self.heads + hd
                    if n > 1:
                        dve.wait_ge(done.sem, self.d0 + n - 1)
                    self.nc.vector.tensor_tensor_reduce(
                        out=self.scratch[:TP, (n % 2) * D:(n % 2) * D + self.c], in0=self.h[:, t, cs],
                        in1=self.loads[s].dst[:TP, 0, cs], scale=1.0, scalar=0.0, op0=ALU.mult, op1=ALU.add,
                        accum_out=self.coef[:, s, self.head0 + hd, t:t + 1]).then_inc(done.sem, done.one())


FIRST = "first"


class Heads(Stage):

    def schedule(self, n_heads, first, prior):
        net = self.net
        self.order = {e: [] for e in ("pe", "act", "dve", "pool")}
        self.side = last = first < 0 and prior is FIRST
        for k in range(first, 0 if last else n_heads):
            self.step(k, k + 1 < n_heads, k >= 0)
        bases = dict(pe=net.pe.planned, act=net.act.planned, dve=net.dve.planned, pool=net.pool.planned)
        self.at = {e: {q: bases[e] + i + 1 for i, q in enumerate(seq)} for e, seq in self.order.items()}
        if first >= 0:
            for e in self.at:
                self.at[e].update(prior.at[e])
        self.bank = {}
        for q in self.order["pe"]:
            b = self.bank[q] = net.bank()
            engine, entry = self.reader(q)
            net.freed[b] = ({"act": net.act, "dve": net.dve}[engine].sem, self.at[engine][entry])
        self.take(**{e: len(seq) for e, seq in self.order.items()})
        if n_heads > 1 and not last:
            net.barrier(self)


    def ps(self, q, p, w):
        return self.net.ps[:p, self.bank[q] % BANKS, 0:w]

    def wait(self, eng, engine, *entry):
        ticks = {"pe": self.net.pe, "act": self.net.act, "dve": self.net.dve, "pool": self.net.pool}[engine]
        eng.wait_ge(ticks.sem, self.at[engine][entry])

    def wait_bank(self, pe, q):
        if self.bank[q] >= BANKS:
            pe.wait_ge(*self.free(self.bank[q]))

    def turn_group(self, P, s, t0, t1, q):
        ps = self.ps(q, TP, (t1 - t0) * TP)
        for t in range(t0, t1):
            mm = self.nc.tensor.transpose(ps[:, (t - t0) * TP:(t - t0 + 1) * TP], P[:, t, s * TP:(s + 1) * TP], self.net.ident[:TP, :TP])
        return mm


class GatHeads(Heads):

    def __init__(self, net, heads, P, PT, eps, rows=(), after=None, first=-1, prior=None):
        super().__init__(net, after)
        self.heads, self.P, self.PT, self.eps, self.rows = heads, P, PT, eps, list(rows)
        self.loads = self.rows
        o = 80
        self.mx, self.b1, self.b2, self.sum = (net.st[:TP, o + 5 * k:o + 5 * k + 5] for k in range(4))
        self.rinv = [net.st[:TP, 180 + 5 * k:185 + 5 * k] for k in range(2)]
        self.relu = [net.misc[:TP, N * k:N * (k + 1)] for k in range(2)]
        c = heads[0][2].shape[2]
        self.w = c if c <= 512 else HALF
        self.nw = c // self.w
        self.schedule(len(heads), first, prior)

    def step(self, k, scores, apply):
        pe, act, dve, pool = (self.order[e] for e in ("pe", "act", "dve", "pool"))
        n = k + 1
        if scores:
            pe += [("row", n, j) for j in range(2)]
            act += [("row", n, j) for j in range(2)]
            dve += [("max", n, t) for t in range(NT)] + [("small", n, j) for j in range(4)]
        if apply:
            pe += [("turn", k, s, j) for s in range(NT) for j in range(2)] + [("apply", k, t, j) for t in range(NT) for j in range(self.nw)]
            act += [("turn", k, s, j) for s in range(NT) for j in range(2)]
        if scores:
            act += [("relu", n, 0), ("relu", n, 1)]
            for t in range(NT):
                pool.append(("add", n, t))
                act.append(("exp", n, t))
                if t + 2 < NT:
                    act.append(("relu", n, t + 2))
        for t in range(NT):
            if apply:
                dve += [("out", k, t, j) for j in range(self.nw)]
            if scores:
                dve.append(("count", n, t))
        if scores:
            dve += [("sum", n), ("rinv", n)]

    def reader(self, q):
        return {"row": ("act", q), "turn": ("act", q), "apply": ("dve", ("out",) + q[1:])}[q[0]]

    def tensor(self, pe):
        self.begin(pe)
        nc, done = self.nc, self.net.pe
        for q in self.order["pe"]:
            self.wait_bank(pe, q)
            k = q[1]
            if q[0] == "row":
                t0, t1 = HALVES[q[2]]
                ps = self.ps(q, TP, (t1 - t0) * TP)
                for t in range(t0, t1):
                    mm = nc.tensor.matmul(ps[:, (t - t0) * TP:(t - t0 + 1) * TP], self.heads[k][0][:, t:t + 1].to_broadcast([TP, TP]),
                                          self.net.ident[:TP, :TP], start=True, stop=True)
            elif q[0] == "turn":
                t0, t1 = HALVES[q[3]]
                if q[2] == 0:
                    self.wait(pe, "dve", "count", k, t1 - 1)
                mm = self.turn_group(self.P[k % 2], q[2], t0, t1, q)
            else:
                t, j = q[2], q[3]
                for s in range(NT):
                    if t == 0 and j == 0:
                        self.wait(pe, "act", "turn", k, s, 1)
                    mm = nc.tensor.matmul(self.ps(q, TP, self.w), self.PT[:, s, t * TP:(t + 1) * TP],
                                          self.heads[k][2][:, s, j * self.w:(j + 1) * self.w], start=(s == 0), stop=(s == NT - 1))
            mm.then_inc(done.sem, done.one())

    def scalar(self, act):
        self.begin(act)
        nc, done = self.nc, self.net.act
        for q in self.order["act"]:
            k = q[1]
            if q[0] == "row":
                t0, t1 = HALVES[q[2]]
                self.wait(act, "pe", *q)
                ins = nc.scalar.activation(self.net.asb[:TP, t0 * TP:t1 * TP], self.ps(q, TP, (t1 - t0) * TP), ACT.Identity)
            elif q[0] == "turn":
                t0, t1 = HALVES[q[3]]
                self.wait(act, "pe", *q)
                ins = nc.scalar.activation(self.PT[:, q[2], t0 * TP:t1 * TP], self.ps(q, TP, (t1 - t0) * TP), ACT.Identity)
            elif q[0] == "relu":
                t = q[2]
                if t == 0:
                    self.wait(act, "dve", "small", k, 3)
                if t >= 2:
                    self.wait(act, "pool", "add", k, t - 2)
                ins = nc.scalar.activation(self.relu[t % 2], self.P[k % 2][:, t], ACT.Relu, bias=self.b1[:, t:t + 1], scale=(1 - SLOPE) / SLOPE)
            else:
                t = q[2]
                self.wait(act, "pool", "add", k, t)
                ins = nc.scalar.activation(self.P[k % 2][:, t], self.P[k % 2][:, t], ACT.Exp, bias=self.b2[:, t:t + 1])
            ins.then_inc(done.sem, done.one())
        self.split_next(self.net.split_high)

    def vector(self, dve):
        self.begin(dve)
        self.landed(dve)
        nc, done, stt = self.nc, self.net.dve, self.nc.vector.scalar_tensor_tensor
        for q in self.order["dve"]:
            k = q[1]
            src, dst, h, out, add, by_tile = self.heads[k]
            if q[0] == "max":
                t = q[2]
                if t == 0:
                    self.wait(dve, "act", "row", k, 1)
                ins = nc.vector.tensor_tensor_reduce(out=self.P[k % 2][:, t], in0=self.net.asb[:TP, :], in1=self.net.mask[:TP, t, :], scale=SLOPE,
                                                     scalar=2 * MASKED, op0=ALU.add, op1=ALU.max, accum_out=self.mx[:, t:t + 1])
            elif q[0] == "small":
                dve.wait_ge(done.sem, done.issued)
                if q[2] == 0:
                    ins = nc.vector.tensor_scalar(self.b1, dst, 1 - SLOPE, None, ALU.mult)
                elif q[2] == 1:
                    ins = stt(out=self.b2, in0=dst, scalar=SLOPE, in1=self.mx, op0=ALU.mult, op1=ALU.add)
                elif q[2] == 2:
                    ins = stt(out=self.mx, in0=self.b2, scalar=1 / SLOPE, in1=self.b2, op0=ALU.mult, op1=ALU.max)
                else:
                    ins = stt(out=self.b2, in0=dst, scalar=SLOPE, in1=self.mx, op0=ALU.mult, op1=ALU.subtract)
            elif q[0] == "count":
                t = q[2]
                self.wait(dve, "act", "exp", k, t)
                ins = nc.vector.tensor_tensor_reduce(out=self.P[k % 2][:, t], in0=self.P[k % 2][:, t], in1=self.net.counts[:TP, t, :], scale=1.0,
                                                     scalar=0.0, op0=ALU.mult, op1=ALU.add, accum_out=self.sum[:, t:t + 1])
            elif q[0] == "sum":
                dve.wait_ge(done.sem, done.issued)
                ins = nc.vector.tensor_scalar(self.sum, self.sum, self.eps, None, ALU.add)
            elif q[0] == "rinv":
                dve.wait_ge(done.sem, done.issued)
                ins = nc.vector.reciprocal(self.rinv[k % 2], self.sum)
            else:
                t, j = q[2], q[3]
                cs = slice(j * self.w, (j + 1) * self.w)
                self.wait(dve, "pe", "apply", k, t, j)
                if t == 0 and j == 0:
                    self.wait(dve, "dve", "rinv", k)
                if add is None:
                    ins = nc.vector.tensor_scalar(out[:, t, cs], self.ps(("apply", k, t, j), TP, self.w), self.rinv[k % 2][:, t:t + 1], None, ALU.mult)
                else:
                    ins = stt(out=out[:, t, cs], in0=self.ps(("apply", k, t, j), TP, self.w), scalar=self.rinv[k % 2][:, t:t + 1],
                              in1=add[:, t, cs] if by_tile else add[:, cs], op0=ALU.mult, op1=ALU.add)
            ins.then_inc(done.sem, done.one())

    def gpsimd(self, pool):
        self.begin(pool)
        for q in self.order["pool"]:
            k, t = q[1], q[2]
            self.wait(pool, "act", "relu", k, t)
            self.nc.gpsimd.tensor_tensor(self.P[k % 2][:, t], self.P[k % 2][:, t], self.relu[t % 2], ALU.add).then_inc(self.net.pool.sem, self.net.pool.one())
        self.split_next(self.net.split_low)


class SoftmaxHeads(Heads):

    def __init__(self, net, heads, P, PT, scale, after=None):
        super().__init__(net, after)
        self.heads, self.P, self.PT, self.scale = heads, P, PT, scale
        self.mx2 = net.st[:TP, 200:210].rearrange("p (t s) -> p t s", t=NT)
        self.nb = net.st[:TP, 210:215]
        self.sum2 = net.st[:TP, 215:225].rearrange("p (t s) -> p t s", t=NT)
        self.rinv = net.st[:TP, 180:185]
        self.schedule(len(heads), -1, None)

    def step(self, k, scores, apply):
        pe, act, dve = (self.order[e] for e in ("pe", "act", "dve"))
        n = k + 1
        for t in range(NT + 1):
            if scores and t < NT:
                pe += [("score", n, t, j) for j in range(2)]
                dve += [("max", n, t, j) for j in range(2)] + [("top", n, t), ("neg", n, t)]
            if apply and t < NT:
                pe += [("turn", k, t, j) for j in range(2)]
                act.append(("turn", k, t, 0))
                dve.append(("turn", k, t, 1))
            if scores and t < NT:
                act += [("exp", n, t, j) for j in range(2)]
            if scores and t > 0:
                dve += [("sum", n, t - 1), ("rinv", n, t - 1), ("norm", n, t - 1)]
        if apply:
            for j in range(2):
                pe.append(("apply", k, j))
                act.append(("out", k, j))
                dve.append(("out", k, j))

    def reader(self, q):
        if q[0] == "score":
            return "act", ("exp",) + q[1:]
        if q[0] == "turn":
            return ("act", "dve")[q[3]], q
        return "dve", ("out",) + q[1:]

    def tensor(self, pe):
        self.begin(pe)
        nc, done = self.nc, self.net.pe
        for q in self.order["pe"]:
            self.wait_bank(pe, q)
            k = q[1]
            qT, kT, v, half, out = self.heads[k]
            if q[0] == "score":
                t0, t1 = HALVES[q[3]]
                mm = nc.tensor.matmul(self.ps(q, TP, (t1 - t0) * TP), qT[:, q[2] * TP:(q[2] + 1) * TP], kT[:, t0 * TP:t1 * TP], start=True, stop=True)
            elif q[0] == "turn":
                if q[2] == 0:
                    self.wait(pe, "dve", "norm", k, HALVES[q[3]][1] - 1)
                mm = self.turn_group(self.P[k % 2], q[2], *HALVES[q[3]], q)
            else:
                t0, t1 = HALVES[q[2]]
                self.wait(pe, "act", "turn", k, NT - 1, 0)
                self.wait(pe, "dve", "turn", k, NT - 1, 1)
                for s in range(NT):
                    mm = nc.tensor.matmul(self.ps(q, 128, (t1 - t0) * TP), v[:, s, :], self.PT[:, s, t0 * TP:t1 * TP], start=(s == 0), stop=(s == NT - 1))
            mm.then_inc(done.sem, done.one())

    def result(self, k, j):
        t0, t1 = HALVES[j]
        qT, kT, v, half, out = self.heads[k]
        ps = self.net.ps[half, self.bank[("apply", k, j)] % BANKS, 0:(t1 - t0) * TP]
        return ps, self.net.r(out.hi[:, t0 * TP:t1 * TP]), self.net.r(out.lo[:, t0 * TP:t1 * TP])

    def scalar(self, act):
        self.begin(act)
        nc, done = self.nc, self.net.act
        for q in self.order["act"]:
            k, j = q[1], q[-1]
            t0, t1 = HALVES[j]
            if q[0] == "turn":
                self.wait(act, "pe", *q)
                ins = nc.scalar.activation(self.PT[:, q[2], t0 * TP:t1 * TP], self.ps(q, TP, (t1 - t0) * TP), ACT.Identity)
            elif q[0] == "out":
                self.wait(act, "pe", "apply", k, j)
                ps, hi, lo = self.result(k, j)
                ins = nc.scalar.activation(hi, ps, ACT.Identity)
            else:
                t = q[2]
                self.wait(act, "dve", "neg", k, t)
                ins = nc.scalar.activation(self.P[k % 2][:, t, t0 * TP:t1 * TP], self.ps(("score", k, t, j), TP, (t1 - t0) * TP), ACT.Exp,
                                           bias=self.nb[:, t:t + 1], scale=self.scale, accum_out=self.sum2[:, t, j:j + 1])
            ins.then_inc(done.sem, done.one())
        self.split_next(self.net.split_high)

    def gpsimd(self, pool):
        self.split_next(self.net.split_low)

    def vector(self, dve):
        self.begin(dve)
        nc, done = self.nc, self.net.dve
        for q in self.order["dve"]:
            k, t = q[1], q[2]
            r = self.rinv[:, t:t + 1]
            if q[0] == "max":
                t0, t1 = HALVES[q[3]]
                self.wait(dve, "pe", "score", *q[1:])
                ins = nc.vector.tensor_reduce(self.mx2[:, t, q[3]:q[3] + 1], self.ps(("score",) + q[1:], TP, (t1 - t0) * TP), AX.X, ALU.max)
            elif q[0] == "top":
                dve.wait_ge(done.sem, done.issued)
                ins = nc.vector.tensor_reduce(self.nb[:, t:t + 1], self.mx2[:, t, :], AX.X, ALU.max)
            elif q[0] == "neg":
                dve.wait_ge(done.sem, done.issued)
                ins = nc.vector.tensor_scalar(self.nb[:, t:t + 1], self.nb[:, t:t + 1], -self.scale, None, ALU.mult)
            elif q[0] == "turn":
                t0, t1 = HALVES[q[3]]
                self.wait(dve, "pe", *q)
                ins = nc.vector.tensor_copy(self.PT[:, t, t0 * TP:t1 * TP], self.ps(q, TP, (t1 - t0) * TP))
            elif q[0] == "out":
                self.wait(dve, "act", *q)
                ps, hi, lo = self.result(k, q[2])
                ins = nc.vector.tensor_tensor(lo, ps, hi, ALU.subtract)
            elif q[0] == "sum":
                self.wait(dve, "act", "exp", k, t, 1)
                ins = nc.vector.tensor_reduce(r, self.sum2[:, t, :], AX.X, ALU.add)
            elif q[0] == "rinv":
                dve.wait_ge(done.sem, done.issued)
                ins = nc.vector.reciprocal(r, r)
            else:
                dve.wait_ge(done.sem, done.issued)
                ins = nc.vector.tensor_scalar(self.P[k % 2][:, t], self.P[k % 2][:, t], r, None, ALU.mult)
            ins.then_inc(done.sem, done.one())


class Apply(Stage):

    def __init__(self, net, P, PT, h, rinv, out, add=None, by_tile=True, rows=(), after=None, evac="ad"):
        super().__init__(net, after)
        self.P, self.PT, self.h, self.rinv, self.out, self.add, self.by_tile, self.rows = P, PT, h, rinv, out, add, by_tile, rows
        self.loads = list(rows)
        c = h.shape[2]
        self.w = c if c <= 512 else HALF
        self.nw = c // self.w
        a, d = self.groups(2 * NT, evac)
        self.turned = [(net.act.sem, net.act.planned + a), (net.dve.sem, net.dve.planned + d)]
        net.dve.planned += d
        _, d2 = self.groups(NT * self.nw, "d")
        net.dve.planned -= d
        self.d_turn = d
        self.take(pe=2 * NT + NT * self.nw, act=a, dve=d + d2)

    def tensor(self, pe):
        self.begin(pe)
        nc, done = self.nc, self.net.pe
        for i in range(2 * NT):
            b, s, (t0, t1) = self.g[i][0], i // 2, HALVES[i % 2]
            if b >= BANKS:
                pe.wait_ge(*self.free(b))
            for t in range(t0, t1):
                mm = nc.tensor.transpose(self.net.ps[:TP, b % BANKS, (t - t0) * TP:(t - t0 + 1) * TP],
                                         self.P[:, t, s * TP:(s + 1) * TP], self.net.ident[:TP, :TP])
            mm.then_inc(done.sem, done.one())
        for sem, value in self.turned:
            pe.wait_ge(sem, value)
        for i in range(NT * self.nw):
            b, t, j = self.g[2 * NT + i][0], i // self.nw, i % self.nw
            if b >= BANKS:
                pe.wait_ge(*self.free(b))
            for s in range(NT):
                mm = nc.tensor.matmul(self.net.ps[:TP, b % BANKS, 0:self.w], self.PT[:, s, t * TP:(t + 1) * TP],
                                      self.h[:, s, j * self.w:(j + 1) * self.w], start=(s == 0), stop=(s == NT - 1))
            mm.then_inc(done.sem, done.one())

    def turn(self, eng, letter, ticks):
        self.begin(eng)
        for i in range(2 * NT):
            b, e = self.g[i]
            if e == letter:
                s, (t0, t1) = i // 2, HALVES[i % 2]
                eng.wait_ge(self.net.pe.sem, self.p0 + i + 1)
                evacuate(self.nc, letter, "copy", self.PT[:, s, t0 * TP:t1 * TP],
                         self.net.ps[:TP, b % BANKS, 0:(t1 - t0) * TP]).then_inc(ticks.sem, ticks.one())

    def scalar(self, act):
        self.turn(act, "a", self.net.act)

    def vector(self, dve):
        self.turn(dve, "d", self.net.dve)
        self.landed(dve)
        done = self.net.dve
        for i in range(NT * self.nw):
            b, t, j = self.g[2 * NT + i][0], i // self.nw, i % self.nw
            cs = slice(j * self.w, (j + 1) * self.w)
            ps, out, r = self.net.ps[:TP, b % BANKS, 0:self.w], self.out[:, t, cs], self.rinv[:, t:t + 1]
            dve.wait_ge(self.net.pe.sem, self.p0 + 2 * NT + i + 1)
            if self.add is None:
                evacuate(self.nc, "d", "scale", out, ps, gate=r).then_inc(done.sem, done.one())
            else:
                add = self.add[:, t, cs] if self.by_tile else self.add[:, cs]
                evacuate(self.nc, "d", "gate", out, ps, gate=r, add=add).then_inc(done.sem, done.one())


class HeadNorm(Stage):
    side = True

    def __init__(self, net, x, tmp, out, gamma, beta, eps, after=None):
        super().__init__(net, after)
        self.x, self.tmp, self.out, self.eps, self.loads = x, tmp, out, eps, [gamma, beta]
        self.mean, self.var = net.st[:TP, 270:330], net.st[:TP, 330:390]
        self.take(dve=9, act=2)

    def bc(self, small):
        return small.unsqueeze(2).to_broadcast([TP, 60, 64])

    def row(self, load):
        return load.dst[:TP, :, :].to_broadcast([TP, 60, 64])

    def vector(self, dve):
        self.begin(dve)
        nc, done, act = self.nc, self.net.dve, self.net.act
        nc.vector.tensor_reduce(self.mean, self.x, AX.X, ALU.add).then_inc(done.sem, done.one())
        dve.wait_ge(done.sem, done.issued)
        nc.vector.tensor_scalar(self.mean, self.mean, 1.0 / 64, None, ALU.mult).then_inc(done.sem, done.one())
        dve.wait_ge(done.sem, done.issued)
        nc.vector.tensor_tensor(self.x, self.x, self.bc(self.mean), ALU.subtract).then_inc(done.sem, done.one())
        dve.wait_ge(act.sem, self.a0 + 1)
        nc.vector.tensor_reduce(self.var, self.tmp, AX.X, ALU.add).then_inc(done.sem, done.one())
        dve.wait_ge(done.sem, done.issued)
        nc.vector.tensor_scalar(self.var, self.var, 1.0 / 64, self.eps, ALU.mult, ALU.add).then_inc(done.sem, done.one())
        dve.wait_ge(act.sem, self.a0 + 2)
        nc.vector.reciprocal(self.var, self.var).then_inc(done.sem, done.one())
        dve.wait_ge(done.sem, done.issued)
        nc.vector.tensor_tensor(self.x, self.x, self.bc(self.var), ALU.mult).then_inc(done.sem, done.one())
        self.landed(dve)
        dve.wait_ge(done.sem, done.issued)
        nc.vector.tensor_tensor(self.x, self.x, self.row(self.loads[0]), ALU.mult).then_inc(done.sem, done.one())
        dve.wait_ge(done.sem, done.issued)
        nc.vector.tensor_tensor(self.out, self.x, self.row(self.loads[1]), ALU.add).then_inc(done.sem, done.one())

    def scalar(self, act):
        self.begin(act)
        done, dve = self.net.act, self.net.dve
        act.wait_ge(dve.sem, self.d0 + 3)
        self.nc.scalar.activation(self.tmp, self.x, ACT.Square).then_inc(done.sem, done.one())
        act.wait_ge(dve.sem, self.d0 + 5)
        self.nc.scalar.activation(self.var, self.var, ACT.Sqrt).then_inc(done.sem, done.one())


class SetOnes(Stage):
    side = True

    def __init__(self, net, v, after=None):
        super().__init__(net, after)
        self.v = v
        self.take(pool=1)

    def gpsimd(self, pool):
        self.begin(pool)
        self.nc.gpsimd.memset(self.v[:, :, 64:65], 1.0).then_inc(self.net.pool.sem, self.net.pool.one())


class Square(Stage):

    def __init__(self, net, x, out, made=None, after=None):
        super().__init__(net, after)
        self.x, self.out, self.made = x, out, made
        self.take(act=x.shape[1])

    def scalar(self, act):
        self.begin(act)
        for c in range(self.x.shape[1]):
            for sem, value in self.made.chunk_done(c) if self.made else ():
                act.wait_ge(sem, value)
            self.nc.scalar.activation(self.out[:, c], self.x[:, c], ACT.Square).then_inc(self.net.act.sem, self.net.act.one())


class Elu1(Stage):
    side = True

    def __init__(self, net, x, tmp, after=None):
        super().__init__(net, after)
        self.x, self.tmp, self.c = x, tmp, x.shape[1]
        self.take(pool=self.c, act=self.c, dve=self.c)

    def gpsimd(self, pool):
        self.begin(pool)
        for c in range(self.c):
            self.nc.gpsimd.tensor_scalar(self.tmp[:, c], self.x[:, c], 0.0, None, ALU.min).then_inc(self.net.pool.sem, self.net.pool.one())

    def scalar(self, act):
        self.begin(act)
        for c in range(self.c):
            act.wait_ge(self.net.pool.sem, self.l0 + c + 1)
            self.nc.scalar.activation(self.tmp[:, c], self.tmp[:, c], ACT.Exp).then_inc(self.net.act.sem, self.net.act.one())

    def vector(self, dve):
        self.begin(dve)
        for c in range(self.c):
            dve.wait_ge(self.net.act.sem, self.a0 + c + 1)
            self.nc.vector.scalar_tensor_tensor(out=self.x[:, c], in0=self.x[:, c], scalar=0.0, in1=self.tmp[:, c],
                                                op0=ALU.max, op1=ALU.add).then_inc(self.net.dve.sem, self.net.dve.one())


class PhiTok(Stage):

    def __init__(self, net, xT, sqT, chunks, out, lnc, waits=(), after=None):
        super().__init__(net, after)
        self.xT, self.sqT, self.chunks, self.out, self.lnc, self.loads = xT, sqT, chunks, out, lnc, list(waits)
        self.groups(NT, "a")
        self.take(pe=NT, act=NT)

    def tensor(self, pe):
        self.begin(pe)
        self.landed(pe)
        for t in range(NT):
            b = self.g[t][0]
            if b >= BANKS:
                pe.wait_ge(*self.free(b))
            for j, terms in enumerate(self.chunks):
                for n, (c, w, norm) in enumerate(terms):
                    ps = self.net.ps[:TP, b % BANKS, j * 128:(j + 1) * 128]
                    self.nc.tensor.matmul(ps, self.xT[:, c, t * TP:(t + 1) * TP], w, start=(n == 0), stop=False)
                    mm = self.nc.tensor.matmul(ps, self.sqT[:, c, t * TP:(t + 1) * TP], norm, start=False, stop=(n == len(terms) - 1))
            mm.then_inc(self.net.pe.sem, self.net.pe.one())

    def scalar(self, act):
        self.begin(act)
        w = 128 * len(self.chunks)
        for t in range(NT):
            act.wait_ge(self.net.pe.sem, self.p0 + t + 1)
            self.nc.scalar.activation(self.out[:, t, 0:w], self.net.ps[:TP, self.g[t][0] % BANKS, 0:w], ACT.Exp,
                                      bias=self.lnc[:TP, :]).then_inc(self.net.act.sem, self.net.act.one())


class PhiFeat(Stage):

    def __init__(self, net, xT, sqT, chunks, out, lnc, waits=(), after=None):
        super().__init__(net, after)
        self.xT, self.sqT, self.chunks, self.out, self.lnc, self.loads = xT, sqT, chunks, out, lnc, list(waits)
        self.groups(2 * len(chunks), "a")
        self.take(pe=2 * len(chunks), act=2 * len(chunks))

    def tensor(self, pe):
        self.begin(pe)
        self.landed(pe)
        for i, (b, _) in enumerate(self.g):
            t0, t1 = HALVES[i % 2]
            terms = self.chunks[i // 2]
            if b >= BANKS:
                pe.wait_ge(*self.free(b))
            ps = self.net.ps[:, b % BANKS, 0:(t1 - t0) * TP]
            for n, (c, w, norm) in enumerate(terms):
                self.nc.tensor.matmul(ps, w, self.xT[:, c, t0 * TP:t1 * TP], start=(n == 0), stop=False)
                mm = self.nc.tensor.matmul(ps, norm, self.sqT[:, c, t0 * TP:t1 * TP], start=False, stop=(n == len(terms) - 1))
            mm.then_inc(self.net.pe.sem, self.net.pe.one())

    def scalar(self, act):
        self.begin(act)
        for i, (b, _) in enumerate(self.g):
            t0, t1 = HALVES[i % 2]
            act.wait_ge(self.net.pe.sem, self.p0 + i + 1)
            self.nc.scalar.activation(self.out[:, i // 2, t0 * TP:t1 * TP], self.net.ps[:, b % BANKS, 0:(t1 - t0) * TP], ACT.Exp,
                                      bias=self.lnc).then_inc(self.net.act.sem, self.net.act.one())


class KvSummary(Stage):

    def __init__(self, net, chunks, v, scale=1.0, clear=None, after=None):
        super().__init__(net, after)
        self.chunks, self.v, self.scale, self.clear = chunks, v, scale, clear
        base = net.dve.planned + (clear is not None)
        for phi, h0, nh, kv, rows in chunks:
            base += nh
            b = net.bank()
            net.freed[b] = (net.dve.sem, base)
            self.g.append((b, "d"))
        self.take(pe=len(chunks), dve=base - net.dve.planned)

    def tensor(self, pe):
        self.begin(pe)
        for (b, _), (phi, h0, nh, kv, rows) in zip(self.g, self.chunks):
            if b >= BANKS:
                pe.wait_ge(*self.free(b))
            for t in range(NT):
                mm = self.nc.tensor.matmul(self.net.ps[:, b % BANKS, 0:nh * 65], phi[:, t],
                                           self.v[:, t * 12 + h0:t * 12 + h0 + nh, :].rearrange("p h c -> p (h c)"),
                                           start=(t == 0), stop=(t == NT - 1))
            mm.then_inc(self.net.pe.sem, self.net.pe.one())

    def vector(self, dve):
        self.begin(dve)
        done = self.net.dve
        if self.clear is not None:
            self.nc.vector.memset(self.clear, 0.0).then_inc(done.sem, done.one())
            dve.wait_ge(done.sem, done.issued)
        for n, ((b, _), (phi, h0, nh, kv, rows)) in enumerate(zip(self.g, self.chunks)):
            dve.wait_ge(self.net.pe.sem, self.p0 + n + 1)
            for i in range(nh):
                r = slice(i * rows, (i + 1) * rows)
                self.nc.vector.tensor_scalar(kv[r, i * 65:(i + 1) * 65], self.net.ps[r, b % BANKS, i * 65:(i + 1) * 65],
                                             self.scale, None, ALU.mult).then_inc(done.sem, done.one())


class KvApply(Stage):

    def __init__(self, net, parts, y, eps, after=None):
        super().__init__(net, after)
        self.parts, self.y, self.eps = parts, y, eps
        self.per = 3 if eps is not None else 1
        n = NT * len(parts)
        for i in range(n):
            b = net.bank()
            net.freed[b] = (net.dve.sem, net.dve.planned + self.per * (i + 1))
            self.g.append((b, "d"))
        self.take(pe=n, dve=self.per * n)

    def tensor(self, pe):
        self.begin(pe)
        i = 0
        for part in self.parts:
            for t in range(NT):
                b, col = self.g[i][0], 0
                if b >= BANKS:
                    pe.wait_ge(*self.free(b))
                for h0, nh, terms in part:
                    for n, (phi, kv) in enumerate(terms):
                        mm = self.nc.tensor.matmul(self.net.ps[:TP, b % BANKS, col:col + nh * 65], phi[:, t * TP:(t + 1) * TP],
                                                   kv, start=(n == 0), stop=(n == len(terms) - 1))
                    col += nh * 65
                mm.then_inc(self.net.pe.sem, self.net.pe.one())
                i += 1

    def vector(self, dve):
        self.begin(dve)
        nc, done = self.nc, self.net.dve
        i = 0
        for part in self.parts:
            h0, nh = part[0][0], sum(q[1] for q in part)
            for t in range(NT):
                ps = self.net.ps[:TP, self.g[i][0] % BANKS, 0:nh * 65].rearrange("p (h c) -> p h c", h=nh)
                y = self.y[:, t, h0 * 64:(h0 + nh) * 64].rearrange("p (h c) -> p h c", h=nh)
                dve.wait_ge(self.net.pe.sem, self.p0 + i + 1)
                if self.eps is None:
                    nc.vector.tensor_copy(y, ps[:, :, 0:64]).then_inc(done.sem, done.one())
                else:
                    o = 270 + 12 * (i % 2)
                    den = self.net.st[:TP, o:o + nh]
                    if i > 1:
                        dve.wait_ge(done.sem, self.d0 + 3 * (i - 1))
                    nc.vector.tensor_scalar(den, ps[:, :, 64], self.eps, None, ALU.add).then_inc(done.sem, done.one())
                    dve.wait_ge(done.sem, done.issued)
                    nc.vector.reciprocal(den, den).then_inc(done.sem, done.one())
                    dve.wait_ge(done.sem, done.issued)
                    nc.vector.tensor_tensor(y, ps[:, :, 0:64], den.unsqueeze(2).to_broadcast([TP, nh, 64]), ALU.mult).then_inc(done.sem, done.one())
                i += 1


class L2Rows(Stage):

    def __init__(self, net, x, scratch, eps, after=None):
        super().__init__(net, after)
        self.x, self.scratch, self.eps = x, scratch, eps
        self.n = net.st[:TP, 270:275]
        self.take(dve=NT + 2 + NT, act=1)

    def vector(self, dve):
        self.begin(dve)
        nc, done = self.nc, self.net.dve
        for t in range(NT):
            nc.vector.tensor_tensor_reduce(out=self.scratch[:, t], in0=self.x[:, t], in1=self.x[:, t], scale=1.0, scalar=0.0,
                                           op0=ALU.mult, op1=ALU.add, accum_out=self.n[:, t:t + 1]).then_inc(done.sem, done.one())
        dve.wait_ge(self.net.act.sem, self.a0 + 1)
        nc.vector.tensor_scalar(self.n, self.n, self.eps, None, ALU.max).then_inc(done.sem, done.one())
        dve.wait_ge(done.sem, done.issued)
        nc.vector.reciprocal(self.n, self.n).then_inc(done.sem, done.one())
        dve.wait_ge(done.sem, done.issued)
        for t in range(NT):
            nc.vector.tensor_scalar(self.x[:, t], self.x[:, t], self.n[:, t:t + 1], None, ALU.mult).then_inc(done.sem, done.one())

    def scalar(self, act):
        self.begin(act)
        act.wait_ge(self.net.dve.sem, self.d0 + NT)
        self.nc.scalar.activation(self.n, self.n, ACT.Sqrt).then_inc(self.net.act.sem, self.net.act.one())


class PhiNorms(Stage):

    def __init__(self, net, phi, sq, rn, scale_col, eps, after=None):
        super().__init__(net, after)
        self.phi, self.sq, self.rn, self.scale_col, self.eps = phi, sq, rn, scale_col, eps
        self.loads = [phi]
        self.groups(1, "a")
        self.take(pe=1, act=1, dve=4)

    def tensor(self, pe):
        self.begin(pe)
        b = self.g[0][0]
        if b >= BANKS:
            pe.wait_ge(*self.free(b))
        pe.wait_ge(self.net.dve.sem, self.d0 + 1)
        for k in range(KC):
            mm = self.nc.tensor.matmul(self.net.ps[:TP, b % BANKS, 0:64], self.net.ones[:, 0:TP], self.sq[:, k, :], start=(k == 0), stop=(k == KC - 1))
        mm.then_inc(self.net.pe.sem, self.net.pe.one())

    def scalar(self, act):
        self.begin(act)
        act.wait_ge(self.net.pe.sem, self.p0 + 1)
        self.nc.scalar.activation(self.rn, self.net.ps[:TP, self.g[0][0] % BANKS, 0:64], ACT.Sqrt).then_inc(self.net.act.sem, self.net.act.one())

    def vector(self, dve):
        self.begin(dve)
        self.landed(dve)
        nc, done = self.nc, self.net.dve
        nc.vector.tensor_tensor(self.sq, self.phi.dst, self.phi.dst, ALU.mult).then_inc(done.sem, done.one())
        dve.wait_ge(self.net.act.sem, self.a0 + 1)
        nc.vector.tensor_scalar(self.rn, self.rn, self.eps, None, ALU.max).then_inc(done.sem, done.one())
        dve.wait_ge(done.sem, done.issued)
        nc.vector.reciprocal(self.rn, self.rn).then_inc(done.sem, done.one())
        dve.wait_ge(done.sem, done.issued)
        nc.vector.tensor_scalar(self.rn, self.rn, self.scale_col, None, ALU.mult).then_inc(done.sem, done.one())


class SoftmaxGroups(Stage):

    def __init__(self, net, x, out, after=None):
        super().__init__(net, after)
        self.x, self.out = x, out
        self.m, self.s = net.st[:TP, 275:280], net.st[:TP, 280:285]
        self.take(dve=5, act=1)

    def bc(self, small):
        return small.unsqueeze(2).to_broadcast(list(self.x.shape))

    def vector(self, dve):
        self.begin(dve)
        nc, done = self.nc, self.net.dve
        nc.vector.tensor_reduce(self.m, self.x, AX.X, ALU.max).then_inc(done.sem, done.one())
        dve.wait_ge(done.sem, done.issued)
        nc.vector.tensor_tensor(self.out, self.x, self.bc(self.m), ALU.subtract).then_inc(done.sem, done.one())
        dve.wait_ge(self.net.act.sem, self.a0 + 1)
        nc.vector.tensor_reduce(self.s, self.out, AX.X, ALU.add).then_inc(done.sem, done.one())
        dve.wait_ge(done.sem, done.issued)
        nc.vector.reciprocal(self.s, self.s).then_inc(done.sem, done.one())
        dve.wait_ge(done.sem, done.issued)
        nc.vector.tensor_tensor(self.out, self.out, self.bc(self.s), ALU.mult).then_inc(done.sem, done.one())

    def scalar(self, act):
        self.begin(act)
        act.wait_ge(self.net.dve.sem, self.d0 + 2)
        self.nc.scalar.activation(self.out, self.out, ACT.Exp).then_inc(self.net.act.sem, self.net.act.one())


class TokenSoftmax(Stage):

    def __init__(self, net, x, after=None):
        super().__init__(net, after)
        self.x = x
        self.m, self.s = net.st[:64, 285:286], net.st[:64, 286:287]
        self.take(dve=4, act=1)

    def vector(self, dve):
        self.begin(dve)
        nc, done = self.nc, self.net.dve
        nc.vector.tensor_reduce(self.m, self.x, AX.X, ALU.max).then_inc(done.sem, done.one())
        dve.wait_ge(done.sem, done.issued)
        nc.vector.tensor_scalar(self.m, self.m, -1.0, None, ALU.mult).then_inc(done.sem, done.one())
        dve.wait_ge(self.net.act.sem, self.a0 + 1)
        nc.vector.reciprocal(self.s, self.s).then_inc(done.sem, done.one())
        dve.wait_ge(done.sem, done.issued)
        nc.vector.tensor_scalar(self.x, self.x, self.s, None, ALU.mult).then_inc(done.sem, done.one())

    def scalar(self, act):
        self.begin(act)
        act.wait_ge(self.net.dve.sem, self.d0 + 2)
        self.nc.scalar.activation(self.x, self.x, ACT.Exp, bias=self.m, accum_out=self.s).then_inc(self.net.act.sem, self.net.act.one())


class ToTokens(Stage):

    def __init__(self, net, x, out, row=None, after=None):
        super().__init__(net, after)
        self.x, self.out, self.row = x, out, row
        self.groups(1, "d")
        self.loads = [row] if row else []
        self.take(pe=1, dve=1)

    def tensor(self, pe):
        self.begin(pe)
        b, w = self.g[0][0], self.x.shape[0]
        if b >= BANKS:
            pe.wait_ge(*self.free(b))
        for t in range(NT):
            mm = self.nc.tensor.transpose(self.net.ps[:TP, b % BANKS, t * w:(t + 1) * w], self.x[:, t * TP:(t + 1) * TP], self.net.ident[:w, :w])
        mm.then_inc(self.net.pe.sem, self.net.pe.one())

    def vector(self, dve):
        self.begin(dve)
        self.landed(dve)
        w = self.x.shape[0]
        dve.wait_ge(self.net.pe.sem, self.p0 + 1)
        ps = self.net.ps[:TP, self.g[0][0] % BANKS, 0:NT * w].rearrange("p (t n) -> p t n", t=NT)
        if self.row:
            ins = self.nc.vector.tensor_tensor(self.out, ps, self.row.dst[:TP, :, :].to_broadcast([TP, NT, w]), ALU.add)
        else:
            ins = self.nc.vector.tensor_copy(self.out, ps)
        ins.then_inc(self.net.dve.sem, self.net.dve.one())


class SlotInputs(Stage):

    def __init__(self, net, x, d, out, after=None):
        super().__init__(net, after)
        self.x, self.d, self.out = x, d, out
        self.groups(1, "d")
        self.take(pe=1, dve=1)

    def tensor(self, pe):
        self.begin(pe)
        b = self.g[0][0]
        if b >= BANKS:
            pe.wait_ge(*self.free(b))
        for c in range(KC):
            for t in range(NT):
                mm = self.nc.tensor.matmul(self.net.ps[:, b % BANKS, c * 64:(c + 1) * 64], self.x[:, t, c * 128:(c + 1) * 128], self.d[:, t, :],
                                           start=(t == 0), stop=(t == NT - 1))
        mm.then_inc(self.net.pe.sem, self.net.pe.one())

    def vector(self, dve):
        self.begin(dve)
        dve.wait_ge(self.net.pe.sem, self.p0 + 1)
        self.nc.vector.tensor_copy(self.out, self.net.ps[:, self.g[0][0] % BANKS, 0:KC * 64].rearrange("p (c n) -> p c n", c=KC)).then_inc(self.net.dve.sem, self.net.dve.one())


class SlotExperts(Stage):
    EXPERTS, DEPTH = 64, 4

    def __init__(self, net, xT, w, kp, masked, out, bias, func, after=None):
        super().__init__(net, after)
        self.xT, self.w, self.kp, self.masked, self.out, self.bias, self.func = xT, w, kp, masked, out, bias, func
        self.kc, self.n = w.shape[1] // kp, w.shape[2]
        self.loads = [bias]
        self.cols = self.n if self.n <= 512 else HALF
        self.nb = self.n // self.cols
        self.held = [s.take(0)[0] for s in net.wring]
        self.held_high = net.high_used[0]
        self.dsts = [net.wbuf[:kp, SLOT * j:SLOT * j + self.kc * self.n].rearrange("p (c n) -> p c n", c=self.kc) for j in range(self.DEPTH)]
        self.base = net.expert_loads
        net.expert_loads += 16 * (self.EXPERTS // self.DEPTH)
        self.before, self.used_at = self, (len(net.stages) - 0.5, 0)
        net.loads.append(self)
        E_, gelu = self.EXPERTS, func == "gelu"
        d_end = net.dve.planned + E_ + self.nb
        for _ in range(self.nb):
            b = net.bank()
            net.freed[b] = (net.dve.sem, d_end)
            self.g.append((b, "d"))
        self.take(pe=1 + E_ + 1, dve=E_ + self.nb, act=1 if gelu else 0)
        for s in net.wring:
            s.last = Load(None, None, None, 0, None)
            s.last.used, s.last.used_at = self.done, (len(net.stages) - 1, 1 << 20)
        net.barrier(self)

    def ps(self, q):
        return self.net.ps[:64, self.g[q][0] % BANKS, 0:self.cols]

    def clear(self, start):
        for q in range(self.nb):
            mm = self.nc.tensor.matmul(self.ps(q), self.net.zeros[:, 0:64], self.net.zeros[:, 0:self.cols], start=start, stop=not start, skip_group_check=True)
        return mm

    def sync(self, sp):
        for before in self.held:
            if before:
                for sem, value in before.used:
                    sp.wait_ge(sem, value)
        for sem, value in self.held_high:
            sp.wait_ge(sem, value)
        dsts, sems = self.dsts, self.net.esem
        for j in range(self.DEPTH):
            sp.dma_start(dsts[j], self.w[j].rearrange("(c p) n -> p c n", p=self.kp)).then_inc(sems[j], 16)
        with self.nc.sync.Fori(1, self.EXPERTS // self.DEPTH) as i:
            for j in range(self.DEPTH):
                sp.wait_ge(self.net.pe.sem, i * self.DEPTH + (self.p0 + 1 + j + 1 - self.DEPTH))
                sp.dma_start(dsts[j], self.w[bass.ds(i * self.DEPTH + j, 1)].rearrange("e (c p) n -> (e p) c n", p=self.kp)).then_inc(sems[j], 16)

    def tensor(self, pe):
        self.begin(pe)
        nc, done = self.nc, self.net.pe
        for b, _ in self.g:
            if b >= BANKS:
                pe.wait_ge(*self.free(b))
        self.clear(True).then_inc(done.sem, done.one())
        with nc.tensor.Fori(0, self.EXPERTS // self.DEPTH) as i:
            for j, w in enumerate(self.dsts):
                pe.wait_ge(self.net.dve.sem, i * self.DEPTH + (self.d0 + j + 1))
                pe.wait_ge(self.net.esem[j], i * 16 + (self.base + 16))
                for k in range(self.kc):
                    for q in range(self.nb):
                        mm = nc.tensor.matmul(self.ps(q), self.masked[j][:, k, :], w[:, k, q * self.cols:(q + 1) * self.cols],
                                              start=False, stop=False, skip_group_check=True)
                mm.then_inc(done.sem, 1)
        done.issued += self.EXPERTS
        self.clear(False).then_inc(done.sem, done.one())

    def vector(self, dve):
        self.begin(dve)
        nc, done = self.nc, self.net.dve
        with nc.vector.Fori(0, self.EXPERTS // self.DEPTH) as i:
            for j in range(self.DEPTH):
                dve.wait_ge(self.net.pe.sem, i * self.DEPTH + (self.p0 + 1 + j + 1 - self.DEPTH))
                nc.vector.scalar_tensor_tensor(out=self.masked[j], in0=self.net.iota64[:self.kp, :].unsqueeze(1).to_broadcast([self.kp, self.kc, 64]),
                                               scalar=self.net.iota64[:self.kp, bass.ds(i * self.DEPTH + j, 1)], in1=self.xT,
                                               op0=ALU.is_equal, op1=ALU.mult).then_inc(done.sem, 1)
        done.issued += self.EXPERTS
        self.landed(dve)
        dve.wait_ge(self.net.pe.sem, self.p0 + self.EXPERTS + 2)
        for q in range(self.nb):
            cs = slice(q * self.cols, (q + 1) * self.cols)
            nc.vector.tensor_tensor(self.out[:, cs], self.ps(q), self.bias.dst[:64, 0, cs], ALU.add).then_inc(done.sem, done.one())

    def scalar(self, act):
        if self.func == "gelu":
            self.begin(act)
            act.wait_ge(self.net.dve.sem, self.d0 + self.EXPERTS + self.nb)
            self.nc.scalar.activation(self.out, self.out, ACT.Gelu).then_inc(self.net.act.sem, self.net.act.one())
        self.split_next(self.net.split_high)

    def gpsimd(self, pool):
        self.split_next(self.net.split_low)


class SlotHidden(Stage):

    def __init__(self, net, x, out, after=None):
        super().__init__(net, after)
        self.x, self.out = x, out
        self.groups(1, "d")
        self.take(pe=1, dve=1)

    def tensor(self, pe):
        self.begin(pe)
        b = self.g[0][0]
        if b >= BANKS:
            pe.wait_ge(*self.free(b))
        for c in range(2):
            mm = self.nc.tensor.transpose(self.net.ps[:96, b % BANKS, c * 64:(c + 1) * 64], self.x[:, c * 96:(c + 1) * 96], self.net.ident[:64, :64])
        mm.then_inc(self.net.pe.sem, self.net.pe.one())

    def vector(self, dve):
        self.begin(dve)
        dve.wait_ge(self.net.pe.sem, self.p0 + 1)
        self.nc.vector.tensor_copy(self.out, self.net.ps[:96, self.g[0][0] % BANKS, 0:128].rearrange("p (c n) -> p c n", c=2)).then_inc(self.net.dve.sem, self.net.dve.one())


class TopTwo(Stage):
    ABSENT = 3.0e38

    def __init__(self, net, logits, gates, norm, sel, first=None, after=None):
        super().__init__(net, after)
        self.x, self.gates, self.norm, self.sel, self.first = logits, gates, norm, sel, first
        s = lambda o, w: net.st[:TP, o:o + NT * w].rearrange("p (t w) -> p t w", t=NT)
        self.top, self.want, self.rep, self.sum = s(310, 8), s(350, 8), s(390, 8), net.st[:TP, 430:435]
        self.n_first = 2 + NT if first is not None else 0
        self.take(dve=NT + 2 + NT + 1 + self.n_first + 1 + 1 + 3, act=1)

    def bc(self, small):
        return small.to_broadcast([TP, NT, 8])

    def vector(self, dve):
        self.begin(dve)
        nc, done = self.nc, self.net.dve
        nc.vector.memset(self.want, self.ABSENT).then_inc(done.sem, done.one())
        for t in range(NT):
            nc.vector.max(self.top[:, t, :], self.x[:, t, :]).then_inc(done.sem, done.one())
        dve.wait_ge(done.sem, done.issued)
        if self.first is not None:
            nc.vector.tensor_copy(self.want[:, :, 0:1], self.top[:, :, 0:1]).then_inc(done.sem, done.one())
            dve.wait_ge(done.sem, done.issued)
            for t in range(NT):
                nc.vector.match_replace(self.first[:, t, :], self.want[:, t, :], self.x[:, t, :], -self.ABSENT).then_inc(done.sem, done.one())
            dve.wait_ge(done.sem, done.issued)
            nc.vector.tensor_tensor(self.first, self.first, self.x, ALU.not_equal).then_inc(done.sem, done.one())
            dve.wait_ge(done.sem, done.issued)
        nc.vector.tensor_copy(self.want[:, :, 0:2], self.top[:, :, 0:2]).then_inc(done.sem, done.one())
        dve.wait_ge(done.sem, done.issued)
        for t in range(NT):
            nc.vector.match_replace(self.rep[:, t, :], self.want[:, t, :], self.x[:, t, :], -self.ABSENT).then_inc(done.sem, done.one())
        nc.vector.tensor_tensor(self.gates, self.x, self.bc(self.top[:, :, 0:1]), ALU.subtract).then_inc(done.sem, done.one())
        dve.wait_ge(done.sem, done.issued)
        nc.vector.tensor_tensor(self.sel, self.rep, self.x, ALU.not_equal).then_inc(done.sem, done.one())
        dve.wait_ge(done.sem, done.issued)
        dve.wait_ge(self.net.act.sem, self.a0 + 1)
        if self.norm == "all":
            nc.vector.tensor_reduce(self.sum, self.gates, AX.X, ALU.add).then_inc(done.sem, done.one())
            dve.wait_ge(done.sem, done.issued)
            nc.vector.tensor_tensor(self.gates, self.gates, self.sel, ALU.mult).then_inc(done.sem, done.one())
        else:
            nc.vector.tensor_tensor(self.gates, self.gates, self.sel, ALU.mult).then_inc(done.sem, done.one())
            dve.wait_ge(done.sem, done.issued)
            nc.vector.tensor_reduce(self.sum, self.gates, AX.X, ALU.add).then_inc(done.sem, done.one())
        dve.wait_ge(done.sem, done.issued)
        nc.vector.reciprocal(self.sum, self.sum).then_inc(done.sem, done.one())
        dve.wait_ge(done.sem, done.issued)
        nc.vector.tensor_tensor(self.gates, self.gates, self.bc(self.sum.unsqueeze(2)), ALU.mult).then_inc(done.sem, done.one())

    def scalar(self, act):
        self.begin(act)
        act.wait_ge(self.net.dve.sem, self.d0 + 1 + NT + self.n_first + 1 + NT + 1)
        self.nc.scalar.activation(self.gates, self.gates, ACT.Exp).then_inc(self.net.act.sem, self.net.act.one())


class Capacity(Stage):

    def __init__(self, net, gates, sel, first, tri, capacity, after=None):
        super().__init__(net, after)
        self.gates, self.sel, self.first, self.tri, self.capacity = gates, sel, first, tri, capacity
        self.hot = net.st[:TP, 350:430].rearrange("p (t k e) -> p t k e", t=NT, k=2)
        self.loads = [tri]
        self.groups(1, "d")
        net.freed[self.g[0][0]] = (net.dve.sem, net.dve.planned + 4)
        self.take(pe=1, dve=6)

    def vector(self, dve):
        self.begin(dve)
        nc, done, ps = self.nc, self.net.dve, self.net.ps
        nc.vector.tensor_copy(self.hot[:, :, 0, :], self.first).then_inc(done.sem, done.one())
        nc.vector.tensor_tensor(self.hot[:, :, 1, :], self.sel, self.first, ALU.subtract).then_inc(done.sem, done.one())
        dve.wait_ge(done.sem, done.issued)
        dve.wait_ge(self.net.pe.sem, self.p0 + 1)
        count = ps[:TP, self.g[0][0] % BANKS, 0:NT * 16].rearrange("p (t k e) -> p t k e", t=NT, k=2)
        for k in range(2):
            nc.vector.scalar_tensor_tensor(out=self.hot[:, :, k, :], in0=count[:, :, k, :], scalar=float(self.capacity), in1=self.hot[:, :, k, :],
                                           op0=ALU.is_le, op1=ALU.mult).then_inc(done.sem, done.one())
        dve.wait_ge(done.sem, done.issued)
        nc.vector.tensor_tensor(self.sel, self.hot[:, :, 0, :], self.hot[:, :, 1, :], ALU.add).then_inc(done.sem, done.one())
        dve.wait_ge(done.sem, done.issued)
        nc.vector.tensor_tensor(self.gates, self.gates, self.sel, ALU.mult).then_inc(done.sem, done.one())

    def tensor(self, pe):
        self.begin(pe)
        self.landed(pe)
        b = self.g[0][0]
        if b >= BANKS:
            pe.wait_ge(*self.free(b))
        pe.wait_ge(self.net.dve.sem, self.d0 + 2)
        for t in range(NT):
            for s in range(t + 1):
                lhs = self.tri.dst[:TP, 0, 0:TP] if s == t else self.net.ones[:TP, 0:TP]
                mm = self.nc.tensor.matmul(self.net.ps[:TP, b % BANKS, t * 16:(t + 1) * 16], lhs, self.hot[:, s].rearrange("p k e -> p (k e)"),
                                           start=(s == 0), stop=(s == t))
        mm.then_inc(self.net.pe.sem, self.net.pe.one())


class GatedRows(Stage):

    def __init__(self, net, x, gate, row, after=None):
        super().__init__(net, after)
        self.x, self.gate, self.row, self.loads = x, gate, row, [row]
        self.take(dve=NT)

    def vector(self, dve):
        self.begin(dve)
        self.landed(dve)
        for t in range(NT):
            self.nc.vector.scalar_tensor_tensor(out=self.x[:, t], in0=self.row.dst[:TP, 0], scalar=self.gate[:, t:t + 1], in1=self.x[:, t],
                                                op0=ALU.mult, op1=ALU.add).then_inc(self.net.dve.sem, self.net.dve.one())


class Multiply(Stage):

    def __init__(self, net, x, y, after=None):
        super().__init__(net, after)
        self.x, self.y = x, y
        self.take(dve=1)

    def vector(self, dve):
        self.begin(dve)
        self.nc.vector.tensor_tensor(self.x, self.x, self.y, ALU.mult).then_inc(self.net.dve.sem, self.net.dve.one())


class Clear(Stage):

    def __init__(self, net, x, value=0.0, after=None):
        super().__init__(net, after)
        self.x, self.value = x, value
        self.take(dve=1)

    def vector(self, dve):
        self.begin(dve)
        self.nc.vector.memset(self.x, self.value).then_inc(self.net.dve.sem, self.net.dve.one())


class Degrees(Stage):
    side = True

    def __init__(self, net, rdeg, after=None):
        super().__init__(net, after)
        self.rdeg = rdeg
        self.take(dve=2, act=1)

    def vector(self, dve):
        self.begin(dve)
        done = self.net.dve
        self.nc.vector.tensor_reduce(self.rdeg, self.net.counts[:TP], AX.X, ALU.add).then_inc(done.sem, done.one())
        dve.wait_ge(self.net.act.sem, self.a0 + 1)
        self.nc.vector.reciprocal(self.rdeg, self.rdeg).then_inc(done.sem, done.one())

    def scalar(self, act):
        self.begin(act)
        act.wait_ge(self.net.dve.sem, self.d0 + 1)
        self.nc.scalar.activation(self.rdeg, self.rdeg, ACT.Sqrt).then_inc(self.net.act.sem, self.net.act.one())


def weight_units(net, w, rows=None, cols=None):
    r0, r1 = rows or (0, w.shape[0])
    c0, c1 = cols or (0, w.shape[1])
    return [net.weights(w[r0:r1, c:min(c + UNIT, c1)]) for c in range(c0, c1, UNIT)]


def linear_T(net, xT, w, out, bias=None, kind="copy", rows=None, cols=None, evac="ad", after=None):
    parts, m = [], 0
    for load in weight_units(net, w, rows, cols):
        for c0 in range(0, load.dst.shape[2], 128):
            parts.append((load, c0, 128, out.chunk(m) if isinstance(out, Pair) else out[:, m], bias[:, m:m + 1] if bias is not None else None, kind))
            m += 1
    return LinearT(net, xT, parts, evac, after)


def linear(net, xT, w, out, kind="copy", add=None, rows=None, cols=None, bias=None, gate=None, evac="ad", kp=128, after=None, stats=None):
    f, units = 0, []
    r0, r1 = rows or (0, w.shape[0])
    c0, c1 = cols or (0, w.shape[1])
    step = min(SLOT // ((r1 - r0) // kp), c1 - c0)
    n = step if step <= 512 else HALF
    for c in range(c0, c1, n):
        if (c - c0) % step == 0:
            load = net.weights(w[r0:r1, c:c + step], kp)
        u = dict(load=load, c0=(c - c0) % step, w=n, out=out[:, :, f:f + n], kind=kind)
        if kind == "row":
            u.update(kind="add", add=bias.dst[:TP, 0, f:f + n], by_tile=False)
        elif kind in ("add", "gate"):
            u["add"] = add[:, :, f:f + n]
        if gate is not None:
            u["gate"] = gate
        units.append(u)
        f += n
    return Linear(net, xT, units, evac if kind in ("copy", "relu") else "d", rows=[bias] if bias else (), after=after, stats=stats)


def linear_heads(net, xT, w, cols, v4, bias=None, evac="ad"):
    units = []
    for j, c in enumerate(range(cols[0], cols[1], UNIT)):
        u = dict(load=net.weights(w[:, c:c + UNIT]), w=UNIT, out=v4[:, :, 4 * j:4 * j + 4, 0:64], kind="copy")
        if bias:
            u.update(kind="add", by_tile=False, add=bias.dst[:TP, 0, j * UNIT:(j + 1) * UNIT].rearrange("p (h c) -> p h c", h=4))
        units.append(u)
    Linear(net, xT, units, "d" if bias else evac, rows=[bias] if bias else ())


def expert_layers(net, xT, n, hidden, gates, out, w2, kp, start):
    gated = net.now()
    made, used = [], []
    for e in range(n + 1):
        if e < n:
            made.append(hidden(e, start if e < 2 else used[e - 2]))
        if e > 0:
            stage, hT = made[e - 1]
            units = []
            load = net.weights(w2[e - 1], kp)
            for j in range(2):
                cs = slice(j * HALF, (j + 1) * HALF)
                units.append(dict(load=load, c0=j * HALF, w=HALF, out=out[:, :, cs], kind="gate", gate=gates[:, :, e - 1], add=out[:, :, cs]))
            product = Linear(net, hT, units, "d", after=gated + stage.ends(), stats=out if e == n else None)
            used.append(product.ends()[:1])


def router(net, xT, w, logits, row=None):
    n = w.shape[1]
    out = net.asb[:n, :]
    LinearT(net, xT, [(net.weights(w), 0, n, out, None, "copy")])
    ToTokens(net, out, logits, row)


def gat_coefs(net, h_parts, c, a_src, a_dst, coef, scratch, after=None):
    head, last = 0, None
    for h, nh in h_parts:
        cs = slice(head * c, (head + nh) * c)
        last = GatCoefs(net, h, nh, c, head, net.row(a_src[:, cs]), net.row(a_dst[:, cs]), coef, scratch, after)
        head += nh
    return last


def gat_heads(net, h_parts, c, coef, P, PT, eps, outs, bias_rows=None, add=None, coefs=()):
    def make(with_rows):
        heads, rows, head = [], [], 0
        for (h, nh), out in zip(h_parts, outs):
            row = net.row(bias_rows[:, head * c:(head + nh) * c]) if with_rows and bias_rows is not None else None
            rows += [row] if row else []
            for i in range(nh):
                cs = slice(i * c, (i + 1) * c)
                heads.append((coef[:, 0, head], coef[:, 1, head], h[:, :, cs], out[:, :, cs], row.dst[:TP, 0, cs] if row else add, not row))
                head += 1
        return heads, rows

    buffers = [net.feat(b, NT, TP) for b in (P, net.P1)]
    first = GatHeads(net, make(False)[0], buffers, net.feat(PT, NT, TP), eps, (), net.now() + list(coefs), -1, FIRST)

    def rest(after=()):
        heads, rows = make(True)
        return GatHeads(net, heads, buffers, net.feat(PT, NT, TP), eps, rows, net.now() + first.ends() + list(after), 0, first)

    return rest


def network(net):
    ins, G, now = net.ins, net.G, net.now
    tok, feat = net.tok, net.feat
    R = tok(net.R)
    pair = lambda hi, lo, c=KC: Pair(feat(hi, c), feat(lo, c))
    small = lambda b, c, p: Pair(feat(b, c, p), feat(b[:, c * N:2 * c * N], c, p))
    net.const(net.ident[:, :], ins["ident"])
    net.const(net.lnc[:, :], ins["lnc"])
    net.const(net.slot_scale[:, :], ins["L0_ffn_scale"].to_broadcast([128, 1]))
    net.const(net.iota64[:, :], ins["iota"][:, 0:64].to_broadcast([128, 64]))
    net.const(R, ins["x"].rearrange("(t p) d -> p t d", p=TP))
    col = {n: net.col(n) for n in ("b_ah_c", "kqv_b_c", "qkv_b_c", "fc1_b_c", "in_b_c")}
    col.update({n: net.col(n, 96) for n in ("mlp_b1_c", "exp_b1_c")})
    heads = lambda b: b[:TP, 0:NT * D].rearrange("p (t c) -> p t c", c=64)
    heads65 = lambda b: b[:TP, 0:NT * 12 * 65].rearrange("p (t c) -> p t c", c=65)
    by_head = lambda v: v.rearrange("p (t h) c -> p t h c", t=NT)
    coef = net.st[:TP, 100:180].rearrange("p (s h t) -> p s h t", s=2, h=8)
    Clear(net, net.ones[:, :], 1.0)
    Clear(net, net.zeros[:, :], 0.0)
    EdgeCounts(net)
    start = now()
    XT = pair(net.XT, G[4])
    norm_T(net, R, tok(G[0]), XT, 1e-5)
    loops = SelfLoops(net, ALU.add, start)
    bias_out = AddRow(net, R, net.row(ins["L0_mix_b_out"]))
    w = ins["L0_mix_w_mapT"]
    v = heads65(G[2])
    linear(net, XT, w, tok(G[1]), cols=(D, 2 * D), evac="a")
    head_norm = HeadNorm(net, heads(G[1]), heads(G[2]), heads(G[1]), net.row(ins["L0_mix_g_k"]), net.row(ins["L0_mix_b_k"]), 1e-5)
    linear(net, XT, w, tok(G[3]), cols=(2 * D, 3 * D), evac="a")
    made = now()
    linear_T(net, XT, ins["L0_gnn_W_ah"], feat(G[5]), bias=col["b_ah_c"], kind="relu", evac="a")
    head_norm = HeadNorm(net, heads(G[3]), v[:, :, 0:64], v[:, :, 0:64], net.row(ins["L0_mix_g_v"]), net.row(ins["L0_mix_b_v"]), 1e-5,
                         made + head_norm.ends())
    ones = SetOnes(net, v, now() + head_norm.ends())
    linear_T(net, XT, w, feat(G[0]), cols=(0, D), evac="a")
    x1 = Split(net, feat(G[5]), feat(G[4]))
    kv = net.kv[:, 0:780].rearrange("p (c w) -> p c w", c=6)
    KvSummary(net, [(tok(G[1])[:, :, j * 128:(j + 1) * 128], 2 * j, 2, kv[:, j], 64) for j in range(6)], v, 1.0 / N, clear=net.kv[:, 0:780],
              after=now() + head_norm.ends() + ones.ends())
    KvApply(net, pairs_of(feat(G[0]), kv), tok(G[3]), None)
    ToFeatures(net, tok(G[3]), pair(G[2], G[1]))
    linear(net, pair(G[2], G[1]), ins["L0_mix_w_outT"], R, "add", add=R, after=now() + bias_out.ends())
    x1T = pair(G[4], G[5])
    hs = [tok(net.XT), tok(G[0]), tok(G[1])]
    coefs3, marks = [net.st[:TP, o:o + 40].rearrange("p (s h t) -> p s h t", s=2, h=4) for o in (100, 140, 600)], []
    for i in range(3):
        linear(net, x1T, ins[f"L0_gnn_W{i}"], hs[i], evac="a", after=now() + x1.ends())
        if i == 1:
            rest = gat_heads(net, [(hs[0], 4)], 192, coefs3[0], G[2], G[3], 1e-16, [tok(G[4])], ins["L0_gnn_b0"], coefs=marks[0].ends() + loops.ends())
        marks.append(gat_coefs(net, [(hs[i], 4)], 192, ins[f"L0_gnn_a_src{i}"], ins[f"L0_gnn_a_dst{i}"], coefs3[i], G[3],
                               now() + (marks[-1].ends() if marks else [])))
    Clear(net, tok(G[5]))
    bias_out = AddRow(net, tok(G[5]), net.row(ins["L0_gnn_b_out"]))
    for i in range(3):
        rest(marks[-1].ends())
        outT = pair((net.XT, G[0], G[1])[i], G[3])
        ToFeatures(net, tok(G[4]), outT, "relu")
        if i < 2:
            rest = gat_heads(net, [(hs[i + 1], 4)], 192, coefs3[i + 1], G[2], G[3], 1e-16, [tok(G[4])], ins[f"L0_gnn_b{i + 1}"], coefs=marks[i + 1].ends())
        linear(net, outT, ins["L0_gnn_W_out"], tok(G[5]), "add", add=tok(G[5]), rows=(i * D, (i + 1) * D), after=now() + bias_out.ends())
    ReluAdd(net, R, tok(G[5]))
    LayerNorm(net, R, tok(G[0]), 1e-5)
    L2Rows(net, tok(G[0]), tok(G[1]), 1e-12)
    XT = feat(net.XT)
    ToFeatures(net, tok(G[0]), XT)
    phi = net.weights(ins["L0_ffn_phi"])
    c64 = lambda b, p=TP, c=NT: b[:p, 0:c * 64].rearrange("p (t n) -> p t n", t=c)
    rn = G[2][:TP, 0:64]
    PhiNorms(net, phi, c64(G[1], 128, KC), rn, net.slot_scale[:TP, :], 1e-12)
    Linear(net, XT, [dict(load=phi, w=64, out=c64(G[3]), kind="mul", add=rn, by_tile=False)], "d")
    ToFeatures(net, c64(G[3]), feat(G[4], 1, 64))
    TokenSoftmax(net, G[4][:64, 0:N])
    ToTokens(net, G[4][:64, 0:N], c64(G[5]))
    xsT = c64(G[1], 128, KC)
    SlotInputs(net, tok(G[0]), c64(G[5]), xsT)
    SoftmaxGroups(net, c64(G[3]), c64(G[3]))
    ToFeatures(net, c64(G[3]), feat(G[4], 1, 64))
    hid = G[5][:64, 0:192]
    masked = [G[2][:, j * HALF:(j + 1) * HALF].rearrange("p (c n) -> p c n", c=KC) for j in range(4)]
    SlotExperts(net, xsT, ins["L0_ffn_w1"], 128, masked, hid, net.rows(ins["L0_ffn_b1"]), "gelu")
    hidT = c64(G[3], 96, 2)
    SlotHidden(net, hid, hidT)
    masked = [G[2][:96, j * 128:(j + 1) * 128].rearrange("p (c n) -> p c n", c=2) for j in range(4)]
    ys = G[0][:64, 0:D]
    SlotExperts(net, hidT, ins["L0_ffn_w2"], 96, masked, ys, net.rows(ins["L0_ffn_b2"]), "copy")
    halves2 = [(Load(None, ys[:, cs].unsqueeze(1), net.pe.sem, 0, None), R[:, :, cs]) for cs in (slice(0, HALF), slice(HALF, D))]
    Linear(net, feat(G[4], 1, 64), [dict(load=held, w=HALF, out=out, kind="add", add=out) for held, out in halves2], "d", stats=R)

    clear = Clear(net, net.fw)
    fw = net.fw.rearrange("p (c m) -> p c m", c=6)
    fn = net.fn[:, 0:256].rearrange("p (i m) -> p i m", i=2)
    fws = [net.into(net.fn[:, 0:256], ins["norms1"], now())]
    for i in range(2):
        for s in range(2):
            dst = net.fw[64 * s:64 * s + 64, :].rearrange("p (j i m) -> p j i m", j=3, i=2)[:, :, i, 64 * i + 32 * s:64 * i + 32 * s + 32]
            fws.append(net.into(dst, ins["L1_mix_wT"].rearrange("(j i s) d m -> i s d j m", i=2, s=2)[i, s], now()))
    XT = pair(net.XT, G[3])
    norm_T(net, R, tok(G[0]), XT, 1e-5, ready=True)
    bias_out = AddRow(net, R, net.row(ins["L1_mix_proj_b"]))
    bias_out2 = AddRow(net, R, net.row(ins["L1_gnn_b"]), now() + bias_out.ends())
    ones = SetOnes(net, heads65(G[4]), now())
    rdeg = net.st[:TP, 180:185]
    degrees = Degrees(net, rdeg)
    chunks = [[(2 * j + i, fw[:, 2 * j + i], fn[:, i]) for i in range(2)] for j in range(3)]
    w = ins["L1_mix_kqv_wT"]
    start = now()
    made = linear_T(net, XT, w, feat(G[0]), bias=col["kqv_b_c"][:, 0:6], cols=(0, D))
    square = Square(net, feat(G[0]), feat(G[1]), made, start)
    made = linear_T(net, XT, w, feat(G[5]), bias=col["kqv_b_c"][:, 6:12], cols=(D, 2 * D))
    phik = G[2][:TP, 0:NT * HALF].rearrange("p (t m) -> p t m", t=NT)
    phi = PhiTok(net, feat(G[0]), feat(G[1]), chunks, phik, net.lnc[:, 0:1], fws)
    v = heads65(G[4])
    linear_heads(net, XT, w, (2 * D, 3 * D), by_head(v), net.row(ins["L1_mix_kqv_b_v"]))
    square = Square(net, feat(G[5]), feat(G[0]), made, phi.ends())
    phiq = feat(G[2][:, NT * HALF + 30:], 3)
    PhiFeat(net, feat(G[5]), feat(G[0]), chunks, phiq, net.lnc[:, 0:1])
    kv = net.kv[:, 0:780].rearrange("p (c w) -> p c w", c=3)
    KvSummary(net, [(phik[:, :, j * 128:(j + 1) * 128], 4 * j, 4, kv[:, j], 32) for j in range(3)], v, 1.0, clear=net.kv[:, 0:780])
    KvApply(net, [[(4 * j, 4, ((phiq[:, j], kv[:, j]),))] for j in range(3)], tok(G[5]), 1e-8)
    units = [dict(load=load, w=UNIT, out=tok(G[1])[:, :, j * UNIT:(j + 1) * UNIT], kind="scale", gate=rdeg) for j, load in enumerate(weight_units(net, ins["L1_gnn_W"]))]
    Linear(net, XT, units, "d", after=now() + degrees.ends())
    Apply(net, net.counts[:TP], feat(G[3], NT, TP), tok(G[1]), rdeg, R, add=R, after=now() + bias_out2.ends())
    ToFeatures(net, tok(G[5]), pair(G[0], G[2]))
    linear(net, pair(G[0], G[2]), ins["L1_mix_proj_wT"], R, "add", add=R, stats=R)
    gates, logits = (net.st[:TP, o:o + 40].rearrange("p (t e) -> p t e", t=NT) for o in (230, 520))
    sel, first = (net.st[:TP, o:o + 40].rearrange("p (t e) -> p t e", t=NT) for o in (440, 480))
    XT = pair(net.XT, G[5])
    norm_T(net, R, tok(G[0]), XT, 1e-5, ready=True)
    start = now()
    router(net, XT, ins["L1_ffn_router_wT"], logits)
    TopTwo(net, logits, gates, "all", sel)

    def hidden1(e, after):
        hT = small(G[e % 2], 2, 96)
        load = net.weights(ins["L1_ffn_w1"][e])
        return LinearT(net, XT, [(load, 96 * k, 96, hT.chunk(k), None, "tanh_gelu") for k in range(2)], "a", after), hT

    expert_layers(net, XT, 8, hidden1, gates, R, ins["L1_ffn_w2"], 96, start)

    loops = SelfLoops(net, ALU.subtract)
    XT = pair(net.XT, G[3])
    norm_T(net, R, tok(G[5]), XT, 1e-5, ready=True)
    bias2 = AddRow(net, R, net.row(ins["L2_gnn_b2"]))
    bias2 = AddRow(net, R, net.row(ins["L2_mix_fc2_b"]), now() + bias2.ends())
    w = ins["L2_gnn_W1T"]
    hA, hB = tok(G[0]), tok(G[1], 256)
    linear(net, XT, w, hA, cols=(0, D), evac="a")
    marks = gat_coefs(net, [(hA, 6)], 128, ins["L2_gnn_att_src1"], ins["L2_gnn_att_dst1"], coef, G[2])
    linear(net, XT, w, hB, cols=(D, 1024), evac="a")
    marks = gat_coefs(net, [(hB, 2)], 128, ins["L2_gnn_att_src1"][:, D:], ins["L2_gnn_att_dst1"][:, D:], coef[:, :, 6:8], G[2], now() + marks.ends())
    outB = G[1][:TP, 1280:2560].rearrange("p (t w) -> p t w", t=NT)
    gat_heads(net, [(hA, 6), (hB, 2)], 128, coef, G[2], G[3], 1e-16, [tok(G[4]), outB], ins["L2_gnn_b1"], coefs=marks.ends())()
    outT = pair(G[0], G[3]), small(G[2], 2, 128)
    ToFeatures(net, tok(G[4]), outT[0], "relu")
    ToFeatures(net, outB, outT[1], "relu")
    linear(net, outT[0], ins["L2_gnn_W2T"], tok(G[4]), rows=(0, D))
    linear(net, outT[1], ins["L2_gnn_W2T"], tok(G[4]), "add", add=tok(G[4]), rows=(D, 1024))
    XT = pair(net.XT, G[1])
    norm_T(net, tok(G[5]), tok(G[0]), XT, 1e-8, net.row(ins["L2_mix_ln1_w"]), net.row(ins["L2_mix_ln1_b"]))
    marks = gat_coefs(net, [(tok(G[4]), 1)], D, ins["L2_gnn_att_src2"], ins["L2_gnn_att_dst2"], coef, G[2])
    rest = gat_heads(net, [(tok(G[4]), 1)], D, coef, G[2], G[3], 1e-16, [R], add=R, coefs=marks.ends())
    bias_p = AddRow(net, tok(G[5]), net.row(ins["L2_mix_proj_b"]))
    w = ins["L2_mix_qkv_w"]
    linear_T(net, XT, w, feat(G[0]), bias=col["qkv_b_c"], cols=(0, D))
    rest(bias2.ends())
    loops = SelfLoops(net, ALU.add)
    elu = Elu1(net, feat(G[0]), feat(G[4]))
    linear(net, XT, w, tok(G[2]), "row", bias=net.row(ins["L2_mix_qkv_b"][:, D:2 * D]), cols=(D, 2 * D))
    v = heads65(G[3])
    ones = SetOnes(net, v, now())
    elu = Elu1(net, tok(G[2]), tok(G[4]), now() + elu.ends())
    linear_heads(net, XT, w, (2 * D, 3 * D), by_head(v), net.row(ins["L2_mix_qkv_b"][:, 2 * D:3 * D]))
    kv = net.kv[:, 0:780].rearrange("p (c w) -> p c w", c=6)
    KvSummary(net, [(tok(G[2])[:, :, j * 128:(j + 1) * 128], 2 * j, 2, kv[:, j], 64) for j in range(6)], v, 1.0, clear=net.kv[:, 0:780],
              after=now() + elu.ends() + ones.ends())
    KvApply(net, pairs_of(feat(G[0]), kv), tok(G[1]), 0.0)
    ToFeatures(net, tok(G[1]), pair(G[0], G[2]))
    linear(net, pair(G[0], G[2]), ins["L2_mix_proj_w"], tok(G[5]), "add", add=tok(G[5]), after=now() + bias_p.ends(), stats=tok(G[5]))
    XT = pair(net.XT, G[4])
    norm_T(net, tok(G[5]), tok(G[0]), XT, 1e-8, net.row(ins["L2_mix_ln2_w"]), net.row(ins["L2_mix_ln2_b"]), ready=True)
    added = Add(net, R, R, tok(G[5]))
    start = now()
    made, used = [], []
    for q in range(5):
        if q < 4:
            made.append(linear_T(net, XT, ins["L2_mix_fc1_w"], pair(G[q % 2], G[2 + q % 2]), bias=col["fc1_b_c"][:, 6 * q:6 * q + 6], kind="gelu",
                                 cols=(q * D, (q + 1) * D), evac="a", after=start if q < 2 else used[q - 2]))
        if q > 0:
            used.append(linear(net, pair(G[(q - 1) % 2], G[2 + (q - 1) % 2]), ins["L2_mix_fc2_w"], R, "add", add=R, rows=((q - 1) * D, q * D),
                               after=start + made[q - 1].ends() + added.ends(), stats=R if q == 4 else None).ends())
    X = tok(G[5])
    LayerNorm(net, R, X, 1e-5, ready=True)
    norm_T(net, X, tok(G[0]), XT, 1e-5, net.row(ins["L2_ffn_ln1_g"]), net.row(ins["L2_ffn_ln1_b"]))
    bias_out = AddRow(net, X, net.row(ins["L2_ffn_out_b"]))
    w = ins["L2_ffn_in_wT"]
    linear_T(net, XT, w, feat(G[0]), bias=col["in_b_c"][:, 0:6], cols=(0, D))
    linear_T(net, XT, w, feat(G[1]), bias=col["in_b_c"][:, 6:12], cols=(D, 2 * D))
    linear(net, XT, w, tok(G[2]), "row", bias=net.row(ins["L2_ffn_in_b"][:, 2 * D:3 * D]), cols=(2 * D, 3 * D))
    halves = [slice(64 * i, 64 * i + 64) for i in range(2)]
    qT, kT = feat(G[0]), feat(G[1])
    parts = [(qT[halves[h % 2], h // 2], kT[halves[h % 2], h // 2]) for h in range(12)]
    SoftmaxHeads(net, [(q, k, tok(G[2])[:, :, h // 2 * 128:(h // 2 + 1) * 128], halves[h % 2], Pair(q, k)) for h, (q, k) in enumerate(parts)],
                 [feat(b, NT, TP) for b in (G[3], net.P1)], feat(G[4], NT, TP), 0.125)
    linear(net, pair(G[0], G[1]), ins["L2_ffn_out_wT"], X, "add", add=X, after=now() + bias_out.ends())
    ToFeatures(net, X, pair(G[0], G[1]))
    bias_out = AddRow(net, X, net.row(ins["L2_ffn_mlp_b2"]))
    load = net.weights(ins["L2_ffn_mlp_w1"])
    hT = small(G[2], 2, 96)
    LinearT(net, pair(G[0], G[1]), [(load, 96 * k, 96, hT.chunk(k), col["mlp_b1_c"][:, k:k + 1], "gelu") for k in range(2)], "a")
    linear(net, hT, ins["L2_ffn_mlp_w2"], X, "add", add=X, kp=96, after=now() + bias_out.ends(), stats=X)
    Clear(net, logits, -1.0e38)
    norm_T(net, X, tok(G[0]), XT, 1e-5, net.row(ins["L2_ffn_ln2_g"]), net.row(ins["L2_ffn_ln2_b"]), ready=True)
    added = Add(net, R, R, X)
    start = now()
    router(net, XT, ins["L2_ffn_gate_wT"], logits[:, :, 0:4], net.row(ins["L2_ffn_gate_b"]))
    TopTwo(net, logits, gates, "top", sel)
    for e in range(4):
        GatedRows(net, R, gates[:, :, e], net.row(ins["L2_ffn_exp_b2"][e:e + 1, :]), now() + added.ends())

    def hidden2(e, after):
        hT = small(G[e % 2], 2, 96)
        load = net.weights(ins["L2_ffn_exp_w1"][e])
        return LinearT(net, XT, [(load, 96 * k, 96, hT.chunk(k), col["exp_b1_c"][:, 2 * e + k:2 * e + k + 1], "gelu") for k in range(2)], "a", after), hT

    expert_layers(net, XT, 4, hidden2, gates, R, ins["L2_ffn_exp_w2"], 96, start)

    XT = pair(net.XT, G[1])
    norm_T(net, R, tok(G[5]), XT, 1e-5, ready=True)
    bias2 = AddRow(net, R, net.row(ins["L3_gnn_b2"]))
    w = ins["L3_mix_W_qkv"]
    linear(net, XT, ins["L3_gnn_W1"], tok(G[0]), evac="a")
    marks = gat_coefs(net, [(tok(G[0]), 1)], D, ins["L3_gnn_att_src1"], ins["L3_gnn_att_dst1"], coef, G[2], now() + loops.ends())
    rest = gat_heads(net, [(tok(G[0]), 1)], D, coef, G[2], G[3], 0.0, [tok(G[1])], ins["L3_gnn_b1"], coefs=marks.ends())
    linear_T(net, XT, w, feat(G[4]), cols=(D, 2 * D), evac="a")
    rest()
    outT = pair(G[3], G[2])
    ToFeatures(net, tok(G[1]), outT, "relu")
    linear(net, outT, ins["L3_gnn_W2"], tok(G[0]), evac="a")
    marks = gat_coefs(net, [(tok(G[0]), 1)], D, ins["L3_gnn_att_src2"], ins["L3_gnn_att_dst2"], coef, G[2])
    rest = gat_heads(net, [(tok(G[0]), 1)], D, coef, G[2], G[3], 0.0, [R], add=R, coefs=marks.ends())
    ToFeatures(net, tok(G[5]), XT)
    rest(bias2.ends())
    Clear(net, net.fw)
    fws = [net.into(net.fn, ins["norms3"], now())]
    for s in range(2):
        fws.append(net.into(net.fw[64 * s:64 * s + 64, 256 * s:256 * s + 256], ins["L3_mix_rfT"], now()))
    wc = lambda m: net.fw[:, m * 128:(m + 1) * 128]
    nc_ = lambda m: net.fn[:, m * 128:(m + 1) * 128]
    v = heads65(G[0])
    ones = SetOnes(net, v, now())
    linear_heads(net, XT, w, (2 * D, 3 * D), by_head(v), evac="a")
    linear_T(net, XT, w, feat(G[2]), cols=(0, D))
    kv = net.kv[:, :].rearrange("p (c w) -> p c w", c=24)
    sqT = feat(net.XT)
    Square(net, feat(G[4]), sqT)
    for c in range(6):
        phik = G[3 - 2 * (c % 2)][:TP, 0:NT * 512].rearrange("p (t m) -> p t m", t=NT)
        PhiTok(net, feat(G[4]), sqT, [[(c, wc(m), nc_(m))] for m in range(4)], phik, net.lnc[:, 1:2], fws, now() + ones.ends())
        KvSummary(net, [(phik[:, :, m * 128:(m + 1) * 128], 2 * c + m // 2, 1, kv[:, 4 * c + m], 128) for m in range(4)], v)
    Square(net, feat(G[2]), sqT)
    for c in range(6):
        phiq = feat(G[3 - 2 * (c % 2)], 4)
        PhiFeat(net, feat(G[2]), sqT, [[(c, wc(m), nc_(m))] for m in range(4)], phiq, net.lnc[:, 1:2])
        KvApply(net, [[(2 * c + s, 1, tuple((phiq[:, 2 * s + m], kv[:, 4 * c + 2 * s + m]) for m in range(2))) for s in range(2)]], tok(G[4]), 1e-6)
    bias_out = AddRow(net, tok(G[5]), net.row(ins["L3_mix_b_proj"]))
    ToFeatures(net, tok(G[4]), pair(G[0], G[1]))
    linear(net, pair(G[0], G[1]), ins["L3_mix_W_proj"], tok(G[5]), "add", add=tok(G[5]), after=now() + bias_out.ends(), stats=tok(G[5]))
    start = now()
    norm = LayerNorm(net, tok(G[5]), tok(G[1]), 1e-5, net.row(ins["L3_mix_gamma"]), net.row(ins["L3_mix_beta"]), ready=True)
    added = Add(net, R, R, tok(G[1]), start, norm.tiles)
    XT = pair(net.XT, G[5])
    norm_T(net, R, tok(G[0]), XT, 1e-5, made=added.made)
    start = now()
    router(net, XT, ins["L3_ffn_Wg"], logits)
    TopTwo(net, logits, gates, "top", sel, first)
    Capacity(net, gates, sel, first, net.rows(ins["tri"]), int(1.2 * N / 8))

    def hidden3(e, after):
        hT = feat(G[e % 2], 3)
        load = net.weights(ins["L3_ffn_W1"][e])
        made = LinearT(net, XT, [(load, 0, 128, hT[:, 0], None, "copy"), (load, 128, 128, hT[:, 1], None, "silu")], "a", after)
        product = Multiply(net, hT[:, 0], hT[:, 1], made.ends())
        return Split(net, hT[:, 0:1], hT[:, 2:3], product.ends()), Pair(hT[:, 2:3], hT[:, 0:1])

    expert_layers(net, XT, 8, hidden3, gates, R, ins["L3_ffn_W2"], 128, start)


def pairs_of(phi, kv):
    return [[(2 * j, 2, ((phi[:, j], kv[:, j]),)) for j in range(3 * q, 3 * q + 3)] for q in range(2)]


def build(nc, ins, out):
    with ExitStack() as ctx:
        net = Net(nc, ctx, ins)
        network(net)
        block = ctx.enter_context(nc.Block())
        n_const = 16 * len(net.consts)

        @block.sync
        def _(sp):
            for dst, src in net.edges:
                sp.dma_start(dst, src).then_inc(net.edges_landed, 16)
            for dst, src in net.consts:
                sp.dma_start(dst, src).then_inc(net.const_landed, 16)
            for load in sorted(net.loads, key=lambda q: q.before.used_at if q.before else (-1, 0)):
                if isinstance(load, SlotExperts):
                    load.sync(sp)
                    continue
                if load.before:
                    for sem, value in load.before.used:
                        if value:
                            sp.wait_ge(sem, value)
                sp.dma_start(load.dst, load.src).then_inc(load.sem, 16)
            for sem, value in net.end():
                sp.wait_ge(sem, value)
            sp.dma_start(out.rearrange("(t p) d -> p t d", p=TP), net.tok(net.R)).then_inc(net.stored, 16)
            sp.wait_ge(net.stored, 16)

        @block.tensor
        def _(pe):
            for stage in net.stages:
                stage.tensor(pe)
                assert net.pe.issued <= net.pe.planned, stage

        @block.scalar
        def _(act):
            act.wait_ge(net.const_landed, n_const)
            for u in range(2):
                net.split_high(u, 0)
            for stage in net.stages:
                stage.scalar(act)

        @block.vector
        def _(dve):
            for stage in net.stages:
                assert net.dve.issued == stage.d0, stage
                stage.vector(dve)

        @block.gpsimd
        def _(pool):
            pool.wait_ge(net.const_landed, n_const)
            for u in range(2):
                net.split_low(u, 0)
            for stage in net.stages:
                stage.gpsimd(pool)

        for ticks in (net.pe, net.act, net.dve, net.pool):
            assert ticks.issued == ticks.planned, (ticks.sem, ticks.issued, ticks.planned)


_TURNED = {"L0_mix_w_mapT": "L0_mix_w_map", "L0_mix_w_outT": "L0_mix_w_out", "L1_mix_kqv_wT": "L1_mix_kqv_w", "L1_mix_proj_wT": "L1_mix_proj_w",
           "L1_ffn_router_wT": "L1_ffn_router_w", "L2_gnn_W1T": "L2_gnn_W1", "L2_gnn_W2T": "L2_gnn_W2", "L2_ffn_in_wT": "L2_ffn_in_w",
           "L2_ffn_out_wT": "L2_ffn_out_w", "L2_ffn_gate_wT": "L2_ffn_gate_w", "L3_mix_rfT": "L3_mix_random_features"}
_ROWS = ["L0_gnn_a_src0", "L0_gnn_a_dst0", "L0_gnn_b0", "L0_gnn_a_src1", "L0_gnn_a_dst1", "L0_gnn_b1", "L0_gnn_a_src2", "L0_gnn_a_dst2", "L0_gnn_b2",
         "L0_gnn_b_out", "L0_mix_g_k", "L0_mix_b_k", "L0_mix_g_v", "L0_mix_b_v", "L0_mix_b_out", "L1_gnn_b", "L1_mix_proj_b",
         "L2_gnn_att_src1", "L2_gnn_att_dst1", "L2_gnn_b1", "L2_gnn_att_src2", "L2_gnn_att_dst2", "L2_gnn_b2", "L2_mix_qkv_b", "L2_mix_proj_b",
         "L2_mix_fc2_b", "L2_mix_ln1_w", "L2_mix_ln1_b", "L2_mix_ln2_w", "L2_mix_ln2_b", "L2_ffn_ln1_g", "L2_ffn_ln1_b", "L2_ffn_in_b",
         "L2_ffn_out_b", "L2_ffn_mlp_b2", "L2_ffn_ln2_g", "L2_ffn_ln2_b", "L2_ffn_gate_b", "L3_gnn_att_src1", "L3_gnn_att_dst1", "L3_gnn_b1",
         "L3_gnn_att_src2", "L3_gnn_att_dst2", "L3_gnn_b2", "L3_mix_b_proj", "L3_mix_gamma", "L3_mix_beta"]
_PLAIN = ["x", "src", "dst", "L0_gnn_W_ah", "L0_gnn_W0", "L0_gnn_W1", "L0_gnn_W2", "L0_gnn_W_out", "L0_ffn_w1", "L0_ffn_b1", "L0_ffn_w2",
          "L0_ffn_b2", "L1_gnn_W", "L1_ffn_w1", "L1_ffn_w2", "L2_mix_qkv_w", "L2_mix_proj_w", "L2_mix_fc1_w", "L2_mix_fc2_w", "L2_ffn_mlp_w1",
          "L2_ffn_mlp_w2", "L2_ffn_exp_w1", "L2_ffn_exp_w2", "L2_ffn_exp_b2", "L3_gnn_W1", "L3_gnn_W2", "L3_mix_W_qkv", "L3_mix_W_proj",
          "L3_ffn_Wg", "L3_ffn_W1", "L3_ffn_W2"]


def kernel(**inputs):
    import math

    import numpy as np
    import concourse.bacc as bacc
    from concourse.bass_utils import run_bass_kernel_spmd

    lay = np.ascontiguousarray
    a = {name: np.asarray(v) for name, v in inputs.items()}
    columns = lambda v, p: lay(v.reshape(-1, p).T)
    arrays = {n: lay(a[n]) for n in _PLAIN}
    arrays.update({n: lay(a[o].T) for n, o in _TURNED.items()})
    arrays.update({n: lay(a[n].reshape(1, -1)) for n in _ROWS})
    arrays["L0_ffn_scale"] = lay(a["L0_ffn_scale"].reshape(1, 1))
    arrays["L0_ffn_phi"] = lay(a["L0_ffn_phi"].reshape(D, 64))
    arrays["L1_mix_wT"] = lay(a["L1_mix_w"].transpose(0, 2, 1))
    arrays["L1_mix_kqv_b_v"] = lay(a["L1_mix_kqv_b"][2 * D:].reshape(1, -1))
    arrays["b_ah_c"] = columns(a["L0_gnn_b_ah"], 128)
    arrays["kqv_b_c"] = columns(a["L1_mix_kqv_b"][:2 * D], 128)
    arrays["qkv_b_c"] = columns(a["L2_mix_qkv_b"][:D], 128)
    arrays["fc1_b_c"] = columns(a["L2_mix_fc1_b"], 128)
    arrays["in_b_c"] = columns(a["L2_ffn_in_b"][:2 * D], 128)
    arrays["mlp_b1_c"] = columns(a["L2_ffn_mlp_b1"], 96)
    arrays["exp_b1_c"] = columns(a["L2_ffn_exp_b1"], 96)
    arrays["ident"] = np.eye(128, dtype=np.float32)
    arrays["iota"] = np.arange(N, dtype=np.float32).reshape(1, N)
    arrays["tri"] = np.triu(np.ones((128, 128), np.float32))
    arrays["lnc"] = np.tile(np.array([[-0.5 * math.log(32.0), -0.5 * math.log(256.0)]], np.float32), (128, 1))
    norms1 = np.zeros((128, 2, 128), np.float32)
    norms3 = np.zeros((128, 512), np.float32)
    for s in range(2):
        norms3[64 * s:64 * s + 64, 256 * s:256 * s + 256] = -0.5
        for i in range(2):
            norms1[64 * s:64 * s + 64, i, 64 * i + 32 * s:64 * i + 32 * s + 32] = -0.5
    arrays["norms1"], arrays["norms3"] = norms1.reshape(128, 256), norms3

    nc = bacc.Bacc("TRN2", target_bir_lowering=False, num_devices=1)
    ins = {n: nc.dram_tensor(f"in_{n}", v.shape, mybir.dt.from_np(v.dtype), kind="ExternalInput").ap() for n, v in arrays.items()}
    out = nc.dram_tensor("out", (N, D), F32, kind="ExternalOutput").ap()
    build(nc, ins, out)
    r = run_bass_kernel_spmd(nc, [{f"in_{n}": v for n, v in arrays.items()}], core_ids=[0])
    return r.results[0]["out"]
```
